# Optimizing a Trainium2 kernel written in Bass

```python
import numpy as np
import jax
import jax.numpy as jnp

def _softmax(x, axis=-1):
    return jax.nn.softmax(x, axis=axis)

def _gelu(x):
    return jax.nn.gelu(x, approximate=True)

def _silu(x):
    return jax.nn.silu(x)

def _sigmoid(x):
    return jax.nn.sigmoid(x)

def _layernorm(x, axis=-1, eps=1e-05):
    m = jnp.mean(x, axis=axis, keepdims=True)
    v = jnp.var(x, axis=axis, keepdims=True)
    return (x - m) / jnp.sqrt(v + eps)

def _scatter_add(tgt, idx, src, axis=0):
    return tgt.at[idx].add(src)

def _segment_sum(src, seg, n):
    return jax.ops.segment_sum(src, seg, n)
kernel_name = 'mk_perceiver_d4_seqx_r4_7e44f1'

def setup_inputs(seed: int=0):
    np.random.seed(seed)
    _w = jnp.asarray

    def _rec_inputs():
        import jax
        import jax.numpy as jnp
        _rk = jax.random.key(seed)
        x = 7.22e-05 + 1 * jax.random.normal(jax.random.fold_in(_rk, 1), (4, 256, 256), jnp.float32)
        _lenS = 256 - jax.random.randint(jax.random.fold_in(_rk, 7), (4,), 0, max(1, 256 // 4) + 1, jnp.int32)
        _lenS2 = 4096 - jax.random.randint(jax.random.fold_in(_rk, 8), (4,), 0, max(1, 4096 // 4) + 1, jnp.int32)
        _ctx_1024P = jax.random.normal(jax.random.fold_in(_rk, 11), (4, 16, 256), jnp.float32)
        _ctx_1024c = jax.random.dirichlet(jax.random.fold_in(_rk, 511), 0.3 * jnp.ones((16,), jnp.float32), (4, 4096))
        _ctx_1024t = jnp.einsum('bsk,bkd->bsd', _ctx_1024c, _ctx_1024P)
        _ctx_1024t = _ctx_1024t * jax.lax.rsqrt(jnp.mean(jnp.square(_ctx_1024t)) + 1e-12) * 0.953939
        ctx_1024 = -0.000107592 + 0.9999 * (_ctx_1024t + 0.3 * jax.random.normal(jax.random.fold_in(_rk, 611), (4, 4096, 256), jnp.float32))
        return (x, ctx_1024)
    x, ctx_1024 = _rec_inputs()

    def _L0_xattn_setup():
        import jax, jax.numpy as jnp
        import numpy as np
        DIM = 256
        N_HEADS = 16
        HEAD_DIM = DIM // N_HEADS
        EPS = 1e-06
        Q_THETA = 32.0
        K_THETA = 1000.0

        def precompute_freqs_1d(dim, seq_len, theta):
            freqs = theta ** (-jnp.arange(0, dim, 2, dtype=jnp.float32) / dim)
            t = jnp.arange(seq_len, dtype=jnp.float32)
            ang = t[:, None] * freqs[None, :]
            return (jnp.cos(ang), jnp.sin(ang))

        def rms_norm(x, w):
            var = jnp.mean(x * x, axis=-1, keepdims=True)
            return x * jax.lax.rsqrt(var + EPS) * w

        def apply_rope(t, cos, sin):
            cos = cos[None, None, :, :]
            sin = sin[None, None, :, :]
            t1, t2 = jnp.split(t, 2, axis=-1)
            return jnp.concatenate([t1 * cos - t2 * sin, t2 * cos + t1 * sin], axis=-1)
        key = jax.random.key(seed)
        ks = jax.random.split(key, 8)
        B, T, S = (128, 64, 96)
        s = 1.0 / np.sqrt(DIM)
        return {'x': jax.random.normal(ks[0], (B, T, DIM), jnp.float32), 'context': jax.random.normal(ks[1], (B, S, DIM), jnp.float32), 'Wq': jax.random.normal(ks[2], (DIM, DIM), jnp.float32) * s, 'Wk': jax.random.normal(ks[3], (DIM, DIM), jnp.float32) * s, 'Wv': jax.random.normal(ks[4], (DIM, DIM), jnp.float32) * s, 'Wo': jax.random.normal(ks[5], (DIM, DIM), jnp.float32) * s, 'q_norm_w': jnp.ones((HEAD_DIM,), jnp.float32), 'k_norm_w': jnp.ones((HEAD_DIM,), jnp.float32)}
    _L0_xattn_all = _L0_xattn_setup()
    _L0_xattn_in = {k: v for k, v in _L0_xattn_all.items() if k in ('Wq', 'Wk', 'Wv', 'Wo', 'q_norm_w', 'k_norm_w')}
    del _L0_xattn_all

    def _L0_attn_setup():
        import jax, jax.numpy as jnp
        import numpy as np
        D_MODEL = 256
        N_HEAD = 16
        HEAD_SIZE = D_MODEL // N_HEAD
        LAYER_ID = 12
        N_LAYER = 24
        HEAD_SIZE_DIVISOR = 8
        TM_DIM = 32
        TD_DIM = 64
        B, T = (4, 256)
        EPS = 1e-05 * HEAD_SIZE_DIVISOR ** 2

        def _wkv6(r, k, v, w, u):
            Bc, Tc, H, K = r.shape
            wdec = jnp.exp(-jnp.exp(w))

            def step(S, inp):
                r_t, k_t, v_t, wd_t = inp
                kv = k_t[:, :, :, None] * v_t[:, :, None, :]
                y = jnp.einsum('bhk,bhkj->bhj', r_t, S + u[None, :, :, None] * kv)
                S = S * wd_t[:, :, :, None] + kv
                return (S, y)
            S0 = jnp.zeros((Bc, H, K, K), r.dtype)
            xs = (jnp.swapaxes(r, 0, 1), jnp.swapaxes(k, 0, 1), jnp.swapaxes(v, 0, 1), jnp.swapaxes(wdec, 0, 1))
            _, ys = jax.lax.scan(step, S0, xs)
            return jnp.swapaxes(ys, 0, 1).reshape(Bc, Tc, H * K)
        key = jax.random.key(seed)
        ks = jax.random.split(key, 12)
        C = D_MODEL
        r0 = LAYER_ID / (N_LAYER - 1)
        r1 = 1.0 - LAYER_ID / N_LAYER
        ddd = np.arange(C, dtype=np.float64) / C
        time_maa_x = (1.0 - ddd ** r1).astype(np.float32)
        time_maa_w = (1.0 - ddd ** r1).astype(np.float32)
        time_maa_k = (1.0 - ddd ** r1).astype(np.float32)
        time_maa_v = (1.0 - (ddd ** r1 + 0.3 * r0)).astype(np.float32)
        time_maa_r = (1.0 - ddd ** (0.5 * r1)).astype(np.float32)
        time_maa_g = (1.0 - ddd ** (0.5 * r1)).astype(np.float32)
        n = np.arange(C, dtype=np.float64)
        time_decay = (-6.0 + 5.0 * (n / (C - 1)) ** (0.7 + 1.3 * r0)).astype(np.float32)
        zig = ((n + 1) % 3 - 1) * 0.1
        time_faaaa = (r0 * (1 - n / (C - 1)) + zig).astype(np.float32).reshape(N_HEAD, HEAD_SIZE)
        s = 1.0 / np.sqrt(C)
        inp = {'x': jax.random.normal(ks[0], (B, T, C), jnp.float32), 'time_maa_x': jnp.asarray(time_maa_x), 'time_maa_w': jnp.asarray(time_maa_w), 'time_maa_k': jnp.asarray(time_maa_k), 'time_maa_v': jnp.asarray(time_maa_v), 'time_maa_r': jnp.asarray(time_maa_r), 'time_maa_g': jnp.asarray(time_maa_g), 'time_maa_w1': jax.random.uniform(ks[1], (C, TM_DIM * 5), jnp.float32, -0.01, 0.01), 'time_maa_w2': jax.random.uniform(ks[2], (5, TM_DIM, C), jnp.float32, -0.01, 0.01), 'time_decay': jnp.asarray(time_decay), 'time_decay_w1': jax.random.uniform(ks[3], (C, TD_DIM), jnp.float32, -0.01, 0.01), 'time_decay_w2': jax.random.uniform(ks[4], (TD_DIM, C), jnp.float32, -0.01, 0.01), 'time_faaaa': jnp.asarray(time_faaaa), 'W_r': jax.random.normal(ks[5], (C, C), jnp.float32) * s, 'W_k': jax.random.normal(ks[6], (C, C), jnp.float32) * s, 'W_v': jax.random.normal(ks[7], (C, C), jnp.float32) * s, 'W_g': jax.random.normal(ks[8], (C, C), jnp.float32) * s, 'W_o': jax.random.normal(ks[9], (C, C), jnp.float32) * s, 'ln_gamma': jnp.ones((C,), jnp.float32), 'ln_beta': jnp.zeros((C,), jnp.float32)}
        return inp
    _L0_attn_all = _L0_attn_setup()
    _L0_attn_in = {k: v for k, v in _L0_attn_all.items() if k in ('time_maa_x', 'time_maa_w', 'time_maa_k', 'time_maa_v', 'time_maa_r', 'time_maa_g', 'time_maa_w1', 'time_maa_w2', 'time_decay', 'time_decay_w1', 'time_decay_w2', 'time_faaaa', 'W_r', 'W_k', 'W_v', 'W_g', 'W_o', 'ln_gamma', 'ln_beta')}
    del _L0_attn_all

    def _L0_ffn_setup():
        import jax, jax.numpy as jnp
        import numpy as np
        TOP_K = 8
        key = jax.random.key(seed)
        k1, k2, k3, k4, k5 = jax.random.split(key, 5)
        B, S, D, F, E = (2, 512, 256, 192, 64)
        return {'hidden_states': jax.random.normal(k1, (B, S, D), dtype=jnp.float32), 'gate_w': jax.random.normal(k2, (E, D), dtype=jnp.float32) * 0.02, 'w_gate': jax.random.normal(k3, (E, F, D), dtype=jnp.float32) * 0.02, 'w_up': jax.random.normal(k4, (E, F, D), dtype=jnp.float32) * 0.02, 'w_down': jax.random.normal(k5, (E, D, F), dtype=jnp.float32) * 0.02}
    _L0_ffn_all = _L0_ffn_setup()
    _L0_ffn_in = {k: v for k, v in _L0_ffn_all.items() if k in ('gate_w', 'w_gate', 'w_up', 'w_down')}
    del _L0_ffn_all

    def _L1_xattn_setup():
        import jax, jax.numpy as jnp
        import numpy as np
        E = 256
        H = 16
        D = E // H
        NUM_BUCKETS = 32
        MAX_DISTANCE = 128

        def _relative_position_bucket(rel, num_buckets=NUM_BUCKETS, max_distance=MAX_DISTANCE):
            nb = num_buckets // 2
            buckets = (rel > 0).astype(jnp.int32) * nb
            rel = jnp.abs(rel)
            max_exact = nb // 2
            is_small = rel < max_exact
            rel_f = jnp.maximum(rel, 1).astype(jnp.float32)
            large = max_exact + (jnp.log(rel_f / max_exact) / np.log(max_distance / max_exact) * (nb - max_exact)).astype(jnp.int32)
            large = jnp.minimum(large, nb - 1)
            return buckets + jnp.where(is_small, rel, large)
        key = jax.random.key(seed)
        ks = jax.random.split(key, 6)
        B, S, K = (2, 512, 512)
        w = 0.02
        return {'hidden_states': jax.random.normal(ks[0], (B, S, E), jnp.float32), 'key_value_states': jax.random.normal(ks[1], (B, K, E), jnp.float32), 'Wq': jax.random.normal(ks[2], (E, E), jnp.float32) * w, 'Wkv': jax.random.normal(ks[3], (E, 2 * E), jnp.float32) * w, 'Wo': jax.random.normal(ks[4], (E, E), jnp.float32) * w, 'rel_bias': jax.random.normal(ks[5], (NUM_BUCKETS, H), jnp.float32) * w}
    _L1_xattn_all = _L1_xattn_setup()
    _L1_xattn_in = {k: v for k, v in _L1_xattn_all.items() if k in ('Wq', 'Wkv', 'Wo', 'rel_bias')}
    del _L1_xattn_all

    def _L1_attn_setup():
        import jax, jax.numpy as jnp
        import numpy as np
        B, L, D = (4, 512, 256)
        E, F, H = (6, 384, 128)
        TOP_K = 2
        LN_EPS = 1e-05
        key = jax.random.key(seed)
        ks = jax.random.split(key, 8)
        s = lambda fan: 1.0 / np.sqrt(fan)
        return {'x': jax.random.normal(ks[0], (B, L, D), jnp.float32), 'r1_w': jax.random.normal(ks[1], (D, H), jnp.float32) * s(D), 'r1_b': jnp.zeros((H,), jnp.float32), 'ln_g': jnp.ones((H,), jnp.float32), 'ln_b': jnp.zeros((H,), jnp.float32), 'r2_w': jax.random.normal(ks[2], (H, E), jnp.float32) * s(H), 'r2_b': jnp.zeros((E,), jnp.float32), 'temp': jnp.ones((1,), jnp.float32), 'route_bias': jnp.zeros((E,), jnp.float32), 'W1': jax.random.normal(ks[3], (E, D, F), jnp.float32) * s(D), 'b1': jnp.zeros((E, F), jnp.float32), 'W2': jax.random.normal(ks[4], (E, F, D), jnp.float32) * s(F), 'b2': jnp.zeros((E, D), jnp.float32)}
    _L1_attn_all = _L1_attn_setup()
    _L1_attn_in = {k: v for k, v in _L1_attn_all.items() if k in ('r1_w', 'r1_b', 'ln_g', 'ln_b', 'r2_w', 'r2_b', 'temp', 'route_bias', 'W1', 'b1', 'W2', 'b2')}
    del _L1_attn_all

    def _L1_ffn_setup():
        import jax, jax.numpy as jnp
        import numpy as np
        TOPK = 4
        N_GROUPS = 4
        TOPK_GROUPS = 2
        ROUTE_SCALE = 2.5

        def _gate(x2, Wg):
            T = x2.shape[0]
            E = Wg.shape[0]
            scores = x2 @ Wg.T
            s = jax.nn.sigmoid(scores)
            g = s.reshape(T, N_GROUPS, E // N_GROUPS)
            group_scores = g.max(axis=-1)
            _, gidx = jax.lax.top_k(group_scores, TOPK_GROUPS)
            group_mask = jnp.any(jax.nn.one_hot(gidx, N_GROUPS, dtype=jnp.bool_), axis=1)
            masked = jnp.where(group_mask[:, :, None], g, -jnp.inf).reshape(T, E)
            _, idx = jax.lax.top_k(masked, TOPK)
            w = jnp.take_along_axis(s, idx, axis=1)
            w = w / jnp.sum(w, axis=-1, keepdims=True)
            w = w * ROUTE_SCALE
            return (w.astype(x2.dtype), idx)
        key = jax.random.key(seed)
        ks = jax.random.split(key, 6)
        B, S, D, I, E = (2, 512, 256, 256, 16)
        scale = 0.02
        return {'x': jax.random.normal(ks[0], (B, S, D), dtype=jnp.float32), 'Wg': jax.random.normal(ks[1], (E, D), dtype=jnp.float32) * scale, 'W1': jax.random.normal(ks[2], (E, I, D), dtype=jnp.float32) * scale, 'b1': jnp.zeros((E, I), dtype=jnp.float32), 'W2': jax.random.normal(ks[3], (E, D, I), dtype=jnp.float32) * scale, 'b2': jnp.zeros((E, D), dtype=jnp.float32), 'W3': jax.random.normal(ks[4], (E, I, D), dtype=jnp.float32) * scale, 'b3': jnp.zeros((E, I), dtype=jnp.float32)}
    _L1_ffn_all = _L1_ffn_setup()
    _L1_ffn_in = {k: v for k, v in _L1_ffn_all.items() if k in ('Wg', 'W1', 'b1', 'W2', 'b2', 'W3', 'b3')}
    del _L1_ffn_all

    def _L2_xattn_setup():
        import jax, jax.numpy as jnp
        import numpy as np
        B, N, L, D, H = (8, 128, 1024, 256, 16)
        key = jax.random.key(seed)
        ks = jax.random.split(key, 7)
        s = 1.0 / np.sqrt(D)
        return {'q': jax.random.normal(ks[0], (B, N, D), dtype=jnp.float32), 'k': jax.random.normal(ks[1], (B, L, D), dtype=jnp.float32), 'v': jax.random.normal(ks[2], (B, L, D), dtype=jnp.float32), 'Wq': jax.random.normal(ks[3], (D, D), dtype=jnp.float32) * s, 'Wk': jax.random.normal(ks[4], (D, D), dtype=jnp.float32) * s, 'Wv': jax.random.normal(ks[5], (D, D), dtype=jnp.float32) * s, 'Wo': jax.random.normal(ks[6], (D, D), dtype=jnp.float32) * s}
    _L2_xattn_all = _L2_xattn_setup()
    _L2_xattn_in = {k: v for k, v in _L2_xattn_all.items() if k in ('Wq', 'Wk', 'Wv', 'Wo')}
    del _L2_xattn_all

    def _L2_attn_setup():
        import jax, jax.numpy as jnp
        import numpy as np
        B, T, D = (1, 1024, 256)
        H, KD, VD = (16, 64, 64)
        MIN_THETA, MAX_THETA = (1.0, 10000.0)

        def _sin_cos(t, d, dtype):
            half = d // 2
            p = jnp.arange(half, dtype=dtype) / (half - 1)
            thetas = MIN_THETA * (MAX_THETA / MIN_THETA) ** p
            pos = jnp.arange(t, dtype=dtype)[:, None] / thetas[None, :]
            return (jnp.sin(pos), jnp.cos(pos))

        def _rope(x, sin, cos):
            d = x.shape[-1] // 2
            x_hi, x_lo = (x[..., :d], x[..., d:])
            y_lo = x_lo * cos + x_hi * sin
            y_hi = x_hi * cos - x_lo * sin
            return jnp.concatenate([y_lo, y_hi], axis=-1)
        key = jax.random.key(seed)
        k0, k1, k2 = jax.random.split(key, 3)
        x = jax.random.normal(k0, (B, T, D), dtype=jnp.float32)
        W_in = jax.random.normal(k1, ((2 * KD + VD) * H, D), dtype=jnp.float32) * 0.02
        b_in = jnp.zeros(((2 * KD + VD) * H,), dtype=jnp.float32)
        W_out = jax.random.normal(k2, (D, H * VD), dtype=jnp.float32) * 0.02
        b_out = jnp.zeros((D,), dtype=jnp.float32)
        return {'x': x, 'W_in': W_in, 'b_in': b_in, 'W_out': W_out, 'b_out': b_out}
    _L2_attn_all = _L2_attn_setup()
    _L2_attn_in = {k: v for k, v in _L2_attn_all.items() if k in ('W_in', 'b_in', 'W_out', 'b_out')}
    del _L2_attn_all

    def _L2_ffn_setup():
        import jax, jax.numpy as jnp
        import numpy as np
        H = 32
        MB = 2
        TOP_K = 2
        key = jax.random.key(seed)
        ks = jax.random.split(key, 8)
        B, S, D, E = (8, 256, 256, 8)
        Fd = 4 * D

        def w(k, shape, fan):
            return jax.random.normal(k, shape, jnp.float32) / np.float32(np.sqrt(fan))
        return dict(x=jax.random.normal(ks[0], (B, S, D), jnp.float32), ln_g=jnp.ones((D,), jnp.float32), ln_b=jnp.zeros((D,), jnp.float32), wq=w(ks[1], (D, D), D), wk=w(ks[2], (D, D), D), wv=w(ks[3], (D, D), D), wo=w(ks[4], (D, D), D), gate_w=w(ks[5], (E, D), D), w1=w(ks[6], (E, D, Fd), D), b1=jnp.zeros((E, Fd), jnp.float32), w2=w(ks[7], (E, Fd, D), Fd), b2=jnp.zeros((E, D), jnp.float32))
    _L2_ffn_all = _L2_ffn_setup()
    _L2_ffn_in = {k: v for k, v in _L2_ffn_all.items() if k in ('ln_g', 'ln_b', 'wq', 'wk', 'wv', 'wo', 'gate_w', 'w1', 'b1', 'w2', 'b2')}
    del _L2_ffn_all

    def _L3_xattn_setup():
        import jax, jax.numpy as jnp
        import numpy as np
        B, T, C, H = (4, 1024, 256, 16)
        D = C // H

        def _heads(t):
            b, n, c = t.shape
            return t.reshape(b, n, H, D).transpose(0, 2, 1, 3)
        key = jax.random.key(seed)
        ks = jax.random.split(key, 10)
        s = 1.0 / np.sqrt(C)
        return {'x': jax.random.normal(ks[0], (B, T, C), jnp.float32), 'y': jax.random.normal(ks[1], (B, T, C), jnp.float32), 'Wq': jax.random.normal(ks[2], (C, C), jnp.float32) * s, 'bq': jnp.zeros((C,), jnp.float32), 'Wk': jax.random.normal(ks[3], (C, C), jnp.float32) * s, 'bk': jnp.zeros((C,), jnp.float32), 'Wv': jax.random.normal(ks[4], (C, C), jnp.float32) * s, 'bv': jnp.zeros((C,), jnp.float32), 'Wp': jax.random.normal(ks[5], (C, C), jnp.float32) * s, 'bp': jnp.zeros((C,), jnp.float32)}
    _L3_xattn_all = _L3_xattn_setup()
    _L3_xattn_in = {k: v for k, v in _L3_xattn_all.items() if k in ('Wq', 'bq', 'Wk', 'bk', 'Wv', 'bv', 'Wp', 'bp')}
    del _L3_xattn_all

    def _L3_attn_setup():
        import jax, jax.numpy as jnp
        import numpy as np
        B_SZ, T, D_IN, H = (8, 256, 256, 256)
        key = jax.random.key(seed)
        ks = jax.random.split(key, 9)
        lim_u = 1.0 / np.sqrt(D_IN)
        return {'x': jax.random.normal(ks[0], (B_SZ, T, D_IN), dtype=jnp.float32), 'W_u': jax.random.uniform(ks[1], (H, D_IN), jnp.float32, -lim_u, lim_u), 'b_u': jax.random.uniform(ks[2], (H,), jnp.float32, -lim_u, lim_u), 'W_g': jax.random.uniform(ks[3], (H, D_IN), jnp.float32, -lim_u, lim_u), 'b_g': jax.random.uniform(ks[4], (H,), jnp.float32, -lim_u, lim_u), 'A': jnp.eye(H, dtype=jnp.float32) * 0.6, 'Bm': jax.random.normal(ks[5], (H, H), dtype=jnp.float32), 'Cm': jax.random.normal(ks[6], (H, H), dtype=jnp.float32), 'D': jax.random.normal(ks[7], (H,), dtype=jnp.float32)}
    _L3_attn_all = _L3_attn_setup()
    _L3_attn_in = {k: v for k, v in _L3_attn_all.items() if k in ('W_u', 'b_u', 'W_g', 'b_g', 'A', 'Bm', 'Cm', 'D')}
    del _L3_attn_all

    def _L3_ffn_setup():
        import jax, jax.numpy as jnp
        import numpy as np
        LORA_DIM = 16
        LORA_TOKEN_INDEX = 1
        B, S, D, H = (4, 512, 256, 1024)
        key = jax.random.key(seed)
        ks = jax.random.split(key, 6)
        x = jax.random.normal(ks[0], (B, S, D), dtype=jnp.float32)
        W1 = jax.random.normal(ks[1], (H, D), dtype=jnp.float32) * 0.02
        b1 = jnp.zeros((H,), dtype=jnp.float32)
        W2 = jax.random.normal(ks[2], (D, H), dtype=jnp.float32) * 0.02
        b2 = jnp.zeros((D,), dtype=jnp.float32)
        scale = jnp.asarray(0.001, dtype=jnp.float32)
        return {'x': x, 'W1': W1, 'b1': b1, 'W2': W2, 'b2': b2, 'scale': scale}
    _L3_ffn_all = _L3_ffn_setup()
    _L3_ffn_in = {k: v for k, v in _L3_ffn_all.items() if k in ('W1', 'b1', 'W2', 'b2', 'scale')}
    del _L3_ffn_all
    return {'x': x, 'ctx_1024': ctx_1024, 'L0_xattn_Wq': _L0_xattn_in['Wq'], 'L0_xattn_Wk': _L0_xattn_in['Wk'], 'L0_xattn_Wv': _L0_xattn_in['Wv'], 'L0_xattn_Wo': _L0_xattn_in['Wo'], 'L0_xattn_q_norm_w': _L0_xattn_in['q_norm_w'], 'L0_xattn_k_norm_w': _L0_xattn_in['k_norm_w'], 'L0_attn_time_maa_x': _L0_attn_in['time_maa_x'], 'L0_attn_time_maa_w': _L0_attn_in['time_maa_w'], 'L0_attn_time_maa_k': _L0_attn_in['time_maa_k'], 'L0_attn_time_maa_v': _L0_attn_in['time_maa_v'], 'L0_attn_time_maa_r': _L0_attn_in['time_maa_r'], 'L0_attn_time_maa_g': _L0_attn_in['time_maa_g'], 'L0_attn_time_maa_w1': _L0_attn_in['time_maa_w1'], 'L0_attn_time_maa_w2': _L0_attn_in['time_maa_w2'], 'L0_attn_time_decay': _L0_attn_in['time_decay'], 'L0_attn_time_decay_w1': _L0_attn_in['time_decay_w1'], 'L0_attn_time_decay_w2': _L0_attn_in['time_decay_w2'], 'L0_attn_time_faaaa': _L0_attn_in['time_faaaa'], 'L0_attn_W_r': _L0_attn_in['W_r'], 'L0_attn_W_k': _L0_attn_in['W_k'], 'L0_attn_W_v': _L0_attn_in['W_v'], 'L0_attn_W_g': _L0_attn_in['W_g'], 'L0_attn_W_o': _L0_attn_in['W_o'], 'L0_attn_ln_gamma': _L0_attn_in['ln_gamma'], 'L0_attn_ln_beta': _L0_attn_in['ln_beta'], 'L0_ffn_gate_w': _L0_ffn_in['gate_w'], 'L0_ffn_w_gate': _L0_ffn_in['w_gate'], 'L0_ffn_w_up': _L0_ffn_in['w_up'], 'L0_ffn_w_down': _L0_ffn_in['w_down'], 'L1_xattn_Wq': _L1_xattn_in['Wq'], 'L1_xattn_Wkv': _L1_xattn_in['Wkv'], 'L1_xattn_Wo': _L1_xattn_in['Wo'], 'L1_xattn_rel_bias': _L1_xattn_in['rel_bias'], 'L1_attn_r1_w': _L1_attn_in['r1_w'], 'L1_attn_r1_b': _L1_attn_in['r1_b'], 'L1_attn_ln_g': _L1_attn_in['ln_g'], 'L1_attn_ln_b': _L1_attn_in['ln_b'], 'L1_attn_r2_w': _L1_attn_in['r2_w'], 'L1_attn_r2_b': _L1_attn_in['r2_b'], 'L1_attn_temp': _L1_attn_in['temp'], 'L1_attn_route_bias': _L1_attn_in['route_bias'], 'L1_attn_W1': _L1_attn_in['W1'], 'L1_attn_b1': _L1_attn_in['b1'], 'L1_attn_W2': _L1_attn_in['W2'], 'L1_attn_b2': _L1_attn_in['b2'], 'L1_ffn_Wg': _L1_ffn_in['Wg'], 'L1_ffn_W1': _L1_ffn_in['W1'], 'L1_ffn_b1': _L1_ffn_in['b1'], 'L1_ffn_W2': _L1_ffn_in['W2'], 'L1_ffn_b2': _L1_ffn_in['b2'], 'L1_ffn_W3': _L1_ffn_in['W3'], 'L1_ffn_b3': _L1_ffn_in['b3'], 'L2_xattn_Wq': _L2_xattn_in['Wq'], 'L2_xattn_Wk': _L2_xattn_in['Wk'], 'L2_xattn_Wv': _L2_xattn_in['Wv'], 'L2_xattn_Wo': _L2_xattn_in['Wo'], 'L2_attn_W_in': _L2_attn_in['W_in'], 'L2_attn_b_in': _L2_attn_in['b_in'], 'L2_attn_W_out': _L2_attn_in['W_out'], 'L2_attn_b_out': _L2_attn_in['b_out'], 'L2_ffn_ln_g': _L2_ffn_in['ln_g'], 'L2_ffn_ln_b': _L2_ffn_in['ln_b'], 'L2_ffn_wq': _L2_ffn_in['wq'], 'L2_ffn_wk': _L2_ffn_in['wk'], 'L2_ffn_wv': _L2_ffn_in['wv'], 'L2_ffn_wo': _L2_ffn_in['wo'], 'L2_ffn_gate_w': _L2_ffn_in['gate_w'], 'L2_ffn_w1': _L2_ffn_in['w1'], 'L2_ffn_b1': _L2_ffn_in['b1'], 'L2_ffn_w2': _L2_ffn_in['w2'], 'L2_ffn_b2': _L2_ffn_in['b2'], 'L3_xattn_Wq': _L3_xattn_in['Wq'], 'L3_xattn_bq': _L3_xattn_in['bq'], 'L3_xattn_Wk': _L3_xattn_in['Wk'], 'L3_xattn_bk': _L3_xattn_in['bk'], 'L3_xattn_Wv': _L3_xattn_in['Wv'], 'L3_xattn_bv': _L3_xattn_in['bv'], 'L3_xattn_Wp': _L3_xattn_in['Wp'], 'L3_xattn_bp': _L3_xattn_in['bp'], 'L3_attn_W_u': _L3_attn_in['W_u'], 'L3_attn_b_u': _L3_attn_in['b_u'], 'L3_attn_W_g': _L3_attn_in['W_g'], 'L3_attn_b_g': _L3_attn_in['b_g'], 'L3_attn_A': _L3_attn_in['A'], 'L3_attn_Bm': _L3_attn_in['Bm'], 'L3_attn_Cm': _L3_attn_in['Cm'], 'L3_attn_D': _L3_attn_in['D'], 'L3_ffn_W1': _L3_ffn_in['W1'], 'L3_ffn_b1': _L3_ffn_in['b1'], 'L3_ffn_W2': _L3_ffn_in['W2'], 'L3_ffn_b2': _L3_ffn_in['b2'], 'L3_ffn_scale': _L3_ffn_in['scale']}

def reference(x, ctx_1024, L0_xattn_Wq, L0_xattn_Wk, L0_xattn_Wv, L0_xattn_Wo, L0_xattn_q_norm_w, L0_xattn_k_norm_w, L0_attn_time_maa_x, L0_attn_time_maa_w, L0_attn_time_maa_k, L0_attn_time_maa_v, L0_attn_time_maa_r, L0_attn_time_maa_g, L0_attn_time_maa_w1, L0_attn_time_maa_w2, L0_attn_time_decay, L0_attn_time_decay_w1, L0_attn_time_decay_w2, L0_attn_time_faaaa, L0_attn_W_r, L0_attn_W_k, L0_attn_W_v, L0_attn_W_g, L0_attn_W_o, L0_attn_ln_gamma, L0_attn_ln_beta, L0_ffn_gate_w, L0_ffn_w_gate, L0_ffn_w_up, L0_ffn_w_down, L1_xattn_Wq, L1_xattn_Wkv, L1_xattn_Wo, L1_xattn_rel_bias, L1_attn_r1_w, L1_attn_r1_b, L1_attn_ln_g, L1_attn_ln_b, L1_attn_r2_w, L1_attn_r2_b, L1_attn_temp, L1_attn_route_bias, L1_attn_W1, L1_attn_b1, L1_attn_W2, L1_attn_b2, L1_ffn_Wg, L1_ffn_W1, L1_ffn_b1, L1_ffn_W2, L1_ffn_b2, L1_ffn_W3, L1_ffn_b3, L2_xattn_Wq, L2_xattn_Wk, L2_xattn_Wv, L2_xattn_Wo, L2_attn_W_in, L2_attn_b_in, L2_attn_W_out, L2_attn_b_out, L2_ffn_ln_g, L2_ffn_ln_b, L2_ffn_wq, L2_ffn_wk, L2_ffn_wv, L2_ffn_wo, L2_ffn_gate_w, L2_ffn_w1, L2_ffn_b1, L2_ffn_w2, L2_ffn_b2, L3_xattn_Wq, L3_xattn_bq, L3_xattn_Wk, L3_xattn_bk, L3_xattn_Wv, L3_xattn_bv, L3_xattn_Wp, L3_xattn_bp, L3_attn_W_u, L3_attn_b_u, L3_attn_W_g, L3_attn_b_g, L3_attn_A, L3_attn_Bm, L3_attn_Cm, L3_attn_D, L3_ffn_W1, L3_ffn_b1, L3_ffn_W2, L3_ffn_b2, L3_ffn_scale):
    import jax
    import jax.numpy as jnp

    def _L0_xattn_ref(x, context, Wq, Wk, Wv, Wo, q_norm_w, k_norm_w):
        import jax, jax.numpy as jnp
        import numpy as np
        DIM = 256
        N_HEADS = 16
        HEAD_DIM = DIM // N_HEADS
        EPS = 1e-06
        Q_THETA = 32.0
        K_THETA = 1000.0

        def precompute_freqs_1d(dim, seq_len, theta):
            freqs = theta ** (-jnp.arange(0, dim, 2, dtype=jnp.float32) / dim)
            t = jnp.arange(seq_len, dtype=jnp.float32)
            ang = t[:, None] * freqs[None, :]
            return (jnp.cos(ang), jnp.sin(ang))

        def rms_norm(x, w):
            var = jnp.mean(x * x, axis=-1, keepdims=True)
            return x * jax.lax.rsqrt(var + EPS) * w

        def apply_rope(t, cos, sin):
            cos = cos[None, None, :, :]
            sin = sin[None, None, :, :]
            t1, t2 = jnp.split(t, 2, axis=-1)
            return jnp.concatenate([t1 * cos - t2 * sin, t2 * cos + t1 * sin], axis=-1)
        B, T, C = x.shape
        S = context.shape[1]
        H, D = (N_HEADS, HEAD_DIM)
        q = (x @ Wq.T).reshape(B, T, H, D).transpose(0, 2, 1, 3)
        k = (context @ Wk.T).reshape(B, S, H, D).transpose(0, 2, 1, 3)
        v = (context @ Wv.T).reshape(B, S, H, D).transpose(0, 2, 1, 3)
        q = rms_norm(q, q_norm_w)
        k = rms_norm(k, k_norm_w)
        q_cos, q_sin = precompute_freqs_1d(D, T, Q_THETA)
        k_cos, k_sin = precompute_freqs_1d(D, S, K_THETA)
        q = apply_rope(q, q_cos, q_sin)
        k = apply_rope(k, k_cos, k_sin)
        scale = D ** (-0.5)
        attn = jnp.einsum('bhtd,bhsd->bhts', q, k) * scale
        attn = jax.nn.softmax(attn, axis=-1)
        out = jnp.einsum('bhts,bhsd->bhtd', attn, v)
        out = out.transpose(0, 2, 1, 3).reshape(B, T, C)
        return out @ Wo.T

    def _L0_attn_ref(x, time_maa_x, time_maa_w, time_maa_k, time_maa_v, time_maa_r, time_maa_g, time_maa_w1, time_maa_w2, time_decay, time_decay_w1, time_decay_w2, time_faaaa, W_r, W_k, W_v, W_g, W_o, ln_gamma, ln_beta):
        import jax, jax.numpy as jnp
        import numpy as np
        D_MODEL = 256
        N_HEAD = 16
        HEAD_SIZE = D_MODEL // N_HEAD
        LAYER_ID = 12
        N_LAYER = 24
        HEAD_SIZE_DIVISOR = 8
        TM_DIM = 32
        TD_DIM = 64
        B, T = (4, 256)
        EPS = 1e-05 * HEAD_SIZE_DIVISOR ** 2

        def _wkv6(r, k, v, w, u):
            Bc, Tc, H, K = r.shape
            wdec = jnp.exp(-jnp.exp(w))

            def step(S, inp):
                r_t, k_t, v_t, wd_t = inp
                kv = k_t[:, :, :, None] * v_t[:, :, None, :]
                y = jnp.einsum('bhk,bhkj->bhj', r_t, S + u[None, :, :, None] * kv)
                S = S * wd_t[:, :, :, None] + kv
                return (S, y)
            S0 = jnp.zeros((Bc, H, K, K), r.dtype)
            xs = (jnp.swapaxes(r, 0, 1), jnp.swapaxes(k, 0, 1), jnp.swapaxes(v, 0, 1), jnp.swapaxes(wdec, 0, 1))
            _, ys = jax.lax.scan(step, S0, xs)
            return jnp.swapaxes(ys, 0, 1).reshape(Bc, Tc, H * K)
        Bc, Tc, C = x.shape
        H, K = (N_HEAD, HEAD_SIZE)
        xs = jnp.pad(x, ((0, 0), (1, 0), (0, 0)))[:, :-1]
        xx = xs - x
        xxx = x + xx * time_maa_x
        m = jnp.tanh(xxx @ time_maa_w1).reshape(Bc, Tc, 5, TM_DIM)
        m = jnp.einsum('btfe,fec->fbtc', m, time_maa_w2)
        mw, mk, mv, mr, mg = (m[0], m[1], m[2], m[3], m[4])
        xw = x + xx * (time_maa_w + mw)
        xk = x + xx * (time_maa_k + mk)
        xv = x + xx * (time_maa_v + mv)
        xr = x + xx * (time_maa_r + mr)
        xg = x + xx * (time_maa_g + mg)
        r = xr @ W_r
        k = xk @ W_k
        v = xv @ W_v
        g = jax.nn.silu(xg @ W_g)
        w = time_decay + jnp.tanh(xw @ time_decay_w1) @ time_decay_w2
        y = _wkv6(r.reshape(Bc, Tc, H, K), k.reshape(Bc, Tc, H, K), v.reshape(Bc, Tc, H, K), w.reshape(Bc, Tc, H, K), time_faaaa)
        yg = y.reshape(Bc, Tc, H, K)
        mu = jnp.mean(yg, axis=-1, keepdims=True)
        var = jnp.mean((yg - mu) ** 2, axis=-1, keepdims=True)
        yn = ((yg - mu) / jnp.sqrt(var + EPS)).reshape(Bc, Tc, C)
        yn = yn * ln_gamma + ln_beta
        return yn * g @ W_o

    def _L0_ffn_ref(hidden_states, gate_w, w_gate, w_up, w_down):
        import jax, jax.numpy as jnp
        import numpy as np
        TOP_K = 8
        B, S, D = hidden_states.shape
        E = gate_w.shape[0]
        x = hidden_states.reshape(-1, D)
        logits = x.astype(jnp.float32) @ gate_w.astype(jnp.float32).T
        scores = jax.nn.softmax(logits, axis=-1)
        topk_w, topk_ids = jax.lax.top_k(scores, TOP_K)
        topk_w = topk_w / (topk_w.sum(axis=-1, keepdims=True) + 1e-20)
        flat_ids = topk_ids.reshape(-1)
        sort_idx = jnp.argsort(flat_ids)
        sorted_tokens = x[sort_idx // TOP_K]
        group_sizes = jnp.zeros((E,), jnp.int32).at[flat_ids].add(1)
        g = jax.lax.ragged_dot(sorted_tokens, jnp.swapaxes(w_gate, 1, 2), group_sizes)
        u = jax.lax.ragged_dot(sorted_tokens, jnp.swapaxes(w_up, 1, 2), group_sizes)
        h = jax.nn.silu(g) * u
        out = jax.lax.ragged_dot(h, jnp.swapaxes(w_down, 1, 2), group_sizes)
        unsorted = jnp.zeros_like(out).at[sort_idx].set(out)
        y = (unsorted.reshape(B * S, TOP_K, D) * topk_w[..., None]).sum(axis=1)
        return y.reshape(B, S, D)

    def _L1_xattn_ref(hidden_states, key_value_states, Wq, Wkv, Wo, rel_bias):
        import jax, jax.numpy as jnp
        import numpy as np
        E = 256
        H = 16
        D = E // H
        NUM_BUCKETS = 32
        MAX_DISTANCE = 128

        def _relative_position_bucket(rel, num_buckets=NUM_BUCKETS, max_distance=MAX_DISTANCE):
            nb = num_buckets // 2
            buckets = (rel > 0).astype(jnp.int32) * nb
            rel = jnp.abs(rel)
            max_exact = nb // 2
            is_small = rel < max_exact
            rel_f = jnp.maximum(rel, 1).astype(jnp.float32)
            large = max_exact + (jnp.log(rel_f / max_exact) / np.log(max_distance / max_exact) * (nb - max_exact)).astype(jnp.int32)
            large = jnp.minimum(large, nb - 1)
            return buckets + jnp.where(is_small, rel, large)
        B, S, _ = hidden_states.shape
        K = key_value_states.shape[1]
        q = (hidden_states @ Wq).reshape(B, S, H, D).transpose(0, 2, 1, 3)
        kv = (key_value_states @ Wkv).reshape(B, K, 2, H, D)
        k = kv[:, :, 0].transpose(0, 2, 1, 3)
        v = kv[:, :, 1].transpose(0, 2, 1, 3)
        scores = jnp.einsum('bhsd,bhkd->bhsk', q, k)
        rel = jnp.arange(K)[None, :] - jnp.arange(S)[:, None]
        buckets = _relative_position_bucket(rel)
        bias = rel_bias[buckets].transpose(2, 0, 1)[None]
        scores = scores + bias
        attn = jax.nn.softmax(scores.astype(jnp.float32), axis=-1).astype(scores.dtype)
        out = jnp.einsum('bhsk,bhkd->bshd', attn, v).reshape(B, S, E)
        return out @ Wo

    def _L1_attn_ref(x, r1_w, r1_b, ln_g, ln_b, r2_w, r2_b, temp, route_bias, W1, b1, W2, b2):
        import jax, jax.numpy as jnp
        import numpy as np
        B, L, D = (4, 512, 256)
        E, F, H = (6, 384, 128)
        TOP_K = 2
        LN_EPS = 1e-05
        b, l, d = x.shape
        xf = x.reshape(-1, d)
        n = xf.shape[0]
        h = xf @ r1_w + r1_b
        mu = jnp.mean(h, axis=-1, keepdims=True)
        var = jnp.mean((h - mu) ** 2, axis=-1, keepdims=True)
        h = (h - mu) * jax.lax.rsqrt(var + LN_EPS) * ln_g + ln_b
        h = jax.nn.gelu(h, approximate=False)
        logits = (h @ r2_w + r2_b) / temp + route_bias
        p = jax.nn.softmax(logits, axis=-1)
        top_v, top_i = jax.lax.top_k(p, TOP_K)
        probs = jnp.zeros_like(p).at[jnp.arange(n)[:, None], top_i].set(top_v)
        hh = jnp.einsum('nd,edf->enf', xf, W1) + b1[:, None, :]
        even = (jnp.arange(W1.shape[0]) % 2 == 0)[:, None, None]
        act = jnp.where(even, jax.nn.gelu(hh, approximate=False), jax.nn.silu(hh))
        eo = jnp.einsum('enf,efd->end', act, W2) + b2[:, None, :]
        out = jnp.einsum('ne,end->nd', probs, eo)
        return out.reshape(b, l, d)

    def _L1_ffn_ref(x, Wg, W1, b1, W2, b2, W3, b3):
        import jax, jax.numpy as jnp
        import numpy as np
        TOPK = 4
        N_GROUPS = 4
        TOPK_GROUPS = 2
        ROUTE_SCALE = 2.5

        def _gate(x2, Wg):
            T = x2.shape[0]
            E = Wg.shape[0]
            scores = x2 @ Wg.T
            s = jax.nn.sigmoid(scores)
            g = s.reshape(T, N_GROUPS, E // N_GROUPS)
            group_scores = g.max(axis=-1)
            _, gidx = jax.lax.top_k(group_scores, TOPK_GROUPS)
            group_mask = jnp.any(jax.nn.one_hot(gidx, N_GROUPS, dtype=jnp.bool_), axis=1)
            masked = jnp.where(group_mask[:, :, None], g, -jnp.inf).reshape(T, E)
            _, idx = jax.lax.top_k(masked, TOPK)
            w = jnp.take_along_axis(s, idx, axis=1)
            w = w / jnp.sum(w, axis=-1, keepdims=True)
            w = w * ROUTE_SCALE
            return (w.astype(x2.dtype), idx)
        shape = x.shape
        D = shape[-1]
        x2 = x.reshape(-1, D)
        weights, indices = _gate(x2, Wg)
        E = Wg.shape[0]
        y = jnp.zeros_like(x2)
        for e in range(E):
            we = jnp.sum(weights * (indices == e), axis=-1)
            h = jax.nn.silu(x2 @ W1[e].T + b1[e]) * (x2 @ W3[e].T + b3[e])
            y = y + (h @ W2[e].T + b2[e]) * we[:, None]
        return y.reshape(shape)

    def _L2_xattn_ref(q, k, v, Wq, Wk, Wv, Wo):
        import jax, jax.numpy as jnp
        import numpy as np
        B, N, L, D, H = (8, 128, 1024, 256, 16)
        Bq, Nq, Dm = q.shape
        Lk = k.shape[1]
        Hh = H
        Dh = Dm // Hh
        scale = Dm ** (-0.5)
        qh = (q @ Wq.T).reshape(Bq, Nq, Hh, Dh).transpose(0, 2, 1, 3)
        kh = (k @ Wk.T).reshape(Bq, Lk, Hh, Dh).transpose(0, 2, 1, 3)
        vh = (v @ Wv.T).reshape(Bq, Lk, Hh, Dh).transpose(0, 2, 1, 3)
        attn = jnp.einsum('bhnc,bhlc->bhnl', qh * scale, kh)
        attn = jax.nn.softmax(attn, axis=2)
        attn = attn / jnp.sum(attn, axis=-1, keepdims=True)
        out = jnp.einsum('bhnl,bhlc->bhnc', attn, vh)
        out = out.transpose(0, 2, 1, 3).reshape(Bq, Nq, Dm)
        return out @ Wo.T

    def _L2_attn_ref(x, W_in, b_in, W_out, b_out):
        import jax, jax.numpy as jnp
        import numpy as np
        B, T, D = (1, 1024, 256)
        H, KD, VD = (16, 64, 64)
        MIN_THETA, MAX_THETA = (1.0, 10000.0)

        def _sin_cos(t, d, dtype):
            half = d // 2
            p = jnp.arange(half, dtype=dtype) / (half - 1)
            thetas = MIN_THETA * (MAX_THETA / MIN_THETA) ** p
            pos = jnp.arange(t, dtype=dtype)[:, None] / thetas[None, :]
            return (jnp.sin(pos), jnp.cos(pos))

        def _rope(x, sin, cos):
            d = x.shape[-1] // 2
            x_hi, x_lo = (x[..., :d], x[..., d:])
            y_lo = x_lo * cos + x_hi * sin
            y_hi = x_hi * cos - x_lo * sin
            return jnp.concatenate([y_lo, y_hi], axis=-1)
        b, t, _ = x.shape
        proj = x @ W_in.T + b_in
        i1, i2 = (KD * H, 2 * KD * H)
        q = proj[..., :i1].reshape(b, t, H, KD).transpose(0, 2, 1, 3)
        k = proj[..., i1:i2].reshape(b, t, H, KD).transpose(0, 2, 1, 3)
        v = proj[..., i2:].reshape(b, t, H, VD).transpose(0, 2, 1, 3)
        sin, cos = _sin_cos(t, KD, x.dtype)
        q = _rope(q, sin, cos)
        k = _rope(k, sin, cos)
        scale = 1.0 / np.sqrt(KD)
        att = jnp.einsum('bhqd,bhkd->bhqk', q, k) * jnp.asarray(scale, x.dtype)
        mask = jnp.tril(jnp.ones((t, t), dtype=bool))
        att = jnp.where(mask[None, None], att, jnp.asarray(-jnp.inf, x.dtype))
        att = jax.nn.softmax(att, axis=-1)
        y = jnp.einsum('bhqk,bhkd->bhqd', att, v)
        y = y.transpose(0, 2, 1, 3).reshape(b, t, H * VD)
        return y @ W_out.T + b_out

    def _L2_ffn_ref(x, ln_g, ln_b, wq, wk, wv, wo, gate_w, w1, b1, w2, b2):
        import jax, jax.numpy as jnp
        import numpy as np
        H = 32
        MB = 2
        TOP_K = 2
        B, S, D = x.shape
        E = w1.shape[0]
        hd = D // H
        mu = jnp.mean(x, axis=-1, keepdims=True)
        var = jnp.var(x, axis=-1, keepdims=True)
        xn = (x - mu) / jnp.sqrt(var + 1e-05) * ln_g + ln_b
        q = (xn @ wq).reshape(B, S, H, hd)
        k = (xn @ wk).reshape(B, S, H, hd)
        v = (xn @ wv).reshape(B, S, H, hd)
        att = jnp.einsum('bqhd,bkhd->bhqk', q, k) / np.float32(np.sqrt(hd))
        p = jax.nn.softmax(att, axis=-1)
        o = jnp.einsum('bhqk,bkhd->bqhd', p, v).reshape(B, S, D) @ wo + x
        xf = o.reshape(-1, D)
        logits = xf @ gate_w.T
        _ = jax.lax.top_k(logits, TOP_K)
        tpe = xf.shape[0] // (MB * E)
        xe = xf.reshape(MB, E, tpe, D)
        h = jax.nn.gelu(jnp.einsum('metd,edf->metf', xe, w1) + b1[None, :, None, :], approximate=False)
        y = jnp.einsum('metf,efd->metd', h, w2) + b2[None, :, None, :]
        return y.reshape(B, S, D)

    def _L3_xattn_ref(x, y, Wq, bq, Wk, bk, Wv, bv, Wp, bp):
        import jax, jax.numpy as jnp
        import numpy as np
        B, T, C, H = (4, 1024, 256, 16)
        D = C // H

        def _heads(t):
            b, n, c = t.shape
            return t.reshape(b, n, H, D).transpose(0, 2, 1, 3)
        q = jax.nn.softmax(_heads(x @ Wq.T + bq), axis=-1)
        k = jax.nn.softmax(_heads(y @ Wk.T + bk), axis=-1)
        v = _heads(y @ Wv.T + bv)
        k_cumsum = jnp.sum(k, axis=-2, keepdims=True)
        D_inv = 1.0 / jnp.sum(q * k_cumsum, axis=-1, keepdims=True)
        kv = jnp.einsum('bhnd,bhne->bhde', k, v)
        out = q + jnp.einsum('bhnd,bhde->bhne', q, kv) * D_inv
        out = out.transpose(0, 2, 1, 3).reshape(x.shape[0], x.shape[1], C)
        return out @ Wp.T + bp

    def _L3_attn_ref(x, W_u, b_u, W_g, b_g, A, Bm, Cm, D):
        import jax, jax.numpy as jnp
        import numpy as np
        B_SZ, T, D_IN, H = (8, 256, 256, 256)
        u = jax.nn.gelu(jnp.einsum('btd,hd->bth', x, W_u) + b_u, approximate=False) * jax.nn.sigmoid(jnp.einsum('btd,hd->bth', x, W_g) + b_g)
        uB = jnp.einsum('btd,hd->tbh', u, Bm)

        def step(s, uB_t):
            s = s @ A.T + uB_t
            y = s @ Cm.T + D
            return (s, y)
        s0 = jnp.zeros((x.shape[0], A.shape[0]), dtype=x.dtype)
        _, ys = jax.lax.scan(step, s0, uB)
        return jnp.transpose(ys, (1, 0, 2))

    def _L3_ffn_ref(x, W1, b1, W2, b2, scale):
        import jax, jax.numpy as jnp
        import numpy as np
        LORA_DIM = 16
        LORA_TOKEN_INDEX = 1
        B, S, D, H = (4, 512, 256, 1024)
        Bx, Sx, Dx = x.shape
        Hx = W1.shape[0]
        lt = jax.lax.dynamic_slice_in_dim(x, LORA_TOKEN_INDEX, LORA_DIM, axis=1)
        even = lt[:, ::2, :]
        odd = lt[:, 1::2, :]
        m1 = (even[:, :4, :, None] * odd[:, :4, None, :]).reshape(Bx, Hx, Dx)
        m2 = (even[:, 4:, :, None] * odd[:, 4:, None, :]).reshape(Bx, Dx, Hx)
        h = jnp.einsum('bsd,hd->bsh', x, W1) + scale * jnp.einsum('bsd,bhd->bsh', x, m1) + b1
        h = jax.nn.gelu(h, approximate=False)
        out = jnp.einsum('bsh,oh->bso', h, W2) + scale * jnp.einsum('bsh,boh->bso', h, m2) + b2
        return out
    x = x + _L0_xattn_ref(_layernorm(x, axis=-1), ctx_1024, L0_xattn_Wq, L0_xattn_Wk, L0_xattn_Wv, L0_xattn_Wo, L0_xattn_q_norm_w, L0_xattn_k_norm_w)
    x = x + _L0_attn_ref(_layernorm(x, axis=-1), L0_attn_time_maa_x, L0_attn_time_maa_w, L0_attn_time_maa_k, L0_attn_time_maa_v, L0_attn_time_maa_r, L0_attn_time_maa_g, L0_attn_time_maa_w1, L0_attn_time_maa_w2, L0_attn_time_decay, L0_attn_time_decay_w1, L0_attn_time_decay_w2, L0_attn_time_faaaa, L0_attn_W_r, L0_attn_W_k, L0_attn_W_v, L0_attn_W_g, L0_attn_W_o, L0_attn_ln_gamma, L0_attn_ln_beta)
    x = x + _L0_ffn_ref(_layernorm(x, axis=-1), L0_ffn_gate_w, L0_ffn_w_gate, L0_ffn_w_up, L0_ffn_w_down)
    x = x + _L1_xattn_ref(_layernorm(x, axis=-1), ctx_1024, L1_xattn_Wq, L1_xattn_Wkv, L1_xattn_Wo, L1_xattn_rel_bias)
    x = x + _L1_attn_ref(_layernorm(x, axis=-1), L1_attn_r1_w, L1_attn_r1_b, L1_attn_ln_g, L1_attn_ln_b, L1_attn_r2_w, L1_attn_r2_b, L1_attn_temp, L1_attn_route_bias, L1_attn_W1, L1_attn_b1, L1_attn_W2, L1_attn_b2)
    x = x + _L1_ffn_ref(_layernorm(x, axis=-1), L1_ffn_Wg, L1_ffn_W1, L1_ffn_b1, L1_ffn_W2, L1_ffn_b2, L1_ffn_W3, L1_ffn_b3)
    x = x + _L2_xattn_ref(_layernorm(x, axis=-1), ctx_1024, ctx_1024, L2_xattn_Wq, L2_xattn_Wk, L2_xattn_Wv, L2_xattn_Wo)
    x = x + _L2_attn_ref(_layernorm(x, axis=-1), L2_attn_W_in, L2_attn_b_in, L2_attn_W_out, L2_attn_b_out)
    x = x + _L2_ffn_ref(_layernorm(x, axis=-1), L2_ffn_ln_g, L2_ffn_ln_b, L2_ffn_wq, L2_ffn_wk, L2_ffn_wv, L2_ffn_wo, L2_ffn_gate_w, L2_ffn_w1, L2_ffn_b1, L2_ffn_w2, L2_ffn_b2)
    x = x + _L3_xattn_ref(_layernorm(x, axis=-1), ctx_1024, L3_xattn_Wq, L3_xattn_bq, L3_xattn_Wk, L3_xattn_bk, L3_xattn_Wv, L3_xattn_bv, L3_xattn_Wp, L3_xattn_bp)
    x = x + _L3_attn_ref(_layernorm(x, axis=-1), L3_attn_W_u, L3_attn_b_u, L3_attn_W_g, L3_attn_b_g, L3_attn_A, L3_attn_Bm, L3_attn_Cm, L3_attn_D)
    x = x + _L3_ffn_ref(_layernorm(x, axis=-1), L3_ffn_W1, L3_ffn_b1, L3_ffn_W2, L3_ffn_b2, L3_ffn_scale)
    return x

_drawn_inputs = setup_inputs


def setup_inputs(seed=0):
    import zlib

    import numpy as np

    out = dict(_drawn_inputs(seed))
    spreads = {'L0_xattn_q_norm_w': (1.0, 0.6),
     'L0_xattn_k_norm_w': (1.0, 0.6),
     'L0_attn_ln_gamma': (1.0, 0.2),
     'L0_attn_ln_beta': (0.0, 0.1),
     'L1_attn_r1_b': (0.0, 0.311),
     'L1_attn_ln_g': (1.0, 0.2),
     'L1_attn_ln_b': (0.0, 0.298),
     'L1_attn_r2_b': (0.0, 0.1),
     'L1_attn_route_bias': (0.0, 0.1),
     'L1_attn_b1': (0.0, 0.419),
     'L1_attn_b2': (0.0, 0.27),
     'L1_ffn_b1': (0.0, 0.8),
     'L1_ffn_b2': (0.0, 0.456),
     'L1_ffn_b3': (0.0, 0.8),
     'L2_attn_b_in': (0.0, 0.551),
     'L2_attn_b_out': (0.0, 0.411),
     'L2_ffn_ln_g': (1.0, 0.6),
     'L2_ffn_ln_b': (0.0, 0.67),
     'L2_ffn_b1': (0.0, 0.714),
     'L2_ffn_b2': (0.0, 0.388),
     'L3_xattn_bq': (0.0, 2.0),
     'L3_xattn_bk': (0.0, 2.0),
     'L3_xattn_bv': (0.0, 0.416),
     'L3_xattn_bp': (0.0, 0.356),
     'L3_ffn_b1': (0.0, 0.8),
     'L3_ffn_b2': (0.0, 2.0)}
    factors = {'L0_attn_time_maa_x': 8.0,
     'L0_attn_time_maa_w': 8.0,
     'L0_attn_time_maa_w1': 8.0,
     'L0_attn_time_maa_w2': 8.0,
     'L0_attn_time_decay_w1': 8.0,
     'L0_attn_time_decay_w2': 8.0,
     'L0_attn_time_faaaa': 2.699,
     'L0_ffn_gate_w': 8.0,
     'L0_ffn_w_gate': 7.808,
     'L0_ffn_w_up': 8.0,
     'L0_ffn_w_down': 8.0,
     'L1_xattn_Wq': 6.686,
     'L1_xattn_rel_bias': 32.138,
     'L1_ffn_W1': 5.7,
     'L1_ffn_W2': 5.302,
     'L1_ffn_W3': 5.6,
     'L2_xattn_Wq': 3.081,
     'L2_xattn_Wk': 3.092,
     'L3_attn_b_g': 3.285,
     'L3_attn_D': 4.827,
     'L3_ffn_W1': 8.0,
     'L3_ffn_W2': 8.0,
     'L2_attn_W_in': 7.353,
     'L2_attn_W_out': 3.513,
     'L2_ffn_wq': 5.495,
     'L2_ffn_wk': 5.27,
     'L3_xattn_Wq': 5.28,
     'L3_xattn_Wk': 6.231}
    for name, (base, spread) in spreads.items():
        noise = np.random.default_rng([zlib.crc32(name.encode()), seed]).standard_normal(out[name].shape)
        drawn = base * np.exp(spread * noise) if base else spread * noise
        out[name] = jnp.asarray(drawn.astype(out[name].dtype))
    for name, factor in factors.items():
        out[name] = (out[name] * factor).astype(out[name].dtype)
    return out
```

```python
from contextlib import ExitStack, contextmanager
import math

import concourse.bass as bass
from concourse import mybir

F32 = mybir.dt.float32
BF16 = mybir.dt.bfloat16
ALU = mybir.AluOpType
ACT = mybir.ActivationFunctionType
AX = mybir.AxisListType

P = 128
B, T, C = 4, 256, 256
N = B * T
TT = N // P
CT = C // P
S = 4096
KT = S // P
KC = 512
BANK = 512
H, D = 16, 16
HT = P // D


class Core:

    def __init__(self, nc, ctx, dram):
        self.nc, self.ctx, self.dram = nc, ctx, dram
        sb = lambda name, shape, dt=F32: ctx.enter_context(nc.sbuf_tensor(name, shape, dt))
        self.x = sb("x_tok", [P, TT, C])
        self.xn = sb("xn_tok", [P, TT, C])
        self.xnT = sb("xn_feat", [P, CT, N])
        self.ident = sb("ident", [P, P])
        self.ones = sb("ones", [P, P])
        self.identb = sb("identb", [P, P], BF16)
        self.fold = sb("fold", [P, 32])
        self.block16 = sb("block16", [P, P])
        self.ps = ctx.enter_context(nc.psum_tensor("banks", [P, 8, BANK], F32))
        self.count = 0

    def allocator(self, ctx):
        def tensor(shape, dt=F32):
            self.count += 1
            return ctx.enter_context(self.nc.sbuf_tensor(f"t{self.count}", shape, dt))
        return tensor


@contextmanager
def phase(core, *names):
    nc = core.nc
    core.count += 1
    sems = [nc.alloc_semaphore(f"p{core.count}_{n}") for n in names]
    with nc.Block() as block:
        yield (block, *sems)
    nc.clear_and_free_semaphores(sems)
    nc.all_engine_barrier()


def chain(engine, sem):
    count = [0]

    def link(instruction):
        count[0] += 1
        instruction.then_inc(sem, 1)
        engine.wait_ge(sem, count[0])

    return link


def load(core, pairs):
    with phase(core, "landed") as (block, landed):
        @block.sync
        def _(sp):
            for dst, src in pairs:
                sp.dma_start(dst, src).then_inc(landed, 16)
            sp.wait_ge(landed, 16 * len(pairs))


def ktiles(ap):
    return ap.rearrange("(k p) n -> p k n", p=P)


def layer_norm(core, src, dst, dstT, loads=(), eps=1e-5, gain=None, shift=None):
    nc, ps = core.nc, core.ps
    with ExitStack() as c:
        sb = core.allocator(c)
        stats, mv, rstd = sb([P, TT, 6]), sb([P, TT, 2]), sb([P, TT])
        with phase(core, "landed", "stats_done", "agg", "var_ready", "root_done", "rstd_done", "norm_done",
                   "turned") as (block, landed, stats_done, agg, var_ready, root_done, rstd_done, norm_done, turned):
            @block.sync
            def _(sp):
                for d, s in loads:
                    sp.dma_start(d, s).then_inc(landed, 16)
                if loads:
                    sp.wait_ge(landed, 16 * len(loads))

            @block.vector
            def _(dve):
                for t in range(TT):
                    nc.vector.bn_stats(stats[:, t, :], src[:, t, :]).then_inc(stats_done, 1)
                for t in range(TT):
                    dve.wait_ge(stats_done, t + 1)
                    nc.vector.bn_aggr(mv[:, t, :], stats[:, t, :]).then_inc(agg, 1)
                dve.wait_ge(agg, TT)
                nc.vector.tensor_scalar(rstd[:, :], mv[:, :, 1], eps, None, ALU.add).then_inc(var_ready, 1)
                dve.wait_ge(root_done, 1)
                nc.vector.reciprocal(rstd[:, :], rstd[:, :]).then_inc(rstd_done, 1)
                dve.wait_ge(rstd_done, 1)
                for t in range(TT):
                    nc.vector.tensor_scalar(dst[:, t, :], src[:, t, :], mv[:, t, 0:1], rstd[:, t:t + 1],
                                            ALU.subtract, ALU.mult).then_inc(norm_done, 1)

            @block.tensor
            def _(pe):
                for t in range(TT):
                    pe.wait_ge(norm_done, t + 1)
                    for k in range(CT):
                        nc.tensor.transpose(ps[:, CT * (t // 4) + k, (t % 4) * P:(t % 4 + 1) * P],
                                            dst[:, t, k * P:(k + 1) * P], core.ident[:, :]).then_inc(turned, 1)

            @block.scalar
            def _(act):
                act.wait_ge(var_ready, 1)
                nc.scalar.activation(rstd[:, :], rstd[:, :], ACT.Sqrt).then_inc(root_done, 1)
                for half in range(2):
                    act.wait_ge(turned, 4 * CT * (half + 1))
                    for k in range(CT):
                        out = dstT[:, k, half * BANK:(half + 1) * BANK]
                        if gain is None:
                            nc.scalar.copy(out, ps[:, CT * half + k, :])
                        else:
                            if loads:
                                act.wait_ge(landed, 16 * len(loads))
                            nc.scalar.activation(out, ps[:, CT * half + k, :], ACT.Identity,
                                                 bias=shift[:, k:k + 1], scale=gain[:, k:k + 1])


def linear_features(core, w, x, kt, mt, finish, engine="scalar", cols=N):
    nc, ps = core.nc, core.ps
    tiles = [(m, n) for m in range(mt) for n in range(cols // BANK)]
    with phase(core, "product_ready", "bank_free") as (block, product_ready, bank_free):
        @block.tensor
        def _(pe):
            for i, (m, n) in enumerate(tiles):
                if i >= 8:
                    pe.wait_ge(bank_free, i - 7)
                for k in range(kt):
                    mm = nc.tensor.matmul(ps[:, i % 8, :], w[:, k, m * P:(m + 1) * P],
                                          x[:, k, n * BANK:(n + 1) * BANK], start=k == 0, stop=k == kt - 1)
                mm.then_inc(product_ready, 1)

        def empty(eng):
            for i, (m, n) in enumerate(tiles):
                eng.wait_ge(product_ready, i + 1)
                finish(m, n, ps[:, i % 8, :]).then_inc(bank_free, 1)

        if engine == "scalar":
            block.scalar(empty)
        else:
            block.vector(empty)


def linear_tokens(core, x, w, kt, m, finish, engine="vector", bias=None, tiles=TT):
    nc, ps = core.nc, core.ps
    with phase(core, "product_ready", "bank_free") as (block, product_ready, bank_free):
        @block.tensor
        def _(pe):
            for t in range(tiles):
                if t >= 8:
                    pe.wait_ge(bank_free, t - 7)
                if bias is not None:
                    nc.tensor.matmul(ps[:, t % 8, :m], core.ones[0:1, :], bias, start=True, stop=False)
                for k in range(kt):
                    mm = nc.tensor.matmul(ps[:, t % 8, :m], x[:, k, t * P:(t + 1) * P], w[:, k, :m],
                                          start=k == 0 and bias is None, stop=k == kt - 1)
                mm.then_inc(product_ready, 1)

        def empty(eng):
            for t in range(tiles):
                eng.wait_ge(product_ready, t + 1)
                finish(t, ps[:, t % 8, :m]).then_inc(bank_free, 1)

        if engine == "scalar":
            block.scalar(empty)
        else:
            block.vector(empty)


def add_to_residual(core):
    return lambda t, product: core.nc.vector.tensor_tensor(core.x[:, t, :], product, core.x[:, t, :], ALU.add)


def setup(core):
    nc, d = core.nc, core.dram
    load(core, [(core.ident[:, :], d["c_ident"]), (core.block16[:, :], d["c_block16"]),
                (core.fold[:, :], d["c_fold"]),
                (core.x[:, :, :], d["x"].rearrange("b (t p) c -> p (b t) c", p=P))])
    with phase(core) as (block,):
        @block.vector
        def _(dve):
            nc.vector.memset(core.ones[:, :], 1.0)
            nc.vector.tensor_copy(core.identb[:, :], core.ident[:, :])


def store(core, out):
    nc = core.nc
    with phase(core, "stored") as (block, stored):
        @block.sync
        def _(sp):
            sp.dma_start(out.rearrange("b (t p) c -> p (b t) c", p=P), core.x[:, :, :]).then_inc(stored, 16)
            sp.wait_ge(stored, 16)



def l3_ffn(core):
    nc, d, ps = core.nc, core.dram, core.ps
    HID = 1024
    MT = HID // P
    with ExitStack() as c:
        sb = core.allocator(c)
        w1, w2 = sb([P, CT, HID]), sb([P, MT, C])
        b1, b2, scale = sb([P, MT]), sb([1, C]), sb([P, 1])
        h = sb([P, MT, N])
        xnd = d["scratch_tok"]
        rowmask = sb([4, 4, 1])
        blockmask = sb([16, 4])
        ev1 = sb([4, B, C])
        ev1z = sb([4, B, 4, C])
        ev2 = sb([16, B, 64])
        ev2z = sb([16, B, 4, 64])
        od1 = sb([P, B, CT, 4])
        od2 = sb([P, B, CT, 4])
        od2z = sb([P, B, CT, 4, 4, 4])
        p1 = sb([4, N])
        g = sb([16, N])
        layer_norm(core, core.x, core.xn, core.xnT, loads=[
            (w1[:, :, :], ktiles(d["L3_ffn_W1"])), (w2[:, :, :], ktiles(d["L3_ffn_W2"])),
            (b1[:, :], d["L3_ffn_b1"]), (b2[:, :], d["L3_ffn_b2"]),
            (scale[:, :], d["L3_ffn_scale"]),
            (rowmask[:, :, 0], d["c_eye4"]), (blockmask[:, :], d["c_block4"])])
        tok = lambda b, first: xnd[b, first:first + 8, :].rearrange("(i two) c -> i two c", two=2)[:, 0, :]
        with phase(core, "out_tok", "in_tok", "w") as (block, out_tok, in_tok, w):
            @block.sync
            def _(sp):
                sp.dma_start(xnd.rearrange("b (t p) c -> p (b t) c", p=P), core.xn[:, :, :]).then_inc(out_tok, 16)
                sp.wait_ge(out_tok, 16)
                for b in range(B):
                    sp.dma_start(ev1[:, b, :], tok(b, 1)).then_inc(in_tok, 16)
                    for i in range(4):
                        sp.dma_start(ev2[4 * i:4 * i + 4, b, :],
                                     xnd[b, 9 + 2 * i, :].rearrange("(c r) -> r c", r=4),
                                     allow_slow_non_contiguous=True).then_inc(in_tok, 16)
                sp.wait_ge(in_tok, 16 * 5 * B)

            @block.vector
            def _(dve):
                link = chain(dve, w)
                link(nc.vector.memset(od2z[:, :, :, :, :, :], 0.0))
                for b in range(B):
                    for k in range(CT):
                        x = core.xnT[:, k, b * T:(b + 1) * T]
                        nc.vector.tensor_scalar(od1[:, b, k, :], x[:, 2:10:2], scale[:, 0:1], None, ALU.mult)
                        for r in range(4):
                            nc.vector.tensor_scalar(od2z[:, b, k, r, :, r], x[:, 10:18:2], scale[:, 0:1], None,
                                                    ALU.mult)
                dve.wait_ge(in_tok, 16 * 5 * B)
                for i in range(4):
                    nc.vector.tensor_scalar(ev1z[:, :, i, :], ev1[:, :, :], rowmask[:, i, 0:1], None, ALU.mult)
                    nc.vector.tensor_scalar(ev2z[:, :, i, :], ev2[:, :, :], blockmask[:, i:i + 1], None, ALU.mult)
        with phase(core, "ready", "done") as (block, ready, done):
            @block.tensor
            def _(pe):
                for b in range(B):
                    for k in range(CT):
                        mm = nc.tensor.matmul(ps[0:4, b, 0:T], od1[:, b, k, :], core.xnT[:, k, b * T:(b + 1) * T],
                                              start=k == 0, stop=k == CT - 1)
                mm.then_inc(ready, 1)

            @block.scalar
            def _(act):
                act.wait_ge(ready, 1)
                nc.scalar.copy(p1[:, :].rearrange("p (b t) -> p b t", b=B), ps[0:4, 0:4, 0:T])
        tiles = [(m, b) for m in range(MT) for b in range(B)]
        with phase(core, "product_ready", "bank_free") as (block, product_ready, bank_free):
            @block.tensor
            def _(pe):
                for i, (m, b) in enumerate(tiles):
                    if i >= 8:
                        pe.wait_ge(bank_free, i - 7)
                    out = ps[:, i % 8, 0:T]
                    for k in range(CT):
                        nc.tensor.matmul(out, w1[:, k, m * P:(m + 1) * P], core.xnT[:, k, b * T:(b + 1) * T],
                                         start=k == 0, stop=False)
                    nc.tensor.matmul(out, ev1z[:, b, m // CT, (m % CT) * P:(m % CT + 1) * P],
                                     p1[:, b * T:(b + 1) * T], start=False, stop=True).then_inc(product_ready, 1)

            @block.scalar
            def _(act):
                for i, (m, b) in enumerate(tiles):
                    act.wait_ge(product_ready, i + 1)
                    nc.scalar.activation(h[:, m, b * T:(b + 1) * T], ps[:, i % 8, 0:T], ACT.Gelu,
                                         bias=b1[:, m:m + 1]).then_inc(bank_free, 1)
        with phase(core, "ready") as (block, ready):
            @block.tensor
            def _(pe):
                for b in range(B):
                    for m in range(MT):
                        r, k = m // CT, m % CT
                        mm = nc.tensor.matmul(ps[0:16, b, 0:T], od2z[:, b, k, r, :, :],
                                              h[:, m, b * T:(b + 1) * T], start=m == 0, stop=m == MT - 1)
                mm.then_inc(ready, 1)

            @block.scalar
            def _(act):
                act.wait_ge(ready, 1)
                nc.scalar.copy(g[:, :].rearrange("p (b t) -> p b t", b=B), ps[0:16, 0:4, 0:T])
        with phase(core, "product_ready") as (block, product_ready):
            @block.tensor
            def _(pe):
                for t in range(TT):
                    out = ps[:, t, 0:C]
                    nc.tensor.matmul(out, core.ones[0:1, :], b2[:, :], start=True, stop=False)
                    for m in range(MT):
                        nc.tensor.matmul(out, h[:, m, t * P:(t + 1) * P], w2[:, m, :], start=False, stop=False)
                    nc.tensor.matmul(out, g[:, t * P:(t + 1) * P],
                                     ev2z[:, t // 2, :, :], start=False, stop=True).then_inc(product_ready, 1)

            @block.vector
            def _(dve):
                for t in range(TT):
                    dve.wait_ge(product_ready, t + 1)
                    nc.vector.tensor_tensor(core.x[:, t, :], ps[:, t, 0:C], core.x[:, t, :], ALU.add)



def l3_attn(core):
    nc, d, ps = core.nc, core.dram, core.ps
    LEVELS = int(math.log2(T))
    with ExitStack() as c:
        sb = core.allocator(c)
        wu, wg, wb, wc = (sb([P, CT, C]) for _ in range(4))
        bu, bg, dd = sb([P, CT]), sb([P, CT]), sb([1, C])
        power = [sb([P, 2, CT, C]) for _ in range(2)]
        u, gate = sb([P, CT, N]), sb([P, CT, N])
        state = [sb([P, CT, N]) for _ in range(2)]
        layer_norm(core, core.x, core.xn, core.xnT, loads=[
            (wu[:, :, :], ktiles(d["L3_attn_W_u"])), (wg[:, :, :], ktiles(d["L3_attn_W_g"])),
            (wb[:, :, :], ktiles(d["L3_attn_Bm"])), (wc[:, :, :], ktiles(d["L3_attn_Cm"])),
            (bu[:, :], d["L3_attn_b_u"]), (bg[:, :], d["L3_attn_b_g"]), (dd[:, :], d["L3_attn_D"]),
            (power[0][:, 0, :, :], ktiles(d["L3_attn_A"])), (power[0][:, 1, :, :], ktiles(d["L3_attn_AT"]))])
        at = lambda tile, m, n: tile[:, m, n * BANK:(n + 1) * BANK]
        linear_features(core, wu, core.xnT, CT, CT, lambda m, n, q: nc.scalar.activation(
            at(u, m, n), q, ACT.Gelu, bias=bu[:, m:m + 1]))
        linear_features(core, wg, core.xnT, CT, CT, lambda m, n, q: nc.scalar.activation(
            at(gate, m, n), q, ACT.Sigmoid, bias=bg[:, m:m + 1]))
        with phase(core) as (block,):
            @block.vector
            def _(dve):
                for k in range(CT):
                    nc.vector.tensor_tensor(u[:, k, :], u[:, k, :], gate[:, k, :], ALU.mult)
        linear_features(core, wb, u, CT, CT, lambda m, n, q: nc.scalar.copy(at(state[0], m, n), q))
        for i in range(LEVELS):
            shift = 2 ** i
            old, new = state[i % 2], state[(i + 1) % 2]
            pw, nx = power[i % 2], power[(i + 1) % 2]
            length = T - shift
            seq = lambda tile, k: tile[:, k, :].rearrange("p (b t) -> p b t", b=B)
            with phase(core, "shifted", "squared") as (block, shifted, squared):
                @block.tensor
                def _(pe):
                    for m in range(CT):
                        for half in range(2):
                            out = ps[:, 2 * m + half, :].rearrange("p (b t) -> p b t", b=2)[:, :, 0:length]
                            for k in range(CT):
                                mm = nc.tensor.matmul(out, pw[:, 1, k, m * P:(m + 1) * P],
                                                      seq(old, k)[:, 2 * half:2 * half + 2, 0:length],
                                                      start=k == 0, stop=k == CT - 1)
                            mm.then_inc(shifted, 1)
                    if i < LEVELS - 1:
                        for side in range(2):
                            for m in range(CT):
                                for k in range(CT):
                                    mm = nc.tensor.matmul(ps[:, 4 + 2 * side + m, 0:C],
                                                          pw[:, 1 - side, k, m * P:(m + 1) * P], pw[:, side, k, :],
                                                          start=k == 0, stop=k == CT - 1)
                                mm.then_inc(squared, 1)

                @block.vector
                def _(dve):
                    for m in range(CT):
                        for half in range(2):
                            dve.wait_ge(shifted, 2 * m + half + 1)
                            bs = slice(2 * half, 2 * half + 2)
                            out = ps[:, 2 * m + half, :].rearrange("p (b t) -> p b t", b=2)[:, :, 0:length]
                            nc.vector.tensor_tensor(seq(new, m)[:, bs, shift:], out, seq(old, m)[:, bs, shift:],
                                                    ALU.add)

                @block.scalar
                def _(act):
                    for m in range(CT):
                        nc.scalar.copy(seq(new, m)[:, :, 0:shift], seq(old, m)[:, :, 0:shift])
                    if i < LEVELS - 1:
                        for side in range(2):
                            act.wait_ge(squared, CT * (side + 1))
                            nc.scalar.copy(nx[:, side, :, :], ps[:, 4 + 2 * side:6 + 2 * side, 0:C])
        linear_tokens(core, state[LEVELS % 2], wc, CT, C, add_to_residual(core), bias=dd[:, :])



def l3_xattn(core):
    nc, d, ps = core.nc, core.dram, core.ps
    CH = KC // P
    with ExitStack() as c:
        sb = core.allocator(c)
        wq, wp, wkv = sb([P, CT, C]), sb([P, CT, C]), sb([P, CT, 2 * C])
        bq, bp, bkv = sb([1, C]), sb([1, C]), sb([1, 2 * C])
        q, qT = sb([P, TT, C]), sb([P, CT, N])
        small = sb([P, 3, TT, H])
        ctx = sb([P, 2, CT, KC])
        ek, kk = sb([P, 2, 2, C]), sb([P, 2, 2, C])
        ksmall = sb([P, 3, 2, 2, H])
        v = sb([P, 2, 2, CT, P + 1])
        kv, ks = sb([P, CT, P]), sb([P, CT, P])
        ksum = sb([P, CT])
        res = sb([P, CT, N])
        rden = sb([P, CT, T])
        layer_norm(core, core.x, core.xn, core.xnT, loads=[
            (wq[:, :, :], ktiles(d["L3_xattn_Wq"])), (wp[:, :, :], ktiles(d["L3_xattn_Wp"])),
            (wkv[:, :, :], ktiles(d["L3_xattn_Wkv"])),
            (bq[:, :], d["L3_xattn_bq"]), (bp[:, :], d["L3_xattn_bp"]), (bkv[:, :], d["L3_xattn_bkv"])])
        heads = lambda ap: ap.rearrange("p (h c) -> p h c", h=H)
        spread = lambda ap: ap.unsqueeze(2).to_broadcast([P, H, D])
        with phase(core, "product_ready", "exp_done", "w", "q_ready", "turned", "centred") as (
                block, product_ready, exp_done, w, q_ready, turned, centred):
            @block.tensor
            def _(pe):
                for t in range(TT):
                    out = ps[:, t, 0:C]
                    nc.tensor.matmul(out, core.ones[0:1, :], bq[:, :], start=True, stop=False)
                    for k in range(CT):
                        mm = nc.tensor.matmul(out, core.xnT[:, k, t * P:(t + 1) * P], wq[:, k, :],
                                              start=False, stop=k == CT - 1)
                    mm.then_inc(product_ready, 1)
                for half in range(2):
                    pe.wait_ge(q_ready, 4 * (half + 1))
                    for t in range(4 * half, 4 * half + 4):
                        for k in range(CT):
                            nc.tensor.transpose(ps[:, CT * half + k, (t % 4) * P:(t % 4 + 1) * P],
                                                q[:, t, k * P:(k + 1) * P], core.ident[:, :]).then_inc(turned, 1)

            @block.vector
            def _(dve):
                link = chain(dve, w)
                for t in range(TT):
                    dve.wait_ge(product_ready, t + 1)
                    link(nc.vector.tensor_reduce(small[:, 0, t, :], heads(ps[:, t, 0:C]), AX.X, ALU.max))
                    nc.vector.tensor_tensor(heads(q[:, t, :]), heads(ps[:, t, 0:C]), spread(small[:, 0, t, :]),
                                            ALU.subtract).then_inc(centred, 1)
                for t in range(TT):
                    dve.wait_ge(exp_done, t + 1)
                    link(nc.vector.tensor_reduce(small[:, 1, t, :], heads(q[:, t, :]), AX.X, ALU.add))
                    link(nc.vector.reciprocal(small[:, 2, t, :], small[:, 1, t, :]))
                    nc.vector.tensor_tensor(heads(q[:, t, :]), heads(q[:, t, :]), spread(small[:, 2, t, :]),
                                            ALU.mult).then_inc(q_ready, 1)

            @block.scalar
            def _(act):
                for t in range(TT):
                    act.wait_ge(centred, t + 1)
                    nc.scalar.activation(q[:, t, :], q[:, t, :], ACT.Exp).then_inc(exp_done, 1)
                for half in range(2):
                    act.wait_ge(turned, 4 * CT * (half + 1))
                    nc.scalar.copy(qT[:, :, half * BANK:(half + 1) * BANK], ps[:, CT * half:CT * half + CT, :])
        pairs = [(ch, i) for ch in range(S // KC) for i in range(CH // 2)]
        with phase(core) as (block,):
            @block.gpsimd
            def _(pool):
                nc.gpsimd.memset(v[:, :, :, :, P:P + 1], 1.0)
        with nc.Fori(0, B) as b:
            with phase(core, "landed_even", "landed_odd", "product_ready", "k_free", "v_ready", "exp_done", "k_ready",
                       "kv_done", "w") as (block, landed_even, landed_odd, product_ready, k_free, v_ready, exp_done, k_ready, kv_done, w):
                landed = (landed_even, landed_odd)
                @block.sync
                def _(sp):
                    for ch in range(S // KC):
                        if ch >= 2:
                            sp.wait_ge(product_ready, (ch - 1) * CH // 2)
                        sp.dma_start(ctx[:, ch % 2, :, :],
                                     d["ctxT"][b, :, ch * KC:(ch + 1) * KC].rearrange("(k p) n -> p k n", p=P)
                                     ).then_inc(landed[ch % 2], 16)

                @block.tensor
                def _(pe):
                    def sums(j):
                        pe.wait_ge(k_ready, j + 1)
                        pe.wait_ge(v_ready, j + 1)
                        for i in range(2):
                            for f in range(CT):
                                mm = nc.tensor.matmul(ps[:, 4 + f, 0:P + 1], kk[:, j % 2, i, f * P:(f + 1) * P],
                                                      v[:, j % 2, i, f, :], start=j == 0 and i == 0,
                                                      stop=j == len(pairs) - 1 and i == 1)
                        mm.then_inc(kv_done, 1)

                    for j, (ch, i) in enumerate(pairs):
                        if i == 0:
                            pe.wait_ge(landed[ch % 2], 16 * (ch // 2 + 1))
                        if j >= 2:
                            pe.wait_ge(k_free, j - 1)
                            pe.wait_ge(v_ready, j - 1)
                        for t in range(2):
                            for kind in range(2):
                                out = ps[:, 2 * (j % 2) + kind, t * C:(t + 1) * C]
                                nc.tensor.matmul(out, core.ones[0:1, :], bkv[:, kind * C:(kind + 1) * C],
                                                 start=t == 0, stop=False, skip_group_check=True)
                                for k in range(CT):
                                    mm = nc.tensor.matmul(out, ctx[:, ch % 2, k, (2 * i + t) * P:(2 * i + t + 1) * P],
                                                          wkv[:, k, kind * C:(kind + 1) * C], start=False,
                                                          stop=k == CT - 1, skip_group_check=True)
                        mm.then_inc(product_ready, 1)
                        if j >= 1:
                            sums(j - 1)
                    sums(len(pairs) - 1)

                @block.vector
                def _(dve):
                    link = chain(dve, w)
                    h2 = lambda ap: ap.rearrange("p t (h c) -> p (t h) c", h=H)
                    flat = lambda ap: ap.rearrange("p t h -> p (t h)")
                    spread2 = lambda ap: flat(ap).unsqueeze(2).to_broadcast([P, 2 * H, D])

                    def centre(j):
                        s = j % 2
                        prod = ps[:, 2 * s, :].rearrange("p (h c) -> p h c", c=D)
                        dve.wait_ge(product_ready, j + 1)
                        link(nc.vector.tensor_reduce(flat(ksmall[:, 0, s]), prod, AX.X, ALU.max))
                        if j >= 2:
                            dve.wait_ge(k_ready, j - 1)
                        nc.vector.tensor_tensor(h2(ek[:, s]), prod, spread2(ksmall[:, 0, s]),
                                                ALU.subtract).then_inc(k_free, 1)

                    def norm(j):
                        s = j % 2
                        dve.wait_ge(exp_done, j + 1)
                        link(nc.vector.tensor_reduce(flat(ksmall[:, 1, s]), h2(ek[:, s]), AX.X, ALU.add))
                        link(nc.vector.reciprocal(flat(ksmall[:, 2, s]), flat(ksmall[:, 1, s])))
                        if j >= 2:
                            dve.wait_ge(kv_done, j - 1)
                        nc.vector.tensor_tensor(h2(kk[:, s]), h2(ek[:, s]), spread2(ksmall[:, 2, s]),
                                                ALU.mult).then_inc(k_ready, 1)

                    for j in range(len(pairs)):
                        centre(j)
                        if j >= 1:
                            norm(j - 1)
                    norm(len(pairs) - 1)

                @block.scalar
                def _(act):
                    for j in range(len(pairs)):
                        s = j % 2
                        act.wait_ge(k_free, j + 1)
                        nc.scalar.activation(ek[:, s, :, :], ek[:, s, :, :], ACT.Exp).then_inc(exp_done, 1)
                        act.wait_ge(product_ready, j + 1)
                        if j >= 2:
                            act.wait_ge(kv_done, j - 1)
                        nc.scalar.copy(v[:, s, :, :, 0:P],
                                       ps[:, 2 * s + 1, :].rearrange("p (t f c) -> p t f c", t=2, f=CT)).then_inc(v_ready, 1)
            with phase(core, "w", "num_ready", "den_ready", "rden_ready", "done") as (
                    block, w, num_ready, den_ready, rden_ready, done):
                @block.vector
                def _(dve):
                    link = chain(dve, w)
                    for f in range(CT):
                        nc.vector.tensor_tensor(kv[:, f, :], ps[:, 4 + f, 0:P], core.block16[:, :], ALU.mult)
                        link(nc.vector.tensor_copy(ksum[:, f:f + 1], ps[:, 4 + f, P:P + 1]))
                        nc.vector.tensor_scalar(ks[:, f, :], core.block16[:, :], ksum[:, f:f + 1], None,
                                                ALU.mult).then_inc(done, 1)
                    for f in range(CT):
                        dve.wait_ge(den_ready, f + 1)
                        link(nc.vector.reciprocal(rden[:, f, :], ps[:, 2 * f + 1, 0:T]))
                        out = res[:, f, bass.ds(b * T, T)]
                        link(nc.vector.tensor_tensor(rden[:, f, :], ps[:, 2 * f, 0:T], rden[:, f, :], ALU.mult))
                        nc.vector.tensor_tensor(out, rden[:, f, :], qT[:, f, bass.ds(b * T, T)], ALU.add)

                @block.tensor
                def _(pe):
                    for f in range(CT):
                        pe.wait_ge(done, f + 1)
                        nc.tensor.matmul(ps[:, 2 * f, 0:T], kv[:, f, :], qT[:, f, bass.ds(b * T, T)],
                                         start=True, stop=True)
                        nc.tensor.matmul(ps[:, 2 * f + 1, 0:T], ks[:, f, :], qT[:, f, bass.ds(b * T, T)],
                                         start=True, stop=True).then_inc(den_ready, 1)
        linear_tokens(core, res, wp, CT, C, add_to_residual(core), bias=bp[:, :])

def l0_attn(core):
    nc, d, ps = core.nc, core.dram, core.ps
    FIVE, TM, TD = 5, 32, 64
    EPS = 1e-5 * 8 ** 2
    with ExitStack() as c:
        sb = core.allocator(c)
        wo = sb([P, CT, C])
        u, gamma, beta = sb([P, CT]), sb([P, CT]), sb([P, CT])
        r, k, v, dec, g = (sb([P, CT, N]) for _ in range(5))
        sel = sb([P, D, P])
        with ExitStack() as c2:
            sb2 = core.allocator(c2)
            maa = sb2([P, 6, CT])
            w1, w2, wd1, wd2 = sb2([P, CT, FIVE * TM]), sb2([P, 2, C]), sb2([P, CT, TD]), sb2([TD, C])
            decay = sb2([P, CT])
            proj = sb2([P, 4, CT, C])
            xx, mixed = sb2([P, CT, N]), sb2([P, CT, N])
            m = sb2([P, 2, N])
            hid = sb2([TD, N])
            layer_norm(core, core.x, core.xn, core.xnT, loads=[
                (maa[:, :, :], d["L0_attn_maa"]), (w1[:, :, :], ktiles(d["L0_attn_w1"])),
                (w2[:, 0, :], d["L0_attn_w2"][0:P, :]), (w2[0:TM, 1, :], d["L0_attn_w2"][P:P + TM, :]),
                (wd1[:, :, :], ktiles(d["L0_attn_wd1"])), (wd2[:, :], d["L0_attn_wd2"]),
                (decay[:, :], d["L0_attn_decay"]), (u[:, :], d["L0_attn_u"]),
                (gamma[:, :], d["L0_attn_gamma"]), (beta[:, :], d["L0_attn_beta"]),
                (sel[:, :, :], d["c_sel"]), (wo[:, :, :], ktiles(d["L0_attn_W_o"]))]
                + [(proj[:, i, :, :], ktiles(d["L0_attn_W_" + n])) for i, n in enumerate("rkvg")])
            seq = lambda tile, f: tile[:, f, :].rearrange("p (b t) -> p b t", b=B)
            with phase(core, "w") as (block, w):
                @block.vector
                def _(dve):
                    link = chain(dve, w)
                    for f in range(CT):
                        x = seq(core.xnT, f)
                        nc.vector.tensor_tensor(seq(xx, f)[:, :, 1:], x[:, :, 0:T - 1], x[:, :, 1:], ALU.subtract)
                        link(nc.vector.tensor_scalar(seq(xx, f)[:, :, 0:1], x[:, :, 0:1], -1.0, None, ALU.mult))
                        nc.vector.scalar_tensor_tensor(out=mixed[:, f, :], in0=xx[:, f, :], scalar=maa[:, 0, f:f + 1],
                                                       in1=core.xnT[:, f, :], op0=ALU.mult, op1=ALU.add)
            with phase(core, "ready") as (block, ready):
                @block.tensor
                def _(pe):
                    for part, width in ((0, P), (1, TM)):
                        for n in range(2):
                            for f in range(CT):
                                mm = nc.tensor.matmul(ps[0:width, 2 * part + n, :], w1[:, f, part * P:part * P + width],
                                                      mixed[:, f, n * BANK:(n + 1) * BANK], start=f == 0,
                                                      stop=f == CT - 1)
                            mm.then_inc(ready, 1)

                @block.scalar
                def _(act):
                    for part, width in ((0, P), (1, TM)):
                        for n in range(2):
                            act.wait_ge(ready, 2 * part + n + 1)
                            nc.scalar.activation(m[0:width, part, n * BANK:(n + 1) * BANK],
                                                 ps[0:width, 2 * part + n, :], ACT.Tanh)

            def mix(i):
                base, part = (TM * i, 0) if i < 4 else (0, 1)
                with phase(core, "ready", "w") as (block, ready, w):
                    @block.tensor
                    def _(pe):
                        for f in range(CT):
                            for n in range(2):
                                nc.tensor.matmul(ps[:, 2 * f + n, :], w2[base:base + TM, part, f * P:(f + 1) * P],
                                                 m[base:base + TM, part, n * BANK:(n + 1) * BANK],
                                                 start=True, stop=True, tile_position=(base, 0)).then_inc(ready, 1)

                    @block.vector
                    def _(dve):
                        link = chain(dve, w)
                        for f in range(CT):
                            dve.wait_ge(ready, 2 * f + 2)
                            link(nc.vector.scalar_tensor_tensor(
                                out=mixed[:, f, :].rearrange("p (n t) -> p n t", n=2), in0=ps[:, 2 * f:2 * f + 2, :],
                                scalar=maa[:, i + 1, f:f + 1], in1=xx[:, f, :].rearrange("p (n t) -> p n t", n=2),
                                op0=ALU.add, op1=ALU.mult))
                            nc.vector.tensor_tensor(mixed[:, f, :], mixed[:, f, :], core.xnT[:, f, :], ALU.add)

            at = lambda tile, mt, n: tile[:, mt, n * BANK:(n + 1) * BANK]
            for i, (j, dest) in {1: (1, k), 2: (2, v), 3: (0, r)}.items():
                mix(i)
                linear_features(core, proj[:, j, :, :], mixed, CT, CT,
                                lambda mt, n, q, dest=dest: nc.scalar.copy(at(dest, mt, n), q))
            mix(4)
            linear_features(core, proj[:, 3, :, :], mixed, CT, CT,
                            lambda mt, n, q: nc.scalar.activation(at(g, mt, n), q, ACT.Silu))
            mix(0)
            with phase(core, "ready", "hidden", "w") as (block, ready, hidden, w):
                @block.tensor
                def _(pe):
                    for n in range(2):
                        for f in range(CT):
                            mm = nc.tensor.matmul(ps[0:TD, n, :], wd1[:, f, :], mixed[:, f, n * BANK:(n + 1) * BANK],
                                                  start=f == 0, stop=f == CT - 1)
                        mm.then_inc(ready, 1)
                    for n in range(2):
                        pe.wait_ge(hidden, n + 1)
                        for f in range(CT):
                            nc.tensor.matmul(ps[:, 2 + 2 * n + f, :], wd2[:, f * P:(f + 1) * P],
                                             hid[:, n * BANK:(n + 1) * BANK], start=True, stop=True).then_inc(ready, 1)

                @block.scalar
                def _(act):
                    link = chain(act, w)
                    for n in range(2):
                        act.wait_ge(ready, n + 1)
                        nc.scalar.activation(hid[:, n * BANK:(n + 1) * BANK], ps[0:TD, n, :], ACT.Tanh).then_inc(hidden, 1)
                    for n in range(2):
                        for f in range(CT):
                            act.wait_ge(ready, 3 + 2 * n + f)
                            link(nc.scalar.activation(at(dec, f, n), ps[:, 2 + 2 * n + f, :], ACT.Exp,
                                                      bias=decay[:, f:f + 1]))
                            nc.scalar.activation(at(dec, f, n), at(dec, f, n), ACT.Exp, scale=-1.0)
        y, bonus, t1 = sb([P, CT, N]), sb([P, CT, N]), sb([P, CT, N])
        scan = sb([P, 2, 2, T + 1])
        kv, prod = sb([P, 2, BANK]), sb([P, 3, BANK])
        with phase(core) as (block,):
            @block.vector
            def _(dve):
                for f in range(CT):
                    nc.vector.scalar_tensor_tensor(out=bonus[:, f, :], in0=r[:, f, :], scalar=u[:, f:f + 1],
                                                   in1=k[:, f, :], op0=ALU.mult, op1=ALU.mult)
                nc.vector.memset(scan[:, :, :, 0:1], 0.0)
        linear_block(core, core.block16, bonus, lambda f, n, q: nc.vector.tensor_tensor(
            at(y, f, n), q, at(v, f, n), ALU.mult), "vector")
        units = [(f, n, i) for f in range(CT) for n in range(2) for i in range(D)]
        with phase(core, "spread", "bank_free", "kv_done", "scan_done", "prod_done", "summed") as (
                block, spread, bank_free, kv_done, scan_done, prod_done, summed):
            @block.tensor
            def _(pe):
                for j, (f, n, i) in enumerate(units):
                    s = 3 * (j % 2)
                    if j >= 2:
                        pe.wait_ge(bank_free, j - 1)
                    for q, src in enumerate((k, dec, r)):
                        nc.tensor.matmul(ps[:, s + q, :], sel[:, i, :], at(src, f, n), start=True,
                                         stop=True).then_inc(spread, 1)

            @block.vector
            def _(dve):
                for j, (f, n, i) in enumerate(units):
                    s, e = 3 * (j % 2), j % 2
                    dve.wait_ge(spread, 3 * j + 1)
                    nc.vector.tensor_tensor(kv[:, e, :], ps[:, s, :], at(v, f, n), ALU.mult).then_inc(kv_done, 1)
                    dve.wait_ge(kv_done, j + 1)
                    dve.wait_ge(spread, 3 * j + 2)
                    for b in range(2):
                        nc.vector.tensor_tensor_scan(scan[:, e, b, 1:T + 1], ps[:, s + 1, b * T:(b + 1) * T],
                                                     kv[:, e, b * T:(b + 1) * T], 0.0, ALU.mult,
                                                     ALU.add).then_inc(scan_done, 1)
                    dve.wait_ge(scan_done, 2 * j + 2)
                    dve.wait_ge(spread, 3 * j + 3)
                    if j >= 3:
                        dve.wait_ge(summed, j - 2)
                    nc.vector.tensor_tensor(prod[:, j % 3, :].rearrange("p (b t) -> p b t", b=2),
                                            ps[:, s + 2, :].rearrange("p (b t) -> p b t", b=2),
                                            scan[:, e, :, 0:T], ALU.mult).then_inc(bank_free, 1)

            @block.gpsimd
            def _(pool):
                for j, (f, n, i) in enumerate(units):
                    pool.wait_ge(bank_free, j + 1)
                    if j >= 1:
                        pool.wait_ge(summed, j)
                    nc.gpsimd.tensor_tensor(at(y, f, n), at(y, f, n), prod[:, j % 3, :], ALU.add).then_inc(summed, 1)
        linear_block(core, core.block16, y, lambda f, n, q: nc.vector.scalar_tensor_tensor(
            out=at(t1, f, n), in0=q, scalar=-1.0 / D, in1=at(y, f, n), op0=ALU.mult, op1=ALU.add), "vector")
        with phase(core) as (block,):
            @block.vector
            def _(dve):
                for f in range(CT):
                    nc.vector.tensor_tensor(y[:, f, :], t1[:, f, :], t1[:, f, :], ALU.mult)
        linear_block(core, core.block16, y, lambda f, n, q: nc.vector.tensor_scalar(
            at(bonus, f, n), q, 1.0 / D, EPS, ALU.mult, ALU.add), "vector")
        with phase(core, "root", "w") as (block, root, w):
            @block.scalar
            def _(act):
                for f in range(CT):
                    nc.scalar.activation(bonus[:, f, :], bonus[:, f, :], ACT.Sqrt).then_inc(root, 1)

            @block.vector
            def _(dve):
                link = chain(dve, w)
                for f in range(CT):
                    dve.wait_ge(root, f + 1)
                    link(nc.vector.reciprocal(bonus[:, f, :], bonus[:, f, :]))
                    link(nc.vector.tensor_tensor(t1[:, f, :], t1[:, f, :], bonus[:, f, :], ALU.mult))
                    link(nc.vector.tensor_scalar(t1[:, f, :], t1[:, f, :], gamma[:, f:f + 1], beta[:, f:f + 1],
                                                 ALU.mult, ALU.add))
                    nc.vector.tensor_tensor(t1[:, f, :], t1[:, f, :], g[:, f, :], ALU.mult)
        linear_tokens(core, t1, wo, CT, C, add_to_residual(core))


def linear_block(core, w, x, finish, engine):
    nc, ps = core.nc, core.ps
    tiles = [(f, n) for f in range(CT) for n in range(N // BANK)]
    with phase(core, "ready") as (block, ready):
        @block.tensor
        def _(pe):
            for i, (f, n) in enumerate(tiles):
                nc.tensor.matmul(ps[:, i, :], w[:, :], x[:, f, n * BANK:(n + 1) * BANK], start=True,
                                 stop=True).then_inc(ready, 1)

        def empty(eng):
            for i, (f, n) in enumerate(tiles):
                eng.wait_ge(ready, i + 1)
                finish(f, n, ps[:, i, :])

        if engine == "scalar":
            block.scalar(empty)
        else:
            block.vector(empty)



def pick_top(core, dve, link, scores, left, top, few):
    nc = core.nc
    for t in range(TT):
        last = nc.vector.max(top[:, t, :], scores[:, t, :])
    link(last)
    if few < 8:
        link(nc.vector.memset(top[:, :, few:8], -1.0))
    for t in range(TT):
        last = nc.vector.match_replace(left[:, t, :], top[:, t, :], scores[:, t, :], -2.0)
    link(last)


def expert_bias(core, weights, bias, e):
    nc, ps = core.nc, core.ps
    with ExitStack() as c:
        wT = core.allocator(c)([e, N])
        with phase(core, "turned", "copied", "ready") as (block, turned, copied, ready):
            @block.tensor
            def _(pe):
                for t in range(TT):
                    nc.tensor.transpose(ps[0:e, t // 4, (t % 4) * P:(t % 4 + 1) * P], weights[:, t, :],
                                        core.ident[:, :]).then_inc(turned, 1)
                for t in range(TT):
                    pe.wait_ge(copied, t // 4 + 1)
                    nc.tensor.matmul(ps[:, 2 + t // 2, (t % 2) * C:(t % 2 + 1) * C], wT[:, t * P:(t + 1) * P],
                                     bias, start=True, stop=True).then_inc(ready, 1)

            @block.scalar
            def _(act):
                for half in range(2):
                    act.wait_ge(turned, 4 * half + 4)
                    nc.scalar.copy(wT[:, half * BANK:(half + 1) * BANK], ps[0:e, half, :]).then_inc(copied, 1)

            @block.vector
            def _(dve):
                for t in range(TT):
                    dve.wait_ge(ready, t // 2 * 2 + 2)
                    nc.vector.tensor_tensor(core.x[:, t, :], ps[:, 2 + t // 2, (t % 2) * C:(t % 2 + 1) * C],
                                            core.x[:, t, :], ALU.add)


def l0_ffn(core):
    nc, d, ps = core.nc, core.dram, core.ps
    E, F, PICK = 64, 192, 8
    with ExitStack() as c:
        sb = core.allocator(c)
        gate = sb([P, CT, E])
        s, left, weights = sb([P, TT, E]), sb([P, TT, E]), sb([P, TT, E])
        top, small = sb([P, TT, 8]), sb([P, 3, TT, 1])
        layer_norm(core, core.x, core.xn, core.xnT, loads=[(gate[:, :, :], ktiles(d["L0_ffn_gate_w"]))])
        linear_tokens(core, core.xnT, gate, CT, E, lambda t, q: nc.vector.tensor_copy(s[:, t, :], q))
        spread = lambda i: small[:, i].to_broadcast([P, TT, E])
        with phase(core, "centred", "exp_done", "w") as (block, centred, exp_done, w):
            @block.vector
            def _(dve):
                link = chain(dve, w)
                link(nc.vector.tensor_reduce(small[:, 0, :, 0], s[:, :, :], AX.X, ALU.max))
                nc.vector.tensor_tensor(s[:, :, :], s[:, :, :], spread(0), ALU.subtract).then_inc(centred, 1)
                dve.wait_ge(exp_done, 1)
                link(nc.vector.tensor_reduce(small[:, 1, :, 0], s[:, :, :], AX.X, ALU.add))
                link(nc.vector.reciprocal(small[:, 1, :, :], small[:, 1, :, :]))
                link(nc.vector.tensor_tensor(s[:, :, :], s[:, :, :], spread(1), ALU.mult))
                pick_top(core, dve, link, s, left, top, PICK)
                link(nc.vector.tensor_reduce(small[:, 2, :, 0], top[:, :, :], AX.X, ALU.add))
                link(nc.vector.tensor_scalar(small[:, 2, :, :], small[:, 2, :, :], 1e-20, None, ALU.add))
                link(nc.vector.reciprocal(small[:, 2, :, :], small[:, 2, :, :]))
                link(nc.vector.tensor_scalar(left[:, :, :], left[:, :, :], -1.0, None, ALU.is_le))
                link(nc.vector.tensor_tensor(weights[:, :, :], s[:, :, :], left[:, :, :], ALU.mult))
                nc.vector.tensor_tensor(weights[:, :, :], weights[:, :, :], spread(2), ALU.mult)

            @block.scalar
            def _(act):
                act.wait_ge(centred, 1)
                nc.scalar.activation(s[:, :, :], s[:, :, :], ACT.Exp).then_inc(exp_done, 1)
        sparse_experts(core, weights, E)


def sparse_experts(core, weights, E):
    nc, d, ps = core.nc, core.dram, core.ps
    HT3 = 3
    with ExitStack() as c:
        sb = core.allocator(c)
        wgu = [sb([P, CT, 2, HT3 * P]) for _ in range(2)]
        wd = [sb([P, HT3, C]) for _ in range(2)]
        gs = sb([P, 2, BANK])
        h = sb([P, HT3, N])
        with nc.Fori(0, E // 4) as q:
            with phase(core, "wgu_a", "wgu_b", "wd_a", "wd_b", "up_ready", "silu_done", "h_ready", "down_ready",
                       "down_used") as (block, wgu_a, wgu_b, wd_a, wd_b, up_ready, silu_done, h_ready, down_ready,
                                        down_used):
                units = [(e, j, n) for e in range(2) for j in range(HT3) for n in range(2)]
                downs = [(e, i, t) for e in range(2) for i in range(2) for t in range(TT)]

                @block.sync
                def _(sp):
                    for e in range(2):
                        sp.dma_start(wgu[e][:, :, :, :], d["L0_ffn_wgu"][2 * q + e]).then_inc((wgu_a, wgu_b)[e], 16)
                        sp.dma_start(wd[e][:, :, :], d["L0_ffn_wd"][2 * q + e]).then_inc((wd_a, wd_b)[e], 16)

                @block.tensor
                def _(pe):
                    dn = 0
                    for e in range(2):
                        pe.wait_ge((wgu_a, wgu_b)[e], 16)
                        for j in range(HT3):
                            for n in range(2):
                                i = (e * HT3 + j) * 2 + n
                                if i >= 2:
                                    pe.wait_ge(h_ready, i - 1)
                                for kind in range(2):
                                    for k in range(CT):
                                        mm = nc.tensor.matmul(ps[:, 2 * (i % 2) + kind, :],
                                                              wgu[e][:, k, kind, j * P:(j + 1) * P],
                                                              core.xnT[:, k, n * BANK:(n + 1) * BANK],
                                                              start=k == 0, stop=k == CT - 1)
                                    mm.then_inc(up_ready, 1)
                        pe.wait_ge((wd_a, wd_b)[e], 16)
                        pe.wait_ge(h_ready, 2 * HT3 * (e + 1))
                        for i in range(2):
                            for t in range(TT):
                                if dn >= 4:
                                    pe.wait_ge(down_used, dn - 3)
                                out = ps[:, 4 + dn % 4, 0:C]
                                nc.tensor.matmul(out, h[:, i, t * P:(t + 1) * P], wd[e][:, i, :], start=True, stop=False)
                                nc.tensor.matmul(out, h[64 * i:64 * i + 64, 2, t * P:(t + 1) * P],
                                                 wd[e][64 * i:64 * i + 64, 2, :], start=False,
                                                 stop=True).then_inc(down_ready, 1)
                                dn += 1

                @block.scalar
                def _(act):
                    for i, (e, j, n) in enumerate(units):
                        act.wait_ge(up_ready, 2 * i + 1)
                        if i >= 2:
                            act.wait_ge(h_ready, i - 1)
                        nc.scalar.activation(gs[:, i % 2, :], ps[:, 2 * (i % 2), :], ACT.Silu).then_inc(silu_done, 1)

                @block.vector
                def _(dve):
                    def add(dn):
                        e, i, t = downs[dn]
                        dve.wait_ge(down_ready, dn + 1)
                        nc.vector.scalar_tensor_tensor(
                            out=core.x[:, t, :], in0=ps[:, 4 + dn % 4, 0:C],
                            scalar=weights[:, t, bass.ds(4 * q + 2 * e + i, 1)], in1=core.x[:, t, :],
                            op0=ALU.mult, op1=ALU.add).then_inc(down_used, 1)

                    for i, (e, j, n) in enumerate(units):
                        dve.wait_ge(silu_done, i + 1)
                        dve.wait_ge(up_ready, 2 * i + 2)
                        if e == 1 and j == 0 and n == 0:
                            dve.wait_ge(down_ready, 2 * TT)
                        nc.vector.tensor_tensor(h[:, j, n * BANK:(n + 1) * BANK], gs[:, i % 2, :],
                                                ps[:, 2 * (i % 2) + 1, :], ALU.mult).then_inc(h_ready, 1)
                        if j == HT3 - 1 and n == 1:
                            for t in range(2 * TT):
                                if t >= 1 or e >= 1:
                                    dve.wait_ge(down_used, 2 * TT * e + t)
                                add(2 * TT * e + t)


def l1_attn(core):
    nc, d, ps = core.nc, core.dram, core.ps
    E, F, HR, PICK, PAD = 6, 384, 128, 2, 16
    FT = F // P
    with ExitStack() as c:
        sb = core.allocator(c)
        r1w, r2w = sb([P, CT, HR]), sb([HR, E])
        rows = sb([1, HR])
        lng, lnb = sb([P, 1]), sb([P, 1])
        r2b, route_bias, temp = sb([P, E]), sb([P, E]), sb([P, 1])
        b1, b2 = sb([P, E, FT]), sb([E, C])
        hr, hn, hT = sb([P, TT, HR]), sb([P, TT, HR]), sb([P, N])
        s, left, weights = sb([P, TT, PAD]), sb([P, TT, PAD]), sb([P, TT, E])
        top, small = sb([P, TT, 8]), sb([P, 3, TT, 1])
        stats, mv, rstd = sb([P, TT, 6]), sb([P, TT, 2]), sb([P, TT])
        layer_norm(core, core.x, core.xn, core.xnT, loads=[
            (r1w[:, :, :], ktiles(d["L1_attn_r1_w"])), (r2w[:, :], d["L1_attn_r2_w"]), (rows[:, :], d["L1_attn_r1_b"]),
            (lng[:, :], d["L1_attn_ln_g"]), (lnb[:, :], d["L1_attn_ln_b"]), (r2b[:, :], d["L1_attn_r2_b"]),
            (route_bias[:, :], d["L1_attn_route_bias"]), (temp[:, :], d["L1_attn_temp"]),
            (b1[:, :, :], d["L1_attn_b1"]), (b2[:, :], d["L1_attn_b2"])])
        linear_tokens(core, core.xnT, r1w, CT, HR, lambda t, q: nc.vector.tensor_copy(hr[:, t, :], q), bias=rows[:, :])
        with phase(core, "w", "var_ready", "root_done", "norm_done", "turned", "gelu_done", "logits", "exp_done",
                   "centred") as (block, w, var_ready, root_done, norm_done, turned, gelu_done, logits, exp_done,
                                  centred):
            @block.vector
            def _(dve):
                link = chain(dve, w)
                for t in range(TT):
                    link(nc.vector.bn_stats(stats[:, t, :], hr[:, t, :]))
                for t in range(TT):
                    link(nc.vector.bn_aggr(mv[:, t, :], stats[:, t, :]))
                nc.vector.tensor_scalar(rstd[:, :], mv[:, :, 1], 1e-5, None, ALU.add).then_inc(var_ready, 1)
                link(nc.vector.reciprocal(temp[:, :], temp[:, :]))
                dve.wait_ge(root_done, 1)
                link(nc.vector.reciprocal(rstd[:, :], rstd[:, :]))
                for t in range(TT):
                    nc.vector.tensor_scalar(hn[:, t, :], hr[:, t, :], mv[:, t, 0:1], rstd[:, t:t + 1],
                                            ALU.subtract, ALU.mult).then_inc(norm_done, 1)
                dve.wait_ge(logits, TT)
                link(nc.vector.memset(s[:, :, E:PAD], -1.0))
                spread_e = lambda ap: ap.unsqueeze(1).to_broadcast([P, TT, E])
                se = s[:, :, 0:E]
                link(nc.vector.tensor_tensor(se, ps[:, 2, 0:TT * E].rearrange("p (t e) -> p t e", e=E),
                                             spread_e(r2b[:, :]), ALU.add))
                link(nc.vector.tensor_scalar(se, se, temp[:, 0:1], None, ALU.mult))
                link(nc.vector.tensor_tensor(se, se, spread_e(route_bias[:, :]), ALU.add))
                spread = lambda i: small[:, i].to_broadcast([P, TT, E])
                link(nc.vector.tensor_reduce(small[:, 0, :, 0], se, AX.X, ALU.max))
                nc.vector.tensor_tensor(se, se, spread(0), ALU.subtract).then_inc(centred, 1)
                dve.wait_ge(exp_done, 1)
                link(nc.vector.tensor_reduce(small[:, 1, :, 0], se, AX.X, ALU.add))
                link(nc.vector.reciprocal(small[:, 1, :, :], small[:, 1, :, :]))
                link(nc.vector.tensor_tensor(se, se, spread(1), ALU.mult))
                pick_top(core, dve, link, s, left, top, PICK)
                link(nc.vector.tensor_scalar(left[:, :, 0:E], left[:, :, 0:E], -1.5, None, ALU.is_le))
                nc.vector.tensor_tensor(weights[:, :, :], se, left[:, :, 0:E], ALU.mult)

            @block.tensor
            def _(pe):
                for t in range(TT):
                    pe.wait_ge(norm_done, t + 1)
                    nc.tensor.transpose(ps[:, t // 4, (t % 4) * P:(t % 4 + 1) * P], hn[:, t, :],
                                        core.ident[:, :]).then_inc(turned, 1)
                for t in range(TT):
                    pe.wait_ge(gelu_done, t // 4 + 1)
                    nc.tensor.matmul(ps[:, 2, t * E:(t + 1) * E], hT[:, t * P:(t + 1) * P], r2w[:, :], start=True,
                                     stop=True).then_inc(logits, 1)

            @block.scalar
            def _(act):
                act.wait_ge(var_ready, 1)
                nc.scalar.activation(rstd[:, :], rstd[:, :], ACT.Sqrt).then_inc(root_done, 1)
                for half in range(2):
                    act.wait_ge(turned, 4 * half + 4)
                    nc.scalar.activation(hT[:, half * BANK:(half + 1) * BANK], ps[:, half, :], ACT.Gelu,
                                         bias=lnb[:, 0:1], scale=lng[:, 0:1]).then_inc(gelu_done, 1)
                act.wait_ge(centred, 1)
                nc.scalar.activation(s[:, :, 0:E], s[:, :, 0:E], ACT.Exp).then_inc(exp_done, 1)
        expert_bias(core, weights, b2[:, :], E)
        w1 = [sb([P, CT, F]) for _ in range(2)]
        w2 = [sb([P, FT, C]) for _ in range(2)]
        h = sb([P, FT, N])
        with nc.Fori(0, E // 2) as q:
            with phase(core, "w_a", "w_b", "up_ready", "h_ready", "down_ready", "down_used") as (
                    block, w_a, w_b, up_ready, h_ready, down_ready, down_used):
                landed = (w_a, w_b)
                units = [(m, n) for m in range(FT) for n in range(2)]

                @block.sync
                def _(sp):
                    for e in range(2):
                        sp.dma_start(w1[e][:, :, :], d["L1_attn_W1"][2 * q + e].rearrange("(k p) f -> p k f", p=P)
                                     ).then_inc(landed[e], 16)
                        sp.dma_start(w2[e][:, :, :], d["L1_attn_W2"][2 * q + e].rearrange("(k p) f -> p k f", p=P)
                                     ).then_inc(landed[e], 16)

                @block.tensor
                def _(pe):
                    for e in range(2):
                        pe.wait_ge(landed[e], 32)
                        for i, (m, n) in enumerate(units):
                            j = len(units) * e + i
                            if j >= 4:
                                pe.wait_ge(h_ready, j - 3)
                            for k in range(CT):
                                mm = nc.tensor.matmul(ps[:, j % 4, :], w1[e][:, k, m * P:(m + 1) * P],
                                                      core.xnT[:, k, n * BANK:(n + 1) * BANK], start=k == 0,
                                                      stop=k == CT - 1)
                            mm.then_inc(up_ready, 1)
                        pe.wait_ge(h_ready, len(units) * (e + 1))
                        for t in range(TT):
                            j = TT * e + t
                            if j >= 4:
                                pe.wait_ge(down_used, j - 3)
                            for m in range(FT):
                                mm = nc.tensor.matmul(ps[:, 4 + j % 4, 0:C], h[:, m, t * P:(t + 1) * P], w2[e][:, m, :],
                                                      start=m == 0, stop=m == FT - 1)
                            mm.then_inc(down_ready, 1)

                @block.scalar
                def _(act):
                    for e in range(2):
                        for i, (m, n) in enumerate(units):
                            j = len(units) * e + i
                            act.wait_ge(up_ready, j + 1)
                            if e == 1 and i == 0:
                                act.wait_ge(down_ready, TT)
                            nc.scalar.activation(h[:, m, n * BANK:(n + 1) * BANK], ps[:, j % 4, :],
                                                 ACT.Gelu if e == 0 else ACT.Silu,
                                                 bias=b1[:, bass.ds(2 * q + e, 1), m]).then_inc(h_ready, 1)

                @block.vector
                def _(dve):
                    for j in range(2 * TT):
                        e, t = j // TT, j % TT
                        dve.wait_ge(down_ready, j + 1)
                        if j >= 1:
                            dve.wait_ge(down_used, j)
                        nc.vector.scalar_tensor_tensor(out=core.x[:, t, :], in0=ps[:, 4 + j % 4, 0:C],
                                                       scalar=weights[:, t, bass.ds(2 * q + e, 1)],
                                                       in1=core.x[:, t, :], op0=ALU.mult,
                                                       op1=ALU.add).then_inc(down_used, 1)


def l1_ffn(core):
    nc, d, ps = core.nc, core.dram, core.ps
    E, G, I, PICK, PICKG, ROUTE = 16, 4, 256, 4, 2, 2.5
    IT, GP = I // P, 16
    with ExitStack() as c:
        sb = core.allocator(c)
        gate = sb([P, CT, E])
        s, masked, left, weights = (sb([P, TT, E]) for _ in range(4))
        gs, gleft = sb([P, TT, GP]), sb([P, TT, GP])
        top, small = sb([P, TT, 8]), sb([P, TT, 1])
        b1, b3, b2 = sb([P, E, IT]), sb([P, E, IT]), sb([E, C])
        layer_norm(core, core.x, core.xn, core.xnT, loads=[
            (gate[:, :, :], ktiles(d["L1_ffn_Wg"])), (b1[:, :, :], d["L1_ffn_b1"]), (b3[:, :, :], d["L1_ffn_b3"]),
            (b2[:, :], d["L1_ffn_b2"])])
        linear_tokens(core, core.xnT, gate, CT, E, lambda t, q: nc.scalar.activation(s[:, t, :], q, ACT.Sigmoid),
                      engine="scalar")
        with phase(core, "w") as (block, w):
            @block.vector
            def _(dve):
                link = chain(dve, w)
                grouped = lambda ap: ap.rearrange("p t (g e) -> p t g e", g=G)
                link(nc.vector.memset(gs[:, :, G:GP], -1.0))
                link(nc.vector.tensor_reduce(gs[:, :, 0:G], grouped(s[:, :, :]), AX.X, ALU.max))
                pick_top(core, dve, link, gs, gleft, top, PICKG)
                link(nc.vector.tensor_scalar(gleft[:, :, :], gleft[:, :, :], -1.5, None, ALU.is_le))
                link(nc.vector.tensor_scalar(masked[:, :, :], s[:, :, :], 1.0, None, ALU.add))
                link(nc.vector.tensor_tensor(grouped(masked[:, :, :]), grouped(masked[:, :, :]),
                                             gleft[:, :, 0:G].unsqueeze(3).to_broadcast([P, TT, G, E // G]), ALU.mult))
                link(nc.vector.tensor_scalar(masked[:, :, :], masked[:, :, :], -1.0, None, ALU.add))
                pick_top(core, dve, link, masked, left, top, PICK)
                link(nc.vector.tensor_tensor(left[:, :, :], masked[:, :, :], left[:, :, :], ALU.subtract))
                link(nc.vector.tensor_scalar(left[:, :, :], left[:, :, :], 1.5, None, ALU.is_ge))
                link(nc.vector.tensor_tensor(weights[:, :, :], s[:, :, :], left[:, :, :], ALU.mult))
                link(nc.vector.tensor_reduce(small[:, :, 0], weights[:, :, :], AX.X, ALU.add))
                link(nc.vector.reciprocal(small[:, :, :], small[:, :, :]))
                link(nc.vector.tensor_scalar(small[:, :, :], small[:, :, :], ROUTE, None, ALU.mult))
                nc.vector.tensor_tensor(weights[:, :, :], weights[:, :, :], small[:, :, :].to_broadcast([P, TT, E]),
                                        ALU.mult)
        expert_bias(core, weights, b2[:, :], E)
        w13 = [sb([P, CT, 2, I]) for _ in range(2)]
        w2 = [sb([P, IT, C]) for _ in range(2)]
        gate_h, h = sb([P, 2, BANK]), sb([P, IT, N])
        with nc.Fori(0, E // 2) as q:
            with phase(core, "w_a", "w_b", "up_ready", "silu_done", "h_ready", "down_ready", "down_used") as (
                    block, w_a, w_b, up_ready, silu_done, h_ready, down_ready, down_used):
                landed = (w_a, w_b)
                units = [(e, m, n) for e in range(2) for m in range(IT) for n in range(2)]

                @block.sync
                def _(sp):
                    for e in range(2):
                        sp.dma_start(w13[e][:, :, :, :], d["L1_ffn_W13"][2 * q + e]).then_inc(landed[e], 16)
                        sp.dma_start(w2[e][:, :, :], d["L1_ffn_W2"][2 * q + e].rearrange("(k p) f -> p k f", p=P)
                                     ).then_inc(landed[e], 16)

                @block.tensor
                def _(pe):
                    for e in range(2):
                        pe.wait_ge(landed[e], 32)
                        for i in range(2 * IT):
                            j = 2 * IT * e + i
                            _, m, n = units[j]
                            if j >= 2:
                                pe.wait_ge(h_ready, j - 1)
                            for kind in range(2):
                                for k in range(CT):
                                    mm = nc.tensor.matmul(ps[:, 2 * (j % 2) + kind, :],
                                                          w13[e][:, k, kind, m * P:(m + 1) * P],
                                                          core.xnT[:, k, n * BANK:(n + 1) * BANK], start=k == 0,
                                                          stop=k == CT - 1)
                                mm.then_inc(up_ready, 1)
                        pe.wait_ge(h_ready, 2 * IT * (e + 1))
                        for t in range(TT):
                            j = TT * e + t
                            if j >= 4:
                                pe.wait_ge(down_used, j - 3)
                            for m in range(IT):
                                mm = nc.tensor.matmul(ps[:, 4 + j % 4, 0:C], h[:, m, t * P:(t + 1) * P], w2[e][:, m, :],
                                                      start=m == 0, stop=m == IT - 1)
                            mm.then_inc(down_ready, 1)

                @block.scalar
                def _(act):
                    for j, (e, m, n) in enumerate(units):
                        act.wait_ge(up_ready, 2 * j + 1)
                        if j >= 2:
                            act.wait_ge(h_ready, j - 1)
                        nc.scalar.activation(gate_h[:, j % 2, :], ps[:, 2 * (j % 2), :], ACT.Silu,
                                             bias=b1[:, bass.ds(2 * q + e, 1), m]).then_inc(silu_done, 1)

                @block.vector
                def _(dve):
                    for j, (e, m, n) in enumerate(units):
                        dve.wait_ge(silu_done, j + 1)
                        dve.wait_ge(up_ready, 2 * j + 2)
                        if e == 1 and m == 0 and n == 0:
                            dve.wait_ge(down_ready, TT)
                        nc.vector.scalar_tensor_tensor(out=h[:, m, n * BANK:(n + 1) * BANK],
                                                       in0=ps[:, 2 * (j % 2) + 1, :],
                                                       scalar=b3[:, bass.ds(2 * q + e, 1), m], in1=gate_h[:, j % 2, :],
                                                       op0=ALU.add, op1=ALU.mult).then_inc(h_ready, 1)
                        if m == IT - 1 and n == 1:
                            for t in range(TT):
                                i = TT * e + t
                                dve.wait_ge(down_ready, i + 1)
                                if i >= 1:
                                    dve.wait_ge(down_used, i)
                                nc.vector.scalar_tensor_tensor(out=core.x[:, t, :], in0=ps[:, 4 + i % 4, 0:C],
                                                               scalar=weights[:, t, bass.ds(2 * q + e, 1)],
                                                               in1=core.x[:, t, :], op0=ALU.mult,
                                                               op1=ALU.add).then_inc(down_used, 1)

def attend(core, heads, spans, score, turns, weigh, per_bank, dest):
    nc, ps = core.nc, core.ps
    total = sum(w for _, w in spans)
    with ExitStack() as c:
        sb = core.allocator(c)
        p, pT = sb([P, 3, BANK]), sb([P, 3, BANK])
        nm, z = sb([P, 4, 2]), sb([P, 4, 2])
        with phase(core, "scored", "max_done", "exp_done", "inv_done", "normed", "turned", "copied", "weighed",
                   "taken") as (block, scored, max_done, exp_done, inv_done, normed, turned, copied, weighed, taken):
            @block.tensor
            def _(pe):
                for i in range(heads + 4):
                    if i < heads:
                        if i >= 2:
                            pe.wait_ge(exp_done, 2 * (i - 1))
                        score(i, ps[:, i % 2, :]).then_inc(scored, 1)
                    j = i - 2
                    if 0 <= j < heads:
                        pe.wait_ge(normed, 2 * (j + 1))
                        if j >= 2:
                            pe.wait_ge(copied, j - 1)
                        for a, b in turns:
                            mm = nc.tensor.transpose(ps[:, 2 + j % 2, b:b + P], p[:, j % 3, a:a + P],
                                                     core.ident[:, :])
                        mm.then_inc(turned, 1)
                    j = i - 4
                    if 0 <= j < heads:
                        group = j // per_bank
                        pe.wait_ge(copied, j + 1)
                        if j % per_bank == 0 and group >= 2:
                            pe.wait_ge(taken, group - 1)
                        weigh(j, pT[:, j % 3, :], ps[:, 4 + group % 2, :]).then_inc(weighed, 1)

            @block.vector
            def _(dve):
                def maxima(i):
                    dve.wait_ge(scored, i + 1)
                    if i >= 4:
                        dve.wait_ge(exp_done, 2 * (i - 3))
                    for s, (a, w) in enumerate(spans):
                        nc.vector.tensor_reduce(nm[:, i % 4, s:s + 1], ps[:, i % 2, a:a + w], AX.X, ALU.max,
                                                negate=True).then_inc(max_done, 1)

                def norm(i):
                    dve.wait_ge(exp_done, 2 * (i + 1))
                    nc.vector.reciprocal(z[:, i % 4, :], z[:, i % 4, :]).then_inc(inv_done, 1)
                    dve.wait_ge(inv_done, i + 1)
                    for s, (a, w) in enumerate(spans):
                        nc.vector.tensor_scalar(p[:, i % 3, a:a + w], p[:, i % 3, a:a + w], z[:, i % 4, s:s + 1], None,
                                                ALU.mult).then_inc(normed, 1)

                def take(g):
                    dve.wait_ge(weighed, per_bank * (g + 1))
                    nc.vector.tensor_copy(dest(g), ps[:, 4 + g % 2, 0:T]).then_inc(taken, 1)

                for i in range(heads + 6):
                    if i < heads:
                        maxima(i)
                    if 1 <= i <= heads:
                        norm(i - 1)
                    if i >= 6 and (i - 5) % per_bank == 0:
                        take((i - 5) // per_bank - 1)

            @block.scalar
            def _(act):
                for i in range(heads + 3):
                    if i < heads:
                        act.wait_ge(max_done, 2 * (i + 1))
                        if i >= 3:
                            act.wait_ge(turned, i - 2)
                        if i >= 4:
                            act.wait_ge(normed, 2 * (i - 3))
                        for s, (a, w) in enumerate(spans):
                            nc.scalar.activation(p[:, i % 3, a:a + w], ps[:, i % 2, a:a + w], ACT.Exp,
                                                 bias=nm[:, i % 4, s:s + 1],
                                                 accum_out=z[:, i % 4, s:s + 1]).then_inc(exp_done, 1)
                    j = i - 2
                    if 0 <= j < heads:
                        act.wait_ge(turned, j + 1)
                        if j >= 3:
                            act.wait_ge(weighed, j - 2)
                        nc.scalar.copy(pT[:, j % 3, 0:total], ps[:, 2 + j % 2, 0:total]).then_inc(copied, 1)


def l2_attn(core):
    nc, d, ps = core.nc, core.dram, core.ps
    HD = 64
    M = H * HD // P
    with ExitStack() as c:
        sb = core.allocator(c)
        w_in, w_out = sb([P, CT, 3 * H * HD]), sb([P, M, C])
        b_qk, b_v, b_out = sb([P, 2 * M]), sb([P, H * HD]), sb([P, C])
        cos, sin, turn = sb([P, T]), sb([P, T]), sb([P, P])
        causal_wide, causal, identb = sb([P, P]), sb([P, P], BF16), sb([P, P], BF16)
        xb = sb([P, CT, T])
        raw, t2 = sb([P, 3, T]), sb([P, 2, T])
        qk, v, o = sb([P, 2 * M, T]), sb([P, 2, H * HD]), sb([P, M, T])
        layer_norm(core, core.x, core.xn, core.xnT, loads=[
            (w_in[:, :, :], ktiles(d["L2_attn_W_in"])), (w_out[:, :, :], ktiles(d["L2_attn_W_out"])),
            (b_qk[:, :], d["L2_attn_b_qk"]), (b_v[:, :], d["L2_attn_b_v"]), (b_out[:, :], d["L2_attn_b_out"]),
            (cos[:, :], d["c_cos64"]), (sin[:, :], d["c_sin64"]), (turn[:, :], d["c_turn64"]),
            (causal_wide[:, :], d["c_causal"])])
        with phase(core, "w") as (block, w):
            @block.vector
            def _(dve):
                nc.vector.tensor_copy(identb[:, :], core.ident[:, :])
                nc.vector.tensor_copy(causal[:, :], causal_wide[:, :])
                nc.vector.tensor_scalar(b_qk[:, 0:M], b_qk[:, 0:M], HD ** -0.5, None, ALU.mult)
                for t in range(TT):
                    nc.vector.tensor_tensor(core.x[:, t, :], core.x[:, t, :], b_out[:, :], ALU.add)
        with nc.Fori(0, B) as b:
            with phase(core, "sliced", "product", "raw_done", "turned", "rot_done", "sum_done", "v_product",
                       "cos_done") as (block, sliced, product, raw_done, turned, rot_done, sum_done, v_product, cos_done):
                vt = [(t, n) for t in range(2) for n in range(2)]

                @block.tensor
                def _(pe):
                    pe.wait_ge(sliced, 1)
                    for i in range(2 * M + 1):
                        if i < 2 * M:
                            if i >= 2:
                                pe.wait_ge(raw_done, i - 1)
                            for k in range(CT):
                                mm = nc.tensor.matmul(ps[:, i % 2, 0:T], w_in[:, k, i * P:(i + 1) * P], xb[:, k, :],
                                                      start=k == 0, stop=k == CT - 1)
                            mm.then_inc(product, 1)
                        if i >= 1:
                            j = i - 1
                            pe.wait_ge(raw_done, j + 1)
                            if j >= 2:
                                pe.wait_ge(rot_done, j - 1)
                            nc.tensor.matmul(ps[:, 2 + j % 2, 0:T], turn[:, :], raw[:, j % 3, :], start=True,
                                             stop=True).then_inc(turned, 1)
                    for j, (t, n) in enumerate(vt):
                        for k in range(CT):
                            mm = nc.tensor.matmul(ps[:, 4 + j, :], xb[:, k, t * P:(t + 1) * P],
                                                  w_in[:, k, 2 * M * P + n * BANK:2 * M * P + (n + 1) * BANK],
                                                  start=k == 0, stop=k == CT - 1)
                        mm.then_inc(v_product, 1)

                @block.scalar
                def _(act):
                    for i in range(2 * M):
                        act.wait_ge(product, i + 1)
                        if i >= 3:
                            act.wait_ge(turned, i - 2)
                            act.wait_ge(sum_done, i - 2)
                        nc.scalar.activation(raw[:, i % 3, :], ps[:, i % 2, 0:T], ACT.Identity, bias=b_qk[:, i:i + 1],
                                             scale=HD ** -0.5 if i < M else 1.0).then_inc(raw_done, 1)

                @block.vector
                def _(dve):
                    nc.vector.tensor_copy(xb[:, :, :], core.xnT[:, :, bass.ds(b * T, T)]).then_inc(sliced, 1)
                    for i in range(2 * M):
                        dve.wait_ge(raw_done, i + 1)
                        nc.vector.tensor_tensor(qk[:, i, :], raw[:, i % 3, :], cos[:, :], ALU.mult).then_inc(cos_done, 1)
                        dve.wait_ge(turned, i + 1)
                        nc.vector.tensor_tensor(t2[:, i % 2, :], ps[:, 2 + i % 2, 0:T], sin[:, :],
                                                ALU.mult).then_inc(rot_done, 1)
                        dve.wait_ge(rot_done, i + 1)
                        dve.wait_ge(cos_done, i + 1)
                        nc.vector.tensor_tensor(qk[:, i, :], qk[:, i, :], t2[:, i % 2, :], ALU.add).then_inc(sum_done, 1)
                    for j, (t, n) in enumerate(vt):
                        dve.wait_ge(v_product, j + 1)
                        nc.vector.tensor_tensor(v[:, t, n * BANK:(n + 1) * BANK], ps[:, 4 + j, :],
                                                b_v[:, n * BANK:(n + 1) * BANK], ALU.add)

            def score(h, bank):
                base, m = HD * (h % 2), h // 2
                for tile, a, w in ((0, 0, P), (1, P, 2 * P)):
                    nc.tensor.matmul(bank[:, a:a + w], qk[base:base + HD, m, tile * P:(tile + 1) * P],
                                     qk[base:base + HD, M + m, 0:w], start=True, stop=False, skip_group_check=True)
                    mm = nc.tensor.matmul(bank[:, a + w - P:a + w], identb[:, :], causal[:, :], start=False,
                                          stop=True, skip_group_check=True)
                return mm

            def weigh(h, probs, out):
                base = HD * (h % 2)
                nc.tensor.matmul(out[base:base + HD, 0:T], v[:, 0, h * HD:(h + 1) * HD], probs[:, 0:T], start=True,
                                 stop=False, skip_group_check=True)
                return nc.tensor.matmul(out[base:base + HD, P:T], v[:, 1, h * HD:(h + 1) * HD], probs[:, T:T + P],
                                        start=False, stop=True, skip_group_check=True)

            attend(core, H, [(0, P), (P, 2 * P)], score, [(0, 0), (P, P), (2 * P, 2 * P)], weigh, 2,
                   lambda g: o[:, g, :])
            with phase(core, "ready") as (block, ready):
                @block.tensor
                def _(pe):
                    for t in range(2):
                        for m in range(M):
                            mm = nc.tensor.matmul(ps[:, t, 0:C], o[:, m, t * P:(t + 1) * P], w_out[:, m, :],
                                                  start=m == 0, stop=m == M - 1)
                        mm.then_inc(ready, 1)

                @block.vector
                def _(dve):
                    for t in range(2):
                        dve.wait_ge(ready, t + 1)
                        x = core.x[:, bass.ds(2 * b + t, 1), :]
                        nc.vector.tensor_tensor(x, ps[:, t:t + 1, 0:C], x, ALU.add)


def l2_ffn(core):
    nc, d, ps = core.nc, core.dram, core.ps
    NH, HD, E, FD, TPE = 32, 8, 8, 1024, 64
    FT = FD // P
    with ExitStack() as c:
        sb = core.allocator(c)
        xfT = sb([P, CT, N])
        with ExitStack() as c2:
            sb2 = core.allocator(c2)
            w = sb2([P, 4, CT, C])
            gain, shift, mask8 = sb2([P, CT]), sb2([P, CT]), sb2([P, 16])
            oT, xaT, xa_tok = sb2([P, CT, N]), sb2([P, CT, N]), sb2([P, TT, C])
            xb, q, k = sb2([P, CT, T]), sb2([P, CT, T]), sb2([P, CT, T])
            qz, vz = sb2([P, NH, T]), sb2([P, 2, NH, 32])
            layer_norm(core, core.x, core.xn, core.xnT, loads=[
                (w[:, i, :, :], ktiles(d["L2_ffn_w" + n])) for i, n in enumerate("qkvo")] + [
                (gain[:, :], d["L2_ffn_ln_g"]), (shift[:, :], d["L2_ffn_ln_b"]), (mask8[:, :], d["c_mask8"])])
            layer_norm(core, core.xn, xa_tok, xaT, gain=gain, shift=shift)
            with phase(core) as (block,):
                @block.gpsimd
                def _(pool):
                    nc.gpsimd.memset(vz[:, :, :, :], 0.0)
            with nc.Fori(0, B) as b:
                with phase(core, "sliced", "product", "q_done") as (block, sliced, product, q_done):
                    @block.tensor
                    def _(pe):
                        pe.wait_ge(sliced, 1)
                        for i in range(2):
                            for m in range(CT):
                                for kk in range(CT):
                                    mm = nc.tensor.matmul(ps[:, 2 * i + m, 0:T], w[:, i, kk, m * P:(m + 1) * P],
                                                          xb[:, kk, :], start=kk == 0, stop=kk == CT - 1)
                                mm.then_inc(product, 1)
                        for t in range(2):
                            for kk in range(CT):
                                mm = nc.tensor.matmul(ps[:, 4 + t, 0:C], xb[:, kk, t * P:(t + 1) * P], w[:, 2, kk, :],
                                                      start=kk == 0, stop=kk == CT - 1)
                            mm.then_inc(product, 1)

                    @block.scalar
                    def _(act):
                        for m in range(CT):
                            act.wait_ge(product, m + 1)
                            nc.scalar.mul(q[:, m, :], ps[:, m, 0:T], HD ** -0.5).then_inc(q_done, 1)
                        for m in range(CT):
                            act.wait_ge(product, CT + m + 1)
                            nc.scalar.copy(k[:, m, :], ps[:, 2 + m, 0:T])

                    @block.vector
                    def _(dve):
                        nc.vector.tensor_copy(xb[:, :, :], xaT[:, :, bass.ds(b * T, T)]).then_inc(sliced, 1)
                        for h in range(NH):
                            dve.wait_ge(q_done, h // 16 + 1)
                            nc.vector.tensor_scalar(qz[:, h, :], q[:, h // 16, :], mask8[:, h % 16:h % 16 + 1], None,
                                                    ALU.mult)
                        for t in range(2):
                            dve.wait_ge(product, 2 * CT + t + 1)
                            src = ps[:, 4 + t, 0:C].rearrange("p (g j c) -> p g j c", j=4, c=HD)
                            dst = vz[:, t, :, :].rearrange("p (g j) c -> p g j c", j=4)
                            for j in range(4):
                                nc.vector.tensor_copy(dst[:, :, j, HD * j:HD * (j + 1)], src[:, :, j, :])

                def score(h, bank):
                    for t in range(2):
                        mm = nc.tensor.matmul(bank[:, t * T:(t + 1) * T], qz[:, h, t * P:(t + 1) * P], k[:, h // 16, :],
                                              start=True, stop=True)
                    return mm

                def weigh(h, probs, out):
                    g = (h % 16) // 4
                    for t in range(2):
                        mm = nc.tensor.matmul(out[32 * g:32 * g + 32, 0:T], vz[:, t, h, :], probs[:, t * T:(t + 1) * T],
                                              start=h % 4 == 0 and t == 0, stop=h % 4 == 3 and t == 1,
                                              skip_group_check=True, tile_position=(0, 32 * g))
                    return mm

                attend(core, NH, [(0, T), (T, T)], score, [(0, 0), (P, T), (T, P), (T + P, T + P)], weigh, 16,
                       lambda g: oT[:, g, bass.ds(b * T, T)])
            linear_features(core, w[:, 3, :, :], oT, CT, CT, lambda m, n, qq: nc.vector.tensor_tensor(
                xfT[:, m, n * BANK:(n + 1) * BANK], qq, core.xnT[:, m, n * BANK:(n + 1) * BANK], ALU.add), "vector")
        w1 = [sb([P, CT, FD]) for _ in range(2)]
        w2 = [sb([P, FT, C]) for _ in range(2)]
        b1, b2 = sb([P, E, FT]), sb([P, C])
        h = sb([P, FT, 2, 2, TPE])
        tmp = sb([P, 2, C])
        load(core, [(b1[:, :, :], d["L2_ffn_b1"])])
        with nc.Fori(0, E // 2) as a:
            with phase(core, "w_a", "w_b", "b2_in", "up_ready", "h_ready", "down_ready", "biased") as (
                    block, w_a, w_b, b2_in, up_ready, h_ready, down_ready, biased):
                landed = (w_a, w_b)

                @block.sync
                def _(sp):
                    for i in range(2):
                        sp.dma_start(w1[i][:, :, :], d["L2_ffn_w1"][2 * a + i].rearrange("(k p) f -> p k f", p=P)
                                     ).then_inc(landed[i], 16)
                        sp.dma_start(w2[i][:, :, :], d["L2_ffn_w2"][2 * a + i].rearrange("(k p) f -> p k f", p=P)
                                     ).then_inc(landed[i], 16)
                    sp.dma_start(b2[:, :], d["L2_ffn_b2"][a]).then_inc(b2_in, 16)

                @block.tensor
                def _(pe):
                    for i in range(2):
                        pe.wait_ge(landed[i], 32)
                        for f in range(FT):
                            j = FT * i + f
                            if j >= 4:
                                pe.wait_ge(h_ready, j - 3)
                            for k2 in range(CT):
                                x = xfT[:, k2, :].rearrange("p (mb t) -> p mb t", mb=2)
                                mm = nc.tensor.matmul(ps[:, j % 4, 0:2 * TPE].rearrange("p (mb t) -> p mb t", mb=2),
                                                      w1[i][:, k2, f * P:(f + 1) * P],
                                                      x[:, :, bass.ds((2 * a + i) * TPE, TPE)],
                                                      start=k2 == 0, stop=k2 == CT - 1)
                            mm.then_inc(up_ready, 1)
                    pe.wait_ge(h_ready, 2 * FT)
                    for mb in range(2):
                        for i in range(2):
                            for f in range(FT):
                                mm = nc.tensor.matmul(ps[TPE * i:TPE * (i + 1), 4 + mb, 0:C], h[:, f, i, mb, :],
                                                      w2[i][:, f, :], start=f == 0, stop=f == FT - 1)
                        mm.then_inc(down_ready, 1)

                @block.scalar
                def _(act):
                    for i in range(2):
                        for f in range(FT):
                            j = FT * i + f
                            act.wait_ge(up_ready, j + 1)
                            nc.scalar.activation(h[:, f, i, :, :],
                                                 ps[:, j % 4, 0:2 * TPE].rearrange("p (mb t) -> p mb t", mb=2),
                                                 ACT.Gelu, bias=b1[:, bass.ds(2 * a + i, 1), f]).then_inc(h_ready, 1)

                @block.vector
                def _(dve):
                    dve.wait_ge(b2_in, 16)
                    for mb in range(2):
                        dve.wait_ge(down_ready, mb + 1)
                        nc.vector.tensor_tensor(tmp[:, mb, :], ps[:, 4 + mb, 0:C], b2[:, :], ALU.add).then_inc(biased, 1)
                    for mb in range(2):
                        dve.wait_ge(biased, mb + 1)
                        x = core.x[:, bass.ds(a + 4 * mb, 1), :]
                        nc.vector.tensor_tensor(x, tmp[:, mb:mb + 1, :], x, ALU.add)

K_SLOTS = (0, 0, 1, 1, 0, 2)
Q_SLOTS = (0, 1, 0, 1, 2, 0)
SLOTS = len(K_SLOTS)
SHIFT = SLOTS * D
ROWS = SHIFT + 1
VW = D + 1
PART = 32


def project_parts(core, w, chunks, source, parts, scale=1.0, values=None, rope=None):
    nc, ps = core.nc, core.ps
    streams = callable(source)
    with ExitStack() as c_:
        sb = core.allocator(c_)
        rest = sb([P, 2, KC])
        if streams:
            ctx = sb([P, 2, CT, KC])
        if rope:
            norm_w, table, turn, eps = rope
            tab = sb([P, 2, 2, KC])
            raw, square, root, mix, turned_ = (sb([P, 2, KC]) for _ in range(5))
        names = ["ctx_a", "ctx_b", "tab_a", "tab_b", "product", "high_done", "rest_done", "middle_done", "low_done",
                 "v_product", "v_done", "copied", "summed", "root_done", "cos_done", "sin_done", "mixed", "inverted",
                 "normed"]
        with phase(core, *names) as (block, ctx_a, ctx_b, tab_a, tab_b, product, high_done, rest_done, middle_done,
                                     low_done, v_product, v_done, copied, summed, root_done, cos_done, sin_done,
                                     mixed, inverted, normed):
            units = [(c, f) for c in range(chunks) for f in range(CT)]
            ctx_in, tab_in = (ctx_a, ctx_b), (tab_a, tab_b)
            x_of = (lambda c: ctx[:, c % 2]) if streams else (lambda c: source[:, :, c * KC:(c + 1) * KC])

            @block.sync
            def _(sp):
                for c in range(chunks):
                    if streams:
                        if c >= 2:
                            sp.wait_ge(product, CT * (c - 1))
                            if values:
                                sp.wait_ge(v_product, 2 * (c - 1))
                        sp.dma_start(ctx[:, c % 2, :, :], source(c)).then_inc(ctx_in[c % 2], 16)
                    if rope:
                        if c >= 2:
                            sp.wait_ge(sin_done, CT * (c - 1))
                            sp.wait_ge(cos_done, CT * (c - 1))
                        sp.dma_start(tab[:, c % 2, :, :], table(c)).then_inc(tab_in[c % 2], 16)

            @block.tensor
            def _(pe):
                def heads_of(i):
                    pe.wait_ge(copied, i + 1)
                    if i >= 2:
                        pe.wait_ge(root_done, i - 1)
                        pe.wait_ge(sin_done, i - 1)
                    b = 2 if i % 2 == 0 else 6
                    nc.tensor.matmul(ps[:, b, :], core.block16[:, :], square[:, i % 2, :], start=True, stop=True)
                    nc.tensor.matmul(ps[:, b + 1, :], turn, raw[:, i % 2, :], start=True, stop=True).then_inc(summed, 1)

                for i, (c, f) in enumerate(units):
                    if streams and f == 0:
                        pe.wait_ge(ctx_in[c % 2], 16 * (c // 2 + 1))
                    if i >= 2:
                        pe.wait_ge(copied if rope else rest_done, i - 1)
                    for k in range(CT):
                        mm = nc.tensor.matmul(ps[:, i % 2, :], w[:, k, f * P:(f + 1) * P], x_of(c)[:, k, :],
                                              start=k == 0, stop=k == CT - 1)
                    mm.then_inc(product, 1)
                    if values:
                        if i >= 2:
                            pe.wait_ge(v_done, i - 1)
                        for t in range(2):
                            for k in range(CT):
                                mm = nc.tensor.matmul(ps[:, 4 + i % 2, t * C:(t + 1) * C],
                                                      x_of(c)[:, k, (2 * f + t) * P:(2 * f + t + 1) * P],
                                                      values[0][:, k, :], start=k == 0, stop=k == CT - 1)
                        mm.then_inc(v_product, 1)
                    if rope and i >= 1:
                        heads_of(i - 1)
                if rope:
                    heads_of(len(units) - 1)

            out = lambda i, part: parts[:, units[i][1], part, units[i][0] * KC:(units[i][0] + 1) * KC]
            whole = (lambda i: mix[:, i % 2, :]) if rope else (lambda i: ps[:, i % 2, :])

            @block.scalar
            def _(act):
                def high(i):
                    act.wait_ge(normed if rope else product, i + 1)
                    nc.scalar.mul(out(i, 0), whole(i), scale).then_inc(high_done, 1)

                for i in range(len(units)):
                    if rope:
                        act.wait_ge(product, i + 1)
                        if i >= 2:
                            act.wait_ge(summed, i - 1)
                            act.wait_ge(cos_done, i - 1)
                        nc.scalar.copy(raw[:, i % 2, :], ps[:, i % 2, :])
                        nc.scalar.activation(square[:, i % 2, :], ps[:, i % 2, :], ACT.Square).then_inc(copied, 1)
                    else:
                        high(i)
                    if values:
                        act.wait_ge(v_product, i + 1)
                        nc.scalar.copy(values[1][:, 2 * i:2 * i + 2, :, 0:D],
                                       ps[:, 4 + i % 2, :].rearrange("p (t h c) -> p t h c", t=2, h=H)
                                       ).then_inc(v_done, 1)
                    if rope:
                        act.wait_ge(summed, i + 1)
                        if i >= 2:
                            act.wait_ge(normed, i - 1)
                        nc.scalar.activation(root[:, i % 2, :], ps[:, 2 if i % 2 == 0 else 6, :], ACT.Sqrt,
                                             bias=eps, scale=1.0 / D).then_inc(root_done, 1)
                        if i >= 1:
                            high(i - 1)
                if rope:
                    high(len(units) - 1)

            @block.vector
            def _(dve):
                def rotate(i):
                    c, s = units[i][0] % 2, i % 2
                    dve.wait_ge(tab_in[c], 16 * (units[i][0] // 2 + 1))
                    dve.wait_ge(copied, i + 1)
                    if i >= 2:
                        dve.wait_ge(rest_done, i - 1)
                        dve.wait_ge(high_done, i - 1)
                    nc.vector.scalar_tensor_tensor(out=mix[:, s, :], in0=raw[:, s, :], scalar=norm_w,
                                                   in1=tab[:, c, 0, :], op0=ALU.mult, op1=ALU.mult).then_inc(cos_done, 1)
                    dve.wait_ge(summed, i + 1)
                    nc.vector.tensor_tensor(turned_[:, s, :], ps[:, 3 if s == 0 else 7, :], tab[:, c, 1, :],
                                            ALU.mult).then_inc(sin_done, 1)
                    dve.wait_ge(sin_done, i + 1)
                    dve.wait_ge(cos_done, i + 1)
                    nc.vector.tensor_tensor(mix[:, s, :], mix[:, s, :], turned_[:, s, :], ALU.add).then_inc(mixed, 1)
                    dve.wait_ge(root_done, i + 1)
                    nc.vector.reciprocal(root[:, s, :], root[:, s, :]).then_inc(inverted, 1)

                def split(i):
                    dve.wait_ge(high_done, i + 1)
                    if i >= 2:
                        dve.wait_ge(low_done, i - 1)
                    nc.vector.scalar_tensor_tensor(out=rest[:, i % 2, :], in0=whole(i), scalar=scale, in1=out(i, 0),
                                                   op0=ALU.mult, op1=ALU.subtract).then_inc(rest_done, 1)

                for i in range(len(units)):
                    if rope:
                        rotate(i)
                        if i >= 1:
                            split(i - 1)
                    else:
                        split(i)
                if rope:
                    split(len(units) - 1)

            @block.gpsimd
            def _(pool):
                def norm(i):
                    pool.wait_ge(mixed, i + 1)
                    pool.wait_ge(inverted, i + 1)
                    nc.gpsimd.tensor_tensor(mix[:, i % 2, :], mix[:, i % 2, :], root[:, i % 2, :],
                                            ALU.mult).then_inc(normed, 1)

                def low(i):
                    pool.wait_ge(rest_done, i + 1)
                    nc.gpsimd.tensor_copy(out(i, 1), rest[:, i % 2, :]).then_inc(middle_done, 1)
                    pool.wait_ge(middle_done, i + 1)
                    nc.gpsimd.tensor_tensor(out(i, 2), rest[:, i % 2, :], out(i, 1), ALU.subtract).then_inc(low_done, 1)

                for i in range(len(units)):
                    if rope:
                        norm(i)
                        if i >= 1:
                            low(i - 1)
                    else:
                        low(i)
                if rope:
                    low(len(units) - 1)


def attend_context(core, kparts, v, qstack, kstack, bias, att):
    nc, ps = core.nc, core.ps
    QT = T // P
    NK = S // KC
    GU = QT * NK
    EU = KT // 4
    with ExitStack() as c:
        sb = core.allocator(c)
        p = sb([P, 3, 4 * T])
        gm, neg = sb([P, 2, QT, NK]), sb([P, 2, QT])
        fold, osum, inv = core.fold, sb([P, 2, T]), sb([P, 2, QT])
        with phase(core, "k_a", "k_b", "scored", "max_done", "neg_done", "neg_row", "shift_done", "guard_free",
                   "qk", "exp_done", "pv", "summed", "out_ready", "inv_done", "out_done", "cleared") as (
                block, k_a, k_b, scored, max_done, neg_done, neg_row, shift_done, guard_free, qk, exp_done, pv,
                summed, out_ready, inv_done, out_done, cleared):
            k_in = (k_a, k_b)

            @block.sync
            def _(sp):
                for h in range(H):
                    if h >= 2:
                        sp.wait_ge(qk, EU * (h - 1))
                    f, row = h // HT, (h % HT) * D
                    for s, part in enumerate(K_SLOTS):
                        sp.dma_start(kstack[s * D:(s + 1) * D, h % 2, :],
                                     kparts[row:row + D, f, part, :]).then_inc(k_in[h % 2], 16)

            @block.tensor
            def _(pe):
                def guard(h, g):
                    t, kc = g // NK, g % NK
                    if g == 0:
                        pe.wait_ge(k_in[h % 2], 16 * SLOTS * (h // 2 + 1))
                        if h >= 1:
                            pe.wait_ge(shift_done, h)
                    if g >= 2:
                        pe.wait_ge(max_done, GU * h + g - 1)
                    if g == 1 and h >= 3:
                        pe.wait_ge(out_done, h - 2)
                    biased = bias is not None and kc == 0
                    mm = nc.tensor.matmul(ps[:, 4 + g % 2, :], qstack[0:SHIFT, h, t * P:(t + 1) * P],
                                          kstack[0:SHIFT, h % 2, kc * KC:(kc + 1) * KC], start=True, stop=True,
                                          skip_group_check=biased)
                    if biased:
                        near = [k for k in range(t + 2)]
                        for k in near:
                            mm = nc.tensor.matmul(ps[:, 4 + g % 2, k * P:(k + 1) * P], core.identb[:, :],
                                                  bias[1][:, k - t + 1, h, :], start=False, stop=True,
                                                  skip_group_check=True)
                    mm.then_inc(scored, 1)

                def shift(h):
                    pe.wait_ge(neg_done, h + 1)
                    for t in range(QT):
                        mm = nc.tensor.matmul(ps[SHIFT:ROWS, 4, t * P:(t + 1) * P], neg[:, h % 2, t:t + 1],
                                              core.ident[:, :], start=True, stop=True, tile_position=(0, SHIFT))
                    mm.then_inc(neg_row, 1)

                def scores(h, e):
                    i = EU * h + e
                    if e == 0:
                        pe.wait_ge(shift_done, h + 1)
                    if i >= 2:
                        pe.wait_ge(exp_done, i - 1)
                    for j in range(4):
                        kt = 4 * e + j
                        out = ps[:, 2 * (i % 2) + j // 2, (j % 2) * T:(j % 2 + 1) * T]
                        near = [t for t in range(QT) if kt - t <= 1] if bias is not None else []
                        mm = nc.tensor.matmul(out, kstack[:, h % 2, kt * P:(kt + 1) * P], qstack[:, h, :],
                                              start=True, stop=True, skip_group_check=bool(near))
                        for t in near:
                            mm = nc.tensor.matmul(out[:, t * P:(t + 1) * P], core.ident[:, :],
                                                  bias[0][:, kt - t + 1, h, :], start=False, stop=True,
                                                  skip_group_check=True)
                    mm.then_inc(qk, 1)

                def weigh(h, e):
                    i = EU * h + e
                    pe.wait_ge(exp_done, i + 1)
                    if i == 0:
                        pe.wait_ge(cleared, 1)
                    if e == 0 and h >= 2:
                        pe.wait_ge(summed, h - 1)
                    for j in range(4):
                        mm = nc.tensor.matmul(ps[PART * j:PART * j + VW, 6 + h % 2, 0:T], v[:, 4 * e + j, h, :],
                                              p[:, i % 3, j * T:(j + 1) * T], start=e == 0, stop=e == EU - 1,
                                              tile_position=(0, PART * j))
                    mm.then_inc(pv, 1)

                def output(h):
                    pe.wait_ge(summed, h + 1)
                    if h >= H - 2:
                        pe.wait_ge(out_done, h)
                    for t in range(QT):
                        mm = nc.tensor.matmul(ps[:, 5, t * VW:(t + 1) * VW], osum[:, h % 2, t * P:(t + 1) * P],
                                              fold[:, 0:VW], start=True, stop=True)
                    mm.then_inc(out_ready, 1)

                for g in range(GU):
                    guard(0, g)
                shift(0)
                for h in range(H + 1):
                    for e in range(EU):
                        if h < H:
                            scores(h, e)
                        if h + 1 < H:
                            guard(h + 1, 2 * e)
                            guard(h + 1, 2 * e + 1)
                        if h < H and e >= 1:
                            weigh(h, e - 1)
                    if h < H:
                        weigh(h, EU - 1)
                    if h + 1 < H:
                        shift(h + 1)
                    if h >= 1:
                        if h + 1 < H:
                            pe.wait_ge(max_done, GU * (h + 2))
                        output(h - 1)

            @block.vector
            def _(dve):
                for q in range(2):
                    last = nc.vector.memset(ps[:, 6 + q, 0:T], 0.0)
                last.then_inc(cleared, 1)

                def maxima(h, g):
                    dve.wait_ge(scored, GU * h + g + 1)
                    nc.vector.tensor_reduce(gm[:, h % 2, g // NK, g % NK:g % NK + 1], ps[:, 4 + g % 2, :], AX.X,
                                            ALU.max).then_inc(max_done, 1)

                def negate(h):
                    dve.wait_ge(max_done, GU * (h + 1))
                    if h >= 2:
                        dve.wait_ge(neg_row, h - 1)
                    nc.vector.tensor_reduce(neg[:, h % 2, :], gm[:, h % 2, :, :], AX.X, ALU.max,
                                            negate=True).then_inc(neg_done, 1)
                    dve.wait_ge(neg_row, h + 1)
                    nc.vector.tensor_copy(qstack[SHIFT:ROWS, h, :], ps[SHIFT:ROWS, 4, 0:T]).then_inc(shift_done, 1)

                def finish(h):
                    dve.wait_ge(out_ready, h + 1)
                    o = ps[:, 5, 0:QT * VW].rearrange("p (t c) -> p t c", t=QT)
                    nc.vector.reciprocal(inv[:, h % 2, :], o[:, :, D]).then_inc(inv_done, 1)
                    dve.wait_ge(inv_done, h + 1)
                    for t in range(QT):
                        last = nc.vector.tensor_scalar(att[:, t, h * D:(h + 1) * D], o[:, t, 0:D],
                                                       inv[:, h % 2, t:t + 1], None, ALU.mult)
                    last.then_inc(out_done, 1)

                for h in range(H + 2):
                    if h < H:
                        for g in range(GU):
                            maxima(h, g)
                        negate(h)
                    if h >= 2:
                        finish(h - 2)

            @block.scalar
            def _(act):
                def take(h):
                    act.wait_ge(pv, EU * (h + 1))
                    if h >= 2:
                        act.wait_ge(out_ready, h - 1)
                    nc.scalar.copy(osum[:, h % 2, :], ps[:, 6 + h % 2, 0:T]).then_inc(summed, 1)

                for h in range(H):
                    for e in range(EU):
                        i = EU * h + e
                        act.wait_ge(qk, i + 1)
                        if i >= 3:
                            act.wait_ge(pv, i - 2)
                        nc.scalar.activation(p[:, i % 3, :].rearrange("p (b t) -> p b t", b=2),
                                             ps[:, 2 * (i % 2):2 * (i % 2) + 2, :], ACT.Exp).then_inc(exp_done, 1)
                        if e == 2 and h >= 1:
                            take(h - 1)
                take(H - 1)


def output_product(core, att, attT, wo, b):
    nc, ps = core.nc, core.ps
    QT = T // P
    with phase(core, "turned", "copied", "ready") as (block, turned, copied, ready):
        @block.tensor
        def _(pe):
            for t in range(QT):
                for k in range(CT):
                    mm = nc.tensor.transpose(ps[:, k, t * P:(t + 1) * P], att[:, t, k * P:(k + 1) * P],
                                             core.ident[:, :])
            mm.then_inc(turned, 1)
            pe.wait_ge(copied, 1)
            for t in range(QT):
                for k in range(CT):
                    mm = nc.tensor.matmul(ps[:, 2 + t, 0:C], attT[:, k, t * P:(t + 1) * P], wo[:, k, :],
                                          start=k == 0, stop=k == CT - 1)
                mm.then_inc(ready, 1)

        @block.scalar
        def _(act):
            act.wait_ge(turned, 1)
            nc.scalar.copy(attT[:, :, :], ps[:, 0:CT, 0:T]).then_inc(copied, 1)

        @block.vector
        def _(dve):
            for t in range(QT):
                dve.wait_ge(ready, t + 1)
                x = core.x[:, bass.ds(QT * b + t, 1), :]
                nc.vector.tensor_tensor(x, ps[:, 2 + t:3 + t, 0:C], x, ALU.add)


def attend_by_key(core, kparts, v, qstack, kstack, att):
    nc, ps = core.nc, core.ps
    QT = T // P
    EU = KT // 4
    with ExitStack() as c:
        sb = core.allocator(c)
        p, scaled = sb([P, 3, 4 * T]), sb([P, 3, 4, VW])
        nm, z, zi = sb([P, 4, 4]), sb([P, 4, 4]), sb([P, 4, 4])
        fold, osum, inv = core.fold, sb([P, 2, T]), sb([P, 2, QT])
        with phase(core, "k_a", "k_b", "max_done", "qk", "exp_done", "z_done", "v_scaled", "pv", "summed",
                   "out_ready", "inv_done", "out_done", "cleared") as (
                block, k_a, k_b, max_done, qk, exp_done, z_done, v_scaled, pv, summed, out_ready, inv_done,
                out_done, cleared):
            k_in = (k_a, k_b)

            @block.sync
            def _(sp):
                for h in range(H):
                    if h >= 2:
                        sp.wait_ge(qk, EU * (h - 1))
                    f, row = h // HT, (h % HT) * D
                    for s, part in enumerate(K_SLOTS):
                        sp.dma_start(kstack[s * D:(s + 1) * D, h % 2, :],
                                     kparts[row:row + D, f, part, :]).then_inc(k_in[h % 2], 16)

            @block.tensor
            def _(pe):
                def scores(i):
                    h, e = i // EU, i % EU
                    if e == 0:
                        pe.wait_ge(k_in[h % 2], 16 * SLOTS * (h // 2 + 1))
                    if i >= 2:
                        pe.wait_ge(exp_done, 4 * (i - 1))
                    for j in range(4):
                        kt = 4 * e + j
                        mm = nc.tensor.matmul(ps[:, 2 * (i % 2) + j // 2, (j % 2) * T:(j % 2 + 1) * T],
                                              kstack[0:SHIFT, h % 2, kt * P:(kt + 1) * P], qstack[0:SHIFT, h, :],
                                              start=True, stop=True)
                    mm.then_inc(qk, 1)

                def weigh(i):
                    h, e = i // EU, i % EU
                    pe.wait_ge(v_scaled, i + 1)
                    if i == 0:
                        pe.wait_ge(cleared, 1)
                    if e == 0 and h >= 2:
                        pe.wait_ge(summed, h - 1)
                    for j in range(4):
                        mm = nc.tensor.matmul(ps[PART * j:PART * j + VW, 6 + h % 2, 0:T], scaled[:, i % 3, j, :],
                                              p[:, i % 3, j * T:(j + 1) * T], start=e == 0, stop=e == EU - 1,
                                              tile_position=(0, PART * j))
                    mm.then_inc(pv, 1)

                def output(h):
                    pe.wait_ge(summed, h + 1)
                    if h >= 2:
                        pe.wait_ge(out_done, h - 1)
                    for t in range(QT):
                        mm = nc.tensor.matmul(ps[:, 4 + h % 2, t * VW:(t + 1) * VW],
                                              osum[:, h % 2, t * P:(t + 1) * P], fold[:, 0:VW], start=True, stop=True)
                    mm.then_inc(out_ready, 1)

                for i in range(H * EU + 2):
                    if i < H * EU:
                        scores(i)
                    if i >= 2:
                        weigh(i - 2)
                    if i >= EU and i % EU == EU - 2:
                        output(i // EU - 1)
                output(H - 1)

            @block.vector
            def _(dve):
                for q in range(2):
                    last = nc.vector.memset(ps[:, 6 + q, 0:T], 0.0)
                last.then_inc(cleared, 1)

                def maxima(i):
                    dve.wait_ge(qk, i + 1)
                    if i >= 4:
                        dve.wait_ge(exp_done, 4 * (i - 3))
                    nc.vector.tensor_reduce(nm[:, i % 4, :],
                                            ps[:, 2 * (i % 2):2 * (i % 2) + 2, :].rearrange("p b (j t) -> p (b j) t", j=2),
                                            AX.X, ALU.max, negate=True).then_inc(max_done, 1)

                def scale_values(i):
                    h, e = i // EU, i % EU
                    dve.wait_ge(exp_done, 4 * (i + 1))
                    nc.vector.reciprocal(zi[:, i % 4, :], z[:, i % 4, :]).then_inc(z_done, 1)
                    dve.wait_ge(z_done, i + 1)
                    if i >= 3:
                        dve.wait_ge(pv, i - 2)
                    nc.vector.tensor_tensor(scaled[:, i % 3, :, :], v[:, 4 * e:4 * e + 4, h, :],
                                            zi[:, i % 4, :].unsqueeze(2).to_broadcast([P, 4, VW]),
                                            ALU.mult).then_inc(v_scaled, 1)

                def finish(h):
                    dve.wait_ge(out_ready, h + 1)
                    o = ps[:, 4 + h % 2, 0:QT * VW].rearrange("p (t c) -> p t c", t=QT)
                    nc.vector.reciprocal(inv[:, h % 2, :], o[:, :, D]).then_inc(inv_done, 1)
                    dve.wait_ge(inv_done, h + 1)
                    for t in range(QT):
                        last = nc.vector.tensor_scalar(att[:, t, h * D:(h + 1) * D], o[:, t, 0:D],
                                                       inv[:, h % 2, t:t + 1], None, ALU.mult)
                    last.then_inc(out_done, 1)

                for i in range(H * EU + 1):
                    if i < H * EU:
                        maxima(i)
                    if i >= 1:
                        scale_values(i - 1)
                    if i >= EU and i % EU == EU - 1 and i < H * EU:
                        finish(i // EU - 1)
                finish(H - 1)

            @block.scalar
            def _(act):
                def take(h):
                    act.wait_ge(pv, EU * (h + 1))
                    if h >= 2:
                        act.wait_ge(out_ready, h - 1)
                    nc.scalar.copy(osum[:, h % 2, :], ps[:, 6 + h % 2, 0:T]).then_inc(summed, 1)

                for i in range(H * EU):
                    h, e = i // EU, i % EU
                    act.wait_ge(max_done, i + 1)
                    if i >= 3:
                        act.wait_ge(pv, i - 2)
                    if i >= 4:
                        act.wait_ge(z_done, i - 3)
                    for j in range(4):
                        nc.scalar.activation(p[:, i % 3, j * T:(j + 1) * T],
                                             ps[:, 2 * (i % 2) + j // 2, (j % 2) * T:(j % 2 + 1) * T], ACT.Exp,
                                             bias=nm[:, i % 4, j:j + 1],
                                             accum_out=z[:, i % 4, j:j + 1]).then_inc(exp_done, 1)
                    if e == 3 and h >= 1:
                        take(h - 1)
                take(H - 1)


def context_attention(core, prefix, by_key=False, scale=1.0, rope=False, bias=False):
    nc, d = core.nc, core.dram
    with ExitStack() as c:
        sb = core.allocator(c)
        tiles = None
        if bias:
            tiles = sb([P, 3, H, P]), sb([P, 3, H, P], BF16)
            distance_bias(core, prefix, *tiles)
        wq, wk, wv, wo = (sb([P, CT, C]) for _ in range(4))
        qstack = sb([P, H, T], BF16)
        qparts, kparts = sb([P, CT, 3, N], BF16), sb([P, CT, 3, S], BF16)
        v, kstack = sb([P, KT, H, VW]), sb([P, 2, S], BF16)
        att, attT = sb([P, T // P, C]), sb([P, CT, T])
        loads = [(t[:, :, :], ktiles(d[prefix + "_W" + n])) for t, n in ((wq, "q"), (wk, "k"), (wv, "v"), (wo, "o"))]
        q_rope = k_rope = None
        if rope:
            qw, kw, qturn, kturn, eps = sb([P, 1]), sb([P, 1]), sb([P, P]), sb([P, P]), sb([P, 1])
            loads += [(qw[:, :], d[prefix + "_q_norm_w"]), (kw[:, :], d[prefix + "_k_norm_w"]),
                      (qturn[:, :], d["c_turn16"]), (kturn[:, :], d["c_turn16"])]
        layer_norm(core, core.x, core.xn, core.xnT, loads=loads)
        with phase(core) as (block,):
            @block.vector
            def _(dve):
                nc.vector.memset(v[:, :, :, D:VW], 1.0)
                nc.vector.memset(kstack[SHIFT:ROWS, :, :], 1.0)
                if rope:
                    nc.vector.memset(eps[:, :], 1e-6)
                    nc.vector.tensor_scalar(qturn[:, :], qturn[:, :], qw[:, 0:1], None, ALU.mult)
                    nc.vector.tensor_scalar(kturn[:, :], kturn[:, :], kw[:, 0:1], None, ALU.mult)
        if rope:
            q_rope = (qw[:, 0:1], lambda i: d["c_rope_q"], qturn[:, :], eps[:, 0:1])
            k_rope = (kw[:, 0:1], lambda i: d["c_rope_k"][:, :, i * KC:(i + 1) * KC], kturn[:, :], eps[:, 0:1])
        project_parts(core, wq, N // KC, core.xnT, qparts, scale=scale, rope=q_rope)
        with nc.Fori(0, B) as b:
            project_parts(core, wk, S // KC, lambda i: d["ctxT"][b, :, i * KC:(i + 1) * KC].rearrange(
                "(k p) n -> p k n", p=P), kparts, values=(wv, v), rope=k_rope)
            with phase(core, "stacked") as (block, stacked):
                @block.sync
                def _(sp):
                    for s, part in enumerate(Q_SLOTS):
                        for h in range(H):
                            row = (h % HT) * D
                            sp.dma_start(qstack[s * D:(s + 1) * D, h, :],
                                         qparts[row:row + D, h // HT, part, bass.ds(b * T, T)]).then_inc(stacked, 16)
                    sp.wait_ge(stacked, 16 * SLOTS * H)
            k97, q97 = kstack[0:ROWS], qstack[0:ROWS]
            if by_key:
                attend_by_key(core, kparts, v, q97, k97, att)
            else:
                attend_context(core, kparts, v, q97, k97, tiles and (tiles[0], tiles[1]), att)
            output_product(core, att, attT, wo, b)


def distance_bias(core, prefix, by_key, by_query):
    nc, d, ps = core.nc, core.dram, core.ps
    W = 4 * P
    HB = BANK // P
    with ExitStack() as c:
        sb = core.allocator(c)
        table, onehot, rows, mirror = sb([32, H]), sb([32, W]), sb([H, W]), sb([P, P])
        slanted = sb([P, 3, H, P])
        scratch = d["scratch_bias"]
        load(core, [(table[:, :], d[prefix + "_rel_bias"]), (onehot[:, :], d["c_buckets"]),
                    (mirror[:, :], d["c_mirror"])])
        banks = [(i, g) for i in range(3) for g in range(H // HB)]
        with phase(core, "ready", "copied", "stored", "read", "query_ready", "key_ready", "query_copied",
                   "key_copied") as (block, ready, copied, stored, read, query_ready, key_ready, query_copied,
                                     key_copied):
            @block.tensor
            def _(pe):
                nc.tensor.matmul(ps[0:H, 0, :], table[:, :], onehot[:, :], start=True, stop=True).then_inc(ready, 1)
                pe.wait_ge(copied, 1)
                pe.wait_ge(read, 48)
                for n, (i, g) in enumerate(banks):
                    if n >= 4:
                        pe.wait_ge(query_copied, n - 3)
                        pe.wait_ge(key_copied, n - 3)
                    nc.tensor.matmul(ps[:, n % 4, :], mirror[:, :], slanted[:, i, g * HB:(g + 1) * HB, :],
                                     start=True, stop=True).then_inc(query_ready, 1)
                    for h in range(HB):
                        mm = nc.tensor.matmul(ps[:, 4 + n % 4, h * P:(h + 1) * P], slanted[:, i, g * HB + h, :],
                                              mirror[:, :], start=True, stop=True)
                    mm.then_inc(key_ready, 1)

            @block.scalar
            def _(act):
                act.wait_ge(ready, 1)
                nc.scalar.copy(rows[:, :], ps[0:H, 0, :]).then_inc(copied, 1)
                for n, (i, g) in enumerate(banks):
                    act.wait_ge(key_ready, n + 1)
                    nc.scalar.copy(by_key[:, i, g * HB:(g + 1) * HB, :], ps[:, 4 + n % 4, :]).then_inc(key_copied, 1)

            @block.sync
            def _(sp):
                sp.wait_ge(copied, 1)
                sp.dma_start(scratch, rows[:, :]).then_inc(stored, 16)
                sp.wait_ge(stored, 16)
                for i in range(3):
                    start = 2 * P + P * (i - 1) - (P - 1)
                    sp.dma_start(slanted[:, i, :, :], bass.AP(tensor=scratch.tensor, offset=start,
                                                              ap=[[1, P], [W, H], [1, P]])).then_inc(read, 16)
                sp.wait_ge(read, 48)

            @block.vector
            def _(dve):
                for n, (i, g) in enumerate(banks):
                    dve.wait_ge(query_ready, n + 1)
                    nc.vector.tensor_copy(by_query[:, i, g * HB:(g + 1) * HB, :],
                                          ps[:, n % 4, :]).then_inc(query_copied, 1)


def l0_xattn(core):
    context_attention(core, "L0_xattn", scale=D ** -0.5, rope=True)


def l1_xattn(core):
    context_attention(core, "L1_xattn", bias=True)


def l2_xattn(core):
    context_attention(core, "L2_xattn", by_key=True, scale=C ** -0.5)

def lay_out(i):
    import numpy as np
    cont = np.ascontiguousarray
    T_ = lambda a: cont(np.swapaxes(a, -1, -2))
    col = lambda a: cont(a.reshape(-1, P).T)
    row = lambda a: cont(a.reshape(1, -1))
    o = {"x": i["x"], "ctxT": T_(i["ctx_1024"])}
    o["L3_ffn_W1"], o["L3_ffn_W2"] = T_(i["L3_ffn_W1"]), T_(i["L3_ffn_W2"])
    o["L3_ffn_b1"], o["L3_ffn_b2"] = col(i["L3_ffn_b1"]), row(i["L3_ffn_b2"])
    o["L3_ffn_scale"] = cont(np.broadcast_to(i["L3_ffn_scale"].reshape(1, 1), (P, 1)))
    for n in ("W_u", "W_g", "Bm", "Cm"):
        o["L3_attn_" + n] = T_(i["L3_attn_" + n])
    o["L3_attn_A"], o["L3_attn_AT"] = i["L3_attn_A"], T_(i["L3_attn_A"])
    o["L3_attn_b_u"], o["L3_attn_b_g"] = col(i["L3_attn_b_u"]), col(i["L3_attn_b_g"])
    o["L3_attn_D"] = row(i["L3_attn_D"])
    o["L3_xattn_Wq"], o["L3_xattn_Wp"] = T_(i["L3_xattn_Wq"]), T_(i["L3_xattn_Wp"])
    o["L3_xattn_Wkv"] = T_(np.concatenate([i["L3_xattn_Wk"], i["L3_xattn_Wv"]], 0))
    o["L3_xattn_bq"], o["L3_xattn_bp"] = row(i["L3_xattn_bq"]), row(i["L3_xattn_bp"])
    o["L3_xattn_bkv"] = row(np.concatenate([i["L3_xattn_bk"], i["L3_xattn_bv"]]))
    o["L0_attn_maa"] = cont(np.stack([col(i["L0_attn_time_maa_" + n]) for n in "xwkvrg"], 1))
    o["L0_attn_w1"] = i["L0_attn_time_maa_w1"]
    o["L0_attn_w2"] = i["L0_attn_time_maa_w2"].reshape(-1, C)
    o["L0_attn_wd1"], o["L0_attn_wd2"] = i["L0_attn_time_decay_w1"], i["L0_attn_time_decay_w2"]
    o["L0_attn_decay"], o["L0_attn_u"] = col(i["L0_attn_time_decay"]), col(i["L0_attn_time_faaaa"])
    o["L0_attn_gamma"], o["L0_attn_beta"] = col(i["L0_attn_ln_gamma"]), col(i["L0_attn_ln_beta"])
    for n in "rkvgo":
        o["L0_attn_W_" + n] = i["L0_attn_W_" + n]
    o["L0_ffn_gate_w"] = T_(i["L0_ffn_gate_w"])

    def paired(w):
        w = w.reshape(32, 2, 192, -1)
        return np.concatenate([w[:, :, 0:P].reshape(32, 2 * P, -1), w[:, :, P:].reshape(32, P, -1)], 1)

    gu = np.stack([paired(i["L0_ffn_w_gate"]), paired(i["L0_ffn_w_up"])], 1)
    o["L0_ffn_wgu"] = cont(gu.reshape(32, 2, 3 * P, CT, P).transpose(0, 4, 3, 1, 2))
    o["L0_ffn_wd"] = cont(paired(T_(i["L0_ffn_w_down"])).reshape(32, 3, P, C).transpose(0, 2, 1, 3))
    for n in ("r1_w", "r2_w", "W1", "W2", "b2"):
        o["L1_attn_" + n] = i["L1_attn_" + n]
    o["L1_attn_r1_b"] = row(i["L1_attn_r1_b"])
    o["L1_attn_ln_g"], o["L1_attn_ln_b"] = col(i["L1_attn_ln_g"]), col(i["L1_attn_ln_b"])
    for n in ("r2_b", "route_bias", "temp"):
        a = i["L1_attn_" + n].reshape(1, -1)
        o["L1_attn_" + n] = cont(np.broadcast_to(a, (P, a.shape[1])))
    expert_col = lambda a: cont(a.reshape(a.shape[0], -1, P).transpose(2, 0, 1))
    o["L1_attn_b1"] = expert_col(i["L1_attn_b1"])
    o["L1_ffn_Wg"], o["L1_ffn_b2"] = T_(i["L1_ffn_Wg"]), i["L1_ffn_b2"]
    o["L1_ffn_b1"], o["L1_ffn_b3"] = expert_col(i["L1_ffn_b1"]), expert_col(i["L1_ffn_b3"])
    w13 = np.stack([i["L1_ffn_W1"], i["L1_ffn_W3"]], 1)
    o["L1_ffn_W13"] = cont(w13.reshape(16, 2, 256, CT, P).transpose(0, 4, 3, 1, 2))
    o["L1_ffn_W2"] = T_(i["L1_ffn_W2"])
    o["L2_attn_W_in"], o["L2_attn_W_out"] = T_(i["L2_attn_W_in"]), T_(i["L2_attn_W_out"])
    spread = lambda a: cont(np.broadcast_to(a.reshape(1, -1), (P, a.size)))
    o["L2_attn_b_qk"], o["L2_attn_b_v"] = col(i["L2_attn_b_in"][:2048]), spread(i["L2_attn_b_in"][2048:])
    o["L2_attn_b_out"] = spread(i["L2_attn_b_out"])
    for n in ("wq", "wk", "wv", "wo", "w1", "w2"):
        o["L2_ffn_" + n] = i["L2_ffn_" + n]
    o["L2_ffn_ln_g"], o["L2_ffn_ln_b"] = col(i["L2_ffn_ln_g"]), col(i["L2_ffn_ln_b"])
    o["L2_ffn_b1"] = expert_col(i["L2_ffn_b1"])
    o["L2_ffn_b2"] = cont(np.broadcast_to(i["L2_ffn_b2"].reshape(4, 2, 1, C), (4, 2, 64, C)).reshape(4, P, C))
    for n in "qkvo":
        o["L0_xattn_W" + n], o["L2_xattn_W" + n] = T_(i["L0_xattn_W" + n]), T_(i["L2_xattn_W" + n])
    for n in "qk":
        o[f"L0_xattn_{n}_norm_w"] = cont(np.tile(i[f"L0_xattn_{n}_norm_w"].reshape(D, 1), (HT, 1)))
    o["L1_xattn_Wq"], o["L1_xattn_Wo"] = i["L1_xattn_Wq"], i["L1_xattn_Wo"]
    o["L1_xattn_Wk"], o["L1_xattn_Wv"] = cont(i["L1_xattn_Wkv"][:, 0:C]), cont(i["L1_xattn_Wkv"][:, C:])
    o["L1_xattn_rel_bias"] = i["L1_xattn_rel_bias"]
    o["c_ident"] = np.eye(P, dtype=np.float32)
    o["c_block16"] = np.kron(np.eye(HT), np.ones((D, D))).astype(np.float32)
    o["c_fold"] = np.tile(np.eye(32), (4, 1)).astype(np.float32)
    o["c_eye4"] = np.eye(4, dtype=np.float32)
    o["c_block4"] = np.kron(np.eye(4), np.ones((4, 1))).astype(np.float32)
    o["c_sel"] = np.stack([np.kron(np.eye(HT), np.eye(D)[:, [n]] * np.ones((1, D))) for n in range(D)],
                          1).astype(np.float32)
    o["c_mask8"] = np.kron(np.eye(16), np.ones((8, 1))).astype(np.float32)
    p64 = np.arange(32, dtype=np.float32) / np.float32(31)
    ang = np.arange(T, dtype=np.float32)[None, :] / (np.float32(10000.0) ** p64)[:, None]
    o["c_cos64"], o["c_sin64"] = (np.tile(f(ang), (4, 1)).astype(np.float32) for f in (np.cos, np.sin))
    t64 = np.zeros((64, 64), np.float32)
    t64[np.arange(32), np.arange(32) + 32] = 1.0
    t64[np.arange(32) + 32, np.arange(32)] = -1.0
    o["c_turn64"] = np.kron(np.eye(2), t64).astype(np.float32)
    o["c_causal"] = np.where(np.arange(P)[:, None] >= np.arange(P)[None, :], 0.0, -1e30).astype(np.float32)
    half = np.arange(D // 2) * 2
    for n, theta, length in (("q", 32.0, T), ("k", 1000.0, S)):
        freqs = np.float32(theta) ** (-half.astype(np.float32) / np.float32(D))
        ang = freqs[:, None] * np.arange(length, dtype=np.float32)[None, :]
        table = np.stack([np.tile(f(ang), (2 * HT, 1)) for f in (np.cos, np.sin)], 1).astype(np.float32)
        o["c_rope_" + n] = np.tile(table, (1, 1, 2)) if n == "q" else table
    t16 = np.zeros((D, D), np.float32)
    t16[np.arange(8) + 8, np.arange(8)] = -1.0
    t16[np.arange(8), np.arange(8) + 8] = 1.0
    o["c_turn16"] = np.kron(np.eye(HT), t16).astype(np.float32)
    rel = np.arange(-256, 256)
    far = np.abs(rel)
    large = 8 + (np.log(np.maximum(far, 1).astype(np.float32) / 8) / np.log(16) * 8).astype(np.int32)
    bucket = (rel > 0) * 16 + np.where(far < 8, far, np.minimum(large, 15))
    hot = np.eye(32)[bucket].T - np.eye(32)[:, [31]]
    o["c_buckets"] = hot.astype(np.float32)
    o["c_mirror"] = np.ascontiguousarray(np.eye(P, dtype=np.float32)[:, ::-1])
    return {k: np.ascontiguousarray(v) for k, v in o.items()}


STAGES = [l0_xattn, l0_attn, l0_ffn, l1_xattn, l1_attn, l1_ffn, l2_xattn, l2_attn, l2_ffn, l3_xattn, l3_attn, l3_ffn]


def perceiver(nc, dram, out, stages=STAGES):
    with ExitStack() as ctx:
        core = Core(nc, ctx, dram)
        setup(core)
        for stage in stages:
            stage(core)
        store(core, out)


def declare(nc, arrays):
    dram = {k: nc.dram_tensor("in_" + k, v.shape, mybir.dt.from_np(v.dtype), kind="ExternalInput").ap()
            for k, v in arrays.items()}
    dram["scratch_tok"] = nc.dram_tensor("scratch_tok", (B, T, C), F32, kind="Internal").ap()
    dram["scratch_bias"] = nc.dram_tensor("scratch_bias", (H, 4 * P), F32, kind="Internal").ap()
    out = nc.dram_tensor("out", (B, T, C), F32, kind="ExternalOutput").ap()
    return dram, out


def kernel(**inputs):
    import numpy as np
    from concourse import bacc
    from concourse.bass_utils import run_bass_kernel_spmd

    nc = bacc.Bacc("TRN2", target_bir_lowering=False, num_devices=1)
    arrays = lay_out({k: np.asarray(v) for k, v in inputs.items()})
    dram, out = declare(nc, arrays)
    perceiver(nc, dram, out)
    r = run_bass_kernel_spmd(nc, [{"in_" + k: v for k, v in arrays.items()}], core_ids=[0])
    return r.results[0]["out"]
```

```python
from contextlib import ExitStack, contextmanager
import math

import concourse.bass as bass
from concourse import mybir

F32 = mybir.dt.float32
BF16 = mybir.dt.bfloat16
ALU = mybir.AluOpType
ACT = mybir.ActivationFunctionType
AX = mybir.AxisListType

P = 128
B, T, C = 4, 256, 256
N = B * T
TT = N // P
CT = C // P
S = 4096
KT = S // P
KC = 512
BANK = 512
H, D = 16, 16
HT = P // D


class Core:

    def __init__(self, nc, ctx, dram):
        self.nc, self.ctx, self.dram = nc, ctx, dram
        sb = lambda name, shape, dt=F32: ctx.enter_context(nc.sbuf_tensor(name, shape, dt))
        self.x = sb("x_tok", [P, TT, C])
        self.xn = sb("xn_tok", [P, TT, C])
        self.xnT = sb("xn_feat", [P, CT, N])
        self.ident = sb("ident", [P, P])
        self.ones = sb("ones", [P, P])
        self.identb = sb("identb", [P, P], BF16)
        self.fold = sb("fold", [P, 32])
        self.block16 = sb("block16", [P, P])
        self.ps = ctx.enter_context(nc.psum_tensor("banks", [P, 8, BANK], F32))
        self.count = 0

    def allocator(self, ctx):
        def tensor(shape, dt=F32):
            self.count += 1
            return ctx.enter_context(self.nc.sbuf_tensor(f"t{self.count}", shape, dt))
        return tensor


@contextmanager
def phase(core, *names):
    nc = core.nc
    core.count += 1
    sems = [nc.alloc_semaphore(f"p{core.count}_{n}") for n in names]
    with nc.Block() as block:
        yield (block, *sems)
    nc.clear_and_free_semaphores(sems)
    nc.all_engine_barrier()


def chain(engine, sem):
    count = [0]

    def link(instruction):
        count[0] += 1
        instruction.then_inc(sem, 1)
        engine.wait_ge(sem, count[0])

    return link


def load(core, pairs):
    with phase(core, "landed") as (block, landed):
        @block.sync
        def _(sp):
            for dst, src in pairs:
                sp.dma_start(dst, src).then_inc(landed, 16)
            sp.wait_ge(landed, 16 * len(pairs))


def ktiles(ap):
    return ap.rearrange("(k p) n -> p k n", p=P)


def layer_norm(core, src, dst, dstT, loads=(), eps=1e-5, gain=None, shift=None, bias=None):
    nc, ps = core.nc, core.ps
    with ExitStack() as c:
        sb = core.allocator(c)
        stats, mv, rstd = sb([P, TT, 6]), sb([P, TT, 2]), sb([P, TT])
        with phase(core, "landed", "stats_done", "agg", "var_ready", "root_done", "rstd_done", "norm_done",
                   "turned") as (block, landed, stats_done, agg, var_ready, root_done, rstd_done, norm_done, turned):
            @block.sync
            def _(sp):
                for d, s in loads:
                    sp.dma_start(d, s).then_inc(landed, 16)
                if loads:
                    sp.wait_ge(landed, 16 * len(loads))

            @block.vector
            def _(dve):
                for t in range(TT):
                    nc.vector.bn_stats(stats[:, t, :], src[:, t, :]).then_inc(stats_done, 1)
                for t in range(TT):
                    dve.wait_ge(stats_done, t + 1)
                    nc.vector.bn_aggr(mv[:, t, :], stats[:, t, :]).then_inc(agg, 1)
                dve.wait_ge(agg, TT)
                nc.vector.tensor_scalar(rstd[:, :], mv[:, :, 1], eps, None, ALU.add).then_inc(var_ready, 1)
                dve.wait_ge(root_done, 1)
                nc.vector.reciprocal(rstd[:, :], rstd[:, :]).then_inc(rstd_done, 1)
                dve.wait_ge(rstd_done, 1)
                for t in range(TT):
                    nc.vector.tensor_scalar(dst[:, t, :], src[:, t, :], mv[:, t, 0:1], rstd[:, t:t + 1],
                                            ALU.subtract, ALU.mult).then_inc(norm_done, 1)

            if bias is not None:
                @block.gpsimd
                def _(pool):
                    pool.wait_ge(landed, 16 * len(loads))
                    for t in range(TT):
                        pool.wait_ge(norm_done, t + 1)
                        nc.gpsimd.tensor_tensor(src[:, t, :], src[:, t, :], bias, ALU.add)

            @block.tensor
            def _(pe):
                for t in range(TT):
                    pe.wait_ge(norm_done, t + 1)
                    for k in range(CT):
                        nc.tensor.transpose(ps[:, CT * (t // 4) + k, (t % 4) * P:(t % 4 + 1) * P],
                                            dst[:, t, k * P:(k + 1) * P], core.ident[:, :]).then_inc(turned, 1)

            @block.scalar
            def _(act):
                act.wait_ge(var_ready, 1)
                nc.scalar.activation(rstd[:, :], rstd[:, :], ACT.Sqrt).then_inc(root_done, 1)
                for half in range(2):
                    act.wait_ge(turned, 4 * CT * (half + 1))
                    for k in range(CT):
                        out = dstT[:, k, half * BANK:(half + 1) * BANK]
                        if gain is None:
                            nc.scalar.copy(out, ps[:, CT * half + k, :])
                        else:
                            if loads:
                                act.wait_ge(landed, 16 * len(loads))
                            nc.scalar.activation(out, ps[:, CT * half + k, :], ACT.Identity,
                                                 bias=shift[:, k:k + 1], scale=gain[:, k:k + 1])


def linear_features(core, w, x, kt, mt, finish, engine="scalar", cols=N):
    nc, ps = core.nc, core.ps
    tiles = [(m, n) for m in range(mt) for n in range(cols // BANK)]
    with phase(core, "product_ready", "bank_free") as (block, product_ready, bank_free):
        @block.tensor
        def _(pe):
            for i, (m, n) in enumerate(tiles):
                if i >= 8:
                    pe.wait_ge(bank_free, i - 7)
                for k in range(kt):
                    mm = nc.tensor.matmul(ps[:, i % 8, :], w[:, k, m * P:(m + 1) * P],
                                          x[:, k, n * BANK:(n + 1) * BANK], start=k == 0, stop=k == kt - 1)
                mm.then_inc(product_ready, 1)

        def empty(eng):
            for i, (m, n) in enumerate(tiles):
                eng.wait_ge(product_ready, i + 1)
                finish(m, n, ps[:, i % 8, :]).then_inc(bank_free, 1)

        if engine == "scalar":
            block.scalar(empty)
        else:
            block.vector(empty)


def linear_tokens(core, x, w, kt, m, finish, engine="vector", tiles=TT):
    nc, ps = core.nc, core.ps
    with phase(core, "product_ready", "bank_free") as (block, product_ready, bank_free):
        @block.tensor
        def _(pe):
            for t in range(tiles):
                if t >= 8:
                    pe.wait_ge(bank_free, t - 7)
                for k in range(kt):
                    mm = nc.tensor.matmul(ps[:, t % 8, :m], x[:, k, t * P:(t + 1) * P], w[:, k, :m],
                                          start=k == 0, stop=k == kt - 1)
                mm.then_inc(product_ready, 1)

        def empty(eng):
            for t in range(tiles):
                eng.wait_ge(product_ready, t + 1)
                finish(t, ps[:, t % 8, :m]).then_inc(bank_free, 1)

        if engine == "scalar":
            block.scalar(empty)
        else:
            block.vector(empty)


def add_to_residual(core):
    return lambda t, product: core.nc.vector.tensor_tensor(core.x[:, t, :], product, core.x[:, t, :], ALU.add)


def setup(core):
    nc, d = core.nc, core.dram
    load(core, [(core.ident[:, :], d["c_ident"]), (core.block16[:, :], d["c_block16"]),
                (core.fold[:, :], d["c_fold"]),
                (core.x[:, :, :], d["x"].rearrange("b (t p) c -> p (b t) c", p=P))])
    with phase(core) as (block,):
        @block.vector
        def _(dve):
            nc.vector.memset(core.ones[:, :], 1.0)
            nc.vector.tensor_copy(core.identb[:, :], core.ident[:, :])


def store(core, out):
    nc = core.nc
    with phase(core, "stored") as (block, stored):
        @block.sync
        def _(sp):
            sp.dma_start(out.rearrange("b (t p) c -> p (b t) c", p=P), core.x[:, :, :]).then_inc(stored, 16)
            sp.wait_ge(stored, 16)



def l3_ffn(core):
    nc, d, ps = core.nc, core.dram, core.ps
    HID = 1024
    MT = HID // P
    with ExitStack() as c:
        sb = core.allocator(c)
        w1, w2 = sb([P, CT, HID]), sb([P, MT, C])
        b1, b2, scale = sb([P, MT]), sb([P, C]), sb([P, 1])
        h = sb([P, MT, N])
        xnd = d["scratch_tok"]
        rowmask = sb([4, 4, 1])
        blockmask = sb([16, 4])
        ev1 = sb([4, B, C])
        ev1z = sb([4, B, 4, C])
        ev2 = sb([16, B, 64])
        ev2z = sb([16, B, 4, 64])
        od1 = sb([P, B, CT, 4])
        od2 = sb([P, B, CT, 4])
        od2z = sb([P, B, CT, 4, 4, 4])
        p1 = sb([4, N])
        g = sb([16, N])
        layer_norm(core, core.x, core.xn, core.xnT, loads=[
            (w1[:, :, :], ktiles(d["L3_ffn_W1"])), (w2[:, :, :], ktiles(d["L3_ffn_W2"])),
            (b1[:, :], d["L3_ffn_b1"]), (b2[:, :], d["L3_ffn_b2"]),
            (scale[:, :], d["L3_ffn_scale"]),
            (rowmask[:, :, 0], d["c_eye4"]), (blockmask[:, :], d["c_block4"])], bias=b2[:, :])
        tok = lambda b, first: xnd[b, first:first + 8, :].rearrange("(i two) c -> i two c", two=2)[:, 0, :]
        with phase(core, "out_tok", "in_tok", "w") as (block, out_tok, in_tok, w):
            @block.sync
            def _(sp):
                sp.dma_start(xnd.rearrange("b (t p) c -> p (b t) c", p=P), core.xn[:, :, :]).then_inc(out_tok, 16)
                sp.wait_ge(out_tok, 16)
                for b in range(B):
                    sp.dma_start(ev1[:, b, :], tok(b, 1)).then_inc(in_tok, 16)
                    for i in range(4):
                        sp.dma_start(ev2[4 * i:4 * i + 4, b, :],
                                     xnd[b, 9 + 2 * i, :].rearrange("(c r) -> r c", r=4),
                                     allow_slow_non_contiguous=True).then_inc(in_tok, 16)
                sp.wait_ge(in_tok, 16 * 5 * B)

            @block.vector
            def _(dve):
                link = chain(dve, w)
                link(nc.vector.memset(od2z[:, :, :, :, :, :], 0.0))
                for b in range(B):
                    for k in range(CT):
                        x = core.xnT[:, k, b * T:(b + 1) * T]
                        nc.vector.tensor_scalar(od1[:, b, k, :], x[:, 2:10:2], scale[:, 0:1], None, ALU.mult)
                        for r in range(4):
                            nc.vector.tensor_scalar(od2z[:, b, k, r, :, r], x[:, 10:18:2], scale[:, 0:1], None,
                                                    ALU.mult)
                dve.wait_ge(in_tok, 16 * 5 * B)
                for i in range(4):
                    nc.vector.tensor_scalar(ev1z[:, :, i, :], ev1[:, :, :], rowmask[:, i, 0:1], None, ALU.mult)
                    nc.vector.tensor_scalar(ev2z[:, :, i, :], ev2[:, :, :], blockmask[:, i:i + 1], None, ALU.mult)
        with phase(core, "ready", "done") as (block, ready, done):
            @block.tensor
            def _(pe):
                for b in range(B):
                    for k in range(CT):
                        mm = nc.tensor.matmul(ps[0:4, b, 0:T], od1[:, b, k, :], core.xnT[:, k, b * T:(b + 1) * T],
                                              start=k == 0, stop=k == CT - 1)
                mm.then_inc(ready, 1)

            @block.scalar
            def _(act):
                act.wait_ge(ready, 1)
                nc.scalar.copy(p1[:, :].rearrange("p (b t) -> p b t", b=B), ps[0:4, 0:4, 0:T])
        tiles = [(m, b) for m in range(MT) for b in range(B)]
        with phase(core, "product_ready", "bank_free") as (block, product_ready, bank_free):
            @block.tensor
            def _(pe):
                for i, (m, b) in enumerate(tiles):
                    if i >= 8:
                        pe.wait_ge(bank_free, i - 7)
                    out = ps[:, i % 8, 0:T]
                    for k in range(CT):
                        nc.tensor.matmul(out, w1[:, k, m * P:(m + 1) * P], core.xnT[:, k, b * T:(b + 1) * T],
                                         start=k == 0, stop=False)
                    nc.tensor.matmul(out, ev1z[:, b, m // CT, (m % CT) * P:(m % CT + 1) * P],
                                     p1[:, b * T:(b + 1) * T], start=False, stop=True).then_inc(product_ready, 1)

            @block.scalar
            def _(act):
                for i, (m, b) in enumerate(tiles):
                    act.wait_ge(product_ready, i + 1)
                    nc.scalar.activation(h[:, m, b * T:(b + 1) * T], ps[:, i % 8, 0:T], ACT.Gelu,
                                         bias=b1[:, m:m + 1]).then_inc(bank_free, 1)
        with phase(core, "ready") as (block, ready):
            @block.tensor
            def _(pe):
                for b in range(B):
                    for m in range(MT):
                        r, k = m // CT, m % CT
                        mm = nc.tensor.matmul(ps[0:16, b, 0:T], od2z[:, b, k, r, :, :],
                                              h[:, m, b * T:(b + 1) * T], start=m == 0, stop=m == MT - 1)
                mm.then_inc(ready, 1)

            @block.scalar
            def _(act):
                act.wait_ge(ready, 1)
                nc.scalar.copy(g[:, :].rearrange("p (b t) -> p b t", b=B), ps[0:16, 0:4, 0:T])
        with phase(core, "product_ready") as (block, product_ready):
            @block.tensor
            def _(pe):
                for t in range(TT):
                    out = ps[:, t, 0:C]
                    for m in range(MT):
                        nc.tensor.matmul(out, h[:, m, t * P:(t + 1) * P], w2[:, m, :], start=m == 0, stop=False)
                    nc.tensor.matmul(out, g[:, t * P:(t + 1) * P],
                                     ev2z[:, t // 2, :, :], start=False, stop=True).then_inc(product_ready, 1)

            @block.vector
            def _(dve):
                for t in range(TT):
                    dve.wait_ge(product_ready, t + 1)
                    nc.vector.tensor_tensor(core.x[:, t, :], ps[:, t, 0:C], core.x[:, t, :], ALU.add)



def l3_attn(core):
    nc, d, ps = core.nc, core.dram, core.ps
    LEVELS = int(math.log2(T))
    with ExitStack() as c:
        sb = core.allocator(c)
        wu, wg, wb, wc = (sb([P, CT, C]) for _ in range(4))
        bu, bg, dd = sb([P, CT]), sb([P, CT]), sb([P, C])
        power = [sb([P, 2, CT, C]) for _ in range(2)]
        u, gate = sb([P, CT, N]), sb([P, CT, N])
        state = [sb([P, CT, N]) for _ in range(2)]
        layer_norm(core, core.x, core.xn, core.xnT, loads=[
            (wu[:, :, :], ktiles(d["L3_attn_W_u"])), (wg[:, :, :], ktiles(d["L3_attn_W_g"])),
            (wb[:, :, :], ktiles(d["L3_attn_Bm"])), (wc[:, :, :], ktiles(d["L3_attn_Cm"])),
            (bu[:, :], d["L3_attn_b_u"]), (bg[:, :], d["L3_attn_b_g"]), (dd[:, :], d["L3_attn_D"]),
            (power[0][:, 0, :, :], ktiles(d["L3_attn_A"])), (power[0][:, 1, :, :], ktiles(d["L3_attn_AT"]))], bias=dd[:, :])
        at = lambda tile, m, n: tile[:, m, n * BANK:(n + 1) * BANK]
        linear_features(core, wu, core.xnT, CT, CT, lambda m, n, q: nc.scalar.activation(
            at(u, m, n), q, ACT.Gelu, bias=bu[:, m:m + 1]))
        linear_features(core, wg, core.xnT, CT, CT, lambda m, n, q: nc.scalar.activation(
            at(gate, m, n), q, ACT.Sigmoid, bias=bg[:, m:m + 1]))
        with phase(core) as (block,):
            @block.vector
            def _(dve):
                for k in range(CT):
                    nc.vector.tensor_tensor(u[:, k, :], u[:, k, :], gate[:, k, :], ALU.mult)
        linear_features(core, wb, u, CT, CT, lambda m, n, q: nc.scalar.copy(at(state[0], m, n), q))
        for i in range(LEVELS):
            shift = 2 ** i
            old, new = state[i % 2], state[(i + 1) % 2]
            pw, nx = power[i % 2], power[(i + 1) % 2]
            length = T - shift
            seq = lambda tile, k: tile[:, k, :].rearrange("p (b t) -> p b t", b=B)
            with phase(core, "shifted", "squared") as (block, shifted, squared):
                @block.tensor
                def _(pe):
                    for m in range(CT):
                        for half in range(2):
                            out = ps[:, 2 * m + half, :].rearrange("p (b t) -> p b t", b=2)[:, :, 0:length]
                            for k in range(CT):
                                mm = nc.tensor.matmul(out, pw[:, 1, k, m * P:(m + 1) * P],
                                                      seq(old, k)[:, 2 * half:2 * half + 2, 0:length],
                                                      start=k == 0, stop=k == CT - 1)
                            mm.then_inc(shifted, 1)
                    if i < LEVELS - 1:
                        for side in range(2):
                            for m in range(CT):
                                for k in range(CT):
                                    mm = nc.tensor.matmul(ps[:, 4 + 2 * side + m, 0:C],
                                                          pw[:, 1 - side, k, m * P:(m + 1) * P], pw[:, side, k, :],
                                                          start=k == 0, stop=k == CT - 1)
                                mm.then_inc(squared, 1)

                @block.vector
                def _(dve):
                    for m in range(CT):
                        for half in range(2):
                            dve.wait_ge(shifted, 2 * m + half + 1)
                            bs = slice(2 * half, 2 * half + 2)
                            out = ps[:, 2 * m + half, :].rearrange("p (b t) -> p b t", b=2)[:, :, 0:length]
                            nc.vector.tensor_tensor(seq(new, m)[:, bs, shift:], out, seq(old, m)[:, bs, shift:],
                                                    ALU.add)

                @block.scalar
                def _(act):
                    for m in range(CT):
                        nc.scalar.copy(seq(new, m)[:, :, 0:shift], seq(old, m)[:, :, 0:shift])
                    if i < LEVELS - 1:
                        for side in range(2):
                            act.wait_ge(squared, CT * (side + 1))
                            nc.scalar.copy(nx[:, side, :, :], ps[:, 4 + 2 * side:6 + 2 * side, 0:C])
        linear_tokens(core, state[LEVELS % 2], wc, CT, C, add_to_residual(core))



def l3_xattn(core):
    nc, d, ps = core.nc, core.dram, core.ps
    CH = KC // P
    with ExitStack() as c:
        sb = core.allocator(c)
        wq, wp, wkv = sb([P, CT, C]), sb([P, CT, C]), sb([P, CT, 2 * C])
        bq, bp, bkv = sb([P, C]), sb([P, C]), sb([P, 2 * C])
        q, qT = sb([P, TT, C]), sb([P, CT, N])
        small = sb([P, 3, TT, H])
        ctx = sb([P, 2, CT, KC])
        ek, kk = sb([P, 4, 2, C]), sb([P, 3, 2, C])
        ksmall = sb([P, 3, 2, 2, H])
        v = sb([P, 4, 2, CT, P + 1])
        kv, ks = sb([P, CT, P]), sb([P, CT, P])
        ksum = sb([P, CT])
        res = sb([P, CT, N])
        rden = sb([P, CT, T])
        layer_norm(core, core.x, core.xn, core.xnT, loads=[
            (wq[:, :, :], ktiles(d["L3_xattn_Wq"])), (wp[:, :, :], ktiles(d["L3_xattn_Wp"])),
            (wkv[:, :, :], ktiles(d["L3_xattn_Wkv"])),
            (bq[:, :], d["L3_xattn_bq"]), (bp[:, :], d["L3_xattn_bp"]), (bkv[:, :], d["L3_xattn_bkv"])],
            bias=bp[:, :])
        heads = lambda ap: ap.rearrange("p (h c) -> p h c", h=H)
        spread = lambda ap: ap.unsqueeze(2).to_broadcast([P, H, D])
        with phase(core, "product_ready", "exp_done", "w", "q_ready", "turned", "centred") as (
                block, product_ready, exp_done, w, q_ready, turned, centred):
            @block.tensor
            def _(pe):
                for t in range(TT):
                    out = ps[:, t, 0:C]
                    for k in range(CT):
                        mm = nc.tensor.matmul(out, core.xnT[:, k, t * P:(t + 1) * P], wq[:, k, :],
                                              start=k == 0, stop=k == CT - 1)
                    mm.then_inc(product_ready, 1)
                for half in range(2):
                    pe.wait_ge(q_ready, 4 * (half + 1))
                    for t in range(4 * half, 4 * half + 4):
                        for k in range(CT):
                            nc.tensor.transpose(ps[:, CT * half + k, (t % 4) * P:(t % 4 + 1) * P],
                                                q[:, t, k * P:(k + 1) * P], core.ident[:, :]).then_inc(turned, 1)

            @block.vector
            def _(dve):
                link = chain(dve, w)
                for t in range(TT):
                    dve.wait_ge(product_ready, t + 1)
                    link(nc.vector.tensor_tensor(q[:, t, :], ps[:, t, 0:C], bq[:, :], ALU.add))
                    link(nc.vector.tensor_reduce(small[:, 0, t, :], heads(q[:, t, :]), AX.X, ALU.max))
                    nc.vector.tensor_tensor(heads(q[:, t, :]), heads(q[:, t, :]), spread(small[:, 0, t, :]),
                                            ALU.subtract).then_inc(centred, 1)
                for t in range(TT):
                    dve.wait_ge(exp_done, t + 1)
                    link(nc.vector.tensor_reduce(small[:, 1, t, :], heads(q[:, t, :]), AX.X, ALU.add))
                    link(nc.vector.reciprocal(small[:, 2, t, :], small[:, 1, t, :]))
                    nc.vector.tensor_tensor(heads(q[:, t, :]), heads(q[:, t, :]), spread(small[:, 2, t, :]),
                                            ALU.mult).then_inc(q_ready, 1)

            @block.scalar
            def _(act):
                for t in range(TT):
                    act.wait_ge(centred, t + 1)
                    nc.scalar.activation(q[:, t, :], q[:, t, :], ACT.Exp).then_inc(exp_done, 1)
                for half in range(2):
                    act.wait_ge(turned, 4 * CT * (half + 1))
                    nc.scalar.copy(qT[:, :, half * BANK:(half + 1) * BANK], ps[:, CT * half:CT * half + CT, :])
        pairs = [(ch, i) for ch in range(S // KC) for i in range(CH // 2)]
        with phase(core) as (block,):
            @block.gpsimd
            def _(pool):
                nc.gpsimd.memset(v[:, :, :, :, P:P + 1], 1.0)
        with nc.Fori(0, B) as b:
            names = ["landed_even", "landed_odd", "product_ready", "k_biased", "max_done", "centred", "exp_done",
                     "sum_done", "inverted", "k_ready", "v_ready", "kv_done"]
            with phase(core, *names) as (block, landed_even, landed_odd, product_ready, k_biased, max_done, centred,
                                         exp_done, sum_done, inverted, k_ready, v_ready, kv_done):
                landed = (landed_even, landed_odd)
                h2 = lambda ap: ap.rearrange("p t (h c) -> p (t h) c", h=H)
                flat = lambda ap: ap.rearrange("p t h -> p (t h)")
                spread2 = lambda ap: flat(ap).unsqueeze(2).to_broadcast([P, 2 * H, D])

                @block.sync
                def _(sp):
                    for ch in range(S // KC):
                        if ch >= 2:
                            sp.wait_ge(product_ready, (ch - 1) * CH // 2)
                        sp.dma_start(ctx[:, ch % 2, :, :],
                                     d["ctxT"][b, :, ch * KC:(ch + 1) * KC].rearrange("(k p) n -> p k n", p=P)
                                     ).then_inc(landed[ch % 2], 16)

                @block.tensor
                def _(pe):
                    def sums(j):
                        pe.wait_ge(k_ready, j + 1)
                        pe.wait_ge(v_ready, j + 1)
                        for i in range(2):
                            for f in range(CT):
                                mm = nc.tensor.matmul(ps[:, 4 + f, 0:P + 1], kk[:, j % 3, i, f * P:(f + 1) * P],
                                                      v[:, j % 4, i, f, :], start=j == 0 and i == 0,
                                                      stop=j == len(pairs) - 1 and i == 1)
                        mm.then_inc(kv_done, 1)

                    for j, (ch, i) in enumerate(pairs):
                        if i == 0:
                            pe.wait_ge(landed[ch % 2], 16 * (ch // 2 + 1))
                        if j >= 2:
                            pe.wait_ge(k_biased, j - 1)
                            pe.wait_ge(v_ready, j - 1)
                        for t in range(2):
                            for kind in range(2):
                                out = ps[:, 2 * (j % 2) + kind, t * C:(t + 1) * C]
                                for k in range(CT):
                                    mm = nc.tensor.matmul(out, ctx[:, ch % 2, k, (2 * i + t) * P:(2 * i + t + 1) * P],
                                                          wkv[:, k, kind * C:(kind + 1) * C], start=k == 0,
                                                          stop=k == CT - 1)
                        mm.then_inc(product_ready, 1)
                        if j >= 3:
                            sums(j - 3)
                    for j in range(len(pairs) - 3, len(pairs)):
                        sums(j)

                @block.vector
                def _(dve):
                    def biased(j):
                        dve.wait_ge(product_ready, j + 1)
                        if j >= 4:
                            dve.wait_ge(k_ready, j - 3)
                        nc.vector.tensor_tensor(ek[:, j % 4], ps[:, 2 * (j % 2), :].rearrange("p (t c) -> p t c", t=2),
                                                bkv[:, 0:C].unsqueeze(1).to_broadcast([P, 2, C]),
                                                ALU.add).then_inc(k_biased, 1)
                        dve.wait_ge(k_biased, j + 1)
                        if j >= 2:
                            dve.wait_ge(centred, j - 1)
                        nc.vector.tensor_reduce(flat(ksmall[:, 0, j % 2]), h2(ek[:, j % 4]), AX.X,
                                                ALU.max).then_inc(max_done, 1)

                    def norm(j):
                        dve.wait_ge(exp_done, j + 1)
                        nc.vector.tensor_reduce(flat(ksmall[:, 1, j % 2]), h2(ek[:, j % 4]), AX.X,
                                                ALU.add).then_inc(sum_done, 1)
                        dve.wait_ge(sum_done, j + 1)
                        nc.vector.reciprocal(flat(ksmall[:, 2, j % 2]), flat(ksmall[:, 1, j % 2])).then_inc(inverted, 1)
                        dve.wait_ge(inverted, j + 1)
                        if j >= 3:
                            dve.wait_ge(kv_done, j - 2)
                        nc.vector.tensor_tensor(h2(kk[:, j % 3]), h2(ek[:, j % 4]), spread2(ksmall[:, 2, j % 2]),
                                                ALU.mult).then_inc(k_ready, 1)

                    for j in range(len(pairs)):
                        biased(j)
                        if j >= 1:
                            norm(j - 1)
                    norm(len(pairs) - 1)

                @block.gpsimd
                def _(pool):
                    for j in range(len(pairs)):
                        pool.wait_ge(max_done, j + 1)
                        nc.gpsimd.tensor_tensor(h2(ek[:, j % 4]), h2(ek[:, j % 4]), spread2(ksmall[:, 0, j % 2]),
                                                ALU.subtract).then_inc(centred, 1)

                @block.scalar
                def _(act):
                    for j in range(len(pairs)):
                        act.wait_ge(product_ready, j + 1)
                        if j >= 4:
                            act.wait_ge(kv_done, j - 3)
                        nc.scalar.copy(v[:, j % 4, :, :, 0:P], ps[:, 2 * (j % 2) + 1, :].rearrange(
                            "p (t f c) -> p t f c", t=2, f=CT)).then_inc(v_ready, 1)
                        act.wait_ge(centred, j + 1)
                        nc.scalar.activation(ek[:, j % 4, :, :], ek[:, j % 4, :, :], ACT.Exp).then_inc(exp_done, 1)
            with phase(core, "w", "num_ready", "den_ready", "rden_ready", "done") as (
                    block, w, num_ready, den_ready, rden_ready, done):
                @block.vector
                def _(dve):
                    link = chain(dve, w)
                    for f in range(CT):
                        link(nc.vector.tensor_copy(ksum[:, f:f + 1], ps[:, 4 + f, P:P + 1]))
                        link(nc.vector.scalar_tensor_tensor(out=kv[:, f, :], in0=bkv[:, C + f * P:C + (f + 1) * P],
                                                            scalar=ksum[:, f:f + 1], in1=ps[:, 4 + f, 0:P],
                                                            op0=ALU.mult, op1=ALU.add))
                        nc.vector.tensor_tensor(kv[:, f, :], kv[:, f, :], core.block16[:, :], ALU.mult)
                        nc.vector.tensor_scalar(ks[:, f, :], core.block16[:, :], ksum[:, f:f + 1], None,
                                                ALU.mult).then_inc(done, 1)
                    for f in range(CT):
                        dve.wait_ge(den_ready, f + 1)
                        link(nc.vector.reciprocal(rden[:, f, :], ps[:, 2 * f + 1, 0:T]))
                        out = res[:, f, bass.ds(b * T, T)]
                        link(nc.vector.tensor_tensor(rden[:, f, :], ps[:, 2 * f, 0:T], rden[:, f, :], ALU.mult))
                        nc.vector.tensor_tensor(out, rden[:, f, :], qT[:, f, bass.ds(b * T, T)], ALU.add)

                @block.tensor
                def _(pe):
                    for f in range(CT):
                        pe.wait_ge(done, f + 1)
                        nc.tensor.matmul(ps[:, 2 * f, 0:T], kv[:, f, :], qT[:, f, bass.ds(b * T, T)],
                                         start=True, stop=True)
                        nc.tensor.matmul(ps[:, 2 * f + 1, 0:T], ks[:, f, :], qT[:, f, bass.ds(b * T, T)],
                                         start=True, stop=True).then_inc(den_ready, 1)
        linear_tokens(core, res, wp, CT, C, add_to_residual(core))

def l0_attn(core):
    nc, d, ps = core.nc, core.dram, core.ps
    FIVE, TM, TD = 5, 32, 64
    EPS = 1e-5 * 8 ** 2
    with ExitStack() as c:
        sb = core.allocator(c)
        wo = sb([P, CT, C])
        u, gamma, beta = sb([P, CT]), sb([P, CT]), sb([P, CT])
        r, k, v, dec, g = (sb([P, CT, N]) for _ in range(5))
        sel = sb([P, D, P])
        with ExitStack() as c2:
            sb2 = core.allocator(c2)
            maa = sb2([P, 6, CT])
            w1, w2, wd1, wd2 = sb2([P, CT, FIVE * TM]), sb2([P, 2, C]), sb2([P, CT, TD]), sb2([TD, C])
            decay = sb2([P, CT])
            proj = sb2([P, 4, CT, C])
            xx, mixed = sb2([P, CT, N]), sb2([P, CT, N])
            m = sb2([P, 2, N])
            hid = sb2([TD, N])
            layer_norm(core, core.x, core.xn, core.xnT, loads=[
                (maa[:, :, :], d["L0_attn_maa"]), (w1[:, :, :], ktiles(d["L0_attn_w1"])),
                (w2[:, 0, :], d["L0_attn_w2"][0:P, :]), (w2[0:TM, 1, :], d["L0_attn_w2"][P:P + TM, :]),
                (wd1[:, :, :], ktiles(d["L0_attn_wd1"])), (wd2[:, :], d["L0_attn_wd2"]),
                (decay[:, :], d["L0_attn_decay"]), (u[:, :], d["L0_attn_u"]),
                (gamma[:, :], d["L0_attn_gamma"]), (beta[:, :], d["L0_attn_beta"]),
                (sel[:, :, :], d["c_sel"]), (wo[:, :, :], ktiles(d["L0_attn_W_o"]))]
                + [(proj[:, i, :, :], ktiles(d["L0_attn_W_" + n])) for i, n in enumerate("rkvg")])
            seq = lambda tile, f: tile[:, f, :].rearrange("p (b t) -> p b t", b=B)
            with phase(core, "w") as (block, w):
                @block.vector
                def _(dve):
                    link = chain(dve, w)
                    for f in range(CT):
                        x = seq(core.xnT, f)
                        nc.vector.tensor_tensor(seq(xx, f)[:, :, 1:], x[:, :, 0:T - 1], x[:, :, 1:], ALU.subtract)
                        link(nc.vector.tensor_scalar(seq(xx, f)[:, :, 0:1], x[:, :, 0:1], -1.0, None, ALU.mult))
                        nc.vector.scalar_tensor_tensor(out=mixed[:, f, :], in0=xx[:, f, :], scalar=maa[:, 0, f:f + 1],
                                                       in1=core.xnT[:, f, :], op0=ALU.mult, op1=ALU.add)
            with phase(core, "ready") as (block, ready):
                @block.tensor
                def _(pe):
                    for part, width in ((0, P), (1, TM)):
                        for n in range(2):
                            for f in range(CT):
                                mm = nc.tensor.matmul(ps[0:width, 2 * part + n, :], w1[:, f, part * P:part * P + width],
                                                      mixed[:, f, n * BANK:(n + 1) * BANK], start=f == 0,
                                                      stop=f == CT - 1)
                            mm.then_inc(ready, 1)

                @block.scalar
                def _(act):
                    for part, width in ((0, P), (1, TM)):
                        for n in range(2):
                            act.wait_ge(ready, 2 * part + n + 1)
                            nc.scalar.activation(m[0:width, part, n * BANK:(n + 1) * BANK],
                                                 ps[0:width, 2 * part + n, :], ACT.Tanh)

            def mix(i):
                base, part = (TM * i, 0) if i < 4 else (0, 1)
                with phase(core, "ready", "w") as (block, ready, w):
                    @block.tensor
                    def _(pe):
                        for f in range(CT):
                            for n in range(2):
                                nc.tensor.matmul(ps[:, 2 * f + n, :], w2[base:base + TM, part, f * P:(f + 1) * P],
                                                 m[base:base + TM, part, n * BANK:(n + 1) * BANK],
                                                 start=True, stop=True, tile_position=(base, 0)).then_inc(ready, 1)

                    @block.vector
                    def _(dve):
                        link = chain(dve, w)
                        for f in range(CT):
                            dve.wait_ge(ready, 2 * f + 2)
                            link(nc.vector.scalar_tensor_tensor(
                                out=mixed[:, f, :].rearrange("p (n t) -> p n t", n=2), in0=ps[:, 2 * f:2 * f + 2, :],
                                scalar=maa[:, i + 1, f:f + 1], in1=xx[:, f, :].rearrange("p (n t) -> p n t", n=2),
                                op0=ALU.add, op1=ALU.mult))
                            nc.vector.tensor_tensor(mixed[:, f, :], mixed[:, f, :], core.xnT[:, f, :], ALU.add)

            at = lambda tile, mt, n: tile[:, mt, n * BANK:(n + 1) * BANK]
            for i, (j, dest) in {1: (1, k), 2: (2, v), 3: (0, r)}.items():
                mix(i)
                linear_features(core, proj[:, j, :, :], mixed, CT, CT,
                                lambda mt, n, q, dest=dest: nc.scalar.copy(at(dest, mt, n), q))
            mix(4)
            linear_features(core, proj[:, 3, :, :], mixed, CT, CT,
                            lambda mt, n, q: nc.scalar.activation(at(g, mt, n), q, ACT.Silu))
            mix(0)
            with phase(core, "ready", "hidden", "w") as (block, ready, hidden, w):
                @block.tensor
                def _(pe):
                    for n in range(2):
                        for f in range(CT):
                            mm = nc.tensor.matmul(ps[0:TD, n, :], wd1[:, f, :], mixed[:, f, n * BANK:(n + 1) * BANK],
                                                  start=f == 0, stop=f == CT - 1)
                        mm.then_inc(ready, 1)
                    for n in range(2):
                        pe.wait_ge(hidden, n + 1)
                        for f in range(CT):
                            nc.tensor.matmul(ps[:, 2 + 2 * n + f, :], wd2[:, f * P:(f + 1) * P],
                                             hid[:, n * BANK:(n + 1) * BANK], start=True, stop=True).then_inc(ready, 1)

                @block.scalar
                def _(act):
                    link = chain(act, w)
                    for n in range(2):
                        act.wait_ge(ready, n + 1)
                        nc.scalar.activation(hid[:, n * BANK:(n + 1) * BANK], ps[0:TD, n, :], ACT.Tanh).then_inc(hidden, 1)
                    for n in range(2):
                        for f in range(CT):
                            act.wait_ge(ready, 3 + 2 * n + f)
                            link(nc.scalar.activation(at(dec, f, n), ps[:, 2 + 2 * n + f, :], ACT.Exp,
                                                      bias=decay[:, f:f + 1]))
                            nc.scalar.activation(at(dec, f, n), at(dec, f, n), ACT.Exp, scale=-1.0)
        y, bonus, t1 = sb([P, CT, N]), sb([P, CT, N]), sb([P, CT, N])
        scan = sb([P, 2, 2, T + 1])
        kv, prod = sb([P, 2, BANK]), sb([P, 3, BANK])
        with phase(core) as (block,):
            @block.vector
            def _(dve):
                for f in range(CT):
                    nc.vector.scalar_tensor_tensor(out=bonus[:, f, :], in0=r[:, f, :], scalar=u[:, f:f + 1],
                                                   in1=k[:, f, :], op0=ALU.mult, op1=ALU.mult)
                nc.vector.memset(scan[:, :, :, 0:1], 0.0)
        linear_block(core, core.block16, bonus, lambda f, n, q: nc.vector.tensor_tensor(
            at(y, f, n), q, at(v, f, n), ALU.mult), "vector")
        units = [(f, n, i) for f in range(CT) for n in range(2) for i in range(D)]
        with phase(core, "spread", "bank_free", "kv_done", "scan_done", "prod_done", "summed") as (
                block, spread, bank_free, kv_done, scan_done, prod_done, summed):
            @block.tensor
            def _(pe):
                for j, (f, n, i) in enumerate(units):
                    s = 3 * (j % 2)
                    if j >= 2:
                        pe.wait_ge(bank_free, j - 1)
                    for q, src in enumerate((k, dec, r)):
                        nc.tensor.matmul(ps[:, s + q, :], sel[:, i, :], at(src, f, n), start=True,
                                         stop=True).then_inc(spread, 1)

            @block.vector
            def _(dve):
                for j, (f, n, i) in enumerate(units):
                    s, e = 3 * (j % 2), j % 2
                    dve.wait_ge(spread, 3 * j + 1)
                    nc.vector.tensor_tensor(kv[:, e, :], ps[:, s, :], at(v, f, n), ALU.mult).then_inc(kv_done, 1)
                    dve.wait_ge(kv_done, j + 1)
                    dve.wait_ge(spread, 3 * j + 2)
                    for b in range(2):
                        nc.vector.tensor_tensor_scan(scan[:, e, b, 1:T + 1], ps[:, s + 1, b * T:(b + 1) * T],
                                                     kv[:, e, b * T:(b + 1) * T], 0.0, ALU.mult,
                                                     ALU.add).then_inc(scan_done, 1)
                    dve.wait_ge(scan_done, 2 * j + 2)
                    dve.wait_ge(spread, 3 * j + 3)
                    if j >= 3:
                        dve.wait_ge(summed, j - 2)
                    nc.vector.tensor_tensor(prod[:, j % 3, :].rearrange("p (b t) -> p b t", b=2),
                                            ps[:, s + 2, :].rearrange("p (b t) -> p b t", b=2),
                                            scan[:, e, :, 0:T], ALU.mult).then_inc(bank_free, 1)

            @block.gpsimd
            def _(pool):
                for j, (f, n, i) in enumerate(units):
                    pool.wait_ge(bank_free, j + 1)
                    if j >= 1:
                        pool.wait_ge(summed, j)
                    nc.gpsimd.tensor_tensor(at(y, f, n), at(y, f, n), prod[:, j % 3, :], ALU.add).then_inc(summed, 1)
        linear_block(core, core.block16, y, lambda f, n, q: nc.vector.scalar_tensor_tensor(
            out=at(t1, f, n), in0=q, scalar=-1.0 / D, in1=at(y, f, n), op0=ALU.mult, op1=ALU.add), "vector")
        with phase(core) as (block,):
            @block.vector
            def _(dve):
                for f in range(CT):
                    nc.vector.tensor_tensor(y[:, f, :], t1[:, f, :], t1[:, f, :], ALU.mult)
        linear_block(core, core.block16, y, lambda f, n, q: nc.vector.tensor_scalar(
            at(bonus, f, n), q, 1.0 / D, EPS, ALU.mult, ALU.add), "vector")
        with phase(core, "root", "w") as (block, root, w):
            @block.scalar
            def _(act):
                for f in range(CT):
                    nc.scalar.activation(bonus[:, f, :], bonus[:, f, :], ACT.Sqrt).then_inc(root, 1)

            @block.vector
            def _(dve):
                link = chain(dve, w)
                for f in range(CT):
                    dve.wait_ge(root, f + 1)
                    link(nc.vector.reciprocal(bonus[:, f, :], bonus[:, f, :]))
                    link(nc.vector.tensor_tensor(t1[:, f, :], t1[:, f, :], bonus[:, f, :], ALU.mult))
                    link(nc.vector.tensor_scalar(t1[:, f, :], t1[:, f, :], gamma[:, f:f + 1], beta[:, f:f + 1],
                                                 ALU.mult, ALU.add))
                    nc.vector.tensor_tensor(t1[:, f, :], t1[:, f, :], g[:, f, :], ALU.mult)
        linear_tokens(core, t1, wo, CT, C, add_to_residual(core))


def linear_block(core, w, x, finish, engine):
    nc, ps = core.nc, core.ps
    tiles = [(f, n) for f in range(CT) for n in range(N // BANK)]
    with phase(core, "ready") as (block, ready):
        @block.tensor
        def _(pe):
            for i, (f, n) in enumerate(tiles):
                nc.tensor.matmul(ps[:, i, :], w[:, :], x[:, f, n * BANK:(n + 1) * BANK], start=True,
                                 stop=True).then_inc(ready, 1)

        def empty(eng):
            for i, (f, n) in enumerate(tiles):
                eng.wait_ge(ready, i + 1)
                finish(f, n, ps[:, i, :])

        if engine == "scalar":
            block.scalar(empty)
        else:
            block.vector(empty)



def pick_top(core, dve, link, scores, left, top, few):
    nc = core.nc
    for t in range(TT):
        last = nc.vector.max(top[:, t, :], scores[:, t, :])
    link(last)
    if few < 8:
        link(nc.vector.memset(top[:, :, few:8], -1.0))
    for t in range(TT):
        last = nc.vector.match_replace(left[:, t, :], top[:, t, :], scores[:, t, :], -2.0)
    link(last)


def expert_bias(core, weights, bias, e):
    nc, ps = core.nc, core.ps
    with ExitStack() as c:
        wT = core.allocator(c)([e, N])
        with phase(core, "turned", "copied", "ready") as (block, turned, copied, ready):
            @block.tensor
            def _(pe):
                for t in range(TT):
                    nc.tensor.transpose(ps[0:e, t // 4, (t % 4) * P:(t % 4 + 1) * P], weights[:, t, :],
                                        core.ident[:, :]).then_inc(turned, 1)
                for t in range(TT):
                    pe.wait_ge(copied, t // 4 + 1)
                    nc.tensor.matmul(ps[:, 2 + t // 2, (t % 2) * C:(t % 2 + 1) * C], wT[:, t * P:(t + 1) * P],
                                     bias, start=True, stop=True).then_inc(ready, 1)

            @block.scalar
            def _(act):
                for half in range(2):
                    act.wait_ge(turned, 4 * half + 4)
                    nc.scalar.copy(wT[:, half * BANK:(half + 1) * BANK], ps[0:e, half, :]).then_inc(copied, 1)

            @block.vector
            def _(dve):
                for t in range(TT):
                    dve.wait_ge(ready, t // 2 * 2 + 2)
                    nc.vector.tensor_tensor(core.x[:, t, :], ps[:, 2 + t // 2, (t % 2) * C:(t % 2 + 1) * C],
                                            core.x[:, t, :], ALU.add)


def l0_ffn(core):
    nc, d, ps = core.nc, core.dram, core.ps
    E, F, PICK = 64, 192, 8
    with ExitStack() as c:
        sb = core.allocator(c)
        gate = sb([P, CT, E])
        s, left, weights = sb([P, TT, E]), sb([P, TT, E]), sb([P, TT, E])
        top, small = sb([P, TT, 8]), sb([P, 3, TT, 1])
        layer_norm(core, core.x, core.xn, core.xnT, loads=[(gate[:, :, :], ktiles(d["L0_ffn_gate_w"]))])
        linear_tokens(core, core.xnT, gate, CT, E, lambda t, q: nc.vector.tensor_copy(s[:, t, :], q))
        spread = lambda i: small[:, i].to_broadcast([P, TT, E])
        with phase(core, "centred", "exp_done", "w") as (block, centred, exp_done, w):
            @block.vector
            def _(dve):
                link = chain(dve, w)
                link(nc.vector.tensor_reduce(small[:, 0, :, 0], s[:, :, :], AX.X, ALU.max))
                nc.vector.tensor_tensor(s[:, :, :], s[:, :, :], spread(0), ALU.subtract).then_inc(centred, 1)
                dve.wait_ge(exp_done, 1)
                link(nc.vector.tensor_reduce(small[:, 1, :, 0], s[:, :, :], AX.X, ALU.add))
                link(nc.vector.reciprocal(small[:, 1, :, :], small[:, 1, :, :]))
                link(nc.vector.tensor_tensor(s[:, :, :], s[:, :, :], spread(1), ALU.mult))
                pick_top(core, dve, link, s, left, top, PICK)
                link(nc.vector.tensor_reduce(small[:, 2, :, 0], top[:, :, :], AX.X, ALU.add))
                link(nc.vector.tensor_scalar(small[:, 2, :, :], small[:, 2, :, :], 1e-20, None, ALU.add))
                link(nc.vector.reciprocal(small[:, 2, :, :], small[:, 2, :, :]))
                link(nc.vector.tensor_scalar(left[:, :, :], left[:, :, :], -1.0, None, ALU.is_le))
                link(nc.vector.tensor_tensor(weights[:, :, :], s[:, :, :], left[:, :, :], ALU.mult))
                nc.vector.tensor_tensor(weights[:, :, :], weights[:, :, :], spread(2), ALU.mult)

            @block.scalar
            def _(act):
                act.wait_ge(centred, 1)
                nc.scalar.activation(s[:, :, :], s[:, :, :], ACT.Exp).then_inc(exp_done, 1)
        sparse_experts(core, weights, E)


def sparse_experts(core, weights, E):
    nc, d, ps = core.nc, core.dram, core.ps
    HT3 = 3
    AHEAD = 2
    ORDER = (2, 0, 1)
    with ExitStack() as c:
        sb = core.allocator(c)
        wgu = [sb([P, CT, 2, HT3 * P]) for _ in range(AHEAD)]
        wd = [sb([P, HT3, C]) for _ in range(AHEAD)]
        shares = [sb([P, N]) for _ in range(AHEAD)]
        gs = sb([P, 3, BANK])
        h = sb([P, AHEAD, HT3, N])
        wT = sb([E, N])

        def share_loads(pair, slot):
            return [(shares[slot][64 * i:64 * i + 64, :],
                     d["scratch_w"][bass.ds(2 * pair + i, 1), :].to_broadcast([64, N])) for i in range(2)]

        with phase(core, "turned", "copied", "stored", "landed") as (block, turned, copied, stored, landed):
            @block.tensor
            def _(pe):
                for t in range(TT):
                    nc.tensor.transpose(ps[0:E, t // 4, (t % 4) * P:(t % 4 + 1) * P], weights[:, t, :],
                                        core.ident[:, :]).then_inc(turned, 1)

            @block.scalar
            def _(act):
                for half in range(2):
                    act.wait_ge(turned, 4 * half + 4)
                    nc.scalar.copy(wT[:, half * BANK:(half + 1) * BANK], ps[0:E, half, :]).then_inc(copied, 1)

            @block.sync
            def _(sp):
                sp.dma_start(wgu[0][:, :, :, :], d["L0_ffn_wgu"][0]).then_inc(landed, 16)
                sp.dma_start(wd[0][:, :, :], d["L0_ffn_wd"][0]).then_inc(landed, 16)
                sp.wait_ge(copied, 2)
                sp.dma_start(d["scratch_w"][0:E], wT[:, :]).then_inc(stored, 16)
                sp.dma_start(d["scratch_w"][E:E + 2], wT[0:2, :]).then_inc(stored, 16)
                sp.wait_ge(stored, 32)
                for dst, src in share_loads(0, 0):
                    sp.dma_start(dst, src).then_inc(landed, 16)
                sp.wait_ge(landed, 64)

        UPS = 2 * HT3
        DOWNS = 3 * TT
        with nc.Fori(0, E // (2 * AHEAD)) as q:
            with phase(core, "wgu_b", "wd_b", "shares_b", "refilled", "up_ready", "silu_done", "shared", "h_ready",
                       "down_ready", "down_used") as (block, wgu_b, wd_b, shares_b, refilled, up_ready, silu_done,
                                                      shared, h_ready, down_ready, down_used):
                units = [(e, j, n) for e in range(AHEAD) for j in ORDER for n in range(2)]
                downs = [(e, j, t) for e in range(AHEAD) for j in ORDER for t in range(TT)]

                @block.sync
                def _(sp):
                    sp.dma_start(wgu[1][:, :, :, :], d["L0_ffn_wgu"][AHEAD * q + 1]).then_inc(wgu_b, 16)
                    for dst, src in share_loads(AHEAD * q + 1, 1):
                        sp.dma_start(dst, src).then_inc(shares_b, 16)
                    sp.dma_start(wd[1][:, :, :], d["L0_ffn_wd"][AHEAD * q + 1]).then_inc(wd_b, 16)
                    sp.wait_ge(up_ready, 2 * UPS)
                    sp.dma_start(wgu[0][:, :, :, :], d["L0_ffn_wgu"][AHEAD * q + 2]).then_inc(refilled, 16)
                    sp.wait_ge(shared, 2)
                    for dst, src in share_loads(AHEAD * q + 2, 0):
                        sp.dma_start(dst, src).then_inc(refilled, 16)
                    sp.wait_ge(down_ready, DOWNS)
                    sp.dma_start(wd[0][:, :, :], d["L0_ffn_wd"][AHEAD * q + 2]).then_inc(refilled, 16)
                    sp.wait_ge(refilled, 64)

                @block.tensor
                def _(pe):
                    for i, (e, j, n) in enumerate(units):
                        if i == UPS:
                            pe.wait_ge(wgu_b, 16)
                        if i >= 2:
                            pe.wait_ge(h_ready, i - 1)
                        for kind in range(2):
                            for k in range(CT):
                                mm = nc.tensor.matmul(ps[:, 2 * (i % 2) + kind, :],
                                                      wgu[e][:, k, kind, j * P:(j + 1) * P],
                                                      core.xnT[:, k, n * BANK:(n + 1) * BANK],
                                                      start=k == 0, stop=k == CT - 1)
                            mm.then_inc(up_ready, 1)
                    for i, (e, j, t) in enumerate(downs):
                        if i == 0:
                            pe.wait_ge(h_ready, UPS)
                        if i == DOWNS:
                            pe.wait_ge(h_ready, 2 * UPS)
                            pe.wait_ge(wd_b, 16)
                        if i >= 4:
                            pe.wait_ge(down_used, i - 3)
                        nc.tensor.matmul(ps[:, 4 + i % 4, 0:C], h[:, e, j, t * P:(t + 1) * P], wd[e][:, j, :],
                                         start=True, stop=True).then_inc(down_ready, 1)

                @block.scalar
                def _(act):
                    for i, (e, j, n) in enumerate(units):
                        act.wait_ge(up_ready, 2 * i + 1)
                        if i >= 3:
                            act.wait_ge(h_ready, i - 2)
                        nc.scalar.activation(gs[:, i % 3, :], ps[:, 2 * (i % 2), :], ACT.Silu).then_inc(silu_done, 1)

                @block.gpsimd
                def _(pool):
                    for i, (e, j, n) in enumerate(units):
                        if j == 2:
                            if e == 1 and n == 0:
                                pool.wait_ge(shares_b, 32)
                            pool.wait_ge(silu_done, i + 1)
                            nc.gpsimd.tensor_tensor(gs[:, i % 3, :], gs[:, i % 3, :],
                                                    shares[e][:, n * BANK:(n + 1) * BANK], ALU.mult).then_inc(shared, 1)

                @block.vector
                def _(dve):
                    for i, (e, j, n) in enumerate(units):
                        dve.wait_ge(silu_done, i + 1)
                        dve.wait_ge(up_ready, 2 * i + 2)
                        if j == 2:
                            dve.wait_ge(shared, 2 * e + n + 1)
                        nc.vector.tensor_tensor(h[:, e, j, n * BANK:(n + 1) * BANK], gs[:, i % 3, :],
                                                ps[:, 2 * (i % 2) + 1, :], ALU.mult).then_inc(h_ready, 1)
                    for i, (e, j, t) in enumerate(downs):
                        dve.wait_ge(down_ready, i + 1)
                        if i >= TT:
                            dve.wait_ge(down_used, i - TT + 1)
                        product, x = ps[:, 4 + i % 4, 0:C], core.x[:, t, :]
                        if j == 2:
                            nc.vector.tensor_tensor(x, product, x, ALU.add).then_inc(down_used, 1)
                        else:
                            nc.vector.scalar_tensor_tensor(out=x, in0=product,
                                                           scalar=weights[:, t, bass.ds(2 * AHEAD * q + 2 * e + j, 1)],
                                                           in1=x, op0=ALU.mult, op1=ALU.add).then_inc(down_used, 1)


def l1_attn(core):
    nc, d, ps = core.nc, core.dram, core.ps
    E, F, HR, PICK, PAD = 6, 384, 128, 2, 16
    FT = F // P
    with ExitStack() as c:
        sb = core.allocator(c)
        r1w, r2w = sb([P, CT, HR]), sb([HR, E])
        rows = sb([P, HR])
        lng, lnb = sb([P, 1]), sb([P, 1])
        r2b, route_bias, temp = sb([P, E]), sb([P, E]), sb([P, 1])
        b1, b2 = sb([P, E, FT]), sb([E, C])
        hr, hn, hT = sb([P, TT, HR]), sb([P, TT, HR]), sb([P, N])
        s, left, weights = sb([P, TT, PAD]), sb([P, TT, PAD]), sb([P, TT, E])
        top, small = sb([P, TT, 8]), sb([P, 3, TT, 1])
        stats, mv, rstd = sb([P, TT, 6]), sb([P, TT, 2]), sb([P, TT])
        layer_norm(core, core.x, core.xn, core.xnT, loads=[
            (r1w[:, :, :], ktiles(d["L1_attn_r1_w"])), (r2w[:, :], d["L1_attn_r2_w"]), (rows[:, :], d["L1_attn_r1_b"]),
            (lng[:, :], d["L1_attn_ln_g"]), (lnb[:, :], d["L1_attn_ln_b"]), (r2b[:, :], d["L1_attn_r2_b"]),
            (route_bias[:, :], d["L1_attn_route_bias"]), (temp[:, :], d["L1_attn_temp"]),
            (b1[:, :, :], d["L1_attn_b1"]), (b2[:, :], d["L1_attn_b2"])])
        linear_tokens(core, core.xnT, r1w, CT, HR, lambda t, q: nc.vector.tensor_tensor(
            hr[:, t, :], q, rows[:, :], ALU.add))
        with phase(core, "w", "var_ready", "root_done", "norm_done", "turned", "gelu_done", "logits", "exp_done",
                   "centred") as (block, w, var_ready, root_done, norm_done, turned, gelu_done, logits, exp_done,
                                  centred):
            @block.vector
            def _(dve):
                link = chain(dve, w)
                for t in range(TT):
                    link(nc.vector.bn_stats(stats[:, t, :], hr[:, t, :]))
                for t in range(TT):
                    link(nc.vector.bn_aggr(mv[:, t, :], stats[:, t, :]))
                nc.vector.tensor_scalar(rstd[:, :], mv[:, :, 1], 1e-5, None, ALU.add).then_inc(var_ready, 1)
                link(nc.vector.reciprocal(temp[:, :], temp[:, :]))
                dve.wait_ge(root_done, 1)
                link(nc.vector.reciprocal(rstd[:, :], rstd[:, :]))
                for t in range(TT):
                    nc.vector.tensor_scalar(hn[:, t, :], hr[:, t, :], mv[:, t, 0:1], rstd[:, t:t + 1],
                                            ALU.subtract, ALU.mult).then_inc(norm_done, 1)
                dve.wait_ge(logits, TT)
                link(nc.vector.memset(s[:, :, E:PAD], -1.0))
                spread_e = lambda ap: ap.unsqueeze(1).to_broadcast([P, TT, E])
                se = s[:, :, 0:E]
                link(nc.vector.tensor_tensor(se, ps[:, 2, 0:TT * E].rearrange("p (t e) -> p t e", e=E),
                                             spread_e(r2b[:, :]), ALU.add))
                link(nc.vector.tensor_scalar(se, se, temp[:, 0:1], None, ALU.mult))
                link(nc.vector.tensor_tensor(se, se, spread_e(route_bias[:, :]), ALU.add))
                spread = lambda i: small[:, i].to_broadcast([P, TT, E])
                link(nc.vector.tensor_reduce(small[:, 0, :, 0], se, AX.X, ALU.max))
                nc.vector.tensor_tensor(se, se, spread(0), ALU.subtract).then_inc(centred, 1)
                dve.wait_ge(exp_done, 1)
                link(nc.vector.tensor_reduce(small[:, 1, :, 0], se, AX.X, ALU.add))
                link(nc.vector.reciprocal(small[:, 1, :, :], small[:, 1, :, :]))
                link(nc.vector.tensor_tensor(se, se, spread(1), ALU.mult))
                pick_top(core, dve, link, s, left, top, PICK)
                link(nc.vector.tensor_scalar(left[:, :, 0:E], left[:, :, 0:E], -1.5, None, ALU.is_le))
                nc.vector.tensor_tensor(weights[:, :, :], se, left[:, :, 0:E], ALU.mult)

            @block.tensor
            def _(pe):
                for t in range(TT):
                    pe.wait_ge(norm_done, t + 1)
                    nc.tensor.transpose(ps[:, t // 4, (t % 4) * P:(t % 4 + 1) * P], hn[:, t, :],
                                        core.ident[:, :]).then_inc(turned, 1)
                for t in range(TT):
                    pe.wait_ge(gelu_done, t // 4 + 1)
                    nc.tensor.matmul(ps[:, 2, t * E:(t + 1) * E], hT[:, t * P:(t + 1) * P], r2w[:, :], start=True,
                                     stop=True).then_inc(logits, 1)

            @block.scalar
            def _(act):
                act.wait_ge(var_ready, 1)
                nc.scalar.activation(rstd[:, :], rstd[:, :], ACT.Sqrt).then_inc(root_done, 1)
                for half in range(2):
                    act.wait_ge(turned, 4 * half + 4)
                    nc.scalar.activation(hT[:, half * BANK:(half + 1) * BANK], ps[:, half, :], ACT.Gelu,
                                         bias=lnb[:, 0:1], scale=lng[:, 0:1]).then_inc(gelu_done, 1)
                act.wait_ge(centred, 1)
                nc.scalar.activation(s[:, :, 0:E], s[:, :, 0:E], ACT.Exp).then_inc(exp_done, 1)
        expert_bias(core, weights, b2[:, :], E)
        w1 = [sb([P, CT, F]) for _ in range(2)]
        w2 = [sb([P, FT, C]) for _ in range(2)]
        h = sb([P, FT, N])
        with nc.Fori(0, E // 2) as q:
            with phase(core, "w_a", "w_b", "up_ready", "h_ready", "down_ready", "down_used") as (
                    block, w_a, w_b, up_ready, h_ready, down_ready, down_used):
                landed = (w_a, w_b)
                units = [(m, n) for m in range(FT) for n in range(2)]

                @block.sync
                def _(sp):
                    for e in range(2):
                        sp.dma_start(w1[e][:, :, :], d["L1_attn_W1"][2 * q + e].rearrange("(k p) f -> p k f", p=P)
                                     ).then_inc(landed[e], 16)
                        sp.dma_start(w2[e][:, :, :], d["L1_attn_W2"][2 * q + e].rearrange("(k p) f -> p k f", p=P)
                                     ).then_inc(landed[e], 16)

                @block.tensor
                def _(pe):
                    for e in range(2):
                        pe.wait_ge(landed[e], 32)
                        for i, (m, n) in enumerate(units):
                            j = len(units) * e + i
                            if j >= 4:
                                pe.wait_ge(h_ready, j - 3)
                            for k in range(CT):
                                mm = nc.tensor.matmul(ps[:, j % 4, :], w1[e][:, k, m * P:(m + 1) * P],
                                                      core.xnT[:, k, n * BANK:(n + 1) * BANK], start=k == 0,
                                                      stop=k == CT - 1)
                            mm.then_inc(up_ready, 1)
                        pe.wait_ge(h_ready, len(units) * (e + 1))
                        for t in range(TT):
                            j = TT * e + t
                            if j >= 4:
                                pe.wait_ge(down_used, j - 3)
                            for m in range(FT):
                                mm = nc.tensor.matmul(ps[:, 4 + j % 4, 0:C], h[:, m, t * P:(t + 1) * P], w2[e][:, m, :],
                                                      start=m == 0, stop=m == FT - 1)
                            mm.then_inc(down_ready, 1)

                @block.scalar
                def _(act):
                    for e in range(2):
                        for i, (m, n) in enumerate(units):
                            j = len(units) * e + i
                            act.wait_ge(up_ready, j + 1)
                            if e == 1 and i == 0:
                                act.wait_ge(down_ready, TT)
                            nc.scalar.activation(h[:, m, n * BANK:(n + 1) * BANK], ps[:, j % 4, :],
                                                 ACT.Gelu if e == 0 else ACT.Silu,
                                                 bias=b1[:, bass.ds(2 * q + e, 1), m]).then_inc(h_ready, 1)

                @block.vector
                def _(dve):
                    for j in range(2 * TT):
                        e, t = j // TT, j % TT
                        dve.wait_ge(down_ready, j + 1)
                        if j >= 1:
                            dve.wait_ge(down_used, j)
                        nc.vector.scalar_tensor_tensor(out=core.x[:, t, :], in0=ps[:, 4 + j % 4, 0:C],
                                                       scalar=weights[:, t, bass.ds(2 * q + e, 1)],
                                                       in1=core.x[:, t, :], op0=ALU.mult,
                                                       op1=ALU.add).then_inc(down_used, 1)


def l1_ffn(core):
    nc, d, ps = core.nc, core.dram, core.ps
    E, G, I, PICK, PICKG, ROUTE = 16, 4, 256, 4, 2, 2.5
    IT, GP = I // P, 16
    with ExitStack() as c:
        sb = core.allocator(c)
        gate = sb([P, CT, E])
        s, masked, left, weights = (sb([P, TT, E]) for _ in range(4))
        gs, gleft = sb([P, TT, GP]), sb([P, TT, GP])
        top, small = sb([P, TT, 8]), sb([P, TT, 1])
        b1, b3, b2 = sb([P, E, IT]), sb([P, E, IT]), sb([E, C])
        layer_norm(core, core.x, core.xn, core.xnT, loads=[
            (gate[:, :, :], ktiles(d["L1_ffn_Wg"])), (b1[:, :, :], d["L1_ffn_b1"]), (b3[:, :, :], d["L1_ffn_b3"]),
            (b2[:, :], d["L1_ffn_b2"])])
        linear_tokens(core, core.xnT, gate, CT, E, lambda t, q: nc.scalar.activation(s[:, t, :], q, ACT.Sigmoid),
                      engine="scalar")
        with phase(core, "w") as (block, w):
            @block.vector
            def _(dve):
                link = chain(dve, w)
                grouped = lambda ap: ap.rearrange("p t (g e) -> p t g e", g=G)
                link(nc.vector.memset(gs[:, :, G:GP], -1.0))
                link(nc.vector.tensor_reduce(gs[:, :, 0:G], grouped(s[:, :, :]), AX.X, ALU.max))
                pick_top(core, dve, link, gs, gleft, top, PICKG)
                link(nc.vector.tensor_scalar(gleft[:, :, :], gleft[:, :, :], -1.5, None, ALU.is_le))
                link(nc.vector.tensor_scalar(masked[:, :, :], s[:, :, :], 1.0, None, ALU.add))
                link(nc.vector.tensor_tensor(grouped(masked[:, :, :]), grouped(masked[:, :, :]),
                                             gleft[:, :, 0:G].unsqueeze(3).to_broadcast([P, TT, G, E // G]), ALU.mult))
                link(nc.vector.tensor_scalar(masked[:, :, :], masked[:, :, :], -1.0, None, ALU.add))
                pick_top(core, dve, link, masked, left, top, PICK)
                link(nc.vector.tensor_tensor(left[:, :, :], masked[:, :, :], left[:, :, :], ALU.subtract))
                link(nc.vector.tensor_scalar(left[:, :, :], left[:, :, :], 1.5, None, ALU.is_ge))
                link(nc.vector.tensor_tensor(weights[:, :, :], s[:, :, :], left[:, :, :], ALU.mult))
                link(nc.vector.tensor_reduce(small[:, :, 0], weights[:, :, :], AX.X, ALU.add))
                link(nc.vector.reciprocal(small[:, :, :], small[:, :, :]))
                link(nc.vector.tensor_scalar(small[:, :, :], small[:, :, :], ROUTE, None, ALU.mult))
                nc.vector.tensor_tensor(weights[:, :, :], weights[:, :, :], small[:, :, :].to_broadcast([P, TT, E]),
                                        ALU.mult)
        expert_bias(core, weights, b2[:, :], E)
        w13 = [sb([P, CT, 2, I]) for _ in range(2)]
        w2 = [sb([P, IT, C]) for _ in range(2)]
        gate_h, h = sb([P, 2, BANK]), sb([P, IT, N])
        with nc.Fori(0, E // 2) as q:
            with phase(core, "w_a", "w_b", "up_ready", "silu_done", "h_ready", "down_ready", "down_used") as (
                    block, w_a, w_b, up_ready, silu_done, h_ready, down_ready, down_used):
                landed = (w_a, w_b)
                units = [(e, m, n) for e in range(2) for m in range(IT) for n in range(2)]

                @block.sync
                def _(sp):
                    for e in range(2):
                        sp.dma_start(w13[e][:, :, :, :], d["L1_ffn_W13"][2 * q + e]).then_inc(landed[e], 16)
                        sp.dma_start(w2[e][:, :, :], d["L1_ffn_W2"][2 * q + e].rearrange("(k p) f -> p k f", p=P)
                                     ).then_inc(landed[e], 16)

                @block.tensor
                def _(pe):
                    for e in range(2):
                        pe.wait_ge(landed[e], 32)
                        for i in range(2 * IT):
                            j = 2 * IT * e + i
                            _, m, n = units[j]
                            if j >= 2:
                                pe.wait_ge(h_ready, j - 1)
                            for kind in range(2):
                                for k in range(CT):
                                    mm = nc.tensor.matmul(ps[:, 2 * (j % 2) + kind, :],
                                                          w13[e][:, k, kind, m * P:(m + 1) * P],
                                                          core.xnT[:, k, n * BANK:(n + 1) * BANK], start=k == 0,
                                                          stop=k == CT - 1)
                                mm.then_inc(up_ready, 1)
                        pe.wait_ge(h_ready, 2 * IT * (e + 1))
                        for t in range(TT):
                            j = TT * e + t
                            if j >= 4:
                                pe.wait_ge(down_used, j - 3)
                            for m in range(IT):
                                mm = nc.tensor.matmul(ps[:, 4 + j % 4, 0:C], h[:, m, t * P:(t + 1) * P], w2[e][:, m, :],
                                                      start=m == 0, stop=m == IT - 1)
                            mm.then_inc(down_ready, 1)

                @block.scalar
                def _(act):
                    for j, (e, m, n) in enumerate(units):
                        act.wait_ge(up_ready, 2 * j + 1)
                        if j >= 2:
                            act.wait_ge(h_ready, j - 1)
                        nc.scalar.activation(gate_h[:, j % 2, :], ps[:, 2 * (j % 2), :], ACT.Silu,
                                             bias=b1[:, bass.ds(2 * q + e, 1), m]).then_inc(silu_done, 1)

                @block.vector
                def _(dve):
                    for j, (e, m, n) in enumerate(units):
                        dve.wait_ge(silu_done, j + 1)
                        dve.wait_ge(up_ready, 2 * j + 2)
                        if e == 1 and m == 0 and n == 0:
                            dve.wait_ge(down_ready, TT)
                        nc.vector.scalar_tensor_tensor(out=h[:, m, n * BANK:(n + 1) * BANK],
                                                       in0=ps[:, 2 * (j % 2) + 1, :],
                                                       scalar=b3[:, bass.ds(2 * q + e, 1), m], in1=gate_h[:, j % 2, :],
                                                       op0=ALU.add, op1=ALU.mult).then_inc(h_ready, 1)
                        if m == IT - 1 and n == 1:
                            for t in range(TT):
                                i = TT * e + t
                                dve.wait_ge(down_ready, i + 1)
                                if i >= 1:
                                    dve.wait_ge(down_used, i)
                                nc.vector.scalar_tensor_tensor(out=core.x[:, t, :], in0=ps[:, 4 + i % 4, 0:C],
                                                               scalar=weights[:, t, bass.ds(2 * q + e, 1)],
                                                               in1=core.x[:, t, :], op0=ALU.mult,
                                                               op1=ALU.add).then_inc(down_used, 1)

def attend(core, heads, spans, score, turns, weigh, per_bank, dest):
    nc, ps = core.nc, core.ps
    total = sum(w for _, w in spans)
    with ExitStack() as c:
        sb = core.allocator(c)
        p, pT = sb([P, 3, BANK]), sb([P, 3, BANK])
        nm, z = sb([P, 4, 2]), sb([P, 4, 2])
        with phase(core, "scored", "max_done", "exp_done", "inv_done", "normed", "turned", "copied", "weighed",
                   "taken") as (block, scored, max_done, exp_done, inv_done, normed, turned, copied, weighed, taken):
            @block.tensor
            def _(pe):
                for i in range(heads + 4):
                    if i < heads:
                        if i >= 2:
                            pe.wait_ge(exp_done, 2 * (i - 1))
                        score(i, ps[:, i % 2, :]).then_inc(scored, 1)
                    j = i - 2
                    if 0 <= j < heads:
                        pe.wait_ge(normed, 2 * (j + 1))
                        if j >= 2:
                            pe.wait_ge(copied, j - 1)
                        for a, b in turns:
                            mm = nc.tensor.transpose(ps[:, 2 + j % 2, b:b + P], p[:, j % 3, a:a + P],
                                                     core.ident[:, :])
                        mm.then_inc(turned, 1)
                    j = i - 4
                    if 0 <= j < heads:
                        group = j // per_bank
                        pe.wait_ge(copied, j + 1)
                        if j % per_bank == 0 and group >= 2:
                            pe.wait_ge(taken, group - 1)
                        weigh(j, pT[:, j % 3, :], ps[:, 4 + group % 2, :]).then_inc(weighed, 1)

            @block.vector
            def _(dve):
                def maxima(i):
                    dve.wait_ge(scored, i + 1)
                    if i >= 4:
                        dve.wait_ge(exp_done, 2 * (i - 3))
                    for s, (a, w) in enumerate(spans):
                        nc.vector.tensor_reduce(nm[:, i % 4, s:s + 1], ps[:, i % 2, a:a + w], AX.X, ALU.max,
                                                negate=True).then_inc(max_done, 1)

                def norm(i):
                    dve.wait_ge(exp_done, 2 * (i + 1))
                    nc.vector.reciprocal(z[:, i % 4, :], z[:, i % 4, :]).then_inc(inv_done, 1)
                    dve.wait_ge(inv_done, i + 1)
                    for s, (a, w) in enumerate(spans):
                        nc.vector.tensor_scalar(p[:, i % 3, a:a + w], p[:, i % 3, a:a + w], z[:, i % 4, s:s + 1], None,
                                                ALU.mult).then_inc(normed, 1)

                def take(g):
                    dve.wait_ge(weighed, per_bank * (g + 1))
                    nc.vector.tensor_copy(dest(g), ps[:, 4 + g % 2, 0:T]).then_inc(taken, 1)

                for i in range(heads + 6):
                    if i < heads:
                        maxima(i)
                    if 1 <= i <= heads:
                        norm(i - 1)
                    if i >= 6 and (i - 5) % per_bank == 0:
                        take((i - 5) // per_bank - 1)

            @block.scalar
            def _(act):
                for i in range(heads + 3):
                    if i < heads:
                        act.wait_ge(max_done, 2 * (i + 1))
                        if i >= 3:
                            act.wait_ge(turned, i - 2)
                        if i >= 4:
                            act.wait_ge(normed, 2 * (i - 3))
                        for s, (a, w) in enumerate(spans):
                            nc.scalar.activation(p[:, i % 3, a:a + w], ps[:, i % 2, a:a + w], ACT.Exp,
                                                 bias=nm[:, i % 4, s:s + 1],
                                                 accum_out=z[:, i % 4, s:s + 1]).then_inc(exp_done, 1)
                    j = i - 2
                    if 0 <= j < heads:
                        act.wait_ge(turned, j + 1)
                        if j >= 3:
                            act.wait_ge(weighed, j - 2)
                        nc.scalar.copy(pT[:, j % 3, 0:total], ps[:, 2 + j % 2, 0:total]).then_inc(copied, 1)


def l2_attn(core):
    nc, d, ps = core.nc, core.dram, core.ps
    HD = 64
    M = H * HD // P
    with ExitStack() as c:
        sb = core.allocator(c)
        w_in, w_out = sb([P, CT, 3 * H * HD]), sb([P, M, C])
        b_qk, b_v, b_out = sb([P, 2 * M]), sb([P, H * HD]), sb([P, C])
        cos, sin, turn = sb([P, T]), sb([P, T]), sb([P, P])
        causal_wide, causal, identb = sb([P, P]), sb([P, P], BF16), sb([P, P], BF16)
        xb = sb([P, CT, T])
        raw, t2 = sb([P, 3, T]), sb([P, 2, T])
        qk, v, o = sb([P, 2 * M, T]), sb([P, 2, H * HD]), sb([P, M, T])
        layer_norm(core, core.x, core.xn, core.xnT, loads=[
            (w_in[:, :, :], ktiles(d["L2_attn_W_in"])), (w_out[:, :, :], ktiles(d["L2_attn_W_out"])),
            (b_qk[:, :], d["L2_attn_b_qk"]), (b_v[:, :], d["L2_attn_b_v"]), (b_out[:, :], d["L2_attn_b_out"]),
            (cos[:, :], d["c_cos64"]), (sin[:, :], d["c_sin64"]), (turn[:, :], d["c_turn64"]),
            (causal_wide[:, :], d["c_causal"])])
        with phase(core, "w") as (block, w):
            @block.vector
            def _(dve):
                nc.vector.tensor_copy(identb[:, :], core.ident[:, :])
                nc.vector.tensor_copy(causal[:, :], causal_wide[:, :])
                nc.vector.tensor_scalar(b_qk[:, 0:M], b_qk[:, 0:M], HD ** -0.5, None, ALU.mult)
                for t in range(TT):
                    nc.vector.tensor_tensor(core.x[:, t, :], core.x[:, t, :], b_out[:, :], ALU.add)
        with nc.Fori(0, B) as b:
            with phase(core, "sliced", "product", "raw_done", "turned", "rot_done", "sum_done", "v_product",
                       "cos_done") as (block, sliced, product, raw_done, turned, rot_done, sum_done, v_product, cos_done):
                vt = [(t, n) for t in range(2) for n in range(2)]

                @block.tensor
                def _(pe):
                    pe.wait_ge(sliced, 1)
                    for i in range(2 * M + 1):
                        if i < 2 * M:
                            if i >= 2:
                                pe.wait_ge(raw_done, i - 1)
                            for k in range(CT):
                                mm = nc.tensor.matmul(ps[:, i % 2, 0:T], w_in[:, k, i * P:(i + 1) * P], xb[:, k, :],
                                                      start=k == 0, stop=k == CT - 1)
                            mm.then_inc(product, 1)
                        if i >= 1:
                            j = i - 1
                            pe.wait_ge(raw_done, j + 1)
                            if j >= 2:
                                pe.wait_ge(rot_done, j - 1)
                            nc.tensor.matmul(ps[:, 2 + j % 2, 0:T], turn[:, :], raw[:, j % 3, :], start=True,
                                             stop=True).then_inc(turned, 1)
                    for j, (t, n) in enumerate(vt):
                        for k in range(CT):
                            mm = nc.tensor.matmul(ps[:, 4 + j, :], xb[:, k, t * P:(t + 1) * P],
                                                  w_in[:, k, 2 * M * P + n * BANK:2 * M * P + (n + 1) * BANK],
                                                  start=k == 0, stop=k == CT - 1)
                        mm.then_inc(v_product, 1)

                @block.scalar
                def _(act):
                    for i in range(2 * M):
                        act.wait_ge(product, i + 1)
                        if i >= 3:
                            act.wait_ge(turned, i - 2)
                            act.wait_ge(sum_done, i - 2)
                        nc.scalar.activation(raw[:, i % 3, :], ps[:, i % 2, 0:T], ACT.Identity, bias=b_qk[:, i:i + 1],
                                             scale=HD ** -0.5 if i < M else 1.0).then_inc(raw_done, 1)

                @block.vector
                def _(dve):
                    nc.vector.tensor_copy(xb[:, :, :], core.xnT[:, :, bass.ds(b * T, T)]).then_inc(sliced, 1)
                    for i in range(2 * M):
                        dve.wait_ge(raw_done, i + 1)
                        nc.vector.tensor_tensor(qk[:, i, :], raw[:, i % 3, :], cos[:, :], ALU.mult).then_inc(cos_done, 1)
                        dve.wait_ge(turned, i + 1)
                        nc.vector.tensor_tensor(t2[:, i % 2, :], ps[:, 2 + i % 2, 0:T], sin[:, :],
                                                ALU.mult).then_inc(rot_done, 1)
                        dve.wait_ge(rot_done, i + 1)
                        dve.wait_ge(cos_done, i + 1)
                        nc.vector.tensor_tensor(qk[:, i, :], qk[:, i, :], t2[:, i % 2, :], ALU.add).then_inc(sum_done, 1)
                    for j, (t, n) in enumerate(vt):
                        dve.wait_ge(v_product, j + 1)
                        nc.vector.tensor_tensor(v[:, t, n * BANK:(n + 1) * BANK], ps[:, 4 + j, :],
                                                b_v[:, n * BANK:(n + 1) * BANK], ALU.add)

            def score(h, bank):
                base, m = HD * (h % 2), h // 2
                for tile, a, w in ((0, 0, P), (1, P, 2 * P)):
                    nc.tensor.matmul(bank[:, a:a + w], qk[base:base + HD, m, tile * P:(tile + 1) * P],
                                     qk[base:base + HD, M + m, 0:w], start=True, stop=False, skip_group_check=True)
                    mm = nc.tensor.matmul(bank[:, a + w - P:a + w], identb[:, :], causal[:, :], start=False,
                                          stop=True, skip_group_check=True)
                return mm

            def weigh(h, probs, out):
                base = HD * (h % 2)
                nc.tensor.matmul(out[base:base + HD, 0:T], v[:, 0, h * HD:(h + 1) * HD], probs[:, 0:T], start=True,
                                 stop=False, skip_group_check=True)
                return nc.tensor.matmul(out[base:base + HD, P:T], v[:, 1, h * HD:(h + 1) * HD], probs[:, T:T + P],
                                        start=False, stop=True, skip_group_check=True)

            attend(core, H, [(0, P), (P, 2 * P)], score, [(0, 0), (P, P), (2 * P, 2 * P)], weigh, 2,
                   lambda g: o[:, g, :])
            with phase(core, "ready") as (block, ready):
                @block.tensor
                def _(pe):
                    for t in range(2):
                        for m in range(M):
                            mm = nc.tensor.matmul(ps[:, t, 0:C], o[:, m, t * P:(t + 1) * P], w_out[:, m, :],
                                                  start=m == 0, stop=m == M - 1)
                        mm.then_inc(ready, 1)

                @block.vector
                def _(dve):
                    for t in range(2):
                        dve.wait_ge(ready, t + 1)
                        x = core.x[:, bass.ds(2 * b + t, 1), :]
                        nc.vector.tensor_tensor(x, ps[:, t:t + 1, 0:C], x, ALU.add)


def l2_ffn(core):
    nc, d, ps = core.nc, core.dram, core.ps
    NH, HD, E, FD, TPE = 32, 8, 8, 1024, 64
    FT = FD // P
    with ExitStack() as c:
        sb = core.allocator(c)
        xfT = sb([P, CT, N])
        with ExitStack() as c2:
            sb2 = core.allocator(c2)
            w = sb2([P, 4, CT, C])
            gain, shift, mask8 = sb2([P, CT]), sb2([P, CT]), sb2([P, 16])
            oT, xaT, xa_tok = sb2([P, CT, N]), sb2([P, CT, N]), sb2([P, TT, C])
            xb, q, k = sb2([P, CT, T]), sb2([P, CT, T]), sb2([P, CT, T])
            qz, vz = sb2([P, NH, T]), sb2([P, 2, NH, 32])
            layer_norm(core, core.x, core.xn, core.xnT, loads=[
                (w[:, i, :, :], ktiles(d["L2_ffn_w" + n])) for i, n in enumerate("qkvo")] + [
                (gain[:, :], d["L2_ffn_ln_g"]), (shift[:, :], d["L2_ffn_ln_b"]), (mask8[:, :], d["c_mask8"])])
            layer_norm(core, core.xn, xa_tok, xaT, gain=gain, shift=shift)
            with phase(core) as (block,):
                @block.gpsimd
                def _(pool):
                    nc.gpsimd.memset(vz[:, :, :, :], 0.0)
            with nc.Fori(0, B) as b:
                with phase(core, "sliced", "product", "q_done") as (block, sliced, product, q_done):
                    @block.tensor
                    def _(pe):
                        pe.wait_ge(sliced, 1)
                        for i in range(2):
                            for m in range(CT):
                                for kk in range(CT):
                                    mm = nc.tensor.matmul(ps[:, 2 * i + m, 0:T], w[:, i, kk, m * P:(m + 1) * P],
                                                          xb[:, kk, :], start=kk == 0, stop=kk == CT - 1)
                                mm.then_inc(product, 1)
                        for t in range(2):
                            for kk in range(CT):
                                mm = nc.tensor.matmul(ps[:, 4 + t, 0:C], xb[:, kk, t * P:(t + 1) * P], w[:, 2, kk, :],
                                                      start=kk == 0, stop=kk == CT - 1)
                            mm.then_inc(product, 1)

                    @block.scalar
                    def _(act):
                        for m in range(CT):
                            act.wait_ge(product, m + 1)
                            nc.scalar.mul(q[:, m, :], ps[:, m, 0:T], HD ** -0.5).then_inc(q_done, 1)
                        for m in range(CT):
                            act.wait_ge(product, CT + m + 1)
                            nc.scalar.copy(k[:, m, :], ps[:, 2 + m, 0:T])

                    @block.vector
                    def _(dve):
                        nc.vector.tensor_copy(xb[:, :, :], xaT[:, :, bass.ds(b * T, T)]).then_inc(sliced, 1)
                        for h in range(NH):
                            dve.wait_ge(q_done, h // 16 + 1)
                            nc.vector.tensor_scalar(qz[:, h, :], q[:, h // 16, :], mask8[:, h % 16:h % 16 + 1], None,
                                                    ALU.mult)
                        for t in range(2):
                            dve.wait_ge(product, 2 * CT + t + 1)
                            src = ps[:, 4 + t, 0:C].rearrange("p (g j c) -> p g j c", j=4, c=HD)
                            dst = vz[:, t, :, :].rearrange("p (g j) c -> p g j c", j=4)
                            for j in range(4):
                                nc.vector.tensor_copy(dst[:, :, j, HD * j:HD * (j + 1)], src[:, :, j, :])

                def score(h, bank):
                    for t in range(2):
                        mm = nc.tensor.matmul(bank[:, t * T:(t + 1) * T], qz[:, h, t * P:(t + 1) * P], k[:, h // 16, :],
                                              start=True, stop=True)
                    return mm

                def weigh(h, probs, out):
                    g = (h % 16) // 4
                    for t in range(2):
                        mm = nc.tensor.matmul(out[32 * g:32 * g + 32, 0:T], vz[:, t, h, :], probs[:, t * T:(t + 1) * T],
                                              start=h % 4 == 0 and t == 0, stop=h % 4 == 3 and t == 1,
                                              skip_group_check=True, tile_position=(0, 32 * g))
                    return mm

                attend(core, NH, [(0, T), (T, T)], score, [(0, 0), (P, T), (T, P), (T + P, T + P)], weigh, 16,
                       lambda g: oT[:, g, bass.ds(b * T, T)])
            linear_features(core, w[:, 3, :, :], oT, CT, CT, lambda m, n, qq: nc.vector.tensor_tensor(
                xfT[:, m, n * BANK:(n + 1) * BANK], qq, core.xnT[:, m, n * BANK:(n + 1) * BANK], ALU.add), "vector")
        w1 = [sb([P, CT, FD]) for _ in range(2)]
        w2 = [sb([P, FT, C]) for _ in range(2)]
        b1, b2 = sb([P, E, FT]), sb([P, C])
        h = sb([P, FT, 2, 2, TPE])
        tmp = sb([P, 2, C])
        load(core, [(b1[:, :, :], d["L2_ffn_b1"])])
        with nc.Fori(0, E // 2) as a:
            with phase(core, "w_a", "w_b", "b2_in", "up_ready", "h_ready", "down_ready", "biased") as (
                    block, w_a, w_b, b2_in, up_ready, h_ready, down_ready, biased):
                landed = (w_a, w_b)

                @block.sync
                def _(sp):
                    for i in range(2):
                        sp.dma_start(w1[i][:, :, :], d["L2_ffn_w1"][2 * a + i].rearrange("(k p) f -> p k f", p=P)
                                     ).then_inc(landed[i], 16)
                        sp.dma_start(w2[i][:, :, :], d["L2_ffn_w2"][2 * a + i].rearrange("(k p) f -> p k f", p=P)
                                     ).then_inc(landed[i], 16)
                    sp.dma_start(b2[:, :], d["L2_ffn_b2"][a]).then_inc(b2_in, 16)

                @block.tensor
                def _(pe):
                    for i in range(2):
                        pe.wait_ge(landed[i], 32)
                        for f in range(FT):
                            j = FT * i + f
                            if j >= 4:
                                pe.wait_ge(h_ready, j - 3)
                            for k2 in range(CT):
                                x = xfT[:, k2, :].rearrange("p (mb t) -> p mb t", mb=2)
                                mm = nc.tensor.matmul(ps[:, j % 4, 0:2 * TPE].rearrange("p (mb t) -> p mb t", mb=2),
                                                      w1[i][:, k2, f * P:(f + 1) * P],
                                                      x[:, :, bass.ds((2 * a + i) * TPE, TPE)],
                                                      start=k2 == 0, stop=k2 == CT - 1)
                            mm.then_inc(up_ready, 1)
                    pe.wait_ge(h_ready, 2 * FT)
                    for mb in range(2):
                        for i in range(2):
                            for f in range(FT):
                                mm = nc.tensor.matmul(ps[TPE * i:TPE * (i + 1), 4 + mb, 0:C], h[:, f, i, mb, :],
                                                      w2[i][:, f, :], start=f == 0, stop=f == FT - 1)
                        mm.then_inc(down_ready, 1)

                @block.scalar
                def _(act):
                    for i in range(2):
                        for f in range(FT):
                            j = FT * i + f
                            act.wait_ge(up_ready, j + 1)
                            nc.scalar.activation(h[:, f, i, :, :],
                                                 ps[:, j % 4, 0:2 * TPE].rearrange("p (mb t) -> p mb t", mb=2),
                                                 ACT.Gelu, bias=b1[:, bass.ds(2 * a + i, 1), f]).then_inc(h_ready, 1)

                @block.vector
                def _(dve):
                    dve.wait_ge(b2_in, 16)
                    for mb in range(2):
                        dve.wait_ge(down_ready, mb + 1)
                        nc.vector.tensor_tensor(tmp[:, mb, :], ps[:, 4 + mb, 0:C], b2[:, :], ALU.add).then_inc(biased, 1)
                    for mb in range(2):
                        dve.wait_ge(biased, mb + 1)
                        x = core.x[:, bass.ds(a + 4 * mb, 1), :]
                        nc.vector.tensor_tensor(x, tmp[:, mb:mb + 1, :], x, ALU.add)

K_SLOTS = (0, 0, 1, 1, 0, 2)
Q_SLOTS = (0, 1, 0, 1, 2, 0)
SLOTS = len(K_SLOTS)
SHIFT = SLOTS * D
ROWS = SHIFT + 1
VW = D + 1
PART = 32


def part_columns(dest, c, f):
    return dest[:, f * P:(f + 1) * P, c * KC:(c + 1) * KC].rearrange("s p n -> p s n")


def project_parts(core, w, chunks, source, dest, scale=1.0, values=None, rope=None):
    nc, ps = core.nc, core.ps
    streams = callable(source)
    with ExitStack() as c_:
        sb = core.allocator(c_)
        rest, parts = sb([P, 2, KC]), sb([P, 2, 3, KC], BF16)
        if streams:
            ctx = sb([P, 2, CT, KC])
        if rope:
            norm_w, table, turn, eps = rope
            tab = sb([P, 2, 2, KC])
            raw, square, root, mix, turned_ = (sb([P, 2, KC]) for _ in range(5))
        names = ["ctx_a", "ctx_b", "tab_a", "tab_b", "product", "high_done", "rest_done", "middle_done", "low_done",
                 "v_product", "v_done", "copied", "summed", "root_done", "cos_done", "sin_done", "mixed", "inverted",
                 "normed", "stored_a", "stored_b"]
        with phase(core, *names) as (block, ctx_a, ctx_b, tab_a, tab_b, product, high_done, rest_done, middle_done,
                                     low_done, v_product, v_done, copied, summed, root_done, cos_done, sin_done,
                                     mixed, inverted, normed, stored_a, stored_b):
            stored = (stored_a, stored_b)
            units = [(c, f) for c in range(chunks) for f in range(CT)]
            ctx_in, tab_in = (ctx_a, ctx_b), (tab_a, tab_b)
            x_of = (lambda c: ctx[:, c % 2]) if streams else (lambda c: source[:, :, c * KC:(c + 1) * KC])

            @block.sync
            def _(sp):
                for c in range(chunks + 2):
                    if streams and c < chunks:
                        if c >= 2:
                            sp.wait_ge(product, CT * (c - 1))
                            if values:
                                sp.wait_ge(v_product, CT * (c - 1))
                        sp.dma_start(ctx[:, c % 2, :, :], source(c)).then_inc(ctx_in[c % 2], 16)
                    if rope and c < chunks:
                        if c >= 2:
                            sp.wait_ge(sin_done, CT * (c - 1))
                            sp.wait_ge(cos_done, CT * (c - 1))
                        sp.dma_start(tab[:, c % 2, :, :], table(c)).then_inc(tab_in[c % 2], 16)
                    if c >= 2:
                        for f in range(CT):
                            i = CT * (c - 2) + f
                            sp.wait_ge(low_done, i + 1)
                            sp.dma_start(part_columns(dest, c - 2, f), parts[:, i % 2, :, :]).then_inc(
                                stored[i % 2], 16)
                for slot in range(2):
                    sp.wait_ge(stored[slot], 16 * (len(units) // 2))

            @block.tensor
            def _(pe):
                def heads_of(i):
                    pe.wait_ge(copied, i + 1)
                    if i >= 2:
                        pe.wait_ge(root_done, i - 1)
                        pe.wait_ge(sin_done, i - 1)
                    b = 2 if i % 2 == 0 else 6
                    nc.tensor.matmul(ps[:, b, :], core.block16[:, :], square[:, i % 2, :], start=True, stop=True)
                    nc.tensor.matmul(ps[:, b + 1, :], turn, raw[:, i % 2, :], start=True, stop=True).then_inc(summed, 1)

                for i, (c, f) in enumerate(units):
                    if streams and f == 0:
                        pe.wait_ge(ctx_in[c % 2], 16 * (c // 2 + 1))
                    if i >= 2:
                        pe.wait_ge(copied if rope else rest_done, i - 1)
                    for k in range(CT):
                        mm = nc.tensor.matmul(ps[:, i % 2, :], w[:, k, f * P:(f + 1) * P], x_of(c)[:, k, :],
                                              start=k == 0, stop=k == CT - 1)
                    mm.then_inc(product, 1)
                    if values:
                        if i >= 2:
                            pe.wait_ge(v_done, i - 1)
                        for t in range(2):
                            for k in range(CT):
                                mm = nc.tensor.matmul(ps[:, 4 + i % 2, t * C:(t + 1) * C],
                                                      x_of(c)[:, k, (2 * f + t) * P:(2 * f + t + 1) * P],
                                                      values[0][:, k, :], start=k == 0, stop=k == CT - 1)
                        mm.then_inc(v_product, 1)
                    if rope and i >= 1:
                        heads_of(i - 1)
                if rope:
                    heads_of(len(units) - 1)

            out = lambda i, part: parts[:, i % 2, part, :]
            whole = (lambda i: mix[:, i % 2, :]) if rope else (lambda i: ps[:, i % 2, :])

            @block.scalar
            def _(act):
                def high(i):
                    act.wait_ge(normed if rope else product, i + 1)
                    if i >= 2:
                        act.wait_ge(stored[i % 2], 16 * (i // 2))
                    nc.scalar.mul(out(i, 0), whole(i), scale).then_inc(high_done, 1)

                for i in range(len(units)):
                    if rope:
                        act.wait_ge(product, i + 1)
                        if i >= 2:
                            act.wait_ge(summed, i - 1)
                            act.wait_ge(cos_done, i - 1)
                        nc.scalar.copy(raw[:, i % 2, :], ps[:, i % 2, :])
                        nc.scalar.activation(square[:, i % 2, :], ps[:, i % 2, :], ACT.Square).then_inc(copied, 1)
                    else:
                        high(i)
                    if values:
                        act.wait_ge(v_product, i + 1)
                        nc.scalar.copy(values[1][:, 2 * i:2 * i + 2, :, 0:D],
                                       ps[:, 4 + i % 2, :].rearrange("p (t h c) -> p t h c", t=2, h=H)
                                       ).then_inc(v_done, 1)
                    if rope:
                        act.wait_ge(summed, i + 1)
                        if i >= 2:
                            act.wait_ge(normed, i - 1)
                        nc.scalar.activation(root[:, i % 2, :], ps[:, 2 if i % 2 == 0 else 6, :], ACT.Sqrt,
                                             bias=eps, scale=1.0 / D).then_inc(root_done, 1)
                        if i >= 1:
                            high(i - 1)
                if rope:
                    high(len(units) - 1)

            @block.vector
            def _(dve):
                def rotate(i):
                    c, s = units[i][0] % 2, i % 2
                    dve.wait_ge(tab_in[c], 16 * (units[i][0] // 2 + 1))
                    dve.wait_ge(copied, i + 1)
                    if i >= 2:
                        dve.wait_ge(rest_done, i - 1)
                        dve.wait_ge(high_done, i - 1)
                    nc.vector.scalar_tensor_tensor(out=mix[:, s, :], in0=raw[:, s, :], scalar=norm_w,
                                                   in1=tab[:, c, 0, :], op0=ALU.mult, op1=ALU.mult).then_inc(cos_done, 1)
                    dve.wait_ge(summed, i + 1)
                    nc.vector.tensor_tensor(turned_[:, s, :], ps[:, 3 if s == 0 else 7, :], tab[:, c, 1, :],
                                            ALU.mult).then_inc(sin_done, 1)
                    dve.wait_ge(sin_done, i + 1)
                    dve.wait_ge(cos_done, i + 1)
                    nc.vector.tensor_tensor(mix[:, s, :], mix[:, s, :], turned_[:, s, :], ALU.add).then_inc(mixed, 1)
                    dve.wait_ge(root_done, i + 1)
                    nc.vector.reciprocal(root[:, s, :], root[:, s, :]).then_inc(inverted, 1)

                def split(i):
                    dve.wait_ge(high_done, i + 1)
                    if i >= 2:
                        dve.wait_ge(low_done, i - 1)
                    nc.vector.scalar_tensor_tensor(out=rest[:, i % 2, :], in0=whole(i), scalar=scale, in1=out(i, 0),
                                                   op0=ALU.mult, op1=ALU.subtract).then_inc(rest_done, 1)

                for i in range(len(units)):
                    if rope:
                        rotate(i)
                        if i >= 1:
                            split(i - 1)
                    else:
                        split(i)
                if rope:
                    split(len(units) - 1)

            @block.gpsimd
            def _(pool):
                def norm(i):
                    pool.wait_ge(mixed, i + 1)
                    pool.wait_ge(inverted, i + 1)
                    nc.gpsimd.tensor_tensor(mix[:, i % 2, :], mix[:, i % 2, :], root[:, i % 2, :],
                                            ALU.mult).then_inc(normed, 1)

                def low(i):
                    pool.wait_ge(rest_done, i + 1)
                    nc.gpsimd.tensor_copy(out(i, 1), rest[:, i % 2, :]).then_inc(middle_done, 1)
                    pool.wait_ge(middle_done, i + 1)
                    nc.gpsimd.tensor_tensor(out(i, 2), rest[:, i % 2, :], out(i, 1), ALU.subtract).then_inc(low_done, 1)

                for i in range(len(units)):
                    if rope:
                        norm(i)
                        if i >= 1:
                            low(i - 1)
                    else:
                        low(i)
                if rope:
                    low(len(units) - 1)


class NextKeys:

    NAMES = ("ctx_a", "ctx_b", "tab_a", "tab_b", "product", "copied", "summed", "turned", "root_done", "cos_done",
             "sin_done", "mixed", "inverted", "normed", "high_done", "rest_done", "middle_done", "low_done", "stored_a",
             "stored_b", "v_product", "v_done")

    def __init__(self, core, sb, sems, w, w_v, v, source, dest, rope, spare, v_bank):
        self.core, self.w, self.w_v, self.v, self.source, self.dest = core, w, w_v, v, source, dest
        self.rope, self.out, self.v_out = rope, core.ps[:, spare, :], core.ps[:, v_bank, :]
        self.ctx, self.rest, self.parts = sb([P, 2, CT, KC]), sb([P, 2, KC]), sb([P, 2, 3, KC], BF16)
        if rope:
            self.norm_w, self.table, self.turn, self.eps = rope
            self.tab = sb([P, 2, 2, KC])
            self.raw, self.square, self.root, self.mix, self.spun = (sb([P, 2, KC]) for _ in range(5))
        (ctx_a, ctx_b, tab_a, tab_b, self.product, self.copied, self.summed, self.turned, self.root_done,
         self.cos_done, self.sin_done, self.mixed, self.inverted, self.normed, self.high_done, self.rest_done,
         self.middle_done, self.low_done, stored_a, stored_b, self.v_product, self.v_done) = sems
        self.ctx_in, self.tab_in, self.stored = (ctx_a, ctx_b), (tab_a, tab_b), (stored_a, stored_b)
        self.chunks, self.units = S // KC, CT * S // KC

    def load_chunk(self, sp, c):
        if c >= 2:
            sp.wait_ge(self.product, CT * (c - 1))
            sp.wait_ge(self.v_product, CT * (c - 1))
        sp.dma_start(self.ctx[:, c % 2, :, :], self.source(c)).then_inc(self.ctx_in[c % 2], 16)
        if self.rope:
            if c >= 2:
                sp.wait_ge(self.cos_done, CT * (c - 1))
                sp.wait_ge(self.sin_done, CT * (c - 1))
            sp.dma_start(self.tab[:, c % 2, :, :], self.table(c)).then_inc(self.tab_in[c % 2], 16)

    def store(self, sp, u):
        sp.wait_ge(self.low_done, u + 1)
        sp.dma_start(part_columns(self.dest, u // CT, u % CT), self.parts[:, u % 2, :, :]).then_inc(
            self.stored[u % 2], 16)

    def all_stored(self, sp):
        for slot in range(2):
            sp.wait_ge(self.stored[slot], 16 * (self.units // 2))

    def multiply(self, pe, u, k):
        c, f = u // CT, u % CT
        pe.wait_ge(self.ctx_in[c % 2], 16 * (c // 2 + 1))
        mm = self.core.nc.tensor.matmul(self.out, self.w[:, k, f * P:(f + 1) * P], self.ctx[:, c % 2, k, :],
                                        start=k == 0, stop=k == CT - 1)
        if k == CT - 1:
            mm.then_inc(self.product, 1)

    def sum_heads(self, pe, u):
        pe.wait_ge(self.copied, u + 1)
        self.core.nc.tensor.matmul(self.out, self.core.block16[:, :], self.square[:, u % 2, :], start=True,
                                   stop=True).then_inc(self.summed, 1)

    def turn_pairs(self, pe, u):
        pe.wait_ge(self.root_done, u + 1)
        self.core.nc.tensor.matmul(self.out, self.turn, self.raw[:, u % 2, :], start=True, stop=True).then_inc(
            self.turned, 1)

    def product_used(self, pe, u):
        pe.wait_ge(self.sin_done if self.rope else self.rest_done, u + 1)

    def multiply_values(self, pe, u, t):
        c, f, nc = u // CT, u % CT, self.core.nc
        for k in range(CT):
            mm = nc.tensor.matmul(self.v_out[:, t * C:(t + 1) * C],
                                  self.ctx[:, c % 2, k, (2 * f + t) * P:(2 * f + t + 1) * P], self.w_v[:, k, :],
                                  start=k == 0, stop=k == CT - 1)
        if t == 1:
            mm.then_inc(self.v_product, 1)

    def copy_product(self, act, u):
        nc, s = self.core.nc, u % 2
        act.wait_ge(self.product, u + 1)
        if u >= 2:
            act.wait_ge(self.summed, u - 1)
            act.wait_ge(self.turned, u - 1)
            act.wait_ge(self.cos_done, u - 1)
        nc.scalar.copy(self.raw[:, s, :], self.out)
        nc.scalar.activation(self.square[:, s, :], self.out, ACT.Square).then_inc(self.copied, 1)

    def take_root(self, act, u):
        act.wait_ge(self.summed, u + 1)
        if u >= 2:
            act.wait_ge(self.normed, u - 1)
        self.core.nc.scalar.activation(self.root[:, u % 2, :], self.out, ACT.Sqrt, bias=self.eps,
                                       scale=1.0 / D).then_inc(self.root_done, 1)

    def whole(self, u):
        return self.mix[:, u % 2, :] if self.rope else self.out

    def high(self, act, u):
        act.wait_ge(self.normed if self.rope else self.product, u + 1)
        if u >= 2:
            act.wait_ge(self.stored[u % 2], 16 * (u // 2))
        self.core.nc.scalar.copy(self.parts[:, u % 2, 0, :], self.whole(u)).then_inc(self.high_done, 1)

    def copy_values(self, act, u):
        act.wait_ge(self.v_product, u + 1)
        self.core.nc.scalar.copy(self.v[:, 2 * u:2 * u + 2, :, 0:D],
                                 self.v_out.rearrange("p (t h c) -> p t h c", t=2, h=H)).then_inc(self.v_done, 1)

    def scale_cos(self, dve, u):
        c, s = u // CT, u % 2
        dve.wait_ge(self.tab_in[c % 2], 16 * (c // 2 + 1))
        dve.wait_ge(self.copied, u + 1)
        if u >= 2:
            dve.wait_ge(self.rest_done, u - 1)
            dve.wait_ge(self.high_done, u - 1)
        self.core.nc.vector.scalar_tensor_tensor(out=self.mix[:, s, :], in0=self.raw[:, s, :], scalar=self.norm_w,
                                                 in1=self.tab[:, c % 2, 0, :], op0=ALU.mult,
                                                 op1=ALU.mult).then_inc(self.cos_done, 1)

    def scale_sin(self, dve, u):
        nc, c, s = self.core.nc, u // CT, u % 2
        dve.wait_ge(self.turned, u + 1)
        nc.vector.tensor_tensor(self.spun[:, s, :], self.out, self.tab[:, c % 2, 1, :], ALU.mult).then_inc(
            self.sin_done, 1)
        dve.wait_ge(self.sin_done, u + 1)
        dve.wait_ge(self.cos_done, u + 1)
        nc.vector.tensor_tensor(self.mix[:, s, :], self.mix[:, s, :], self.spun[:, s, :], ALU.add).then_inc(
            self.mixed, 1)

    def invert(self, dve, u):
        dve.wait_ge(self.root_done, u + 1)
        self.core.nc.vector.reciprocal(self.root[:, u % 2, :], self.root[:, u % 2, :]).then_inc(self.inverted, 1)

    def take_rest(self, dve, u):
        dve.wait_ge(self.high_done, u + 1)
        if u >= 2:
            dve.wait_ge(self.low_done, u - 1)
        self.core.nc.vector.tensor_tensor(self.rest[:, u % 2, :], self.whole(u), self.parts[:, u % 2, 0, :],
                                          ALU.subtract).then_inc(self.rest_done, 1)

    def low_parts(self, pool, u):
        nc, s = self.core.nc, u % 2
        if self.rope:
            pool.wait_ge(self.mixed, u + 1)
            pool.wait_ge(self.inverted, u + 1)
            nc.gpsimd.tensor_tensor(self.mix[:, s, :], self.mix[:, s, :], self.root[:, s, :], ALU.mult).then_inc(
                self.normed, 1)
        pool.wait_ge(self.rest_done, u + 1)
        nc.gpsimd.tensor_copy(self.parts[:, s, 1, :], self.rest[:, s, :]).then_inc(self.middle_done, 1)
        pool.wait_ge(self.middle_done, u + 1)
        nc.gpsimd.tensor_tensor(self.parts[:, s, 2, :], self.rest[:, s, :], self.parts[:, s, 1, :],
                                ALU.subtract).then_inc(self.low_done, 1)


def load_queries(sp, queries, qstack, landed):
    for s, part in enumerate(Q_SLOTS):
        sp.dma_start(qstack[s * D:(s + 1) * D, :, :], queries[part].rearrange("(h c) n -> c h n", h=H)).then_inc(
            landed, 16)


def load_keys(sp, keys, kstack, h, landed):
    for s, part in enumerate(K_SLOTS):
        sp.dma_start(kstack[s * D:(s + 1) * D, h % 3, :], keys[part, h * D:(h + 1) * D, :]).then_inc(landed, 16)


def attend_context(core, queries, keys, v, qstack, kstack, bias, att, coming=None):
    nc, ps = core.nc, core.ps
    QT = T // P
    NK = S // KC
    GU = QT * NK
    EU = KT // 4
    rope = coming is not None and coming["rope"] is not None
    GUARDS = (3, 3, 2, 3, 3, 2, 0, 0) if rope else (3, 3, 3, 3, 2, 2, 0, 0)
    units_of = [range(sum(GUARDS[:e]), sum(GUARDS[:e + 1])) for e in range(EU)]
    OUT, SPARE = 6, 7
    V_BANK = 5 if rope else SPARE
    with ExitStack() as c:
        sb = core.allocator(c)
        p = sb([P, 3, 4 * T])
        gm, neg = sb([P, 2, QT, NK]), sb([P, 2, QT])
        fold, osum, inv = core.fold, sb([P, 2, T]), sb([P, 2, QT])
        with phase(core, "q_in", "k_a", "k_b", "k_c", "scored", "max_done", "neg_done", "neg_row", "shift_done", "qk",
                   "exp_done", "pv", "taken", "out_ready", "inv_done", "out_done", "cleared",
                   *(NextKeys.NAMES if coming else ())) as (
                block, q_in, k_a, k_b, k_c, scored, max_done, neg_done, neg_row, shift_done, qk, exp_done, pv,
                taken, out_ready, inv_done, out_done, cleared, *next_sems):
            k_in = (k_a, k_b, k_c)
            new = NextKeys(core, sb, next_sems, spare=SPARE, v_bank=V_BANK, **coming) if coming else None

            @block.sync
            def _(sp):
                load_keys(sp, keys, kstack, 0, k_in[0])
                load_queries(sp, queries, qstack, q_in)
                load_keys(sp, keys, kstack, 1, k_in[1])
                if new:
                    new.load_chunk(sp, 0)
                    new.load_chunk(sp, 1)
                for h in range(H):
                    if h + 2 < H:
                        if h >= 1:
                            sp.wait_ge(qk, EU * h)
                        load_keys(sp, keys, kstack, h + 2, k_in[(h + 2) % 3])
                    if new:
                        if h % CT == 0 and 2 <= h // CT + 1 < new.chunks:
                            new.load_chunk(sp, h // CT + 1)
                        if h >= 1:
                            new.store(sp, h - 1)
                if new:
                    new.store(sp, H - 1)
                    new.all_stored(sp)

            @block.tensor
            def _(pe):
                def guard(h, g):
                    t, kc = g // NK, g % NK
                    if g == 0:
                        pe.wait_ge(k_in[h % 3], 16 * SLOTS * (h // 3 + 1))
                        if h == 0:
                            pe.wait_ge(q_in, 16 * SLOTS)
                        if h >= 1:
                            pe.wait_ge(shift_done, h)
                    if g == 1 and new and rope and h >= 2:
                        pe.wait_ge(new.v_done, h - 1)
                    if g >= 2:
                        pe.wait_ge(max_done, GU * h + g - 1)
                    biased = bias is not None and kc == 0
                    mm = nc.tensor.matmul(ps[:, 4 + g % 2, :], qstack[0:SHIFT, h, t * P:(t + 1) * P],
                                          kstack[0:SHIFT, h % 3, kc * KC:(kc + 1) * KC], start=True, stop=True,
                                          skip_group_check=biased)
                    if biased:
                        for k in range(t + 2):
                            mm = nc.tensor.matmul(ps[:, 4 + g % 2, k * P:(k + 1) * P], core.identb[:, :],
                                                  bias[1][:, k - t + 1, h, :], start=False, stop=True,
                                                  skip_group_check=True)
                    mm.then_inc(scored, 1)

                def shift(h):
                    pe.wait_ge(neg_done, h + 1)
                    for t in range(QT):
                        mm = nc.tensor.matmul(ps[SHIFT:ROWS, 4, t * P:(t + 1) * P], neg[:, h % 2, t:t + 1],
                                              core.ident[:, :], start=True, stop=True, tile_position=(0, SHIFT))
                    mm.then_inc(neg_row, 1)

                def scores(i):
                    h, e = i // EU, i % EU
                    if e == 0:
                        pe.wait_ge(shift_done, h + 1)
                    if i >= 2:
                        pe.wait_ge(exp_done, i - 1)
                    for j in range(4):
                        kt = 4 * e + j
                        out = ps[:, 2 * (i % 2) + j // 2, (j % 2) * T:(j % 2 + 1) * T]
                        near = [t for t in range(QT) if kt - t <= 1] if bias is not None else []
                        mm = nc.tensor.matmul(out, kstack[:, h % 3, kt * P:(kt + 1) * P], qstack[:, h, :],
                                              start=True, stop=True, skip_group_check=bool(near))
                        for t in near:
                            mm = nc.tensor.matmul(out[:, t * P:(t + 1) * P], core.ident[:, :],
                                                  bias[0][:, kt - t + 1, h, :], start=False, stop=True,
                                                  skip_group_check=True)
                    mm.then_inc(qk, 1)

                def weigh(i):
                    h, e = i // EU, i % EU
                    pe.wait_ge(exp_done, i + 1)
                    if i == 0:
                        pe.wait_ge(cleared, 1)
                    if e == 0 and h >= 1:
                        pe.wait_ge(taken, h)
                    for j in range(4):
                        mm = nc.tensor.matmul(ps[PART * j:PART * j + VW, OUT, 0:T], v[:, 4 * e + j, h, :],
                                              p[:, i % 3, j * T:(j + 1) * T], start=e == 0, stop=e == EU - 1,
                                              tile_position=(0, PART * j))
                    mm.then_inc(pv, 1)

                def output(h):
                    pe.wait_ge(taken, h + 1)
                    if new:
                        new.product_used(pe, min(h + 1, H - 1))
                        pe.wait_ge(new.v_done, min(h + 1, H) if rope else min(h + 2, H))
                    if h >= 1:
                        pe.wait_ge(out_done, h)
                    for t in range(QT):
                        mm = nc.tensor.matmul(ps[:, SPARE, t * VW:(t + 1) * VW], osum[:, h % 2, t * P:(t + 1) * P],
                                              fold[:, 0:VW], start=True, stop=True)
                    mm.then_inc(out_ready, 1)

                for g in range(GU):
                    guard(0, g)
                shift(0)
                for i in range(H * EU):
                    h, e = i // EU, i % EU
                    guards = list(units_of[e]) if h + 1 < H else []
                    for g in guards[0:1]:
                        guard(h + 1, g)
                    scores(i)
                    for g in guards[1:2]:
                        guard(h + 1, g)
                    if i >= 1:
                        weigh(i - 1)
                    for g in guards[2:]:
                        guard(h + 1, g)
                    if new and e in (0, 1):
                        if e == 0 and h >= 2:
                            pe.wait_ge(out_done, h - 1)
                        if e == 0 and h == 1:
                            new.product_used(pe, 0)
                            if not rope:
                                pe.wait_ge(new.v_done, 1)
                        new.multiply(pe, h, e)
                    if new and not rope and e in (4, 5):
                        new.product_used(pe, h)
                        new.multiply_values(pe, h, e - 4)
                    if new and rope and e == 2:
                        new.sum_heads(pe, h)
                    if new and rope and e == 3:
                        new.turn_pairs(pe, h)
                    if e == 6:
                        if h + 1 < H:
                            shift(h + 1)
                        if h >= 1:
                            output(h - 1)
                    if new and rope and e in (6, 7):
                        if e == 6 and h + 1 < H:
                            pe.wait_ge(max_done, GU * (h + 2))
                        elif e == 6:
                            pe.wait_ge(new.v_done, h)
                        new.multiply_values(pe, h, e - 6)
                weigh(H * EU - 1)
                output(H - 1)

            @block.vector
            def _(dve):
                nc.vector.memset(ps[:, OUT, 0:T], 0.0).then_inc(cleared, 1)

                def maxima(h, g):
                    dve.wait_ge(scored, GU * h + g + 1)
                    nc.vector.tensor_reduce(gm[:, h % 2, g // NK, g % NK:g % NK + 1], ps[:, 4 + g % 2, :], AX.X,
                                            ALU.max).then_inc(max_done, 1)

                def negate(h):
                    dve.wait_ge(max_done, GU * (h + 1))
                    if h >= 2:
                        dve.wait_ge(neg_row, h - 1)
                    nc.vector.tensor_reduce(neg[:, h % 2, :], gm[:, h % 2, :, :], AX.X, ALU.max,
                                            negate=True).then_inc(neg_done, 1)

                def place_shift(h):
                    dve.wait_ge(neg_row, h + 1)
                    if h == 0:
                        dve.wait_ge(q_in, 16 * SLOTS)
                    nc.vector.tensor_copy(qstack[SHIFT:ROWS, h, :], ps[SHIFT:ROWS, 4, 0:T]).then_inc(shift_done, 1)

                def finish(h):
                    dve.wait_ge(out_ready, h + 1)
                    o = ps[:, SPARE, 0:QT * VW].rearrange("p (t c) -> p t c", t=QT)
                    nc.vector.reciprocal(inv[:, h % 2, :], o[:, :, D]).then_inc(inv_done, 1)
                    dve.wait_ge(inv_done, h + 1)
                    for t in range(QT):
                        last = nc.vector.tensor_scalar(att[:, t, h * D:(h + 1) * D], o[:, t, 0:D],
                                                       inv[:, h % 2, t:t + 1], None, ALU.mult)
                    last.then_inc(out_done, 1)

                for g in range(GU):
                    maxima(0, g)
                negate(0)
                place_shift(0)
                for i in range(H * EU):
                    h, e = i // EU, i % EU
                    if h + 1 < H:
                        for g in units_of[e]:
                            maxima(h + 1, g)
                    if new and e == 2:
                        if new.rope:
                            if h >= 1:
                                new.take_rest(dve, h - 1)
                            new.scale_cos(dve, h)
                        else:
                            new.take_rest(dve, h)
                    if new and new.rope and e == 4:
                        new.scale_sin(dve, h)
                    if e == 6:
                        if h + 1 < H:
                            negate(h + 1)
                        if new and new.rope:
                            new.invert(dve, h)
                        if h + 1 < H:
                            place_shift(h + 1)
                    if e == 7 and h >= 1:
                        finish(h - 1)
                if new and new.rope:
                    new.take_rest(dve, H - 1)
                finish(H - 1)

            @block.scalar
            def _(act):
                def take(h):
                    act.wait_ge(pv, EU * (h + 1))
                    if h >= 2:
                        act.wait_ge(out_ready, h - 1)
                    nc.scalar.copy(osum[:, h % 2, :], ps[:, OUT, 0:T]).then_inc(taken, 1)

                for i in range(H * EU):
                    h, e = i // EU, i % EU
                    if new and not rope and e == 2:
                        new.high(act, h)
                    if new and not rope and e == 6:
                        new.copy_values(act, h)
                    if new and rope and e == 2:
                        new.copy_product(act, h)
                    if new and rope and e == 3:
                        new.take_root(act, h)
                    if new and rope and e == 0 and h >= 1:
                        new.copy_values(act, h - 1)
                    act.wait_ge(qk, i + 1)
                    if i >= 3:
                        act.wait_ge(pv, i - 2)
                    nc.scalar.activation(p[:, i % 3, :].rearrange("p (b t) -> p b t", b=2),
                                         ps[:, 2 * (i % 2):2 * (i % 2) + 2, :], ACT.Exp).then_inc(exp_done, 1)
                    if e == 0 and h >= 1:
                        take(h - 1)
                    if new and rope and e == 1 and h >= 1:
                        new.high(act, h - 1)
                if new and rope:
                    new.copy_values(act, H - 1)
                take(H - 1)
                if new and new.rope:
                    new.high(act, H - 1)

            if new:
                @block.gpsimd
                def _(pool):
                    for u in range(new.units):
                        new.low_parts(pool, u)


def output_product(core, att, attT, wo, b, moved=None):
    nc, ps = core.nc, core.ps
    QT = T // P
    CUT, CUT2 = KT // 2, KT * 13 // 16
    with phase(core, "turned", "copied", "ready") as (block, turned, copied, ready):
        @block.tensor
        def _(pe):
            for t in range(QT):
                for k in range(CT):
                    mm = nc.tensor.transpose(ps[:, k, t * P:(t + 1) * P], att[:, t, k * P:(k + 1) * P],
                                             core.ident[:, :])
            mm.then_inc(turned, 1)
            pe.wait_ge(copied, 1)
            for t in range(QT):
                for k in range(CT):
                    mm = nc.tensor.matmul(ps[:, 2 + t, 0:C], attT[:, k, t * P:(t + 1) * P], wo[:, k, :],
                                          start=k == 0, stop=k == CT - 1)
                mm.then_inc(ready, 1)

        @block.scalar
        def _(act):
            act.wait_ge(turned, 1)
            nc.scalar.copy(attT[:, :, :], ps[:, 0:CT, 0:T]).then_inc(copied, 1)
            if moved:
                nc.scalar.copy(moved[1][:, CUT:CUT2], moved[0][:, CUT:CUT2])

        if moved:
            @block.gpsimd
            def _(pool):
                nc.gpsimd.tensor_copy(moved[1][:, CUT2:], moved[0][:, CUT2:])

        @block.vector
        def _(dve):
            if moved:
                nc.vector.tensor_copy(moved[1][:, 0:CUT], moved[0][:, 0:CUT])
            for t in range(QT):
                dve.wait_ge(ready, t + 1)
                x = core.x[:, bass.ds(QT * b + t, 1), :]
                nc.vector.tensor_tensor(x, ps[:, 2 + t:3 + t, 0:C], x, ALU.add)


def attend_by_key(core, queries, keys, v, qstack, kstack, att, coming=None):
    nc, ps = core.nc, core.ps
    QT = T // P
    EU = KT // 4
    OUT, SPARE = 6, 7
    with ExitStack() as c:
        sb = core.allocator(c)
        p, scaled = sb([P, 3, 4 * T]), sb([P, 3, 4, VW])
        nm, z, zi = sb([P, 4, 4]), sb([P, 4, 4]), sb([P, 4, 4])
        fold, osum, inv = core.fold, sb([P, 2, T]), sb([P, 2, QT])
        with phase(core, "q_in", "k_a", "k_b", "k_c", "max_done", "qk", "exp_done", "z_done", "v_scaled", "pv",
                   "taken", "out_ready", "inv_done", "out_done", "cleared", *(NextKeys.NAMES if coming else ())) as (
                block, q_in, k_a, k_b, k_c, max_done, qk, exp_done, z_done, v_scaled, pv, taken, out_ready, inv_done,
                out_done, cleared, *next_sems):
            k_in = (k_a, k_b, k_c)
            new = NextKeys(core, sb, next_sems, spare=SPARE, v_bank=SPARE, **coming) if coming else None

            @block.sync
            def _(sp):
                load_keys(sp, keys, kstack, 0, k_in[0])
                load_queries(sp, queries, qstack, q_in)
                load_keys(sp, keys, kstack, 1, k_in[1])
                if new:
                    new.load_chunk(sp, 0)
                    new.load_chunk(sp, 1)
                for h in range(H):
                    if h + 2 < H:
                        if h >= 1:
                            sp.wait_ge(qk, EU * h)
                        load_keys(sp, keys, kstack, h + 2, k_in[(h + 2) % 3])
                    if new:
                        if h % CT == 0 and 2 <= h // CT + 1 < new.chunks:
                            new.load_chunk(sp, h // CT + 1)
                        if h >= 1:
                            new.store(sp, h - 1)
                if new:
                    new.store(sp, H - 1)
                    new.all_stored(sp)

            @block.tensor
            def _(pe):
                def scores(i):
                    h, e = i // EU, i % EU
                    if i == 0:
                        pe.wait_ge(q_in, 16 * SLOTS)
                    if e == 0:
                        pe.wait_ge(k_in[h % 3], 16 * SLOTS * (h // 3 + 1))
                    if i >= 3:
                        pe.wait_ge(exp_done, 4 * (i - 2))
                    for j in range(4):
                        kt = 4 * e + j
                        mm = nc.tensor.matmul(ps[:, 2 * (i % 3) + j // 2, (j % 2) * T:(j % 2 + 1) * T],
                                              kstack[0:SHIFT, h % 3, kt * P:(kt + 1) * P], qstack[0:SHIFT, h, :],
                                              start=True, stop=True)
                    mm.then_inc(qk, 1)

                def weigh(i):
                    h, e = i // EU, i % EU
                    pe.wait_ge(v_scaled, i + 1)
                    if i == 0:
                        pe.wait_ge(cleared, 1)
                    if e == 0 and h >= 1:
                        pe.wait_ge(taken, h)
                    for j in range(4):
                        mm = nc.tensor.matmul(ps[PART * j:PART * j + VW, OUT, 0:T], scaled[:, i % 3, j, :],
                                              p[:, i % 3, j * T:(j + 1) * T], start=e == 0, stop=e == EU - 1,
                                              tile_position=(0, PART * j))
                    mm.then_inc(pv, 1)

                def output(h):
                    pe.wait_ge(taken, h + 1)
                    if h >= 1:
                        pe.wait_ge(out_done, h)
                    for t in range(QT):
                        mm = nc.tensor.matmul(ps[:, SPARE, t * VW:(t + 1) * VW],
                                              osum[:, h % 2, t * P:(t + 1) * P], fold[:, 0:VW], start=True, stop=True)
                    mm.then_inc(out_ready, 1)

                for i in range(H * EU + 2):
                    h, e = i // EU, i % EU
                    if i < H * EU:
                        scores(i)
                    if i >= 2:
                        weigh(i - 2)
                    if i >= H * EU:
                        continue
                    if new and e in (0, 1):
                        if e == 0 and h >= 2:
                            pe.wait_ge(out_done, h - 1)
                        if e == 0 and h == 1:
                            pe.wait_ge(new.v_done, 1)
                        new.multiply(pe, h, e)
                    if new and e in (4, 5):
                        new.product_used(pe, h)
                        new.multiply_values(pe, h, e - 4)
                    if e == 7 and h >= 1:
                        if new:
                            pe.wait_ge(new.v_done, h + 1)
                        output(h - 1)
                output(H - 1)

            @block.vector
            def _(dve):
                nc.vector.memset(ps[:, OUT, 0:T], 0.0).then_inc(cleared, 1)

                def maxima(i):
                    dve.wait_ge(qk, i + 1)
                    if i >= 4:
                        dve.wait_ge(exp_done, 4 * (i - 3))
                    nc.vector.tensor_reduce(nm[:, i % 4, :],
                                            ps[:, 2 * (i % 3):2 * (i % 3) + 2, :].rearrange("p b (j t) -> p (b j) t", j=2),
                                            AX.X, ALU.max, negate=True).then_inc(max_done, 1)

                def scale_values(i):
                    h, e = i // EU, i % EU
                    dve.wait_ge(exp_done, 4 * (i + 1))
                    nc.vector.reciprocal(zi[:, i % 4, :], z[:, i % 4, :]).then_inc(z_done, 1)
                    dve.wait_ge(z_done, i + 1)
                    if i >= 3:
                        dve.wait_ge(pv, i - 2)
                    nc.vector.tensor_tensor(scaled[:, i % 3, :, :], v[:, 4 * e:4 * e + 4, h, :],
                                            zi[:, i % 4, :].unsqueeze(2).to_broadcast([P, 4, VW]),
                                            ALU.mult).then_inc(v_scaled, 1)

                def finish(h):
                    dve.wait_ge(out_ready, h + 1)
                    o = ps[:, SPARE, 0:QT * VW].rearrange("p (t c) -> p t c", t=QT)
                    nc.vector.reciprocal(inv[:, h % 2, :], o[:, :, D]).then_inc(inv_done, 1)
                    dve.wait_ge(inv_done, h + 1)
                    for t in range(QT):
                        last = nc.vector.tensor_scalar(att[:, t, h * D:(h + 1) * D], o[:, t, 0:D],
                                                       inv[:, h % 2, t:t + 1], None, ALU.mult)
                    last.then_inc(out_done, 1)

                for i in range(H * EU + 1):
                    h, e = i // EU, i % EU
                    if i < H * EU:
                        maxima(i)
                    if i >= 1:
                        scale_values(i - 1)
                    if i < H * EU:
                        if new and e == 3:
                            new.take_rest(dve, h)
                        if e == 0 and h >= 2:
                            finish(h - 2)
                finish(H - 2)
                finish(H - 1)

            @block.scalar
            def _(act):
                def take(h):
                    act.wait_ge(pv, EU * (h + 1))
                    if h >= 2:
                        act.wait_ge(out_ready, h - 1)
                    nc.scalar.copy(osum[:, h % 2, :], ps[:, OUT, 0:T]).then_inc(taken, 1)

                for i in range(H * EU):
                    h, e = i // EU, i % EU
                    act.wait_ge(max_done, i + 1)
                    if i >= 3:
                        act.wait_ge(pv, i - 2)
                    if i >= 4:
                        act.wait_ge(z_done, i - 3)
                    for j in range(4):
                        nc.scalar.activation(p[:, i % 3, j * T:(j + 1) * T],
                                             ps[:, 2 * (i % 3) + j // 2, (j % 2) * T:(j % 2 + 1) * T], ACT.Exp,
                                             bias=nm[:, i % 4, j:j + 1],
                                             accum_out=z[:, i % 4, j:j + 1]).then_inc(exp_done, 1)
                    if e == 1 and h >= 1:
                        take(h - 1)
                    if new and e == 2:
                        new.high(act, h)
                    if new and e == 6:
                        new.copy_values(act, h)
                take(H - 1)

            if new:
                @block.gpsimd
                def _(pool):
                    for u in range(new.units):
                        new.low_parts(pool, u)


def context_attention(core, prefix, by_key=False, scale=1.0, rope=False, bias=False):
    nc, d = core.nc, core.dram
    queries, keys = d["scratch_q"], d["scratch_k"]
    with ExitStack() as c:
        sb = core.allocator(c)
        tiles = None
        if bias:
            tiles = sb([P, 3, H, P]), sb([P, 3, H, P], BF16)
            distance_bias(core, prefix, *tiles)
        wk, wv, wo = (sb([P, CT, C]) for _ in range(3))
        v, v_next, kstack = sb([P, KT, H, VW]), sb([P, KT, H, VW]), sb([P, 3, S], BF16)
        loads = [(t[:, :, :], ktiles(d[prefix + "_W" + n])) for t, n in ((wk, "k"), (wv, "v"), (wo, "o"))]
        q_rope = k_rope = None
        if rope:
            qw, kw, qturn, kturn, eps = sb([P, 1]), sb([P, 1]), sb([P, P]), sb([P, P]), sb([P, 1])
            loads += [(qw[:, :], d[prefix + "_q_norm_w"]), (kw[:, :], d[prefix + "_k_norm_w"]),
                      (qturn[:, :], d["c_turn16"]), (kturn[:, :], d["c_turn16"])]
            q_rope = (qw[:, 0:1], lambda i: d["c_rope_q"], qturn[:, :], eps[:, 0:1])
            k_rope = (kw[:, 0:1], lambda i: d["c_rope_k"][:, :, i * KC:(i + 1) * KC], kturn[:, :], eps[:, 0:1])
        context = lambda b: (lambda i: d["ctxT"][b, :, i * KC:(i + 1) * KC].rearrange("(k p) n -> p k n", p=P))
        with ExitStack() as early:
            wq = core.allocator(early)([P, CT, C])
            layer_norm(core, core.x, core.xn, core.xnT, loads=loads + [(wq[:, :, :], ktiles(d[prefix + "_Wq"]))])
            with phase(core, "w") as (block, w):
                @block.gpsimd
                def _(pool):
                    chain(pool, w)(nc.gpsimd.memset(kstack[SHIFT:ROWS, 0:2, :], 1.0))
                    nc.gpsimd.memset(v[:, :, :, D:VW], 1.0)
                    nc.gpsimd.memset(v_next[:, :, :, D:VW], 1.0)

                @block.vector
                def _(dve):
                    nc.vector.memset(kstack[SHIFT:ROWS, 2, :], 1.0)
                    if rope:
                        nc.vector.memset(eps[:, :], 1e-6)
                        nc.vector.tensor_scalar(qturn[:, :], qturn[:, :], qw[:, 0:1], None, ALU.mult)
                        nc.vector.tensor_scalar(kturn[:, :], kturn[:, :], kw[:, 0:1], None, ALU.mult)
            project_parts(core, wq, N // KC, core.xnT, queries, scale=scale, rope=q_rope)
        project_parts(core, wk, S // KC, context(0), keys[0], values=(wv, v), rope=k_rope)
        qstack, att, attT = sb([P, H, T], BF16), sb([P, T // P, C]), sb([P, CT, T])
        k97, q97 = kstack[0:ROWS], qstack[0:ROWS]

        def attend_batch(b, coming):
            mine = queries[:, :, bass.ds(b * T, T)]
            if by_key:
                attend_by_key(core, mine, keys[b], v, q97, k97, att, coming)
            else:
                attend_context(core, mine, keys[b], v, q97, k97, tiles, att, coming)
            output_product(core, att, attT, wo, b, (v_next, v) if coming else None)

        with nc.Fori(0, B - 1) as b:
            attend_batch(b, dict(w=wk, w_v=wv, v=v_next, source=context(b + 1), dest=keys[b + 1], rope=k_rope))
        attend_batch(B - 1, None)


def distance_bias(core, prefix, by_key, by_query):
    nc, d, ps = core.nc, core.dram, core.ps
    W = 4 * P
    HB = BANK // P
    with ExitStack() as c:
        sb = core.allocator(c)
        table, onehot, rows, mirror = sb([32, H]), sb([32, W]), sb([H, W]), sb([P, P])
        slanted = sb([P, 3, H, P])
        scratch = d["scratch_bias"]
        load(core, [(table[:, :], d[prefix + "_rel_bias"]), (onehot[:, :], d["c_buckets"]),
                    (mirror[:, :], d["c_mirror"])])
        banks = [(i, g) for i in range(3) for g in range(H // HB)]
        with phase(core, "ready", "copied", "stored", "read", "query_ready", "key_ready", "query_copied",
                   "key_copied") as (block, ready, copied, stored, read, query_ready, key_ready, query_copied,
                                     key_copied):
            @block.tensor
            def _(pe):
                nc.tensor.matmul(ps[0:H, 0, :], table[:, :], onehot[:, :], start=True, stop=True).then_inc(ready, 1)
                pe.wait_ge(copied, 1)
                pe.wait_ge(read, 48)
                for n, (i, g) in enumerate(banks):
                    if n >= 4:
                        pe.wait_ge(query_copied, n - 3)
                        pe.wait_ge(key_copied, n - 3)
                    nc.tensor.matmul(ps[:, n % 4, :], mirror[:, :], slanted[:, i, g * HB:(g + 1) * HB, :],
                                     start=True, stop=True).then_inc(query_ready, 1)
                    for h in range(HB):
                        mm = nc.tensor.matmul(ps[:, 4 + n % 4, h * P:(h + 1) * P], slanted[:, i, g * HB + h, :],
                                              mirror[:, :], start=True, stop=True)
                    mm.then_inc(key_ready, 1)

            @block.scalar
            def _(act):
                act.wait_ge(ready, 1)
                nc.scalar.copy(rows[:, :], ps[0:H, 0, :]).then_inc(copied, 1)
                for n, (i, g) in enumerate(banks):
                    act.wait_ge(key_ready, n + 1)
                    nc.scalar.copy(by_key[:, i, g * HB:(g + 1) * HB, :], ps[:, 4 + n % 4, :]).then_inc(key_copied, 1)

            @block.sync
            def _(sp):
                sp.wait_ge(copied, 1)
                sp.dma_start(scratch, rows[:, :]).then_inc(stored, 16)
                sp.wait_ge(stored, 16)
                for i in range(3):
                    start = 2 * P + P * (i - 1) - (P - 1)
                    sp.dma_start(slanted[:, i, :, :], bass.AP(tensor=scratch.tensor, offset=start,
                                                              ap=[[1, P], [W, H], [1, P]])).then_inc(read, 16)
                sp.wait_ge(read, 48)

            @block.vector
            def _(dve):
                for n, (i, g) in enumerate(banks):
                    dve.wait_ge(query_ready, n + 1)
                    nc.vector.tensor_copy(by_query[:, i, g * HB:(g + 1) * HB, :],
                                          ps[:, n % 4, :]).then_inc(query_copied, 1)


def l0_xattn(core):
    context_attention(core, "L0_xattn", scale=D ** -0.5, rope=True)


def l1_xattn(core):
    context_attention(core, "L1_xattn", bias=True)


def l2_xattn(core):
    context_attention(core, "L2_xattn", by_key=True, scale=C ** -0.5)

def lay_out(i):
    import numpy as np
    cont = np.ascontiguousarray
    T_ = lambda a: cont(np.swapaxes(a, -1, -2))
    col = lambda a: cont(a.reshape(-1, P).T)
    spread = lambda a: cont(np.broadcast_to(a.reshape(1, -1), (P, a.size)))
    o = {"x": i["x"], "ctxT": T_(i["ctx_1024"])}
    o["L3_ffn_W1"], o["L3_ffn_W2"] = T_(i["L3_ffn_W1"]), T_(i["L3_ffn_W2"])
    o["L3_ffn_b1"], o["L3_ffn_b2"] = col(i["L3_ffn_b1"]), spread(i["L3_ffn_b2"])
    o["L3_ffn_scale"] = cont(np.broadcast_to(i["L3_ffn_scale"].reshape(1, 1), (P, 1)))
    for n in ("W_u", "W_g", "Bm", "Cm"):
        o["L3_attn_" + n] = T_(i["L3_attn_" + n])
    o["L3_attn_A"], o["L3_attn_AT"] = i["L3_attn_A"], T_(i["L3_attn_A"])
    o["L3_attn_b_u"], o["L3_attn_b_g"] = col(i["L3_attn_b_u"]), col(i["L3_attn_b_g"])
    o["L3_attn_D"] = spread(i["L3_attn_D"])
    o["L3_xattn_Wq"], o["L3_xattn_Wp"] = T_(i["L3_xattn_Wq"]), T_(i["L3_xattn_Wp"])
    o["L3_xattn_Wkv"] = T_(np.concatenate([i["L3_xattn_Wk"], i["L3_xattn_Wv"]], 0))
    o["L3_xattn_bq"], o["L3_xattn_bp"] = spread(i["L3_xattn_bq"]), spread(i["L3_xattn_bp"])
    o["L3_xattn_bkv"] = spread(np.concatenate([i["L3_xattn_bk"], i["L3_xattn_bv"]]))
    o["L0_attn_maa"] = cont(np.stack([col(i["L0_attn_time_maa_" + n]) for n in "xwkvrg"], 1))
    o["L0_attn_w1"] = i["L0_attn_time_maa_w1"]
    o["L0_attn_w2"] = i["L0_attn_time_maa_w2"].reshape(-1, C)
    o["L0_attn_wd1"], o["L0_attn_wd2"] = i["L0_attn_time_decay_w1"], i["L0_attn_time_decay_w2"]
    o["L0_attn_decay"], o["L0_attn_u"] = col(i["L0_attn_time_decay"]), col(i["L0_attn_time_faaaa"])
    o["L0_attn_gamma"], o["L0_attn_beta"] = col(i["L0_attn_ln_gamma"]), col(i["L0_attn_ln_beta"])
    for n in "rkvgo":
        o["L0_attn_W_" + n] = i["L0_attn_W_" + n]
    o["L0_ffn_gate_w"] = T_(i["L0_ffn_gate_w"])

    def paired(w):
        w = w.reshape(32, 2, 192, -1)
        return np.concatenate([w[:, :, 0:P].reshape(32, 2 * P, -1), w[:, :, P:].reshape(32, P, -1)], 1)

    gu = np.stack([paired(i["L0_ffn_w_gate"]), paired(i["L0_ffn_w_up"])], 1)
    again = lambda a: np.concatenate([a, a[:1]], 0)
    o["L0_ffn_wgu"] = again(gu.reshape(32, 2, 3 * P, CT, P).transpose(0, 4, 3, 1, 2))
    o["L0_ffn_wd"] = again(paired(T_(i["L0_ffn_w_down"])).reshape(32, 3, P, C).transpose(0, 2, 1, 3))
    for n in ("r1_w", "r2_w", "W1", "W2", "b2"):
        o["L1_attn_" + n] = i["L1_attn_" + n]
    o["L1_attn_r1_b"] = spread(i["L1_attn_r1_b"])
    o["L1_attn_ln_g"], o["L1_attn_ln_b"] = col(i["L1_attn_ln_g"]), col(i["L1_attn_ln_b"])
    for n in ("r2_b", "route_bias", "temp"):
        a = i["L1_attn_" + n].reshape(1, -1)
        o["L1_attn_" + n] = cont(np.broadcast_to(a, (P, a.shape[1])))
    expert_col = lambda a: cont(a.reshape(a.shape[0], -1, P).transpose(2, 0, 1))
    o["L1_attn_b1"] = expert_col(i["L1_attn_b1"])
    o["L1_ffn_Wg"], o["L1_ffn_b2"] = T_(i["L1_ffn_Wg"]), i["L1_ffn_b2"]
    o["L1_ffn_b1"], o["L1_ffn_b3"] = expert_col(i["L1_ffn_b1"]), expert_col(i["L1_ffn_b3"])
    w13 = np.stack([i["L1_ffn_W1"], i["L1_ffn_W3"]], 1)
    o["L1_ffn_W13"] = cont(w13.reshape(16, 2, 256, CT, P).transpose(0, 4, 3, 1, 2))
    o["L1_ffn_W2"] = T_(i["L1_ffn_W2"])
    o["L2_attn_W_in"], o["L2_attn_W_out"] = T_(i["L2_attn_W_in"]), T_(i["L2_attn_W_out"])
    o["L2_attn_b_qk"], o["L2_attn_b_v"] = col(i["L2_attn_b_in"][:2048]), spread(i["L2_attn_b_in"][2048:])
    o["L2_attn_b_out"] = spread(i["L2_attn_b_out"])
    for n in ("wq", "wk", "wv", "wo", "w1", "w2"):
        o["L2_ffn_" + n] = i["L2_ffn_" + n]
    o["L2_ffn_ln_g"], o["L2_ffn_ln_b"] = col(i["L2_ffn_ln_g"]), col(i["L2_ffn_ln_b"])
    o["L2_ffn_b1"] = expert_col(i["L2_ffn_b1"])
    o["L2_ffn_b2"] = cont(np.broadcast_to(i["L2_ffn_b2"].reshape(4, 2, 1, C), (4, 2, 64, C)).reshape(4, P, C))
    for n in "qkvo":
        o["L0_xattn_W" + n], o["L2_xattn_W" + n] = T_(i["L0_xattn_W" + n]), T_(i["L2_xattn_W" + n])
    for n in "qk":
        o[f"L0_xattn_{n}_norm_w"] = cont(np.tile(i[f"L0_xattn_{n}_norm_w"].reshape(D, 1), (HT, 1)))
    o["L1_xattn_Wq"], o["L1_xattn_Wo"] = i["L1_xattn_Wq"], i["L1_xattn_Wo"]
    o["L1_xattn_Wk"], o["L1_xattn_Wv"] = cont(i["L1_xattn_Wkv"][:, 0:C]), cont(i["L1_xattn_Wkv"][:, C:])
    o["L1_xattn_rel_bias"] = i["L1_xattn_rel_bias"]
    o["c_ident"] = np.eye(P, dtype=np.float32)
    o["c_block16"] = np.kron(np.eye(HT), np.ones((D, D))).astype(np.float32)
    o["c_fold"] = np.tile(np.eye(32), (4, 1)).astype(np.float32)
    o["c_eye4"] = np.eye(4, dtype=np.float32)
    o["c_block4"] = np.kron(np.eye(4), np.ones((4, 1))).astype(np.float32)
    o["c_sel"] = np.stack([np.kron(np.eye(HT), np.eye(D)[:, [n]] * np.ones((1, D))) for n in range(D)],
                          1).astype(np.float32)
    o["c_mask8"] = np.kron(np.eye(16), np.ones((8, 1))).astype(np.float32)
    p64 = np.arange(32, dtype=np.float32) / np.float32(31)
    ang = np.arange(T, dtype=np.float32)[None, :] / (np.float32(10000.0) ** p64)[:, None]
    o["c_cos64"], o["c_sin64"] = (np.tile(f(ang), (4, 1)).astype(np.float32) for f in (np.cos, np.sin))
    t64 = np.zeros((64, 64), np.float32)
    t64[np.arange(32), np.arange(32) + 32] = 1.0
    t64[np.arange(32) + 32, np.arange(32)] = -1.0
    o["c_turn64"] = np.kron(np.eye(2), t64).astype(np.float32)
    o["c_causal"] = np.where(np.arange(P)[:, None] >= np.arange(P)[None, :], 0.0, -1e30).astype(np.float32)
    half = np.arange(D // 2) * 2
    for n, theta, length in (("q", 32.0, T), ("k", 1000.0, S)):
        freqs = np.float32(theta) ** (-half.astype(np.float32) / np.float32(D))
        ang = freqs[:, None] * np.arange(length, dtype=np.float32)[None, :]
        table = np.stack([np.tile(f(ang), (2 * HT, 1)) for f in (np.cos, np.sin)], 1).astype(np.float32)
        o["c_rope_" + n] = np.tile(table, (1, 1, 2)) if n == "q" else table
    t16 = np.zeros((D, D), np.float32)
    t16[np.arange(8) + 8, np.arange(8)] = -1.0
    t16[np.arange(8), np.arange(8) + 8] = 1.0
    o["c_turn16"] = np.kron(np.eye(HT), t16).astype(np.float32)
    rel = np.arange(-256, 256)
    far = np.abs(rel)
    large = 8 + (np.log(np.maximum(far, 1).astype(np.float32) / 8) / np.log(16) * 8).astype(np.int32)
    bucket = (rel > 0) * 16 + np.where(far < 8, far, np.minimum(large, 15))
    hot = np.eye(32)[bucket].T - np.eye(32)[:, [31]]
    o["c_buckets"] = hot.astype(np.float32)
    o["c_mirror"] = np.ascontiguousarray(np.eye(P, dtype=np.float32)[:, ::-1])
    return {k: np.ascontiguousarray(v) for k, v in o.items()}


STAGES = [l0_xattn, l0_attn, l0_ffn, l1_xattn, l1_attn, l1_ffn, l2_xattn, l2_attn, l2_ffn, l3_xattn, l3_attn, l3_ffn]


def perceiver(nc, dram, out, stages=STAGES):
    with ExitStack() as ctx:
        core = Core(nc, ctx, dram)
        setup(core)
        for stage in stages:
            stage(core)
        store(core, out)


def declare(nc, arrays):
    dram = {k: nc.dram_tensor("in_" + k, v.shape, mybir.dt.from_np(v.dtype), kind="ExternalInput").ap()
            for k, v in arrays.items()}
    dram["scratch_tok"] = nc.dram_tensor("scratch_tok", (B, T, C), F32, kind="Internal").ap()
    dram["scratch_bias"] = nc.dram_tensor("scratch_bias", (H, 4 * P), F32, kind="Internal").ap()
    dram["scratch_q"] = nc.dram_tensor("scratch_q", (3, C, N), BF16, kind="Internal").ap()
    dram["scratch_k"] = nc.dram_tensor("scratch_k", (B, 3, C, S), BF16, kind="Internal").ap()
    dram["scratch_w"] = nc.dram_tensor("scratch_w", (66, N), F32, kind="Internal").ap()
    out = nc.dram_tensor("out", (B, T, C), F32, kind="ExternalOutput").ap()
    return dram, out


def kernel(**inputs):
    import numpy as np
    from concourse import bacc
    from concourse.bass_utils import run_bass_kernel_spmd

    nc = bacc.Bacc("TRN2", target_bir_lowering=False, num_devices=1)
    arrays = lay_out({k: np.asarray(v) for k, v in inputs.items()})
    dram, out = declare(nc, arrays)
    perceiver(nc, dram, out)
    r = run_bass_kernel_spmd(nc, [{"in_" + k: v for k, v in arrays.items()}], core_ids=[0])
    return r.results[0]["out"]
```

```python
from contextlib import ExitStack, contextmanager
import math

import concourse.bass as bass
from concourse import mybir

F32 = mybir.dt.float32
BF16 = mybir.dt.bfloat16
ALU = mybir.AluOpType
ACT = mybir.ActivationFunctionType
AX = mybir.AxisListType

P = 128
B, T, C = 4, 256, 256
N = B * T
TT = N // P
CT = C // P
S = 4096
KT = S // P
KC = 512
BANK = 512
H, D = 16, 16
HT = P // D


class Core:

    def __init__(self, nc, ctx, dram):
        self.nc, self.ctx, self.dram = nc, ctx, dram
        sb = lambda name, shape, dt=F32: ctx.enter_context(nc.sbuf_tensor(name, shape, dt))
        self.x = sb("x_tok", [P, TT, C])
        self.xn = sb("xn_tok", [P, TT, C])
        self.xnT = sb("xn_feat", [P, CT, N])
        self.ident = sb("ident", [P, P])
        self.ones = sb("ones", [P, P])
        self.identb = sb("identb", [P, P], BF16)
        self.fold = sb("fold", [P, 32])
        self.block16 = sb("block16", [P, P])
        self.ps = ctx.enter_context(nc.psum_tensor("banks", [P, 8, BANK], F32))
        self.count = 0

    def allocator(self, ctx):
        def tensor(shape, dt=F32):
            self.count += 1
            return ctx.enter_context(self.nc.sbuf_tensor(f"t{self.count}", shape, dt))
        return tensor


@contextmanager
def phase(core, *names):
    nc = core.nc
    core.count += 1
    sems = [nc.alloc_semaphore(f"p{core.count}_{n}") for n in names]
    with nc.Block() as block:
        yield (block, *sems)
    nc.clear_and_free_semaphores(sems)
    nc.all_engine_barrier()


def chain(engine, sem):
    count = [0]

    def link(instruction):
        count[0] += 1
        instruction.then_inc(sem, 1)
        engine.wait_ge(sem, count[0])

    return link


def load(core, pairs):
    with phase(core, "landed") as (block, landed):
        @block.sync
        def _(sp):
            for dst, src in pairs:
                sp.dma_start(dst, src).then_inc(landed, 16)
            sp.wait_ge(landed, 16 * len(pairs))


def ktiles(ap):
    return ap.rearrange("(k p) n -> p k n", p=P)


def layer_norm(core, src, dst, dstT, loads=(), eps=1e-5, gain=None, shift=None, bias=None,
               constants=()):
    nc, ps = core.nc, core.ps
    with ExitStack() as c:
        sb = core.allocator(c)
        stats, mv, rstd = sb([P, TT, 6]), sb([P, TT, 2]), sb([P, TT])
        with phase(core, "landed", "stats_done", "agg", "var_ready", "root_done", "rstd_done", "norm_done",
                   "turned", "set_done") as (block, landed, stats_done, agg, var_ready, root_done, rstd_done, norm_done,
                                             turned, set_done):
            @block.sync
            def _(sp):
                for d, s in loads:
                    sp.dma_start(d, s).then_inc(landed, 16)
                if loads:
                    sp.wait_ge(landed, 16 * len(loads))

            @block.vector
            def _(dve):
                for t in range(TT):
                    nc.vector.bn_stats(stats[:, t, :], src[:, t, :]).then_inc(stats_done, 1)
                for t in range(TT):
                    dve.wait_ge(stats_done, t + 1)
                    nc.vector.bn_aggr(mv[:, t, :], stats[:, t, :]).then_inc(agg, 1)
                dve.wait_ge(agg, TT)
                nc.vector.tensor_scalar(rstd[:, :], mv[:, :, 1], eps, None, ALU.add).then_inc(var_ready, 1)
                dve.wait_ge(root_done, 1)
                nc.vector.reciprocal(rstd[:, :], rstd[:, :]).then_inc(rstd_done, 1)
                dve.wait_ge(rstd_done, 1)
                for t in range(TT):
                    nc.vector.tensor_scalar(dst[:, t, :], src[:, t, :], mv[:, t, 0:1], rstd[:, t:t + 1],
                                            ALU.subtract, ALU.mult).then_inc(norm_done, 1)

            if constants:
                @block.gpsimd
                def _(pool):
                    link = chain(pool, set_done)
                    for d, value in constants:
                        link(nc.gpsimd.memset(d, value))

            if bias is not None:
                @block.gpsimd
                def _(pool):
                    pool.wait_ge(landed, 16 * len(loads))
                    for t in range(TT):
                        pool.wait_ge(norm_done, t + 1)
                        nc.gpsimd.tensor_tensor(src[:, t, :], src[:, t, :], bias, ALU.add)

            @block.tensor
            def _(pe):
                for t in range(TT):
                    pe.wait_ge(norm_done, t + 1)
                    for k in range(CT):
                        nc.tensor.transpose(ps[:, CT * (t // 4) + k, (t % 4) * P:(t % 4 + 1) * P],
                                            dst[:, t, k * P:(k + 1) * P], core.ident[:, :]).then_inc(turned, 1)

            @block.scalar
            def _(act):
                act.wait_ge(var_ready, 1)
                nc.scalar.activation(rstd[:, :], rstd[:, :], ACT.Sqrt).then_inc(root_done, 1)
                for half in range(2):
                    act.wait_ge(turned, 4 * CT * (half + 1))
                    for k in range(CT):
                        out = dstT[:, k, half * BANK:(half + 1) * BANK]
                        if gain is None:
                            nc.scalar.copy(out, ps[:, CT * half + k, :])
                        else:
                            if loads:
                                act.wait_ge(landed, 16 * len(loads))
                            nc.scalar.activation(out, ps[:, CT * half + k, :], ACT.Identity,
                                                 bias=shift[:, k:k + 1], scale=gain[:, k:k + 1])


def linear_features(core, w, x, kt, mt, finish, engine="scalar", cols=N):
    nc, ps = core.nc, core.ps
    tiles = [(m, n) for m in range(mt) for n in range(cols // BANK)]
    with phase(core, "product_ready", "bank_free") as (block, product_ready, bank_free):
        @block.tensor
        def _(pe):
            for i, (m, n) in enumerate(tiles):
                if i >= 8:
                    pe.wait_ge(bank_free, i - 7)
                for k in range(kt):
                    mm = nc.tensor.matmul(ps[:, i % 8, :], w[:, k, m * P:(m + 1) * P],
                                          x[:, k, n * BANK:(n + 1) * BANK], start=k == 0, stop=k == kt - 1)
                mm.then_inc(product_ready, 1)

        def empty(eng):
            for i, (m, n) in enumerate(tiles):
                eng.wait_ge(product_ready, i + 1)
                finish(m, n, ps[:, i % 8, :]).then_inc(bank_free, 1)

        if engine == "scalar":
            block.scalar(empty)
        else:
            block.vector(empty)


def linear_tokens(core, x, w, kt, m, finish, engine="vector", tiles=TT):
    nc, ps = core.nc, core.ps
    with phase(core, "product_ready", "bank_free") as (block, product_ready, bank_free):
        @block.tensor
        def _(pe):
            for t in range(tiles):
                if t >= 8:
                    pe.wait_ge(bank_free, t - 7)
                for k in range(kt):
                    mm = nc.tensor.matmul(ps[:, t % 8, :m], x[:, k, t * P:(t + 1) * P], w[:, k, :m],
                                          start=k == 0, stop=k == kt - 1)
                mm.then_inc(product_ready, 1)

        def empty(eng):
            for t in range(tiles):
                eng.wait_ge(product_ready, t + 1)
                finish(t, ps[:, t % 8, :m]).then_inc(bank_free, 1)

        if engine == "scalar":
            block.scalar(empty)
        else:
            block.vector(empty)


def add_to_residual(core):
    return lambda t, product: core.nc.vector.tensor_tensor(core.x[:, t, :], product, core.x[:, t, :], ALU.add)


def setup(core):
    nc, d = core.nc, core.dram
    load(core, [(core.ident[:, :], d["c_ident"]), (core.block16[:, :], d["c_block16"]),
                (core.fold[:, :], d["c_fold"]),
                (core.x[:, :, :], d["x"].rearrange("b (t p) c -> p (b t) c", p=P))])
    with phase(core) as (block,):
        @block.vector
        def _(dve):
            nc.vector.memset(core.ones[:, :], 1.0)
            nc.vector.tensor_copy(core.identb[:, :], core.ident[:, :])


def store(core, out):
    nc = core.nc
    with phase(core, "stored") as (block, stored):
        @block.sync
        def _(sp):
            sp.dma_start(out.rearrange("b (t p) c -> p (b t) c", p=P), core.x[:, :, :]).then_inc(stored, 16)
            sp.wait_ge(stored, 16)



def l3_ffn(core):
    nc, d, ps = core.nc, core.dram, core.ps
    HID = 1024
    MT = HID // P
    with ExitStack() as c:
        sb = core.allocator(c)
        w1, w2 = sb([P, CT, HID]), sb([P, MT, C])
        b1, b2, scale = sb([P, MT]), sb([P, C]), sb([P, 1])
        h = sb([P, MT, N])
        xnd = d["scratch_tok"]
        rowmask = sb([4, 4, 1])
        blockmask = sb([16, 4])
        ev1 = sb([4, B, C])
        ev1z = sb([4, B, 4, C])
        ev2 = sb([16, B, 64])
        ev2z = sb([16, B, 4, 64])
        od1 = sb([P, B, CT, 4])
        od2 = sb([P, B, CT, 4])
        od2z = sb([P, B, CT, 4, 4, 4])
        p1 = sb([4, N])
        g = sb([16, N])
        layer_norm(core, core.x, core.xn, core.xnT, loads=[
            (w1[:, :, :], ktiles(d["L3_ffn_W1"])), (w2[:, :, :], ktiles(d["L3_ffn_W2"])),
            (b1[:, :], d["L3_ffn_b1"]), (b2[:, :], d["L3_ffn_b2"]),
            (scale[:, :], d["L3_ffn_scale"]),
            (rowmask[:, :, 0], d["c_eye4"]), (blockmask[:, :], d["c_block4"])], bias=b2[:, :])
        tok = lambda b, first: xnd[b, first:first + 8, :].rearrange("(i two) c -> i two c", two=2)[:, 0, :]
        with phase(core, "out_tok", "in_tok", "w") as (block, out_tok, in_tok, w):
            @block.sync
            def _(sp):
                sp.dma_start(xnd.rearrange("b (t p) c -> p (b t) c", p=P), core.xn[:, :, :]).then_inc(out_tok, 16)
                sp.wait_ge(out_tok, 16)
                for b in range(B):
                    sp.dma_start(ev1[:, b, :], tok(b, 1)).then_inc(in_tok, 16)
                    for i in range(4):
                        sp.dma_start(ev2[4 * i:4 * i + 4, b, :],
                                     xnd[b, 9 + 2 * i, :].rearrange("(c r) -> r c", r=4),
                                     allow_slow_non_contiguous=True).then_inc(in_tok, 16)
                sp.wait_ge(in_tok, 16 * 5 * B)

            @block.vector
            def _(dve):
                link = chain(dve, w)
                link(nc.vector.memset(od2z[:, :, :, :, :, :], 0.0))
                for b in range(B):
                    for k in range(CT):
                        x = core.xnT[:, k, b * T:(b + 1) * T]
                        nc.vector.tensor_scalar(od1[:, b, k, :], x[:, 2:10:2], scale[:, 0:1], None, ALU.mult)
                        for r in range(4):
                            nc.vector.tensor_scalar(od2z[:, b, k, r, :, r], x[:, 10:18:2], scale[:, 0:1], None,
                                                    ALU.mult)
                dve.wait_ge(in_tok, 16 * 5 * B)
                for i in range(4):
                    nc.vector.tensor_scalar(ev1z[:, :, i, :], ev1[:, :, :], rowmask[:, i, 0:1], None, ALU.mult)
                    nc.vector.tensor_scalar(ev2z[:, :, i, :], ev2[:, :, :], blockmask[:, i:i + 1], None, ALU.mult)
        with phase(core, "ready", "done") as (block, ready, done):
            @block.tensor
            def _(pe):
                for b in range(B):
                    for k in range(CT):
                        mm = nc.tensor.matmul(ps[0:4, b, 0:T], od1[:, b, k, :], core.xnT[:, k, b * T:(b + 1) * T],
                                              start=k == 0, stop=k == CT - 1)
                mm.then_inc(ready, 1)

            @block.scalar
            def _(act):
                act.wait_ge(ready, 1)
                nc.scalar.copy(p1[:, :].rearrange("p (b t) -> p b t", b=B), ps[0:4, 0:4, 0:T])
        tiles = [(m, b) for m in range(MT) for b in range(B)]
        with phase(core, "product_ready", "bank_free") as (block, product_ready, bank_free):
            @block.tensor
            def _(pe):
                for i, (m, b) in enumerate(tiles):
                    if i >= 8:
                        pe.wait_ge(bank_free, i - 7)
                    out = ps[:, i % 8, 0:T]
                    for k in range(CT):
                        nc.tensor.matmul(out, w1[:, k, m * P:(m + 1) * P], core.xnT[:, k, b * T:(b + 1) * T],
                                         start=k == 0, stop=False)
                    nc.tensor.matmul(out, ev1z[:, b, m // CT, (m % CT) * P:(m % CT + 1) * P],
                                     p1[:, b * T:(b + 1) * T], start=False, stop=True).then_inc(product_ready, 1)

            @block.scalar
            def _(act):
                for i, (m, b) in enumerate(tiles):
                    act.wait_ge(product_ready, i + 1)
                    nc.scalar.activation(h[:, m, b * T:(b + 1) * T], ps[:, i % 8, 0:T], ACT.Gelu,
                                         bias=b1[:, m:m + 1]).then_inc(bank_free, 1)
        with phase(core, "ready") as (block, ready):
            @block.tensor
            def _(pe):
                for b in range(B):
                    for m in range(MT):
                        r, k = m // CT, m % CT
                        mm = nc.tensor.matmul(ps[0:16, b, 0:T], od2z[:, b, k, r, :, :],
                                              h[:, m, b * T:(b + 1) * T], start=m == 0, stop=m == MT - 1)
                mm.then_inc(ready, 1)

            @block.scalar
            def _(act):
                act.wait_ge(ready, 1)
                nc.scalar.copy(g[:, :].rearrange("p (b t) -> p b t", b=B), ps[0:16, 0:4, 0:T])
        with phase(core, "product_ready") as (block, product_ready):
            @block.tensor
            def _(pe):
                for t in range(TT):
                    out = ps[:, t, 0:C]
                    for m in range(MT):
                        nc.tensor.matmul(out, h[:, m, t * P:(t + 1) * P], w2[:, m, :], start=m == 0, stop=False)
                    nc.tensor.matmul(out, g[:, t * P:(t + 1) * P],
                                     ev2z[:, t // 2, :, :], start=False, stop=True).then_inc(product_ready, 1)

            @block.vector
            def _(dve):
                for t in range(TT):
                    dve.wait_ge(product_ready, t + 1)
                    nc.vector.tensor_tensor(core.x[:, t, :], ps[:, t, 0:C], core.x[:, t, :], ALU.add)



def l3_attn(core):
    nc, d, ps = core.nc, core.dram, core.ps
    LEVELS = int(math.log2(T))
    with ExitStack() as c:
        sb = core.allocator(c)
        wu, wg, wb, wc = (sb([P, CT, C]) for _ in range(4))
        bu, bg, dd = sb([P, CT]), sb([P, CT]), sb([P, C])
        power = [sb([P, 2, CT, C]) for _ in range(2)]
        u, gate = sb([P, CT, N]), sb([P, CT, N])
        state = [sb([P, CT, N]) for _ in range(2)]
        layer_norm(core, core.x, core.xn, core.xnT, loads=[
            (wu[:, :, :], ktiles(d["L3_attn_W_u"])), (wg[:, :, :], ktiles(d["L3_attn_W_g"])),
            (wb[:, :, :], ktiles(d["L3_attn_Bm"])), (wc[:, :, :], ktiles(d["L3_attn_Cm"])),
            (bu[:, :], d["L3_attn_b_u"]), (bg[:, :], d["L3_attn_b_g"]), (dd[:, :], d["L3_attn_D"]),
            (power[0][:, 0, :, :], ktiles(d["L3_attn_A"])), (power[0][:, 1, :, :], ktiles(d["L3_attn_AT"]))], bias=dd[:, :])
        at = lambda tile, m, n: tile[:, m, n * BANK:(n + 1) * BANK]
        linear_features(core, wu, core.xnT, CT, CT, lambda m, n, q: nc.scalar.activation(
            at(u, m, n), q, ACT.Gelu, bias=bu[:, m:m + 1]))
        linear_features(core, wg, core.xnT, CT, CT, lambda m, n, q: nc.scalar.activation(
            at(gate, m, n), q, ACT.Sigmoid, bias=bg[:, m:m + 1]))
        with phase(core) as (block,):
            @block.vector
            def _(dve):
                for k in range(CT):
                    nc.vector.tensor_tensor(u[:, k, :], u[:, k, :], gate[:, k, :], ALU.mult)
        linear_features(core, wb, u, CT, CT, lambda m, n, q: nc.scalar.copy(at(state[0], m, n), q))
        for i in range(LEVELS):
            shift = 2 ** i
            old, new = state[i % 2], state[(i + 1) % 2]
            pw, nx = power[i % 2], power[(i + 1) % 2]
            length = T - shift
            seq = lambda tile, k: tile[:, k, :].rearrange("p (b t) -> p b t", b=B)
            with phase(core, "shifted", "squared") as (block, shifted, squared):
                @block.tensor
                def _(pe):
                    for m in range(CT):
                        for half in range(2):
                            out = ps[:, 2 * m + half, :].rearrange("p (b t) -> p b t", b=2)[:, :, 0:length]
                            for k in range(CT):
                                mm = nc.tensor.matmul(out, pw[:, 1, k, m * P:(m + 1) * P],
                                                      seq(old, k)[:, 2 * half:2 * half + 2, 0:length],
                                                      start=k == 0, stop=k == CT - 1)
                            mm.then_inc(shifted, 1)
                    if i < LEVELS - 1:
                        for side in range(2):
                            for m in range(CT):
                                for k in range(CT):
                                    mm = nc.tensor.matmul(ps[:, 4 + 2 * side + m, 0:C],
                                                          pw[:, 1 - side, k, m * P:(m + 1) * P], pw[:, side, k, :],
                                                          start=k == 0, stop=k == CT - 1)
                                mm.then_inc(squared, 1)

                @block.vector
                def _(dve):
                    for m in range(CT):
                        for half in range(2):
                            dve.wait_ge(shifted, 2 * m + half + 1)
                            bs = slice(2 * half, 2 * half + 2)
                            out = ps[:, 2 * m + half, :].rearrange("p (b t) -> p b t", b=2)[:, :, 0:length]
                            nc.vector.tensor_tensor(seq(new, m)[:, bs, shift:], out, seq(old, m)[:, bs, shift:],
                                                    ALU.add)

                @block.scalar
                def _(act):
                    for m in range(CT):
                        nc.scalar.copy(seq(new, m)[:, :, 0:shift], seq(old, m)[:, :, 0:shift])
                    if i < LEVELS - 1:
                        for side in range(2):
                            act.wait_ge(squared, CT * (side + 1))
                            nc.scalar.copy(nx[:, side, :, :], ps[:, 4 + 2 * side:6 + 2 * side, 0:C])
        linear_tokens(core, state[LEVELS % 2], wc, CT, C, add_to_residual(core))



def l3_xattn(core):
    nc, d, ps = core.nc, core.dram, core.ps
    CH = KC // P
    with ExitStack() as c:
        sb = core.allocator(c)
        wq, wp, wkv = sb([P, CT, C]), sb([P, CT, C]), sb([P, CT, 2 * C])
        bq, bp, bkv = sb([P, C]), sb([P, C]), sb([P, 2 * C])
        q, qT = sb([P, TT, C]), sb([P, CT, N])
        small = sb([P, 3, TT, H])
        ctx = sb([P, 2, CT, KC])
        ek, kk = sb([P, 4, 2, C]), sb([P, 3, 2, C])
        ksmall = sb([P, 3, 2, 2, H])
        v = sb([P, 4, 2, CT, P + 1])
        kv, ks = sb([P, CT, P]), sb([P, CT, P])
        ksum = sb([P, CT])
        res = sb([P, CT, N])
        rden = sb([P, CT, T])
        layer_norm(core, core.x, core.xn, core.xnT, loads=[
            (wq[:, :, :], ktiles(d["L3_xattn_Wq"])), (wp[:, :, :], ktiles(d["L3_xattn_Wp"])),
            (wkv[:, :, :], ktiles(d["L3_xattn_Wkv"])),
            (bq[:, :], d["L3_xattn_bq"]), (bp[:, :], d["L3_xattn_bp"]), (bkv[:, :], d["L3_xattn_bkv"])],
            bias=bp[:, :])
        heads = lambda ap: ap.rearrange("p (h c) -> p h c", h=H)
        spread = lambda ap: ap.unsqueeze(2).to_broadcast([P, H, D])
        with phase(core, "product_ready", "exp_done", "w", "q_ready", "turned", "centred") as (
                block, product_ready, exp_done, w, q_ready, turned, centred):
            @block.tensor
            def _(pe):
                for t in range(TT):
                    out = ps[:, t, 0:C]
                    for k in range(CT):
                        mm = nc.tensor.matmul(out, core.xnT[:, k, t * P:(t + 1) * P], wq[:, k, :],
                                              start=k == 0, stop=k == CT - 1)
                    mm.then_inc(product_ready, 1)
                for half in range(2):
                    pe.wait_ge(q_ready, 4 * (half + 1))
                    for t in range(4 * half, 4 * half + 4):
                        for k in range(CT):
                            nc.tensor.transpose(ps[:, CT * half + k, (t % 4) * P:(t % 4 + 1) * P],
                                                q[:, t, k * P:(k + 1) * P], core.ident[:, :]).then_inc(turned, 1)

            @block.vector
            def _(dve):
                link = chain(dve, w)
                for t in range(TT):
                    dve.wait_ge(product_ready, t + 1)
                    link(nc.vector.tensor_tensor(q[:, t, :], ps[:, t, 0:C], bq[:, :], ALU.add))
                    link(nc.vector.tensor_reduce(small[:, 0, t, :], heads(q[:, t, :]), AX.X, ALU.max))
                    nc.vector.tensor_tensor(heads(q[:, t, :]), heads(q[:, t, :]), spread(small[:, 0, t, :]),
                                            ALU.subtract).then_inc(centred, 1)
                for t in range(TT):
                    dve.wait_ge(exp_done, t + 1)
                    link(nc.vector.tensor_reduce(small[:, 1, t, :], heads(q[:, t, :]), AX.X, ALU.add))
                    link(nc.vector.reciprocal(small[:, 2, t, :], small[:, 1, t, :]))
                    nc.vector.tensor_tensor(heads(q[:, t, :]), heads(q[:, t, :]), spread(small[:, 2, t, :]),
                                            ALU.mult).then_inc(q_ready, 1)

            @block.scalar
            def _(act):
                for t in range(TT):
                    act.wait_ge(centred, t + 1)
                    nc.scalar.activation(q[:, t, :], q[:, t, :], ACT.Exp).then_inc(exp_done, 1)
                for half in range(2):
                    act.wait_ge(turned, 4 * CT * (half + 1))
                    nc.scalar.copy(qT[:, :, half * BANK:(half + 1) * BANK], ps[:, CT * half:CT * half + CT, :])
        pairs = [(ch, i) for ch in range(S // KC) for i in range(CH // 2)]
        with phase(core) as (block,):
            @block.gpsimd
            def _(pool):
                nc.gpsimd.memset(v[:, :, :, :, P:P + 1], 1.0)
        with nc.Fori(0, B) as b:
            names = ["landed_even", "landed_odd", "product_ready", "k_biased", "max_done", "centred", "exp_done",
                     "sum_done", "inverted", "k_ready", "v_ready", "kv_done"]
            with phase(core, *names) as (block, landed_even, landed_odd, product_ready, k_biased, max_done, centred,
                                         exp_done, sum_done, inverted, k_ready, v_ready, kv_done):
                landed = (landed_even, landed_odd)
                h2 = lambda ap: ap.rearrange("p t (h c) -> p (t h) c", h=H)
                flat = lambda ap: ap.rearrange("p t h -> p (t h)")
                spread2 = lambda ap: flat(ap).unsqueeze(2).to_broadcast([P, 2 * H, D])

                @block.sync
                def _(sp):
                    for ch in range(S // KC):
                        if ch >= 2:
                            sp.wait_ge(product_ready, (ch - 1) * CH // 2)
                        sp.dma_start(ctx[:, ch % 2, :, :],
                                     d["ctxT"][b, :, ch * KC:(ch + 1) * KC].rearrange("(k p) n -> p k n", p=P)
                                     ).then_inc(landed[ch % 2], 16)

                @block.tensor
                def _(pe):
                    def sums(j):
                        pe.wait_ge(k_ready, j + 1)
                        pe.wait_ge(v_ready, j + 1)
                        for i in range(2):
                            for f in range(CT):
                                mm = nc.tensor.matmul(ps[:, 4 + f, 0:P + 1], kk[:, j % 3, i, f * P:(f + 1) * P],
                                                      v[:, j % 4, i, f, :], start=j == 0 and i == 0,
                                                      stop=j == len(pairs) - 1 and i == 1)
                        mm.then_inc(kv_done, 1)

                    for j, (ch, i) in enumerate(pairs):
                        if i == 0:
                            pe.wait_ge(landed[ch % 2], 16 * (ch // 2 + 1))
                        if j >= 2:
                            pe.wait_ge(k_biased, j - 1)
                            pe.wait_ge(v_ready, j - 1)
                        for t in range(2):
                            for kind in range(2):
                                out = ps[:, 2 * (j % 2) + kind, t * C:(t + 1) * C]
                                for k in range(CT):
                                    mm = nc.tensor.matmul(out, ctx[:, ch % 2, k, (2 * i + t) * P:(2 * i + t + 1) * P],
                                                          wkv[:, k, kind * C:(kind + 1) * C], start=k == 0,
                                                          stop=k == CT - 1)
                        mm.then_inc(product_ready, 1)
                        if j >= 3:
                            sums(j - 3)
                    for j in range(len(pairs) - 3, len(pairs)):
                        sums(j)

                @block.vector
                def _(dve):
                    def biased(j):
                        dve.wait_ge(product_ready, j + 1)
                        if j >= 4:
                            dve.wait_ge(k_ready, j - 3)
                        nc.vector.tensor_tensor(ek[:, j % 4], ps[:, 2 * (j % 2), :].rearrange("p (t c) -> p t c", t=2),
                                                bkv[:, 0:C].unsqueeze(1).to_broadcast([P, 2, C]),
                                                ALU.add).then_inc(k_biased, 1)
                        dve.wait_ge(k_biased, j + 1)
                        if j >= 2:
                            dve.wait_ge(centred, j - 1)
                        nc.vector.tensor_reduce(flat(ksmall[:, 0, j % 2]), h2(ek[:, j % 4]), AX.X,
                                                ALU.max).then_inc(max_done, 1)

                    def norm(j):
                        dve.wait_ge(exp_done, j + 1)
                        nc.vector.tensor_reduce(flat(ksmall[:, 1, j % 2]), h2(ek[:, j % 4]), AX.X,
                                                ALU.add).then_inc(sum_done, 1)
                        dve.wait_ge(sum_done, j + 1)
                        nc.vector.reciprocal(flat(ksmall[:, 2, j % 2]), flat(ksmall[:, 1, j % 2])).then_inc(inverted, 1)
                        dve.wait_ge(inverted, j + 1)
                        if j >= 3:
                            dve.wait_ge(kv_done, j - 2)
                        nc.vector.tensor_tensor(h2(kk[:, j % 3]), h2(ek[:, j % 4]), spread2(ksmall[:, 2, j % 2]),
                                                ALU.mult).then_inc(k_ready, 1)

                    for j in range(len(pairs)):
                        biased(j)
                        if j >= 1:
                            norm(j - 1)
                    norm(len(pairs) - 1)

                @block.gpsimd
                def _(pool):
                    for j in range(len(pairs)):
                        pool.wait_ge(max_done, j + 1)
                        nc.gpsimd.tensor_tensor(h2(ek[:, j % 4]), h2(ek[:, j % 4]), spread2(ksmall[:, 0, j % 2]),
                                                ALU.subtract).then_inc(centred, 1)

                @block.scalar
                def _(act):
                    for j in range(len(pairs)):
                        act.wait_ge(product_ready, j + 1)
                        if j >= 4:
                            act.wait_ge(kv_done, j - 3)
                        nc.scalar.copy(v[:, j % 4, :, :, 0:P], ps[:, 2 * (j % 2) + 1, :].rearrange(
                            "p (t f c) -> p t f c", t=2, f=CT)).then_inc(v_ready, 1)
                        act.wait_ge(centred, j + 1)
                        nc.scalar.activation(ek[:, j % 4, :, :], ek[:, j % 4, :, :], ACT.Exp).then_inc(exp_done, 1)
            with phase(core, "w", "num_ready", "den_ready", "rden_ready", "done") as (
                    block, w, num_ready, den_ready, rden_ready, done):
                @block.vector
                def _(dve):
                    link = chain(dve, w)
                    for f in range(CT):
                        link(nc.vector.tensor_copy(ksum[:, f:f + 1], ps[:, 4 + f, P:P + 1]))
                        link(nc.vector.scalar_tensor_tensor(out=kv[:, f, :], in0=bkv[:, C + f * P:C + (f + 1) * P],
                                                            scalar=ksum[:, f:f + 1], in1=ps[:, 4 + f, 0:P],
                                                            op0=ALU.mult, op1=ALU.add))
                        nc.vector.tensor_tensor(kv[:, f, :], kv[:, f, :], core.block16[:, :], ALU.mult)
                        nc.vector.tensor_scalar(ks[:, f, :], core.block16[:, :], ksum[:, f:f + 1], None,
                                                ALU.mult).then_inc(done, 1)
                    for f in range(CT):
                        dve.wait_ge(den_ready, f + 1)
                        link(nc.vector.reciprocal(rden[:, f, :], ps[:, 2 * f + 1, 0:T]))
                        out = res[:, f, bass.ds(b * T, T)]
                        link(nc.vector.tensor_tensor(rden[:, f, :], ps[:, 2 * f, 0:T], rden[:, f, :], ALU.mult))
                        nc.vector.tensor_tensor(out, rden[:, f, :], qT[:, f, bass.ds(b * T, T)], ALU.add)

                @block.tensor
                def _(pe):
                    for f in range(CT):
                        pe.wait_ge(done, f + 1)
                        nc.tensor.matmul(ps[:, 2 * f, 0:T], kv[:, f, :], qT[:, f, bass.ds(b * T, T)],
                                         start=True, stop=True)
                        nc.tensor.matmul(ps[:, 2 * f + 1, 0:T], ks[:, f, :], qT[:, f, bass.ds(b * T, T)],
                                         start=True, stop=True).then_inc(den_ready, 1)
        linear_tokens(core, res, wp, CT, C, add_to_residual(core))

def l0_attn(core):
    nc, d, ps = core.nc, core.dram, core.ps
    FIVE, TM, TD = 5, 32, 64
    EPS = 1e-5 * 8 ** 2
    with ExitStack() as c:
        sb = core.allocator(c)
        wo = sb([P, CT, C])
        u, gamma, beta = sb([P, CT]), sb([P, CT]), sb([P, CT])
        r, k, v, dec, g = (sb([P, CT, N]) for _ in range(5))
        sel = sb([P, D, P])
        with ExitStack() as c2:
            sb2 = core.allocator(c2)
            maa = sb2([P, 6, CT])
            w1, w2, wd1, wd2 = sb2([P, CT, FIVE * TM]), sb2([P, 2, C]), sb2([P, CT, TD]), sb2([TD, C])
            decay = sb2([P, CT])
            proj = sb2([P, 4, CT, C])
            xx, mixed = sb2([P, CT, N]), sb2([P, CT, N])
            m = sb2([P, 2, N])
            hid = sb2([TD, N])
            layer_norm(core, core.x, core.xn, core.xnT, loads=[
                (maa[:, :, :], d["L0_attn_maa"]), (w1[:, :, :], ktiles(d["L0_attn_w1"])),
                (w2[:, 0, :], d["L0_attn_w2"][0:P, :]), (w2[0:TM, 1, :], d["L0_attn_w2"][P:P + TM, :]),
                (wd1[:, :, :], ktiles(d["L0_attn_wd1"])), (wd2[:, :], d["L0_attn_wd2"]),
                (decay[:, :], d["L0_attn_decay"]), (u[:, :], d["L0_attn_u"]),
                (gamma[:, :], d["L0_attn_gamma"]), (beta[:, :], d["L0_attn_beta"]),
                (sel[:, :, :], d["c_sel"]), (wo[:, :, :], ktiles(d["L0_attn_W_o"]))]
                + [(proj[:, i, :, :], ktiles(d["L0_attn_W_" + n])) for i, n in enumerate("rkvg")])
            seq = lambda tile, f: tile[:, f, :].rearrange("p (b t) -> p b t", b=B)
            with phase(core, "w") as (block, w):
                @block.vector
                def _(dve):
                    link = chain(dve, w)
                    for f in range(CT):
                        x = seq(core.xnT, f)
                        nc.vector.tensor_tensor(seq(xx, f)[:, :, 1:], x[:, :, 0:T - 1], x[:, :, 1:], ALU.subtract)
                        link(nc.vector.tensor_scalar(seq(xx, f)[:, :, 0:1], x[:, :, 0:1], -1.0, None, ALU.mult))
                        nc.vector.scalar_tensor_tensor(out=mixed[:, f, :], in0=xx[:, f, :], scalar=maa[:, 0, f:f + 1],
                                                       in1=core.xnT[:, f, :], op0=ALU.mult, op1=ALU.add)
            with phase(core, "ready") as (block, ready):
                @block.tensor
                def _(pe):
                    for part, width in ((0, P), (1, TM)):
                        for n in range(2):
                            for f in range(CT):
                                mm = nc.tensor.matmul(ps[0:width, 2 * part + n, :], w1[:, f, part * P:part * P + width],
                                                      mixed[:, f, n * BANK:(n + 1) * BANK], start=f == 0,
                                                      stop=f == CT - 1)
                            mm.then_inc(ready, 1)

                @block.scalar
                def _(act):
                    for part, width in ((0, P), (1, TM)):
                        for n in range(2):
                            act.wait_ge(ready, 2 * part + n + 1)
                            nc.scalar.activation(m[0:width, part, n * BANK:(n + 1) * BANK],
                                                 ps[0:width, 2 * part + n, :], ACT.Tanh)

            def mix(i):
                base, part = (TM * i, 0) if i < 4 else (0, 1)
                with phase(core, "ready", "w") as (block, ready, w):
                    @block.tensor
                    def _(pe):
                        for f in range(CT):
                            for n in range(2):
                                nc.tensor.matmul(ps[:, 2 * f + n, :], w2[base:base + TM, part, f * P:(f + 1) * P],
                                                 m[base:base + TM, part, n * BANK:(n + 1) * BANK],
                                                 start=True, stop=True, tile_position=(base, 0)).then_inc(ready, 1)

                    @block.vector
                    def _(dve):
                        link = chain(dve, w)
                        for f in range(CT):
                            dve.wait_ge(ready, 2 * f + 2)
                            link(nc.vector.scalar_tensor_tensor(
                                out=mixed[:, f, :].rearrange("p (n t) -> p n t", n=2), in0=ps[:, 2 * f:2 * f + 2, :],
                                scalar=maa[:, i + 1, f:f + 1], in1=xx[:, f, :].rearrange("p (n t) -> p n t", n=2),
                                op0=ALU.add, op1=ALU.mult))
                            nc.vector.tensor_tensor(mixed[:, f, :], mixed[:, f, :], core.xnT[:, f, :], ALU.add)

            at = lambda tile, mt, n: tile[:, mt, n * BANK:(n + 1) * BANK]
            for i, (j, dest) in {1: (1, k), 2: (2, v), 3: (0, r)}.items():
                mix(i)
                linear_features(core, proj[:, j, :, :], mixed, CT, CT,
                                lambda mt, n, q, dest=dest: nc.scalar.copy(at(dest, mt, n), q))
            mix(4)
            linear_features(core, proj[:, 3, :, :], mixed, CT, CT,
                            lambda mt, n, q: nc.scalar.activation(at(g, mt, n), q, ACT.Silu))
            mix(0)
            with phase(core, "ready", "hidden", "w") as (block, ready, hidden, w):
                @block.tensor
                def _(pe):
                    for n in range(2):
                        for f in range(CT):
                            mm = nc.tensor.matmul(ps[0:TD, n, :], wd1[:, f, :], mixed[:, f, n * BANK:(n + 1) * BANK],
                                                  start=f == 0, stop=f == CT - 1)
                        mm.then_inc(ready, 1)
                    for n in range(2):
                        pe.wait_ge(hidden, n + 1)
                        for f in range(CT):
                            nc.tensor.matmul(ps[:, 2 + 2 * n + f, :], wd2[:, f * P:(f + 1) * P],
                                             hid[:, n * BANK:(n + 1) * BANK], start=True, stop=True).then_inc(ready, 1)

                @block.scalar
                def _(act):
                    link = chain(act, w)
                    for n in range(2):
                        act.wait_ge(ready, n + 1)
                        nc.scalar.activation(hid[:, n * BANK:(n + 1) * BANK], ps[0:TD, n, :], ACT.Tanh).then_inc(hidden, 1)
                    for n in range(2):
                        for f in range(CT):
                            act.wait_ge(ready, 3 + 2 * n + f)
                            link(nc.scalar.activation(at(dec, f, n), ps[:, 2 + 2 * n + f, :], ACT.Exp,
                                                      bias=decay[:, f:f + 1]))
                            nc.scalar.activation(at(dec, f, n), at(dec, f, n), ACT.Exp, scale=-1.0)
        y, bonus, t1 = sb([P, CT, N]), sb([P, CT, N]), sb([P, CT, N])
        scan = sb([P, 2, 2, T + 1])
        kv, prod = sb([P, 2, BANK]), sb([P, 3, BANK])
        with phase(core) as (block,):
            @block.vector
            def _(dve):
                for f in range(CT):
                    nc.vector.scalar_tensor_tensor(out=bonus[:, f, :], in0=r[:, f, :], scalar=u[:, f:f + 1],
                                                   in1=k[:, f, :], op0=ALU.mult, op1=ALU.mult)
                nc.vector.memset(scan[:, :, :, 0:1], 0.0)
        linear_block(core, core.block16, bonus, lambda f, n, q: nc.vector.tensor_tensor(
            at(y, f, n), q, at(v, f, n), ALU.mult), "vector")
        units = [(f, n, i) for f in range(CT) for n in range(2) for i in range(D)]
        with phase(core, "spread", "bank_free", "kv_done", "scan_done", "prod_done", "summed") as (
                block, spread, bank_free, kv_done, scan_done, prod_done, summed):
            @block.tensor
            def _(pe):
                for j, (f, n, i) in enumerate(units):
                    s = 3 * (j % 2)
                    if j >= 2:
                        pe.wait_ge(bank_free, j - 1)
                    for q, src in enumerate((k, dec, r)):
                        nc.tensor.matmul(ps[:, s + q, :], sel[:, i, :], at(src, f, n), start=True,
                                         stop=True).then_inc(spread, 1)

            @block.vector
            def _(dve):
                for j, (f, n, i) in enumerate(units):
                    s, e = 3 * (j % 2), j % 2
                    dve.wait_ge(spread, 3 * j + 1)
                    nc.vector.tensor_tensor(kv[:, e, :], ps[:, s, :], at(v, f, n), ALU.mult).then_inc(kv_done, 1)
                    dve.wait_ge(kv_done, j + 1)
                    dve.wait_ge(spread, 3 * j + 2)
                    for b in range(2):
                        nc.vector.tensor_tensor_scan(scan[:, e, b, 1:T + 1], ps[:, s + 1, b * T:(b + 1) * T],
                                                     kv[:, e, b * T:(b + 1) * T], 0.0, ALU.mult,
                                                     ALU.add).then_inc(scan_done, 1)
                    dve.wait_ge(scan_done, 2 * j + 2)
                    dve.wait_ge(spread, 3 * j + 3)
                    if j >= 3:
                        dve.wait_ge(summed, j - 2)
                    nc.vector.tensor_tensor(prod[:, j % 3, :].rearrange("p (b t) -> p b t", b=2),
                                            ps[:, s + 2, :].rearrange("p (b t) -> p b t", b=2),
                                            scan[:, e, :, 0:T], ALU.mult).then_inc(bank_free, 1)

            @block.gpsimd
            def _(pool):
                for j, (f, n, i) in enumerate(units):
                    pool.wait_ge(bank_free, j + 1)
                    if j >= 1:
                        pool.wait_ge(summed, j)
                    nc.gpsimd.tensor_tensor(at(y, f, n), at(y, f, n), prod[:, j % 3, :], ALU.add).then_inc(summed, 1)
        linear_block(core, core.block16, y, lambda f, n, q: nc.vector.scalar_tensor_tensor(
            out=at(t1, f, n), in0=q, scalar=-1.0 / D, in1=at(y, f, n), op0=ALU.mult, op1=ALU.add), "vector")
        with phase(core) as (block,):
            @block.vector
            def _(dve):
                for f in range(CT):
                    nc.vector.tensor_tensor(y[:, f, :], t1[:, f, :], t1[:, f, :], ALU.mult)
        linear_block(core, core.block16, y, lambda f, n, q: nc.vector.tensor_scalar(
            at(bonus, f, n), q, 1.0 / D, EPS, ALU.mult, ALU.add), "vector")
        with phase(core, "root", "w") as (block, root, w):
            @block.scalar
            def _(act):
                for f in range(CT):
                    nc.scalar.activation(bonus[:, f, :], bonus[:, f, :], ACT.Sqrt).then_inc(root, 1)

            @block.vector
            def _(dve):
                link = chain(dve, w)
                for f in range(CT):
                    dve.wait_ge(root, f + 1)
                    link(nc.vector.reciprocal(bonus[:, f, :], bonus[:, f, :]))
                    link(nc.vector.tensor_tensor(t1[:, f, :], t1[:, f, :], bonus[:, f, :], ALU.mult))
                    link(nc.vector.tensor_scalar(t1[:, f, :], t1[:, f, :], gamma[:, f:f + 1], beta[:, f:f + 1],
                                                 ALU.mult, ALU.add))
                    nc.vector.tensor_tensor(t1[:, f, :], t1[:, f, :], g[:, f, :], ALU.mult)
        linear_tokens(core, t1, wo, CT, C, add_to_residual(core))


def linear_block(core, w, x, finish, engine):
    nc, ps = core.nc, core.ps
    tiles = [(f, n) for f in range(CT) for n in range(N // BANK)]
    with phase(core, "ready") as (block, ready):
        @block.tensor
        def _(pe):
            for i, (f, n) in enumerate(tiles):
                nc.tensor.matmul(ps[:, i, :], w[:, :], x[:, f, n * BANK:(n + 1) * BANK], start=True,
                                 stop=True).then_inc(ready, 1)

        def empty(eng):
            for i, (f, n) in enumerate(tiles):
                eng.wait_ge(ready, i + 1)
                finish(f, n, ps[:, i, :])

        if engine == "scalar":
            block.scalar(empty)
        else:
            block.vector(empty)



def pick_top(core, dve, link, scores, left, top, few):
    nc = core.nc
    for t in range(TT):
        last = nc.vector.max(top[:, t, :], scores[:, t, :])
    link(last)
    if few < 8:
        link(nc.vector.memset(top[:, :, few:8], -1.0))
    for t in range(TT):
        last = nc.vector.match_replace(left[:, t, :], top[:, t, :], scores[:, t, :], -2.0)
    link(last)


def expert_bias(core, weights, bias, e):
    nc, ps = core.nc, core.ps
    with ExitStack() as c:
        wT = core.allocator(c)([e, N])
        with phase(core, "turned", "copied", "ready") as (block, turned, copied, ready):
            @block.tensor
            def _(pe):
                for t in range(TT):
                    nc.tensor.transpose(ps[0:e, t // 4, (t % 4) * P:(t % 4 + 1) * P], weights[:, t, :],
                                        core.ident[:, :]).then_inc(turned, 1)
                for t in range(TT):
                    pe.wait_ge(copied, t // 4 + 1)
                    nc.tensor.matmul(ps[:, 2 + t // 2, (t % 2) * C:(t % 2 + 1) * C], wT[:, t * P:(t + 1) * P],
                                     bias, start=True, stop=True).then_inc(ready, 1)

            @block.scalar
            def _(act):
                for half in range(2):
                    act.wait_ge(turned, 4 * half + 4)
                    nc.scalar.copy(wT[:, half * BANK:(half + 1) * BANK], ps[0:e, half, :]).then_inc(copied, 1)

            @block.vector
            def _(dve):
                for t in range(TT):
                    dve.wait_ge(ready, t // 2 * 2 + 2)
                    nc.vector.tensor_tensor(core.x[:, t, :], ps[:, 2 + t // 2, (t % 2) * C:(t % 2 + 1) * C],
                                            core.x[:, t, :], ALU.add)


def l0_ffn(core):
    nc, d, ps = core.nc, core.dram, core.ps
    E, F, PICK = 64, 192, 8
    with ExitStack() as c:
        sb = core.allocator(c)
        gate = sb([P, CT, E])
        s, left, weights = sb([P, TT, E]), sb([P, TT, E]), sb([P, TT, E])
        top, small = sb([P, TT, 8]), sb([P, 3, TT, 1])
        layer_norm(core, core.x, core.xn, core.xnT, loads=[(gate[:, :, :], ktiles(d["L0_ffn_gate_w"]))])
        linear_tokens(core, core.xnT, gate, CT, E, lambda t, q: nc.vector.tensor_copy(s[:, t, :], q))
        spread = lambda i: small[:, i].to_broadcast([P, TT, E])
        with phase(core, "centred", "exp_done", "w") as (block, centred, exp_done, w):
            @block.vector
            def _(dve):
                link = chain(dve, w)
                link(nc.vector.tensor_reduce(small[:, 0, :, 0], s[:, :, :], AX.X, ALU.max))
                nc.vector.tensor_tensor(s[:, :, :], s[:, :, :], spread(0), ALU.subtract).then_inc(centred, 1)
                dve.wait_ge(exp_done, 1)
                link(nc.vector.tensor_reduce(small[:, 1, :, 0], s[:, :, :], AX.X, ALU.add))
                link(nc.vector.reciprocal(small[:, 1, :, :], small[:, 1, :, :]))
                link(nc.vector.tensor_tensor(s[:, :, :], s[:, :, :], spread(1), ALU.mult))
                pick_top(core, dve, link, s, left, top, PICK)
                link(nc.vector.tensor_reduce(small[:, 2, :, 0], top[:, :, :], AX.X, ALU.add))
                link(nc.vector.tensor_scalar(small[:, 2, :, :], small[:, 2, :, :], 1e-20, None, ALU.add))
                link(nc.vector.reciprocal(small[:, 2, :, :], small[:, 2, :, :]))
                link(nc.vector.tensor_scalar(left[:, :, :], left[:, :, :], -1.0, None, ALU.is_le))
                link(nc.vector.tensor_tensor(weights[:, :, :], s[:, :, :], left[:, :, :], ALU.mult))
                nc.vector.tensor_tensor(weights[:, :, :], weights[:, :, :], spread(2), ALU.mult)

            @block.scalar
            def _(act):
                act.wait_ge(centred, 1)
                nc.scalar.activation(s[:, :, :], s[:, :, :], ACT.Exp).then_inc(exp_done, 1)
        sparse_experts(core, weights, E)


def sparse_experts(core, weights, E):
    nc, d, ps = core.nc, core.dram, core.ps
    HT3 = 3
    AHEAD = 2
    ORDER = (2, 0, 1)
    with ExitStack() as c:
        sb = core.allocator(c)
        wgu = [sb([P, CT, 2, HT3 * P]) for _ in range(AHEAD)]
        wd = [sb([P, HT3, C]) for _ in range(AHEAD)]
        shares = [sb([P, N]) for _ in range(AHEAD)]
        gs = sb([P, 3, BANK])
        h = sb([P, AHEAD, HT3, N])
        wT = sb([E, N])

        def share_loads(pair, slot):
            return [(shares[slot][64 * i:64 * i + 64, :],
                     d["scratch_w"][bass.ds(2 * pair + i, 1), :].to_broadcast([64, N])) for i in range(2)]

        with phase(core, "turned", "copied", "stored", "landed") as (block, turned, copied, stored, landed):
            @block.tensor
            def _(pe):
                for t in range(TT):
                    nc.tensor.transpose(ps[0:E, t // 4, (t % 4) * P:(t % 4 + 1) * P], weights[:, t, :],
                                        core.ident[:, :]).then_inc(turned, 1)

            @block.scalar
            def _(act):
                for half in range(2):
                    act.wait_ge(turned, 4 * half + 4)
                    nc.scalar.copy(wT[:, half * BANK:(half + 1) * BANK], ps[0:E, half, :]).then_inc(copied, 1)

            @block.sync
            def _(sp):
                sp.dma_start(wgu[0][:, :, :, :], d["L0_ffn_wgu"][0]).then_inc(landed, 16)
                sp.dma_start(wd[0][:, :, :], d["L0_ffn_wd"][0]).then_inc(landed, 16)
                sp.wait_ge(copied, 2)
                sp.dma_start(d["scratch_w"][0:E], wT[:, :]).then_inc(stored, 16)
                sp.dma_start(d["scratch_w"][E:E + 2], wT[0:2, :]).then_inc(stored, 16)
                sp.wait_ge(stored, 32)
                for dst, src in share_loads(0, 0):
                    sp.dma_start(dst, src).then_inc(landed, 16)
                sp.wait_ge(landed, 64)

        UPS = 2 * HT3
        DOWNS = 3 * TT
        with nc.Fori(0, E // (2 * AHEAD)) as q:
            with phase(core, "wgu_b", "wd_b", "shares_b", "refilled", "up_ready", "silu_done", "shared", "h_ready",
                       "down_ready", "down_used") as (block, wgu_b, wd_b, shares_b, refilled, up_ready, silu_done,
                                                      shared, h_ready, down_ready, down_used):
                units = [(e, j, n) for e in range(AHEAD) for j in ORDER for n in range(2)]
                downs = [(e, j, t) for e in range(AHEAD) for j in ORDER for t in range(TT)]

                @block.sync
                def _(sp):
                    sp.dma_start(wgu[1][:, :, :, :], d["L0_ffn_wgu"][AHEAD * q + 1]).then_inc(wgu_b, 16)
                    for dst, src in share_loads(AHEAD * q + 1, 1):
                        sp.dma_start(dst, src).then_inc(shares_b, 16)
                    sp.dma_start(wd[1][:, :, :], d["L0_ffn_wd"][AHEAD * q + 1]).then_inc(wd_b, 16)
                    sp.wait_ge(up_ready, 2 * UPS)
                    sp.dma_start(wgu[0][:, :, :, :], d["L0_ffn_wgu"][AHEAD * q + 2]).then_inc(refilled, 16)
                    sp.wait_ge(shared, 2)
                    for dst, src in share_loads(AHEAD * q + 2, 0):
                        sp.dma_start(dst, src).then_inc(refilled, 16)
                    sp.wait_ge(down_ready, DOWNS)
                    sp.dma_start(wd[0][:, :, :], d["L0_ffn_wd"][AHEAD * q + 2]).then_inc(refilled, 16)
                    sp.wait_ge(refilled, 64)

                @block.tensor
                def _(pe):
                    for i, (e, j, n) in enumerate(units):
                        if i == UPS:
                            pe.wait_ge(wgu_b, 16)
                        if i >= 2:
                            pe.wait_ge(h_ready, i - 1)
                        for kind in range(2):
                            for k in range(CT):
                                mm = nc.tensor.matmul(ps[:, 2 * (i % 2) + kind, :],
                                                      wgu[e][:, k, kind, j * P:(j + 1) * P],
                                                      core.xnT[:, k, n * BANK:(n + 1) * BANK],
                                                      start=k == 0, stop=k == CT - 1)
                            mm.then_inc(up_ready, 1)
                    for i, (e, j, t) in enumerate(downs):
                        if i == 0:
                            pe.wait_ge(h_ready, UPS)
                        if i == DOWNS:
                            pe.wait_ge(h_ready, 2 * UPS)
                            pe.wait_ge(wd_b, 16)
                        if i >= 4:
                            pe.wait_ge(down_used, i - 3)
                        nc.tensor.matmul(ps[:, 4 + i % 4, 0:C], h[:, e, j, t * P:(t + 1) * P], wd[e][:, j, :],
                                         start=True, stop=True).then_inc(down_ready, 1)

                @block.scalar
                def _(act):
                    for i, (e, j, n) in enumerate(units):
                        act.wait_ge(up_ready, 2 * i + 1)
                        if i >= 3:
                            act.wait_ge(h_ready, i - 2)
                        nc.scalar.activation(gs[:, i % 3, :], ps[:, 2 * (i % 2), :], ACT.Silu).then_inc(silu_done, 1)

                @block.gpsimd
                def _(pool):
                    for i, (e, j, n) in enumerate(units):
                        if j == 2:
                            if e == 1 and n == 0:
                                pool.wait_ge(shares_b, 32)
                            pool.wait_ge(silu_done, i + 1)
                            nc.gpsimd.tensor_tensor(gs[:, i % 3, :], gs[:, i % 3, :],
                                                    shares[e][:, n * BANK:(n + 1) * BANK], ALU.mult).then_inc(shared, 1)

                @block.vector
                def _(dve):
                    for i, (e, j, n) in enumerate(units):
                        dve.wait_ge(silu_done, i + 1)
                        dve.wait_ge(up_ready, 2 * i + 2)
                        if j == 2:
                            dve.wait_ge(shared, 2 * e + n + 1)
                        nc.vector.tensor_tensor(h[:, e, j, n * BANK:(n + 1) * BANK], gs[:, i % 3, :],
                                                ps[:, 2 * (i % 2) + 1, :], ALU.mult).then_inc(h_ready, 1)
                    for i, (e, j, t) in enumerate(downs):
                        dve.wait_ge(down_ready, i + 1)
                        if i >= TT:
                            dve.wait_ge(down_used, i - TT + 1)
                        product, x = ps[:, 4 + i % 4, 0:C], core.x[:, t, :]
                        if j == 2:
                            nc.vector.tensor_tensor(x, product, x, ALU.add).then_inc(down_used, 1)
                        else:
                            nc.vector.scalar_tensor_tensor(out=x, in0=product,
                                                           scalar=weights[:, t, bass.ds(2 * AHEAD * q + 2 * e + j, 1)],
                                                           in1=x, op0=ALU.mult, op1=ALU.add).then_inc(down_used, 1)


def l1_attn(core):
    nc, d, ps = core.nc, core.dram, core.ps
    E, F, HR, PICK, PAD = 6, 384, 128, 2, 16
    FT = F // P
    with ExitStack() as c:
        sb = core.allocator(c)
        r1w, r2w = sb([P, CT, HR]), sb([HR, E])
        rows = sb([P, HR])
        lng, lnb = sb([P, 1]), sb([P, 1])
        r2b, route_bias, temp = sb([P, E]), sb([P, E]), sb([P, 1])
        b1, b2 = sb([P, E, FT]), sb([E, C])
        hr, hn, hT = sb([P, TT, HR]), sb([P, TT, HR]), sb([P, N])
        s, left, weights = sb([P, TT, PAD]), sb([P, TT, PAD]), sb([P, TT, E])
        top, small = sb([P, TT, 8]), sb([P, 3, TT, 1])
        stats, mv, rstd = sb([P, TT, 6]), sb([P, TT, 2]), sb([P, TT])
        w1 = [sb([P, CT, F]) for _ in range(2)]
        w2 = [sb([P, FT, C]) for _ in range(2)]
        h = sb([P, 2, FT, N])
        layer_norm(core, core.x, core.xn, core.xnT, loads=[
            (r1w[:, :, :], ktiles(d["L1_attn_r1_w"])), (r2w[:, :], d["L1_attn_r2_w"]), (rows[:, :], d["L1_attn_r1_b"]),
            (lng[:, :], d["L1_attn_ln_g"]), (lnb[:, :], d["L1_attn_ln_b"]), (r2b[:, :], d["L1_attn_r2_b"]),
            (route_bias[:, :], d["L1_attn_route_bias"]), (temp[:, :], d["L1_attn_temp"]),
            (b1[:, :, :], d["L1_attn_b1"]), (b2[:, :], d["L1_attn_b2"]),
            (w1[0][:, :, :], ktiles(d["L1_attn_W1"][0])), (w2[0][:, :, :], ktiles(d["L1_attn_W2"][0]))])
        linear_tokens(core, core.xnT, r1w, CT, HR, lambda t, q: nc.vector.tensor_tensor(
            hr[:, t, :], q, rows[:, :], ALU.add))
        with phase(core, "w", "var_ready", "root_done", "norm_done", "turned", "gelu_done", "logits", "exp_done",
                   "centred") as (block, w, var_ready, root_done, norm_done, turned, gelu_done, logits, exp_done,
                                  centred):
            @block.vector
            def _(dve):
                link = chain(dve, w)
                for t in range(TT):
                    link(nc.vector.bn_stats(stats[:, t, :], hr[:, t, :]))
                for t in range(TT):
                    link(nc.vector.bn_aggr(mv[:, t, :], stats[:, t, :]))
                nc.vector.tensor_scalar(rstd[:, :], mv[:, :, 1], 1e-5, None, ALU.add).then_inc(var_ready, 1)
                link(nc.vector.reciprocal(temp[:, :], temp[:, :]))
                dve.wait_ge(root_done, 1)
                link(nc.vector.reciprocal(rstd[:, :], rstd[:, :]))
                for t in range(TT):
                    nc.vector.tensor_scalar(hn[:, t, :], hr[:, t, :], mv[:, t, 0:1], rstd[:, t:t + 1],
                                            ALU.subtract, ALU.mult).then_inc(norm_done, 1)
                dve.wait_ge(logits, TT)
                link(nc.vector.memset(s[:, :, E:PAD], -1.0))
                spread_e = lambda ap: ap.unsqueeze(1).to_broadcast([P, TT, E])
                se = s[:, :, 0:E]
                link(nc.vector.tensor_tensor(se, ps[:, 2, 0:TT * E].rearrange("p (t e) -> p t e", e=E),
                                             spread_e(r2b[:, :]), ALU.add))
                link(nc.vector.tensor_scalar(se, se, temp[:, 0:1], None, ALU.mult))
                link(nc.vector.tensor_tensor(se, se, spread_e(route_bias[:, :]), ALU.add))
                spread = lambda i: small[:, i].to_broadcast([P, TT, E])
                link(nc.vector.tensor_reduce(small[:, 0, :, 0], se, AX.X, ALU.max))
                nc.vector.tensor_tensor(se, se, spread(0), ALU.subtract).then_inc(centred, 1)
                dve.wait_ge(exp_done, 1)
                link(nc.vector.tensor_reduce(small[:, 1, :, 0], se, AX.X, ALU.add))
                link(nc.vector.reciprocal(small[:, 1, :, :], small[:, 1, :, :]))
                link(nc.vector.tensor_tensor(se, se, spread(1), ALU.mult))
                pick_top(core, dve, link, s, left, top, PICK)
                link(nc.vector.tensor_scalar(left[:, :, 0:E], left[:, :, 0:E], -1.5, None, ALU.is_le))
                nc.vector.tensor_tensor(weights[:, :, :], se, left[:, :, 0:E], ALU.mult)

            @block.tensor
            def _(pe):
                for t in range(TT):
                    pe.wait_ge(norm_done, t + 1)
                    nc.tensor.transpose(ps[:, t // 4, (t % 4) * P:(t % 4 + 1) * P], hn[:, t, :],
                                        core.ident[:, :]).then_inc(turned, 1)
                for t in range(TT):
                    pe.wait_ge(gelu_done, t // 4 + 1)
                    nc.tensor.matmul(ps[:, 2, t * E:(t + 1) * E], hT[:, t * P:(t + 1) * P], r2w[:, :], start=True,
                                     stop=True).then_inc(logits, 1)

            @block.scalar
            def _(act):
                act.wait_ge(var_ready, 1)
                nc.scalar.activation(rstd[:, :], rstd[:, :], ACT.Sqrt).then_inc(root_done, 1)
                for half in range(2):
                    act.wait_ge(turned, 4 * half + 4)
                    nc.scalar.activation(hT[:, half * BANK:(half + 1) * BANK], ps[:, half, :], ACT.Gelu,
                                         bias=lnb[:, 0:1], scale=lng[:, 0:1]).then_inc(gelu_done, 1)
                act.wait_ge(centred, 1)
                nc.scalar.activation(s[:, :, 0:E], s[:, :, 0:E], ACT.Exp).then_inc(exp_done, 1)
        expert_bias(core, weights, b2[:, :], E)
        with nc.Fori(0, E // 2) as q:
            with phase(core, "w_b", "refilled", "up_ready", "h_ready", "down_ready", "down_used") as (
                    block, w_b, refilled, up_ready, h_ready, down_ready, down_used):
                units = [(e, m, n) for e in range(2) for m in range(FT) for n in range(2)]
                outs = [(e, t) for e in range(2) for t in range(TT)]

                @block.sync
                def _(sp):
                    sp.dma_start(w1[1][:, :, :], ktiles(d["L1_attn_W1"][2 * q + 1])).then_inc(w_b, 16)
                    sp.dma_start(w2[1][:, :, :], ktiles(d["L1_attn_W2"][2 * q + 1])).then_inc(w_b, 16)
                    sp.wait_ge(up_ready, 2 * FT)
                    sp.dma_start(w1[0][:, :, :], ktiles(d["L1_attn_W1"][2 * q + 2])).then_inc(refilled, 16)
                    sp.wait_ge(down_ready, TT)
                    sp.dma_start(w2[0][:, :, :], ktiles(d["L1_attn_W2"][2 * q + 2])).then_inc(refilled, 16)
                    sp.wait_ge(refilled, 32)

                @block.tensor
                def _(pe):
                    for i, (e, m, n) in enumerate(units):
                        if i == 2 * FT:
                            pe.wait_ge(w_b, 32)
                        if i >= 4:
                            pe.wait_ge(h_ready, i - 3)
                        for k in range(CT):
                            mm = nc.tensor.matmul(ps[:, i % 4, :], w1[e][:, k, m * P:(m + 1) * P],
                                                  core.xnT[:, k, n * BANK:(n + 1) * BANK], start=k == 0,
                                                  stop=k == CT - 1)
                        mm.then_inc(up_ready, 1)
                    for i, (e, t) in enumerate(outs):
                        if t == 0:
                            pe.wait_ge(h_ready, 2 * FT * (e + 1))
                        if i >= 4:
                            pe.wait_ge(down_used, i - 3)
                        for m in range(FT):
                            mm = nc.tensor.matmul(ps[:, 4 + i % 4, 0:C], h[:, e, m, t * P:(t + 1) * P],
                                                  w2[e][:, m, :], start=m == 0, stop=m == FT - 1)
                        mm.then_inc(down_ready, 1)

                @block.scalar
                def _(act):
                    for i, (e, m, n) in enumerate(units):
                        act.wait_ge(up_ready, i + 1)
                        nc.scalar.activation(h[:, e, m, n * BANK:(n + 1) * BANK], ps[:, i % 4, :],
                                             ACT.Gelu if e == 0 else ACT.Silu,
                                             bias=b1[:, bass.ds(2 * q + e, 1), m]).then_inc(h_ready, 1)

                @block.vector
                def _(dve):
                    for i, (e, t) in enumerate(outs):
                        dve.wait_ge(down_ready, i + 1)
                        if e == 1:
                            dve.wait_ge(down_used, t + 1)
                        nc.vector.scalar_tensor_tensor(out=core.x[:, t, :], in0=ps[:, 4 + i % 4, 0:C],
                                                       scalar=weights[:, t, bass.ds(2 * q + e, 1)],
                                                       in1=core.x[:, t, :], op0=ALU.mult,
                                                       op1=ALU.add).then_inc(down_used, 1)


def l1_ffn(core):
    nc, d, ps = core.nc, core.dram, core.ps
    E, G, I, PICK, PICKG, ROUTE = 16, 4, 256, 4, 2, 2.5
    IT, GP = I // P, 16
    with ExitStack() as c:
        sb = core.allocator(c)
        gate = sb([P, CT, E])
        s, masked, left, weights = (sb([P, TT, E]) for _ in range(4))
        gs, gleft = sb([P, TT, GP]), sb([P, TT, GP])
        top, small = sb([P, TT, 8]), sb([P, TT, 1])
        b1, b3, b2 = sb([P, E, IT]), sb([P, E, IT]), sb([E, C])
        w13 = [sb([P, CT, 2, I]) for _ in range(2)]
        w2 = [sb([P, IT, C]) for _ in range(2)]
        gate_h, h = sb([P, 2, BANK]), sb([P, 2, IT, N])
        layer_norm(core, core.x, core.xn, core.xnT, loads=[
            (gate[:, :, :], ktiles(d["L1_ffn_Wg"])), (b1[:, :, :], d["L1_ffn_b1"]), (b3[:, :, :], d["L1_ffn_b3"]),
            (b2[:, :], d["L1_ffn_b2"]),
            (w13[0][:, :, :, :], d["L1_ffn_W13"][0]), (w2[0][:, :, :], ktiles(d["L1_ffn_W2"][0]))])
        linear_tokens(core, core.xnT, gate, CT, E, lambda t, q: nc.scalar.activation(s[:, t, :], q, ACT.Sigmoid),
                      engine="scalar")
        with phase(core, "w") as (block, w):
            @block.vector
            def _(dve):
                link = chain(dve, w)
                grouped = lambda ap: ap.rearrange("p t (g e) -> p t g e", g=G)
                link(nc.vector.memset(gs[:, :, G:GP], -1.0))
                link(nc.vector.tensor_reduce(gs[:, :, 0:G], grouped(s[:, :, :]), AX.X, ALU.max))
                pick_top(core, dve, link, gs, gleft, top, PICKG)
                link(nc.vector.tensor_scalar(gleft[:, :, :], gleft[:, :, :], -1.5, None, ALU.is_le))
                link(nc.vector.tensor_scalar(masked[:, :, :], s[:, :, :], 1.0, None, ALU.add))
                link(nc.vector.tensor_tensor(grouped(masked[:, :, :]), grouped(masked[:, :, :]),
                                             gleft[:, :, 0:G].unsqueeze(3).to_broadcast([P, TT, G, E // G]), ALU.mult))
                link(nc.vector.tensor_scalar(masked[:, :, :], masked[:, :, :], -1.0, None, ALU.add))
                pick_top(core, dve, link, masked, left, top, PICK)
                link(nc.vector.tensor_tensor(left[:, :, :], masked[:, :, :], left[:, :, :], ALU.subtract))
                link(nc.vector.tensor_scalar(left[:, :, :], left[:, :, :], 1.5, None, ALU.is_ge))
                link(nc.vector.tensor_tensor(weights[:, :, :], s[:, :, :], left[:, :, :], ALU.mult))
                link(nc.vector.tensor_reduce(small[:, :, 0], weights[:, :, :], AX.X, ALU.add))
                link(nc.vector.reciprocal(small[:, :, :], small[:, :, :]))
                link(nc.vector.tensor_scalar(small[:, :, :], small[:, :, :], ROUTE, None, ALU.mult))
                nc.vector.tensor_tensor(weights[:, :, :], weights[:, :, :], small[:, :, :].to_broadcast([P, TT, E]),
                                        ALU.mult)
        expert_bias(core, weights, b2[:, :], E)
        with nc.Fori(0, E // 2) as q:
            with phase(core, "w_b", "refilled", "up_ready", "silu_done", "h_ready", "down_ready", "down_used") as (
                    block, w_b, refilled, up_ready, silu_done, h_ready, down_ready, down_used):
                units = [(e, m, n) for e in range(2) for m in range(IT) for n in range(2)]
                outs = [(e, t) for e in range(2) for t in range(TT)]

                @block.sync
                def _(sp):
                    sp.dma_start(w13[1][:, :, :, :], d["L1_ffn_W13"][2 * q + 1]).then_inc(w_b, 16)
                    sp.dma_start(w2[1][:, :, :], ktiles(d["L1_ffn_W2"][2 * q + 1])).then_inc(w_b, 16)
                    sp.wait_ge(up_ready, 4 * IT)
                    sp.dma_start(w13[0][:, :, :, :], d["L1_ffn_W13"][2 * q + 2]).then_inc(refilled, 16)
                    sp.wait_ge(down_ready, TT)
                    sp.dma_start(w2[0][:, :, :], ktiles(d["L1_ffn_W2"][2 * q + 2])).then_inc(refilled, 16)
                    sp.wait_ge(refilled, 32)

                @block.tensor
                def _(pe):
                    for i, (e, m, n) in enumerate(units):
                        if i == 2 * IT:
                            pe.wait_ge(w_b, 32)
                        if i >= 2:
                            pe.wait_ge(h_ready, i - 1)
                        for kind in range(2):
                            for k in range(CT):
                                mm = nc.tensor.matmul(ps[:, 2 * (i % 2) + kind, :],
                                                      w13[e][:, k, kind, m * P:(m + 1) * P],
                                                      core.xnT[:, k, n * BANK:(n + 1) * BANK], start=k == 0,
                                                      stop=k == CT - 1)
                            mm.then_inc(up_ready, 1)
                    for i, (e, t) in enumerate(outs):
                        if t == 0:
                            pe.wait_ge(h_ready, 2 * IT * (e + 1))
                        if i >= 4:
                            pe.wait_ge(down_used, i - 3)
                        for m in range(IT):
                            mm = nc.tensor.matmul(ps[:, 4 + i % 4, 0:C], h[:, e, m, t * P:(t + 1) * P],
                                                  w2[e][:, m, :], start=m == 0, stop=m == IT - 1)
                        mm.then_inc(down_ready, 1)

                @block.scalar
                def _(act):
                    for i, (e, m, n) in enumerate(units):
                        act.wait_ge(up_ready, 2 * i + 1)
                        if i >= 2:
                            act.wait_ge(h_ready, i - 1)
                        nc.scalar.activation(gate_h[:, i % 2, :], ps[:, 2 * (i % 2), :], ACT.Silu,
                                             bias=b1[:, bass.ds(2 * q + e, 1), m]).then_inc(silu_done, 1)

                @block.vector
                def _(dve):
                    for i, (e, m, n) in enumerate(units):
                        dve.wait_ge(silu_done, i + 1)
                        dve.wait_ge(up_ready, 2 * i + 2)
                        nc.vector.scalar_tensor_tensor(out=h[:, e, m, n * BANK:(n + 1) * BANK],
                                                       in0=ps[:, 2 * (i % 2) + 1, :],
                                                       scalar=b3[:, bass.ds(2 * q + e, 1), m], in1=gate_h[:, i % 2, :],
                                                       op0=ALU.add, op1=ALU.mult).then_inc(h_ready, 1)
                    for i, (e, t) in enumerate(outs):
                        dve.wait_ge(down_ready, i + 1)
                        if e == 1:
                            dve.wait_ge(down_used, t + 1)
                        nc.vector.scalar_tensor_tensor(out=core.x[:, t, :], in0=ps[:, 4 + i % 4, 0:C],
                                                       scalar=weights[:, t, bass.ds(2 * q + e, 1)],
                                                       in1=core.x[:, t, :], op0=ALU.mult,
                                                       op1=ALU.add).then_inc(down_used, 1)

def attend(core, heads, spans, score, turns, weigh, per_bank, dest):
    nc, ps = core.nc, core.ps
    total = sum(w for _, w in spans)
    with ExitStack() as c:
        sb = core.allocator(c)
        p, pT = sb([P, 3, BANK]), sb([P, 3, BANK])
        nm, z = sb([P, 4, 2]), sb([P, 4, 2])
        with phase(core, "scored", "max_done", "exp_done", "inv_done", "normed", "turned", "copied", "weighed",
                   "taken") as (block, scored, max_done, exp_done, inv_done, normed, turned, copied, weighed, taken):
            @block.tensor
            def _(pe):
                for i in range(heads + 4):
                    if i < heads:
                        if i >= 2:
                            pe.wait_ge(exp_done, 2 * (i - 1))
                        score(i, ps[:, i % 2, :]).then_inc(scored, 1)
                    j = i - 2
                    if 0 <= j < heads:
                        pe.wait_ge(normed, 2 * (j + 1))
                        if j >= 2:
                            pe.wait_ge(copied, j - 1)
                        for a, b in turns:
                            mm = nc.tensor.transpose(ps[:, 2 + j % 2, b:b + P], p[:, j % 3, a:a + P],
                                                     core.ident[:, :])
                        mm.then_inc(turned, 1)
                    j = i - 4
                    if 0 <= j < heads:
                        group = j // per_bank
                        pe.wait_ge(copied, j + 1)
                        if j % per_bank == 0 and group >= 2:
                            pe.wait_ge(taken, group - 1)
                        weigh(j, pT[:, j % 3, :], ps[:, 4 + group % 2, :]).then_inc(weighed, 1)

            @block.vector
            def _(dve):
                def maxima(i):
                    dve.wait_ge(scored, i + 1)
                    if i >= 4:
                        dve.wait_ge(exp_done, 2 * (i - 3))
                    for s, (a, w) in enumerate(spans):
                        nc.vector.tensor_reduce(nm[:, i % 4, s:s + 1], ps[:, i % 2, a:a + w], AX.X, ALU.max,
                                                negate=True).then_inc(max_done, 1)

                def norm(i):
                    dve.wait_ge(exp_done, 2 * (i + 1))
                    nc.vector.reciprocal(z[:, i % 4, :], z[:, i % 4, :]).then_inc(inv_done, 1)
                    dve.wait_ge(inv_done, i + 1)
                    for s, (a, w) in enumerate(spans):
                        nc.vector.tensor_scalar(p[:, i % 3, a:a + w], p[:, i % 3, a:a + w], z[:, i % 4, s:s + 1], None,
                                                ALU.mult).then_inc(normed, 1)

                def take(g):
                    dve.wait_ge(weighed, per_bank * (g + 1))
                    nc.vector.tensor_copy(dest(g), ps[:, 4 + g % 2, 0:T]).then_inc(taken, 1)

                for i in range(heads + 6):
                    if i < heads:
                        maxima(i)
                    if 1 <= i <= heads:
                        norm(i - 1)
                    if i >= 6 and (i - 5) % per_bank == 0:
                        take((i - 5) // per_bank - 1)

            @block.scalar
            def _(act):
                for i in range(heads + 3):
                    if i < heads:
                        act.wait_ge(max_done, 2 * (i + 1))
                        if i >= 3:
                            act.wait_ge(turned, i - 2)
                        if i >= 4:
                            act.wait_ge(normed, 2 * (i - 3))
                        for s, (a, w) in enumerate(spans):
                            nc.scalar.activation(p[:, i % 3, a:a + w], ps[:, i % 2, a:a + w], ACT.Exp,
                                                 bias=nm[:, i % 4, s:s + 1],
                                                 accum_out=z[:, i % 4, s:s + 1]).then_inc(exp_done, 1)
                    j = i - 2
                    if 0 <= j < heads:
                        act.wait_ge(turned, j + 1)
                        if j >= 3:
                            act.wait_ge(weighed, j - 2)
                        nc.scalar.copy(pT[:, j % 3, 0:total], ps[:, 2 + j % 2, 0:total]).then_inc(copied, 1)


def l2_attn(core):
    nc, d, ps = core.nc, core.dram, core.ps
    HD = 64
    M = H * HD // P
    with ExitStack() as c:
        sb = core.allocator(c)
        w_in, w_out = sb([P, CT, 3 * H * HD]), sb([P, M, C])
        b_qk, b_v, b_out = sb([P, 2 * M]), sb([P, H * HD]), sb([P, C])
        cos, sin, turn = sb([P, T]), sb([P, T]), sb([P, P])
        causal_wide, causal, identb = sb([P, P]), sb([P, P], BF16), sb([P, P], BF16)
        xb = sb([P, CT, T])
        raw, t2 = sb([P, 3, T]), sb([P, 2, T])
        qk, v, o = sb([P, 2 * M, T]), sb([P, 2, H * HD]), sb([P, M, T])
        layer_norm(core, core.x, core.xn, core.xnT, loads=[
            (w_in[:, :, :], ktiles(d["L2_attn_W_in"])), (w_out[:, :, :], ktiles(d["L2_attn_W_out"])),
            (b_qk[:, :], d["L2_attn_b_qk"]), (b_v[:, :], d["L2_attn_b_v"]), (b_out[:, :], d["L2_attn_b_out"]),
            (cos[:, :], d["c_cos64"]), (sin[:, :], d["c_sin64"]), (turn[:, :], d["c_turn64"]),
            (causal_wide[:, :], d["c_causal"])])
        with phase(core, "w") as (block, w):
            @block.vector
            def _(dve):
                nc.vector.tensor_copy(identb[:, :], core.ident[:, :])
                nc.vector.tensor_copy(causal[:, :], causal_wide[:, :])
                nc.vector.tensor_scalar(b_qk[:, 0:M], b_qk[:, 0:M], HD ** -0.5, None, ALU.mult)
                for t in range(TT):
                    nc.vector.tensor_tensor(core.x[:, t, :], core.x[:, t, :], b_out[:, :], ALU.add)
        with nc.Fori(0, B) as b:
            with phase(core, "sliced", "product", "raw_done", "turned", "rot_done", "sum_done", "v_product",
                       "cos_done") as (block, sliced, product, raw_done, turned, rot_done, sum_done, v_product, cos_done):
                vt = [(t, n) for t in range(2) for n in range(2)]

                @block.tensor
                def _(pe):
                    pe.wait_ge(sliced, 1)
                    for i in range(2 * M + 1):
                        if i < 2 * M:
                            if i >= 2:
                                pe.wait_ge(raw_done, i - 1)
                            for k in range(CT):
                                mm = nc.tensor.matmul(ps[:, i % 2, 0:T], w_in[:, k, i * P:(i + 1) * P], xb[:, k, :],
                                                      start=k == 0, stop=k == CT - 1)
                            mm.then_inc(product, 1)
                        if i >= 1:
                            j = i - 1
                            pe.wait_ge(raw_done, j + 1)
                            if j >= 2:
                                pe.wait_ge(rot_done, j - 1)
                            nc.tensor.matmul(ps[:, 2 + j % 2, 0:T], turn[:, :], raw[:, j % 3, :], start=True,
                                             stop=True).then_inc(turned, 1)
                    for j, (t, n) in enumerate(vt):
                        for k in range(CT):
                            mm = nc.tensor.matmul(ps[:, 4 + j, :], xb[:, k, t * P:(t + 1) * P],
                                                  w_in[:, k, 2 * M * P + n * BANK:2 * M * P + (n + 1) * BANK],
                                                  start=k == 0, stop=k == CT - 1)
                        mm.then_inc(v_product, 1)

                @block.scalar
                def _(act):
                    for i in range(2 * M):
                        act.wait_ge(product, i + 1)
                        if i >= 3:
                            act.wait_ge(turned, i - 2)
                            act.wait_ge(sum_done, i - 2)
                        nc.scalar.activation(raw[:, i % 3, :], ps[:, i % 2, 0:T], ACT.Identity, bias=b_qk[:, i:i + 1],
                                             scale=HD ** -0.5 if i < M else 1.0).then_inc(raw_done, 1)

                @block.vector
                def _(dve):
                    nc.vector.tensor_copy(xb[:, :, :], core.xnT[:, :, bass.ds(b * T, T)]).then_inc(sliced, 1)
                    for i in range(2 * M):
                        dve.wait_ge(raw_done, i + 1)
                        nc.vector.tensor_tensor(qk[:, i, :], raw[:, i % 3, :], cos[:, :], ALU.mult).then_inc(cos_done, 1)
                        dve.wait_ge(turned, i + 1)
                        nc.vector.tensor_tensor(t2[:, i % 2, :], ps[:, 2 + i % 2, 0:T], sin[:, :],
                                                ALU.mult).then_inc(rot_done, 1)
                        dve.wait_ge(rot_done, i + 1)
                        dve.wait_ge(cos_done, i + 1)
                        nc.vector.tensor_tensor(qk[:, i, :], qk[:, i, :], t2[:, i % 2, :], ALU.add).then_inc(sum_done, 1)
                    for j, (t, n) in enumerate(vt):
                        dve.wait_ge(v_product, j + 1)
                        nc.vector.tensor_tensor(v[:, t, n * BANK:(n + 1) * BANK], ps[:, 4 + j, :],
                                                b_v[:, n * BANK:(n + 1) * BANK], ALU.add)

            def score(h, bank):
                base, m = HD * (h % 2), h // 2
                for tile, a, w in ((0, 0, P), (1, P, 2 * P)):
                    nc.tensor.matmul(bank[:, a:a + w], qk[base:base + HD, m, tile * P:(tile + 1) * P],
                                     qk[base:base + HD, M + m, 0:w], start=True, stop=False, skip_group_check=True)
                    mm = nc.tensor.matmul(bank[:, a + w - P:a + w], identb[:, :], causal[:, :], start=False,
                                          stop=True, skip_group_check=True)
                return mm

            def weigh(h, probs, out):
                base = HD * (h % 2)
                nc.tensor.matmul(out[base:base + HD, 0:T], v[:, 0, h * HD:(h + 1) * HD], probs[:, 0:T], start=True,
                                 stop=False, skip_group_check=True)
                return nc.tensor.matmul(out[base:base + HD, P:T], v[:, 1, h * HD:(h + 1) * HD], probs[:, T:T + P],
                                        start=False, stop=True, skip_group_check=True)

            attend(core, H, [(0, P), (P, 2 * P)], score, [(0, 0), (P, P), (2 * P, 2 * P)], weigh, 2,
                   lambda g: o[:, g, :])
            with phase(core, "ready") as (block, ready):
                @block.tensor
                def _(pe):
                    for t in range(2):
                        for m in range(M):
                            mm = nc.tensor.matmul(ps[:, t, 0:C], o[:, m, t * P:(t + 1) * P], w_out[:, m, :],
                                                  start=m == 0, stop=m == M - 1)
                        mm.then_inc(ready, 1)

                @block.vector
                def _(dve):
                    for t in range(2):
                        dve.wait_ge(ready, t + 1)
                        x = core.x[:, bass.ds(2 * b + t, 1), :]
                        nc.vector.tensor_tensor(x, ps[:, t:t + 1, 0:C], x, ALU.add)


def l2_ffn(core):
    nc, d, ps = core.nc, core.dram, core.ps
    NH, HD, E, FD, TPE = 32, 8, 8, 1024, 64
    FT = FD // P
    with ExitStack() as c:
        sb = core.allocator(c)
        xfT = sb([P, CT, N])
        with ExitStack() as c2:
            sb2 = core.allocator(c2)
            w = sb2([P, 4, CT, C])
            gain, shift, mask8 = sb2([P, CT]), sb2([P, CT]), sb2([P, 16])
            oT, xaT, xa_tok = sb2([P, CT, N]), sb2([P, CT, N]), sb2([P, TT, C])
            xb, q, k = sb2([P, CT, T]), sb2([P, CT, T]), sb2([P, CT, T])
            qz, vz = sb2([P, NH, T]), sb2([P, 2, NH, 32])
            layer_norm(core, core.x, core.xn, core.xnT, loads=[
                (w[:, i, :, :], ktiles(d["L2_ffn_w" + n])) for i, n in enumerate("qkvo")] + [
                (gain[:, :], d["L2_ffn_ln_g"]), (shift[:, :], d["L2_ffn_ln_b"]), (mask8[:, :], d["c_mask8"])])
            layer_norm(core, core.xn, xa_tok, xaT, gain=gain, shift=shift)
            with phase(core) as (block,):
                @block.gpsimd
                def _(pool):
                    nc.gpsimd.memset(vz[:, :, :, :], 0.0)
            with nc.Fori(0, B) as b:
                with phase(core, "sliced", "product", "q_done") as (block, sliced, product, q_done):
                    @block.tensor
                    def _(pe):
                        pe.wait_ge(sliced, 1)
                        for i in range(2):
                            for m in range(CT):
                                for kk in range(CT):
                                    mm = nc.tensor.matmul(ps[:, 2 * i + m, 0:T], w[:, i, kk, m * P:(m + 1) * P],
                                                          xb[:, kk, :], start=kk == 0, stop=kk == CT - 1)
                                mm.then_inc(product, 1)
                        for t in range(2):
                            for kk in range(CT):
                                mm = nc.tensor.matmul(ps[:, 4 + t, 0:C], xb[:, kk, t * P:(t + 1) * P], w[:, 2, kk, :],
                                                      start=kk == 0, stop=kk == CT - 1)
                            mm.then_inc(product, 1)

                    @block.scalar
                    def _(act):
                        for m in range(CT):
                            act.wait_ge(product, m + 1)
                            nc.scalar.mul(q[:, m, :], ps[:, m, 0:T], HD ** -0.5).then_inc(q_done, 1)
                        for m in range(CT):
                            act.wait_ge(product, CT + m + 1)
                            nc.scalar.copy(k[:, m, :], ps[:, 2 + m, 0:T])

                    @block.vector
                    def _(dve):
                        nc.vector.tensor_copy(xb[:, :, :], xaT[:, :, bass.ds(b * T, T)]).then_inc(sliced, 1)
                        for h in range(NH):
                            dve.wait_ge(q_done, h // 16 + 1)
                            nc.vector.tensor_scalar(qz[:, h, :], q[:, h // 16, :], mask8[:, h % 16:h % 16 + 1], None,
                                                    ALU.mult)
                        for t in range(2):
                            dve.wait_ge(product, 2 * CT + t + 1)
                            src = ps[:, 4 + t, 0:C].rearrange("p (g j c) -> p g j c", j=4, c=HD)
                            dst = vz[:, t, :, :].rearrange("p (g j) c -> p g j c", j=4)
                            for j in range(4):
                                nc.vector.tensor_copy(dst[:, :, j, HD * j:HD * (j + 1)], src[:, :, j, :])

                def score(h, bank):
                    for t in range(2):
                        mm = nc.tensor.matmul(bank[:, t * T:(t + 1) * T], qz[:, h, t * P:(t + 1) * P], k[:, h // 16, :],
                                              start=True, stop=True)
                    return mm

                def weigh(h, probs, out):
                    g = (h % 16) // 4
                    for t in range(2):
                        mm = nc.tensor.matmul(out[32 * g:32 * g + 32, 0:T], vz[:, t, h, :], probs[:, t * T:(t + 1) * T],
                                              start=h % 4 == 0 and t == 0, stop=h % 4 == 3 and t == 1,
                                              skip_group_check=True, tile_position=(0, 32 * g))
                    return mm

                attend(core, NH, [(0, T), (T, T)], score, [(0, 0), (P, T), (T, P), (T + P, T + P)], weigh, 16,
                       lambda g: oT[:, g, bass.ds(b * T, T)])
            linear_features(core, w[:, 3, :, :], oT, CT, CT, lambda m, n, qq: nc.vector.tensor_tensor(
                xfT[:, m, n * BANK:(n + 1) * BANK], qq, core.xnT[:, m, n * BANK:(n + 1) * BANK], ALU.add), "vector")
        w1 = [sb([P, CT, FD]) for _ in range(2)]
        w2 = [sb([P, FT, C]) for _ in range(2)]
        b1, b2 = sb([P, E, FT]), sb([P, E // 2, C])
        h = sb([P, FT, 2, 2, TPE])
        tmp = sb([P, 2, C])
        load(core, [(w1[0][:, :, :], ktiles(d["L2_ffn_w1"][0])), (b1[:, :, :], d["L2_ffn_b1"]),
                    (b2[:, :, :], d["L2_ffn_b2"]), (w2[0][:, :, :], ktiles(d["L2_ffn_w2"][0]))])
        with nc.Fori(0, E // 2) as a:
            with phase(core, "w1_b", "w2_b", "refilled", "up_ready", "h_ready", "down_ready", "biased") as (
                    block, w1_b, w2_b, refilled, up_ready, h_ready, down_ready, biased):
                @block.sync
                def _(sp):
                    sp.dma_start(w1[1][:, :, :], ktiles(d["L2_ffn_w1"][2 * a + 1])).then_inc(w1_b, 16)
                    sp.dma_start(w2[1][:, :, :], ktiles(d["L2_ffn_w2"][2 * a + 1])).then_inc(w2_b, 16)
                    sp.wait_ge(up_ready, FT)
                    sp.dma_start(w1[0][:, :, :], ktiles(d["L2_ffn_w1"][2 * a + 2])).then_inc(refilled, 16)
                    sp.wait_ge(down_ready, 2)
                    sp.dma_start(w2[0][:, :, :], ktiles(d["L2_ffn_w2"][2 * a + 2])).then_inc(refilled, 16)
                    sp.wait_ge(refilled, 32)

                @block.tensor
                def _(pe):
                    for i in range(2):
                        if i == 1:
                            pe.wait_ge(w1_b, 16)
                        for f in range(FT):
                            j = FT * i + f
                            if j >= 4:
                                pe.wait_ge(h_ready, j - 3)
                            for k2 in range(CT):
                                x = xfT[:, k2, :].rearrange("p (mb t) -> p mb t", mb=2)
                                mm = nc.tensor.matmul(ps[:, j % 4, 0:2 * TPE].rearrange("p (mb t) -> p mb t", mb=2),
                                                      w1[i][:, k2, f * P:(f + 1) * P],
                                                      x[:, :, bass.ds((2 * a + i) * TPE, TPE)],
                                                      start=k2 == 0, stop=k2 == CT - 1)
                            mm.then_inc(up_ready, 1)
                        pe.wait_ge(h_ready, FT * (i + 1))
                        if i == 1:
                            pe.wait_ge(w2_b, 16)
                        for mb in range(2):
                            for f in range(FT):
                                mm = nc.tensor.matmul(ps[TPE * i:TPE * (i + 1), 4 + mb, 0:C], h[:, f, i, mb, :],
                                                      w2[i][:, f, :], start=f == 0, stop=f == FT - 1)
                            mm.then_inc(down_ready, 1)

                @block.scalar
                def _(act):
                    for i in range(2):
                        for f in range(FT):
                            j = FT * i + f
                            act.wait_ge(up_ready, j + 1)
                            nc.scalar.activation(h[:, f, i, :, :],
                                                 ps[:, j % 4, 0:2 * TPE].rearrange("p (mb t) -> p mb t", mb=2),
                                                 ACT.Gelu, bias=b1[:, bass.ds(2 * a + i, 1), f]).then_inc(h_ready, 1)

                @block.vector
                def _(dve):
                    for mb in range(2):
                        dve.wait_ge(down_ready, 2 + mb + 1)
                        nc.vector.tensor_tensor(tmp[:, mb:mb + 1, :], ps[:, 4 + mb:5 + mb, 0:C],
                                                b2[:, bass.ds(a, 1), :], ALU.add).then_inc(biased, 1)
                    for mb in range(2):
                        dve.wait_ge(biased, mb + 1)
                        x = core.x[:, bass.ds(a + 4 * mb, 1), :]
                        nc.vector.tensor_tensor(x, tmp[:, mb:mb + 1, :], x, ALU.add)

K_SLOTS = (0, 0, 1, 1, 0, 2)
Q_SLOTS = (0, 1, 0, 1, 2, 0)
SLOTS = len(K_SLOTS)
SHIFT = SLOTS * D
ROWS = SHIFT + 1
VW = D + 1
PART = 32


def part_columns(dest, c, f):
    return dest[:, f * P:(f + 1) * P, c * KC:(c + 1) * KC].rearrange("s p n -> p s n")


def project_first(core, wq, queries, q_rope, scale, wk, wv, context, keys, v, k_rope):
    nc, ps = core.nc, core.ps
    rope = q_rope is not None
    with ExitStack() as c_:
        sb = core.allocator(c_)
        rest, parts, ctx = sb([P, 2, KC]), sb([P, 2, 3, KC], BF16), sb([P, 2, CT, KC])
        if rope:
            turn, eps = q_rope[2:]
            tab = sb([P, 2, 2, KC])
            raw, square, root, mix, turned_ = (sb([P, 2, KC]) for _ in range(5))
        names = ["ctx_a", "ctx_b", "tab_a", "tab_b", "product", "high_done", "rest_done", "middle_done", "low_done",
                 "v_product", "v_done", "copied", "summed", "root_done", "cos_done", "sin_done", "mixed", "inverted",
                 "normed", "stored_a", "stored_b"]
        with phase(core, *names) as (block, ctx_a, ctx_b, tab_a, tab_b, product, high_done, rest_done, middle_done,
                                     low_done, v_product, v_done, copied, summed, root_done, cos_done, sin_done,
                                     mixed, inverted, normed, stored_a, stored_b):
            stored, ctx_in, tab_in = (stored_a, stored_b), (ctx_a, ctx_b), (tab_a, tab_b)
            QC, C_ALL = N // KC, N // KC + S // KC
            units, VU = CT * C_ALL, CT * QC
            is_key = lambda c: c >= QC
            x_of = lambda c: ctx[:, c % 2] if is_key(c) else core.xnT[:, :, c * KC:(c + 1) * KC]
            dest = lambda i: part_columns(keys, i // CT - QC, i % CT) if is_key(i // CT) else part_columns(
                queries, i // CT, i % CT)
            scaled = lambda i: 1.0 if is_key(i // CT) else scale
            rope_of = lambda i: k_rope if is_key(i // CT) else q_rope

            @block.sync
            def _(sp):
                for c in range(C_ALL + 2):
                    if c < C_ALL and is_key(c):
                        if c >= QC + 2:
                            sp.wait_ge(product, CT * (c - 1))
                            sp.wait_ge(v_product, CT * (c - 1) - VU)
                        sp.dma_start(ctx[:, c % 2, :, :], context(c - QC)).then_inc(ctx_in[c % 2], 16)
                    if c < C_ALL and rope:
                        if c >= 2:
                            sp.wait_ge(sin_done, CT * (c - 1))
                            sp.wait_ge(cos_done, CT * (c - 1))
                        table = k_rope[1](c - QC) if is_key(c) else q_rope[1](c)
                        sp.dma_start(tab[:, c % 2, :, :], table).then_inc(tab_in[c % 2], 16)
                    if c >= 2:
                        for f in range(CT):
                            i = CT * (c - 2) + f
                            sp.wait_ge(low_done, i + 1)
                            sp.dma_start(dest(i), parts[:, i % 2, :, :]).then_inc(stored[i % 2], 16)
                for slot in range(2):
                    sp.wait_ge(stored[slot], 16 * (units // 2))

            @block.tensor
            def _(pe):
                def heads_of(i):
                    pe.wait_ge(copied, i + 1)
                    if i >= 2:
                        pe.wait_ge(root_done, i - 1)
                        pe.wait_ge(sin_done, i - 1)
                    b = 2 if i % 2 == 0 else 6
                    nc.tensor.matmul(ps[:, b, :], core.block16[:, :], square[:, i % 2, :], start=True, stop=True)
                    nc.tensor.matmul(ps[:, b + 1, :], turn, raw[:, i % 2, :], start=True, stop=True).then_inc(summed, 1)

                for i in range(units):
                    c, f = i // CT, i % CT
                    w = wk if is_key(c) else wq
                    if is_key(c) and f == 0:
                        pe.wait_ge(ctx_in[c % 2], 16 * ((c - QC) // 2 + 1))
                    if i >= 2:
                        pe.wait_ge(copied if rope else rest_done, i - 1)
                    for k in range(CT):
                        mm = nc.tensor.matmul(ps[:, i % 2, :], w[:, k, f * P:(f + 1) * P], x_of(c)[:, k, :],
                                              start=k == 0, stop=k == CT - 1)
                    mm.then_inc(product, 1)
                    if i >= VU:
                        if i >= VU + 2:
                            pe.wait_ge(v_done, i - VU - 1)
                        for t in range(2):
                            for k in range(CT):
                                mm = nc.tensor.matmul(ps[:, 4 + i % 2, t * C:(t + 1) * C],
                                                      x_of(c)[:, k, (2 * f + t) * P:(2 * f + t + 1) * P],
                                                      wv[:, k, :], start=k == 0, stop=k == CT - 1)
                        mm.then_inc(v_product, 1)
                    if rope and i >= 1:
                        heads_of(i - 1)
                if rope:
                    heads_of(units - 1)

            out = lambda i, part: parts[:, i % 2, part, :]
            whole = (lambda i: mix[:, i % 2, :]) if rope else (lambda i: ps[:, i % 2, :])

            @block.scalar
            def _(act):
                def high(i):
                    act.wait_ge(normed if rope else product, i + 1)
                    if i >= 2:
                        act.wait_ge(stored[i % 2], 16 * (i // 2))
                    nc.scalar.mul(out(i, 0), whole(i), scaled(i)).then_inc(high_done, 1)

                for i in range(units):
                    if rope:
                        act.wait_ge(product, i + 1)
                        if i >= 2:
                            act.wait_ge(summed, i - 1)
                            act.wait_ge(cos_done, i - 1)
                        nc.scalar.activation(raw[:, i % 2, :], ps[:, i % 2, :], ACT.Copy, scale=rope_of(i)[0])
                        nc.scalar.activation(square[:, i % 2, :], ps[:, i % 2, :], ACT.Square).then_inc(copied, 1)
                    else:
                        high(i)
                    if i >= VU:
                        j = i - VU
                        act.wait_ge(v_product, j + 1)
                        nc.scalar.copy(v[:, 2 * j:2 * j + 2, :, 0:D],
                                       ps[:, 4 + i % 2, :].rearrange("p (t h c) -> p t h c", t=2, h=H)
                                       ).then_inc(v_done, 1)
                    if rope:
                        act.wait_ge(summed, i + 1)
                        if i >= 2:
                            act.wait_ge(normed, i - 1)
                        nc.scalar.activation(root[:, i % 2, :], ps[:, 2 if i % 2 == 0 else 6, :], ACT.Sqrt,
                                             bias=eps, scale=1.0 / D).then_inc(root_done, 1)
                        if i >= 1:
                            high(i - 1)
                if rope:
                    high(units - 1)

            @block.vector
            def _(dve):
                def rotate(i):
                    c, s = i // CT % 2, i % 2
                    dve.wait_ge(tab_in[c], 16 * (i // CT // 2 + 1))
                    dve.wait_ge(copied, i + 1)
                    if i >= 2:
                        dve.wait_ge(rest_done, i - 1)
                        dve.wait_ge(high_done, i - 1)
                    nc.vector.tensor_tensor(mix[:, s, :], raw[:, s, :], tab[:, c, 0, :], ALU.mult).then_inc(cos_done, 1)
                    dve.wait_ge(summed, i + 1)
                    nc.vector.tensor_tensor(turned_[:, s, :], ps[:, 3 if s == 0 else 7, :], tab[:, c, 1, :],
                                            ALU.mult).then_inc(sin_done, 1)
                    dve.wait_ge(sin_done, i + 1)
                    dve.wait_ge(cos_done, i + 1)
                    nc.vector.tensor_tensor(mix[:, s, :], mix[:, s, :], turned_[:, s, :], ALU.add).then_inc(mixed, 1)
                    dve.wait_ge(root_done, i + 1)
                    nc.vector.reciprocal(root[:, s, :], root[:, s, :]).then_inc(inverted, 1)

                def split(i):
                    dve.wait_ge(high_done, i + 1)
                    if i >= 2:
                        dve.wait_ge(low_done, i - 1)
                    nc.vector.scalar_tensor_tensor(out=rest[:, i % 2, :], in0=whole(i), scalar=scaled(i), in1=out(i, 0),
                                                   op0=ALU.mult, op1=ALU.subtract).then_inc(rest_done, 1)

                for i in range(units):
                    if rope:
                        rotate(i)
                        if i >= 1:
                            split(i - 1)
                    else:
                        split(i)
                if rope:
                    split(units - 1)

            @block.gpsimd
            def _(pool):
                def norm(i):
                    pool.wait_ge(mixed, i + 1)
                    pool.wait_ge(inverted, i + 1)
                    nc.gpsimd.tensor_tensor(mix[:, i % 2, :], mix[:, i % 2, :], root[:, i % 2, :],
                                            ALU.mult).then_inc(normed, 1)

                def low(i):
                    pool.wait_ge(rest_done, i + 1)
                    nc.gpsimd.tensor_copy(out(i, 1), rest[:, i % 2, :]).then_inc(middle_done, 1)
                    pool.wait_ge(middle_done, i + 1)
                    nc.gpsimd.tensor_tensor(out(i, 2), rest[:, i % 2, :], out(i, 1), ALU.subtract).then_inc(low_done, 1)

                for i in range(units):
                    if rope:
                        norm(i)
                        if i >= 1:
                            low(i - 1)
                    else:
                        low(i)
                if rope:
                    low(units - 1)


class NextKeys:

    NAMES = ("ctx_a", "ctx_b", "tab_a", "tab_b", "product", "copied", "summed", "turned", "root_done", "cos_done",
             "sin_done", "mixed", "inverted", "normed", "high_done", "rest_done", "middle_done", "low_done", "stored_a",
             "stored_b", "v_product", "v_done")

    def __init__(self, core, sb, sems, w, w_v, v, source, dest, rope, spare, v_bank):
        self.core, self.w, self.w_v, self.v, self.source, self.dest = core, w, w_v, v, source, dest
        self.rope, self.out, self.v_out = rope, core.ps[:, spare, :], core.ps[:, v_bank, :]
        self.ctx, self.rest, self.parts = sb([P, 2, CT, KC]), sb([P, 2, KC]), sb([P, 2, 3, KC], BF16)
        if rope:
            self.norm_w, self.table, self.turn, self.eps = rope
            self.tab = sb([P, 2, 2, KC])
            self.raw, self.square, self.root, self.mix, self.spun = (sb([P, 2, KC]) for _ in range(5))
        (ctx_a, ctx_b, tab_a, tab_b, self.product, self.copied, self.summed, self.turned, self.root_done,
         self.cos_done, self.sin_done, self.mixed, self.inverted, self.normed, self.high_done, self.rest_done,
         self.middle_done, self.low_done, stored_a, stored_b, self.v_product, self.v_done) = sems
        self.ctx_in, self.tab_in, self.stored = (ctx_a, ctx_b), (tab_a, tab_b), (stored_a, stored_b)
        self.chunks, self.units = S // KC, CT * S // KC

    def load_chunk(self, sp, c):
        if c >= 2:
            sp.wait_ge(self.product, CT * (c - 1))
            sp.wait_ge(self.v_product, CT * (c - 1))
        sp.dma_start(self.ctx[:, c % 2, :, :], self.source(c)).then_inc(self.ctx_in[c % 2], 16)
        if self.rope:
            if c >= 2:
                sp.wait_ge(self.cos_done, CT * (c - 1))
                sp.wait_ge(self.sin_done, CT * (c - 1))
            sp.dma_start(self.tab[:, c % 2, :, :], self.table(c)).then_inc(self.tab_in[c % 2], 16)

    def store(self, sp, u):
        sp.wait_ge(self.low_done, u + 1)
        sp.dma_start(part_columns(self.dest, u // CT, u % CT), self.parts[:, u % 2, :, :]).then_inc(
            self.stored[u % 2], 16)

    def all_stored(self, sp):
        for slot in range(2):
            sp.wait_ge(self.stored[slot], 16 * (self.units // 2))

    def multiply(self, pe, u, k):
        c, f = u // CT, u % CT
        pe.wait_ge(self.ctx_in[c % 2], 16 * (c // 2 + 1))
        mm = self.core.nc.tensor.matmul(self.out, self.w[:, k, f * P:(f + 1) * P], self.ctx[:, c % 2, k, :],
                                        start=k == 0, stop=k == CT - 1)
        if k == CT - 1:
            mm.then_inc(self.product, 1)

    def sum_heads(self, pe, u):
        pe.wait_ge(self.copied, u + 1)
        self.core.nc.tensor.matmul(self.out, self.core.block16[:, :], self.square[:, u % 2, :], start=True,
                                   stop=True).then_inc(self.summed, 1)

    def turn_pairs(self, pe, u):
        pe.wait_ge(self.root_done, u + 1)
        self.core.nc.tensor.matmul(self.out, self.turn, self.raw[:, u % 2, :], start=True, stop=True).then_inc(
            self.turned, 1)

    def product_used(self, pe, u):
        pe.wait_ge(self.sin_done if self.rope else self.rest_done, u + 1)

    def multiply_values(self, pe, u, t):
        c, f, nc = u // CT, u % CT, self.core.nc
        for k in range(CT):
            mm = nc.tensor.matmul(self.v_out[:, t * C:(t + 1) * C],
                                  self.ctx[:, c % 2, k, (2 * f + t) * P:(2 * f + t + 1) * P], self.w_v[:, k, :],
                                  start=k == 0, stop=k == CT - 1)
        if t == 1:
            mm.then_inc(self.v_product, 1)

    def copy_product(self, act, u):
        nc, s = self.core.nc, u % 2
        act.wait_ge(self.product, u + 1)
        if u >= 2:
            act.wait_ge(self.summed, u - 1)
            act.wait_ge(self.turned, u - 1)
            act.wait_ge(self.cos_done, u - 1)
        nc.scalar.activation(self.raw[:, s, :], self.out, ACT.Copy, scale=self.norm_w)
        nc.scalar.activation(self.square[:, s, :], self.out, ACT.Square).then_inc(self.copied, 1)

    def take_root(self, act, u):
        act.wait_ge(self.summed, u + 1)
        if u >= 2:
            act.wait_ge(self.normed, u - 1)
        self.core.nc.scalar.activation(self.root[:, u % 2, :], self.out, ACT.Sqrt, bias=self.eps,
                                       scale=1.0 / D).then_inc(self.root_done, 1)

    def whole(self, u):
        return self.mix[:, u % 2, :] if self.rope else self.out

    def high(self, act, u):
        act.wait_ge(self.normed if self.rope else self.product, u + 1)
        if u >= 2:
            act.wait_ge(self.stored[u % 2], 16 * (u // 2))
        self.core.nc.scalar.copy(self.parts[:, u % 2, 0, :], self.whole(u)).then_inc(self.high_done, 1)

    def copy_values(self, act, u):
        act.wait_ge(self.v_product, u + 1)
        self.core.nc.scalar.copy(self.v[:, 2 * u:2 * u + 2, :, 0:D],
                                 self.v_out.rearrange("p (t h c) -> p t h c", t=2, h=H)).then_inc(self.v_done, 1)

    def scale_sin(self, dve, u):
        dve.wait_ge(self.turned, u + 1)
        if u < CT:
            dve.wait_ge(self.tab_in[0], 16)
        if u >= 2:
            dve.wait_ge(self.mixed, u - 1)
        self.core.nc.vector.tensor_tensor(self.spun[:, u % 2, :], self.out, self.tab[:, u // CT % 2, 1, :],
                                          ALU.mult).then_inc(self.sin_done, 1)

    def invert(self, dve, u, quarter):
        dve.wait_ge(self.root_done, u + 1)
        part = self.root[:, u % 2, quarter * P:(quarter + 1) * P]
        self.core.nc.vector.reciprocal(part, part).then_inc(self.inverted, 1)

    def take_rest(self, dve, u):
        dve.wait_ge(self.high_done, u + 1)
        if u >= 2:
            dve.wait_ge(self.low_done, u - 1)
        self.core.nc.vector.tensor_tensor(self.rest[:, u % 2, :], self.whole(u), self.parts[:, u % 2, 0, :],
                                          ALU.subtract).then_inc(self.rest_done, 1)

    def rotate(self, pool, u):
        nc, c, s = self.core.nc, u // CT, u % 2
        pool.wait_ge(self.tab_in[c % 2], 16 * (c // 2 + 1))
        pool.wait_ge(self.copied, u + 1)
        if u >= 2:
            pool.wait_ge(self.rest_done, u - 1)
        nc.gpsimd.tensor_tensor(self.mix[:, s, :], self.raw[:, s, :], self.tab[:, c % 2, 0, :], ALU.mult).then_inc(
            self.cos_done, 1)
        pool.wait_ge(self.cos_done, u + 1)
        pool.wait_ge(self.sin_done, u + 1)
        nc.gpsimd.tensor_tensor(self.mix[:, s, :], self.mix[:, s, :], self.spun[:, s, :], ALU.add).then_inc(
            self.mixed, 1)
        pool.wait_ge(self.mixed, u + 1)
        pool.wait_ge(self.inverted, KC // P * (u + 1))
        nc.gpsimd.tensor_tensor(self.mix[:, s, :], self.mix[:, s, :], self.root[:, s, :], ALU.mult).then_inc(
            self.normed, 1)

    def low_parts(self, pool, u):
        nc, s = self.core.nc, u % 2
        pool.wait_ge(self.rest_done, u + 1)
        nc.gpsimd.tensor_copy(self.parts[:, s, 1, :], self.rest[:, s, :]).then_inc(self.middle_done, 1)
        pool.wait_ge(self.middle_done, u + 1)
        nc.gpsimd.tensor_tensor(self.parts[:, s, 2, :], self.rest[:, s, :], self.parts[:, s, 1, :],
                                ALU.subtract).then_inc(self.low_done, 1)


def load_queries(engine, queries, qstack, landed):
    for s, part in enumerate(Q_SLOTS):
        engine.dma_start(qstack[s * D:(s + 1) * D, :, :], queries[part].rearrange("(h c) n -> c h n", h=H)).then_inc(
            landed, 16)


def load_keys(sp, keys, kstack, h, landed):
    for s, part in enumerate(K_SLOTS):
        sp.dma_start(kstack[s * D:(s + 1) * D, h % 3, :], keys[part, h * D:(h + 1) * D, :]).then_inc(landed, 16)


def attend_context(core, queries, keys, v, qstack, kstack, bias, att, coming=None):
    nc, ps = core.nc, core.ps
    QT = T // P
    NK = S // KC
    GU = QT * NK
    EU = KT // 4
    rope = coming is not None and coming["rope"] is not None
    GUARDS, SHIFT_AT = ((2, 3, 3, 2, 2, 2, 2, 0), 7) if rope else ((3, 3, 3, 3, 2, 2, 0, 0), 6)
    V_AT = 5 if rope else 4
    units_of = [range(sum(GUARDS[:e]), sum(GUARDS[:e + 1])) for e in range(EU)]
    OUT, SPARE = 6, 7
    with ExitStack() as c:
        sb = core.allocator(c)
        p = sb([P, 3, 4 * T])
        gm, neg = sb([P, 2, QT, NK]), sb([P, 2, QT])
        fold, osum, inv = core.fold, sb([P, 2, T]), sb([P, 2, QT])
        with phase(core, "q_in", "k_a", "k_b", "k_c", "scored", "max_done", "neg_done", "neg_row", "shift_done", "qk",
                   "exp_done", "pv", "taken", "out_ready", "inv_done", "out_done", "cleared",
                   *(NextKeys.NAMES if coming else ())) as (
                block, q_in, k_a, k_b, k_c, scored, max_done, neg_done, neg_row, shift_done, qk, exp_done, pv,
                taken, out_ready, inv_done, out_done, cleared, *next_sems):
            k_in = (k_a, k_b, k_c)
            new = NextKeys(core, sb, next_sems, spare=SPARE, v_bank=SPARE, **coming) if coming else None

            @block.sync
            def _(sp):
                load_keys(sp, keys, kstack, 0, k_in[0])
                if new:
                    new.load_chunk(sp, 0)
                load_keys(sp, keys, kstack, 1, k_in[1])
                if new:
                    new.load_chunk(sp, 1)
                for h in range(H):
                    if h + 2 < H:
                        if h >= 1:
                            sp.wait_ge(qk, EU * h)
                        load_keys(sp, keys, kstack, h + 2, k_in[(h + 2) % 3])
                    if new:
                        if (h + 1) % CT == 0 and (h + 1) // CT + 1 < new.chunks:
                            new.load_chunk(sp, (h + 1) // CT + 1)
                        new.store(sp, h)
                if new:
                    new.all_stored(sp)

            @block.tensor
            def _(pe):
                def guard(h, g):
                    t, kc = g // NK, g % NK
                    if g == 0:
                        pe.wait_ge(k_in[h % 3], 16 * SLOTS * (h // 3 + 1))
                        if h == 0:
                            pe.wait_ge(q_in, 16 * SLOTS)
                        if h >= 1:
                            pe.wait_ge(shift_done, h)
                    if g >= 2:
                        pe.wait_ge(max_done, GU * h + g - 1)
                    biased = bias is not None and kc == 0
                    mm = nc.tensor.matmul(ps[:, 4 + g % 2, :], qstack[0:SHIFT, h, t * P:(t + 1) * P],
                                          kstack[0:SHIFT, h % 3, kc * KC:(kc + 1) * KC], start=True, stop=True,
                                          skip_group_check=biased)
                    if biased:
                        for k in range(t + 2):
                            mm = nc.tensor.matmul(ps[:, 4 + g % 2, k * P:(k + 1) * P], core.identb[:, :],
                                                  bias[1][:, k - t + 1, h, :], start=False, stop=True,
                                                  skip_group_check=True)
                    mm.then_inc(scored, 1)

                def shift(h):
                    pe.wait_ge(neg_done, h + 1)
                    for t in range(QT):
                        mm = nc.tensor.matmul(ps[SHIFT:ROWS, 4, t * P:(t + 1) * P], neg[:, h % 2, t:t + 1],
                                              core.ident[:, :], start=True, stop=True, tile_position=(0, SHIFT))
                    mm.then_inc(neg_row, 1)

                def scores(i):
                    h, e = i // EU, i % EU
                    if e == 0:
                        pe.wait_ge(shift_done, h + 1)
                    if i >= 2:
                        pe.wait_ge(exp_done, i - 1)
                    for j in range(4):
                        kt = 4 * e + j
                        out = ps[:, 2 * (i % 2) + j // 2, (j % 2) * T:(j % 2 + 1) * T]
                        near = [t for t in range(QT) if kt - t <= 1] if bias is not None else []
                        mm = nc.tensor.matmul(out, kstack[:, h % 3, kt * P:(kt + 1) * P], qstack[:, h, :],
                                              start=True, stop=True, skip_group_check=bool(near))
                        for t in near:
                            mm = nc.tensor.matmul(out[:, t * P:(t + 1) * P], core.ident[:, :],
                                                  bias[0][:, kt - t + 1, h, :], start=False, stop=True,
                                                  skip_group_check=True)
                    mm.then_inc(qk, 1)

                def weigh(i):
                    h, e = i // EU, i % EU
                    pe.wait_ge(exp_done, i + 1)
                    if i == 0:
                        pe.wait_ge(cleared, 1)
                    if e == 0 and h >= 1:
                        pe.wait_ge(taken, h)
                    for j in range(4):
                        mm = nc.tensor.matmul(ps[PART * j:PART * j + VW, OUT, 0:T], v[:, 4 * e + j, h, :],
                                              p[:, i % 3, j * T:(j + 1) * T], start=e == 0, stop=e == EU - 1,
                                              tile_position=(0, PART * j))
                    mm.then_inc(pv, 1)

                def output(h):
                    pe.wait_ge(taken, h + 1)
                    if new:
                        pe.wait_ge(new.v_done, min(h + 3, H))
                    if h >= 1:
                        pe.wait_ge(out_done, h)
                    for t in range(QT):
                        mm = nc.tensor.matmul(ps[:, SPARE, t * VW:(t + 1) * VW], osum[:, h % 2, t * P:(t + 1) * P],
                                              fold[:, 0:VW], start=True, stop=True)
                    mm.then_inc(out_ready, 1)

                for g in range(0, GU, 2):
                    guard(0, g)
                    guard(0, g + 1)
                    if new and g == 0:
                        for k in range(CT):
                            new.multiply(pe, 0, k)
                    if new and rope and g == 2:
                        new.sum_heads(pe, 0)
                    if new and rope and g == 4:
                        new.turn_pairs(pe, 0)
                    if new and g in (8, 10):
                        new.product_used(pe, 0)
                        new.multiply_values(pe, 0, g // 2 - 4)
                shift(0)
                for i in range(H * EU):
                    h, e = i // EU, i % EU
                    guards = list(units_of[e]) if h + 1 < H else []
                    for g in guards[0:1]:
                        guard(h + 1, g)
                    scores(i)
                    for g in guards[1:2]:
                        guard(h + 1, g)
                    if i >= 1:
                        weigh(i - 1)
                    for g in guards[2:]:
                        guard(h + 1, g)
                    u = h + 1
                    if new and u < H and e in (0, 1):
                        if e == 0:
                            pe.wait_ge(new.v_done, u)
                        if e == 0 and h >= 2:
                            pe.wait_ge(out_done, h - 1)
                        new.multiply(pe, u, e)
                    if new and rope and u < H and e == 2:
                        new.sum_heads(pe, u)
                    if new and rope and u < H and e == 3:
                        new.turn_pairs(pe, u)
                    if new and u < H and V_AT <= e <= V_AT + 1:
                        new.product_used(pe, u)
                        new.multiply_values(pe, u, e - V_AT)
                    if e == SHIFT_AT:
                        if h + 1 < H:
                            shift(h + 1)
                        if h >= 1:
                            output(h - 1)
                weigh(H * EU - 1)
                output(H - 1)

            @block.vector
            def _(dve):
                nc.vector.memset(ps[:, OUT, 0:T], 0.0).then_inc(cleared, 1)

                def maxima(h, g):
                    dve.wait_ge(scored, GU * h + g + 1)
                    nc.vector.tensor_reduce(gm[:, h % 2, g // NK, g % NK:g % NK + 1], ps[:, 4 + g % 2, :], AX.X,
                                            ALU.max).then_inc(max_done, 1)

                def negate(h):
                    dve.wait_ge(max_done, GU * (h + 1))
                    if h >= 2:
                        dve.wait_ge(neg_row, h - 1)
                    nc.vector.tensor_reduce(neg[:, h % 2, :], gm[:, h % 2, :, :], AX.X, ALU.max,
                                            negate=True).then_inc(neg_done, 1)

                def place_shift(h):
                    dve.wait_ge(neg_row, h + 1)
                    if h == 0:
                        dve.wait_ge(q_in, 16 * SLOTS)
                    nc.vector.tensor_copy(qstack[SHIFT:ROWS, h, :], ps[SHIFT:ROWS, 4, 0:T]).then_inc(shift_done, 1)

                def finish(h):
                    dve.wait_ge(out_ready, h + 1)
                    o = ps[:, SPARE, 0:QT * VW].rearrange("p (t c) -> p t c", t=QT)
                    nc.vector.reciprocal(inv[:, h % 2, :], o[:, :, D]).then_inc(inv_done, 1)
                    dve.wait_ge(inv_done, h + 1)
                    for t in range(QT):
                        last = nc.vector.tensor_scalar(att[:, t, h * D:(h + 1) * D], o[:, t, 0:D],
                                                       inv[:, h % 2, t:t + 1], None, ALU.mult)
                    last.then_inc(out_done, 1)

                for g in range(GU):
                    maxima(0, g)
                    if new and not rope and g == 5:
                        new.take_rest(dve, 0)
                    if new and rope and g == 7:
                        new.scale_sin(dve, 0)
                negate(0)
                place_shift(0)
                if new and rope:
                    for quarter in range(3):
                        new.invert(dve, 0, quarter)
                for i in range(H * EU):
                    h, e = i // EU, i % EU
                    if h + 1 < H:
                        for g in units_of[e]:
                            maxima(h + 1, g)
                    u = h + 1
                    if new and not rope and u < H and e == 2:
                        new.take_rest(dve, u)
                    if new and rope and e == 3:
                        new.take_rest(dve, u - 1)
                    if new and rope and u < H and e == 4:
                        new.scale_sin(dve, u)
                    if e == SHIFT_AT and h + 1 < H:
                        negate(h + 1)
                        place_shift(h + 1)
                    if new and rope and u < H and e >= 5:
                        new.invert(dve, u, e - 5)
                    if new and rope and e == 0:
                        new.invert(dve, u - 1, 3)
                    if e == 7 and h >= 1:
                        finish(h - 1)
                finish(H - 1)

            @block.scalar
            def _(act):
                load_queries(act, queries, qstack, q_in)

                def take(h):
                    act.wait_ge(pv, EU * (h + 1))
                    if h >= 2:
                        act.wait_ge(out_ready, h - 1)
                    nc.scalar.copy(osum[:, h % 2, :], ps[:, OUT, 0:T]).then_inc(taken, 1)

                if new:
                    if rope:
                        new.copy_product(act, 0)
                        new.take_root(act, 0)
                    else:
                        new.high(act, 0)
                    new.copy_values(act, 0)
                for i in range(H * EU):
                    h, e = i // EU, i % EU
                    u = h + 1
                    if new and not rope and u < H and e == 2:
                        new.high(act, u)
                    if new and not rope and u < H and e == 6:
                        new.copy_values(act, u)
                    if new and rope and u < H and e == 2:
                        new.copy_product(act, u)
                    if new and rope and u < H and e == 3:
                        new.take_root(act, u)
                    act.wait_ge(qk, i + 1)
                    if i >= 3:
                        act.wait_ge(pv, i - 2)
                    nc.scalar.activation(p[:, i % 3, :].rearrange("p (b t) -> p b t", b=2),
                                         ps[:, 2 * (i % 2):2 * (i % 2) + 2, :], ACT.Exp).then_inc(exp_done, 1)
                    if e == 0 and h >= 1:
                        take(h - 1)
                    if new and rope and e == 2:
                        new.high(act, u - 1)
                    if new and rope and u < H and e == 6:
                        new.copy_values(act, u)
                take(H - 1)

            if new:
                @block.gpsimd
                def _(pool):
                    for u in range(new.units):
                        if rope:
                            new.rotate(pool, u)
                        new.low_parts(pool, u)


def output_product(core, att, attT, wo, b, moved=None):
    nc, ps = core.nc, core.ps
    QT = T // P
    CUT, CUT2 = KT // 2, KT * 13 // 16
    with phase(core, "turned", "copied", "ready") as (block, turned, copied, ready):
        @block.tensor
        def _(pe):
            for t in range(QT):
                for k in range(CT):
                    mm = nc.tensor.transpose(ps[:, k, t * P:(t + 1) * P], att[:, t, k * P:(k + 1) * P],
                                             core.ident[:, :])
            mm.then_inc(turned, 1)
            pe.wait_ge(copied, 1)
            for t in range(QT):
                for k in range(CT):
                    mm = nc.tensor.matmul(ps[:, 2 + t, 0:C], attT[:, k, t * P:(t + 1) * P], wo[:, k, :],
                                          start=k == 0, stop=k == CT - 1)
                mm.then_inc(ready, 1)

        @block.scalar
        def _(act):
            act.wait_ge(turned, 1)
            nc.scalar.copy(attT[:, :, :], ps[:, 0:CT, 0:T]).then_inc(copied, 1)
            if moved:
                nc.scalar.copy(moved[1][:, CUT:CUT2], moved[0][:, CUT:CUT2])

        if moved:
            @block.gpsimd
            def _(pool):
                nc.gpsimd.tensor_copy(moved[1][:, CUT2:], moved[0][:, CUT2:])

        @block.vector
        def _(dve):
            if moved:
                nc.vector.tensor_copy(moved[1][:, 0:CUT], moved[0][:, 0:CUT])
            for t in range(QT):
                dve.wait_ge(ready, t + 1)
                x = core.x[:, bass.ds(QT * b + t, 1), :]
                nc.vector.tensor_tensor(x, ps[:, 2 + t:3 + t, 0:C], x, ALU.add)


def attend_by_key(core, queries, keys, v, qstack, kstack, att, coming=None):
    nc, ps = core.nc, core.ps
    QT = T // P
    EU = KT // 4
    OUT, SPARE = 6, 7
    with ExitStack() as c:
        sb = core.allocator(c)
        p, scaled = sb([P, 4, 4 * T]), sb([P, 4, 4, VW])
        nm, z, zi = sb([P, 4, 4]), sb([P, 4, 4]), sb([P, 4, 4])
        fold, osum, inv = core.fold, sb([P, H, T]), sb([P, QT, H])
        with phase(core, "q_in", "k_a", "k_b", "k_c", "max_done", "qk", "exp_done", "z_done", "v_scaled", "pv",
                   "taken", "out_ready", "inv_done", "cleared", *(NextKeys.NAMES if coming else ())) as (
                block, q_in, k_a, k_b, k_c, max_done, qk, exp_done, z_done, v_scaled, pv, taken, out_ready, inv_done,
                cleared, *next_sems):
            k_in = (k_a, k_b, k_c)
            new = NextKeys(core, sb, next_sems, spare=SPARE, v_bank=SPARE, **coming) if coming else None

            @block.sync
            def _(sp):
                load_keys(sp, keys, kstack, 0, k_in[0])
                load_keys(sp, keys, kstack, 1, k_in[1])
                if new:
                    new.load_chunk(sp, 0)
                    new.load_chunk(sp, 1)
                for h in range(H):
                    if h + 2 < H:
                        if h >= 1:
                            sp.wait_ge(qk, EU * h)
                        load_keys(sp, keys, kstack, h + 2, k_in[(h + 2) % 3])
                    if new:
                        if h % CT == 0 and 2 <= h // CT + 1 < new.chunks:
                            new.load_chunk(sp, h // CT + 1)
                        if h >= 1:
                            new.store(sp, h - 1)
                if new:
                    new.store(sp, H - 1)
                    new.all_stored(sp)

            @block.tensor
            def _(pe):
                def scores(i):
                    h, e = i // EU, i % EU
                    if i == 0:
                        pe.wait_ge(q_in, 16 * SLOTS)
                    if e == 0:
                        pe.wait_ge(k_in[h % 3], 16 * SLOTS * (h // 3 + 1))
                    if i >= 3:
                        pe.wait_ge(exp_done, 4 * (i - 2))
                    for j in range(4):
                        kt = 4 * e + j
                        mm = nc.tensor.matmul(ps[:, 2 * (i % 3) + j // 2, (j % 2) * T:(j % 2 + 1) * T],
                                              kstack[0:SHIFT, h % 3, kt * P:(kt + 1) * P], qstack[0:SHIFT, h, :],
                                              start=True, stop=True)
                    mm.then_inc(qk, 1)

                def weigh(i):
                    h, e = i // EU, i % EU
                    pe.wait_ge(v_scaled, i + 1)
                    if i == 0:
                        pe.wait_ge(cleared, 1)
                    if e == 0 and h >= 1:
                        pe.wait_ge(taken, h)
                    for j in range(4):
                        mm = nc.tensor.matmul(ps[PART * j:PART * j + VW, OUT, 0:T], scaled[:, i % 4, j, :],
                                              p[:, i % 4, j * T:(j + 1) * T], start=e == 0, stop=e == EU - 1,
                                              tile_position=(0, PART * j))
                    mm.then_inc(pv, 1)

                for i in range(H * EU + 3):
                    h, e = i // EU, i % EU
                    if i < H * EU:
                        scores(i)
                    if i >= 3:
                        weigh(i - 3)
                    if new and i < H * EU and e in (0, 1):
                        if e == 0 and h >= 1:
                            pe.wait_ge(new.v_done, h)
                        new.multiply(pe, h, e)
                    if new and i < H * EU and e in (5, 6):
                        new.product_used(pe, h)
                        new.multiply_values(pe, h, e - 5)
                pe.wait_ge(exp_done, 4 * H * EU)
                for h in range(H):
                    pe.wait_ge(taken, h + 1)
                    for t in range(QT):
                        mm = nc.tensor.matmul(ps[:, h // HT, (QT * (h % HT) + t) * VW:(QT * (h % HT) + t + 1) * VW],
                                              osum[:, h, t * P:(t + 1) * P], fold[:, 0:VW], start=True, stop=True,
                                              skip_group_check=True)
                    mm.then_inc(out_ready, 1)

            @block.vector
            def _(dve):
                nc.vector.memset(ps[:, OUT, 0:T], 0.0).then_inc(cleared, 1)

                def maxima(i):
                    dve.wait_ge(qk, i + 1)
                    if i >= 4:
                        dve.wait_ge(exp_done, 4 * (i - 3))
                    nc.vector.tensor_reduce(nm[:, i % 4, :],
                                            ps[:, 2 * (i % 3):2 * (i % 3) + 2, :].rearrange("p b (j t) -> p (b j) t", j=2),
                                            AX.X, ALU.max, negate=True).then_inc(max_done, 1)

                def scale_values(i):
                    h, e = i // EU, i % EU
                    dve.wait_ge(exp_done, 4 * (i + 1))
                    nc.vector.reciprocal(zi[:, i % 4, :], z[:, i % 4, :]).then_inc(z_done, 1)
                    dve.wait_ge(z_done, i + 1)
                    if i >= 4:
                        dve.wait_ge(pv, i - 3)
                    nc.vector.tensor_tensor(scaled[:, i % 4, :, :], v[:, 4 * e:4 * e + 4, h, :],
                                            zi[:, i % 4, :].unsqueeze(2).to_broadcast([P, 4, VW]),
                                            ALU.mult).then_inc(v_scaled, 1)

                for i in range(H * EU + 2):
                    h, e = i // EU, i % EU
                    if i < H * EU:
                        maxima(i)
                    if i >= 2:
                        scale_values(i - 2)
                    if new and i < H * EU and e == 4:
                        new.take_rest(dve, h)
                for g in range(H // HT):
                    dve.wait_ge(out_ready, HT * (g + 1))
                    o = ps[:, g, 0:HT * QT * VW].rearrange("p (h t c) -> p t h c", h=HT, t=QT)
                    i = inv[:, :, g * HT:(g + 1) * HT]
                    nc.vector.reciprocal(i, o[:, :, :, D]).then_inc(inv_done, 1)
                    dve.wait_ge(inv_done, g + 1)
                    for t in range(QT):
                        nc.vector.tensor_tensor(
                            att[:, t, g * P:(g + 1) * P].rearrange("p (h c) -> p h c", h=HT), o[:, t, :, 0:D],
                            inv[:, t, g * HT:(g + 1) * HT].unsqueeze(2).to_broadcast([P, HT, D]), ALU.mult)

            @block.scalar
            def _(act):
                load_queries(act, queries, qstack, q_in)

                def take(h):
                    act.wait_ge(pv, EU * (h + 1))
                    nc.scalar.copy(osum[:, h, :], ps[:, OUT, 0:T]).then_inc(taken, 1)

                for i in range(H * EU):
                    h, e = i // EU, i % EU
                    act.wait_ge(max_done, i + 1)
                    if i >= 4:
                        act.wait_ge(pv, i - 3)
                        act.wait_ge(z_done, i - 3)
                    for j in range(4):
                        nc.scalar.activation(p[:, i % 4, j * T:(j + 1) * T],
                                             ps[:, 2 * (i % 3) + j // 2, (j % 2) * T:(j % 2 + 1) * T], ACT.Exp,
                                             bias=nm[:, i % 4, j:j + 1],
                                             accum_out=z[:, i % 4, j:j + 1]).then_inc(exp_done, 1)
                    if e == 2 and h >= 1:
                        take(h - 1)
                    if new and e == 1:
                        new.high(act, h)
                    if new and e == 6:
                        new.copy_values(act, h)
                take(H - 1)

            if new:
                @block.gpsimd
                def _(pool):
                    for u in range(new.units):
                        new.low_parts(pool, u)


def context_attention(core, prefix, by_key=False, scale=1.0, rope=False, bias=False):
    nc, d = core.nc, core.dram
    queries, keys = d["scratch_q"], d["scratch_k"]
    with ExitStack() as c:
        sb = core.allocator(c)
        tiles = None
        if bias:
            tiles = sb([P, 3, H, P]), sb([P, 3, H, P], BF16)
            distance_bias(core, prefix, *tiles)
        wk, wv, wo = (sb([P, CT, C]) for _ in range(3))
        v, v_next, kstack = sb([P, KT, H, VW]), sb([P, KT, H, VW]), sb([P, 3, S], BF16)
        loads = [(t[:, :, :], ktiles(d[prefix + "_W" + n])) for t, n in ((wk, "k"), (wv, "v"), (wo, "o"))]
        q_rope = k_rope = None
        if rope:
            qw, kw, turn, eps = sb([P, 1]), sb([P, 1]), sb([P, P]), sb([P, 1])
            loads += [(qw[:, :], d[prefix + "_q_norm_w"]), (kw[:, :], d[prefix + "_k_norm_w"]),
                      (turn[:, :], d["c_turn16"])]
            q_rope = (qw[:, 0:1], lambda i: d["c_rope_q"], turn[:, :], eps[:, 0:1])
            k_rope = (kw[:, 0:1], lambda i: d["c_rope_k"][:, :, i * KC:(i + 1) * KC], turn[:, :], eps[:, 0:1])
        context = lambda b: (lambda i: d["ctxT"][b, :, i * KC:(i + 1) * KC].rearrange("(k p) n -> p k n", p=P))
        with ExitStack() as early:
            wq = core.allocator(early)([P, CT, C])
            layer_norm(core, core.x, core.xn, core.xnT, loads=loads + [(wq[:, :, :], ktiles(d[prefix + "_Wq"]))],
                       constants=[(kstack[SHIFT:ROWS, :, :], 1.0), (v[:, :, :, D:VW], 1.0), (v_next[:, :, :, D:VW], 1.0)]
                       + ([(eps[:, :], 1e-6)] if rope else []))
            project_first(core, wq, queries, q_rope, scale, wk, wv, context(0), keys[0], v, k_rope)
        qstack, att, attT = sb([P, H, T], BF16), sb([P, T // P, C]), sb([P, CT, T])
        k97, q97 = kstack[0:ROWS], qstack[0:ROWS]

        def attend_batch(b, coming):
            mine = queries[:, :, bass.ds(b * T, T)]
            if by_key:
                attend_by_key(core, mine, keys[b], v, q97, k97, att, coming)
            else:
                attend_context(core, mine, keys[b], v, q97, k97, tiles, att, coming)
            output_product(core, att, attT, wo, b, (v_next, v) if coming else None)

        with nc.Fori(0, B - 1) as b:
            attend_batch(b, dict(w=wk, w_v=wv, v=v_next, source=context(b + 1), dest=keys[b + 1], rope=k_rope))
        attend_batch(B - 1, None)


def distance_bias(core, prefix, by_key, by_query):
    nc, d, ps = core.nc, core.dram, core.ps
    W = 4 * P
    HB = BANK // P
    with ExitStack() as c:
        sb = core.allocator(c)
        table, onehot, rows, mirror = sb([32, H]), sb([32, W]), sb([H, W]), sb([P, P])
        slanted = sb([P, 3, H, P])
        scratch = d["scratch_bias"]
        load(core, [(table[:, :], d[prefix + "_rel_bias"]), (onehot[:, :], d["c_buckets"]),
                    (mirror[:, :], d["c_mirror"])])
        banks = [(i, g) for i in range(3) for g in range(H // HB)]
        with phase(core, "ready", "copied", "stored", "read", "query_ready", "key_ready", "query_copied",
                   "key_copied") as (block, ready, copied, stored, read, query_ready, key_ready, query_copied,
                                     key_copied):
            @block.tensor
            def _(pe):
                nc.tensor.matmul(ps[0:H, 0, :], table[:, :], onehot[:, :], start=True, stop=True).then_inc(ready, 1)
                pe.wait_ge(copied, 1)
                pe.wait_ge(read, 48)
                for n, (i, g) in enumerate(banks):
                    if n >= 4:
                        pe.wait_ge(query_copied, n - 3)
                        pe.wait_ge(key_copied, n - 3)
                    nc.tensor.matmul(ps[:, n % 4, :], mirror[:, :], slanted[:, i, g * HB:(g + 1) * HB, :],
                                     start=True, stop=True).then_inc(query_ready, 1)
                    for h in range(HB):
                        mm = nc.tensor.matmul(ps[:, 4 + n % 4, h * P:(h + 1) * P], slanted[:, i, g * HB + h, :],
                                              mirror[:, :], start=True, stop=True)
                    mm.then_inc(key_ready, 1)

            @block.scalar
            def _(act):
                act.wait_ge(ready, 1)
                nc.scalar.copy(rows[:, :], ps[0:H, 0, :]).then_inc(copied, 1)
                for n, (i, g) in enumerate(banks):
                    act.wait_ge(key_ready, n + 1)
                    nc.scalar.copy(by_key[:, i, g * HB:(g + 1) * HB, :], ps[:, 4 + n % 4, :]).then_inc(key_copied, 1)

            @block.sync
            def _(sp):
                sp.wait_ge(copied, 1)
                sp.dma_start(scratch, rows[:, :]).then_inc(stored, 16)
                sp.wait_ge(stored, 16)
                for i in range(3):
                    start = 2 * P + P * (i - 1) - (P - 1)
                    sp.dma_start(slanted[:, i, :, :], bass.AP(tensor=scratch.tensor, offset=start,
                                                              ap=[[1, P], [W, H], [1, P]])).then_inc(read, 16)
                sp.wait_ge(read, 48)

            @block.vector
            def _(dve):
                for n, (i, g) in enumerate(banks):
                    dve.wait_ge(query_ready, n + 1)
                    nc.vector.tensor_copy(by_query[:, i, g * HB:(g + 1) * HB, :],
                                          ps[:, n % 4, :]).then_inc(query_copied, 1)


def l0_xattn(core):
    context_attention(core, "L0_xattn", scale=D ** -0.5, rope=True)


def l1_xattn(core):
    context_attention(core, "L1_xattn", bias=True)


def l2_xattn(core):
    context_attention(core, "L2_xattn", by_key=True, scale=C ** -0.5)

def lay_out(i):
    import numpy as np
    cont = np.ascontiguousarray
    T_ = lambda a: cont(np.swapaxes(a, -1, -2))
    col = lambda a: cont(a.reshape(-1, P).T)
    spread = lambda a: cont(np.broadcast_to(a.reshape(1, -1), (P, a.size)))
    again = lambda a: np.concatenate([a, a[:1]], 0)
    o = {"x": i["x"], "ctxT": T_(i["ctx_1024"])}
    o["L3_ffn_W1"], o["L3_ffn_W2"] = T_(i["L3_ffn_W1"]), T_(i["L3_ffn_W2"])
    o["L3_ffn_b1"], o["L3_ffn_b2"] = col(i["L3_ffn_b1"]), spread(i["L3_ffn_b2"])
    o["L3_ffn_scale"] = cont(np.broadcast_to(i["L3_ffn_scale"].reshape(1, 1), (P, 1)))
    for n in ("W_u", "W_g", "Bm", "Cm"):
        o["L3_attn_" + n] = T_(i["L3_attn_" + n])
    o["L3_attn_A"], o["L3_attn_AT"] = i["L3_attn_A"], T_(i["L3_attn_A"])
    o["L3_attn_b_u"], o["L3_attn_b_g"] = col(i["L3_attn_b_u"]), col(i["L3_attn_b_g"])
    o["L3_attn_D"] = spread(i["L3_attn_D"])
    o["L3_xattn_Wq"], o["L3_xattn_Wp"] = T_(i["L3_xattn_Wq"]), T_(i["L3_xattn_Wp"])
    o["L3_xattn_Wkv"] = T_(np.concatenate([i["L3_xattn_Wk"], i["L3_xattn_Wv"]], 0))
    o["L3_xattn_bq"], o["L3_xattn_bp"] = spread(i["L3_xattn_bq"]), spread(i["L3_xattn_bp"])
    o["L3_xattn_bkv"] = spread(np.concatenate([i["L3_xattn_bk"], i["L3_xattn_bv"]]))
    o["L0_attn_maa"] = cont(np.stack([col(i["L0_attn_time_maa_" + n]) for n in "xwkvrg"], 1))
    o["L0_attn_w1"] = i["L0_attn_time_maa_w1"]
    o["L0_attn_w2"] = i["L0_attn_time_maa_w2"].reshape(-1, C)
    o["L0_attn_wd1"], o["L0_attn_wd2"] = i["L0_attn_time_decay_w1"], i["L0_attn_time_decay_w2"]
    o["L0_attn_decay"], o["L0_attn_u"] = col(i["L0_attn_time_decay"]), col(i["L0_attn_time_faaaa"])
    o["L0_attn_gamma"], o["L0_attn_beta"] = col(i["L0_attn_ln_gamma"]), col(i["L0_attn_ln_beta"])
    for n in "rkvgo":
        o["L0_attn_W_" + n] = i["L0_attn_W_" + n]
    o["L0_ffn_gate_w"] = T_(i["L0_ffn_gate_w"])

    def paired(w):
        w = w.reshape(32, 2, 192, -1)
        return np.concatenate([w[:, :, 0:P].reshape(32, 2 * P, -1), w[:, :, P:].reshape(32, P, -1)], 1)

    gu = np.stack([paired(i["L0_ffn_w_gate"]), paired(i["L0_ffn_w_up"])], 1)
    o["L0_ffn_wgu"] = again(gu.reshape(32, 2, 3 * P, CT, P).transpose(0, 4, 3, 1, 2))
    o["L0_ffn_wd"] = again(paired(T_(i["L0_ffn_w_down"])).reshape(32, 3, P, C).transpose(0, 2, 1, 3))
    for n in ("r1_w", "r2_w", "b2"):
        o["L1_attn_" + n] = i["L1_attn_" + n]
    o["L1_attn_W1"], o["L1_attn_W2"] = again(i["L1_attn_W1"]), again(i["L1_attn_W2"])
    o["L1_attn_r1_b"] = spread(i["L1_attn_r1_b"])
    o["L1_attn_ln_g"], o["L1_attn_ln_b"] = col(i["L1_attn_ln_g"]), col(i["L1_attn_ln_b"])
    for n in ("r2_b", "route_bias", "temp"):
        a = i["L1_attn_" + n].reshape(1, -1)
        o["L1_attn_" + n] = cont(np.broadcast_to(a, (P, a.shape[1])))
    expert_col = lambda a: cont(a.reshape(a.shape[0], -1, P).transpose(2, 0, 1))
    o["L1_attn_b1"] = expert_col(i["L1_attn_b1"])
    o["L1_ffn_Wg"], o["L1_ffn_b2"] = T_(i["L1_ffn_Wg"]), i["L1_ffn_b2"]
    o["L1_ffn_b1"], o["L1_ffn_b3"] = expert_col(i["L1_ffn_b1"]), expert_col(i["L1_ffn_b3"])
    w13 = np.stack([i["L1_ffn_W1"], i["L1_ffn_W3"]], 1)
    o["L1_ffn_W13"] = again(w13.reshape(16, 2, 256, CT, P).transpose(0, 4, 3, 1, 2))
    o["L1_ffn_W2"] = again(T_(i["L1_ffn_W2"]))
    o["L2_attn_W_in"], o["L2_attn_W_out"] = T_(i["L2_attn_W_in"]), T_(i["L2_attn_W_out"])
    o["L2_attn_b_qk"], o["L2_attn_b_v"] = col(i["L2_attn_b_in"][:2048]), spread(i["L2_attn_b_in"][2048:])
    o["L2_attn_b_out"] = spread(i["L2_attn_b_out"])
    for n in ("wq", "wk", "wv", "wo"):
        o["L2_ffn_" + n] = i["L2_ffn_" + n]
    o["L2_ffn_w1"], o["L2_ffn_w2"] = again(i["L2_ffn_w1"]), again(i["L2_ffn_w2"])
    o["L2_ffn_ln_g"], o["L2_ffn_ln_b"] = col(i["L2_ffn_ln_g"]), col(i["L2_ffn_ln_b"])
    o["L2_ffn_b1"] = expert_col(i["L2_ffn_b1"])
    o["L2_ffn_b2"] = cont(np.broadcast_to(i["L2_ffn_b2"].reshape(4, 2, 1, C), (4, 2, 64, C)).reshape(4, P, C).transpose(1, 0, 2))
    for n in "qkvo":
        o["L0_xattn_W" + n], o["L2_xattn_W" + n] = T_(i["L0_xattn_W" + n]), T_(i["L2_xattn_W" + n])
    for n in "qk":
        o[f"L0_xattn_{n}_norm_w"] = cont(np.tile(i[f"L0_xattn_{n}_norm_w"].reshape(D, 1), (HT, 1)))
    o["L1_xattn_Wq"], o["L1_xattn_Wo"] = i["L1_xattn_Wq"], i["L1_xattn_Wo"]
    o["L1_xattn_Wk"], o["L1_xattn_Wv"] = cont(i["L1_xattn_Wkv"][:, 0:C]), cont(i["L1_xattn_Wkv"][:, C:])
    o["L1_xattn_rel_bias"] = i["L1_xattn_rel_bias"]
    o["c_ident"] = np.eye(P, dtype=np.float32)
    o["c_block16"] = np.kron(np.eye(HT), np.ones((D, D))).astype(np.float32)
    o["c_fold"] = np.tile(np.eye(32), (4, 1)).astype(np.float32)
    o["c_eye4"] = np.eye(4, dtype=np.float32)
    o["c_block4"] = np.kron(np.eye(4), np.ones((4, 1))).astype(np.float32)
    o["c_sel"] = np.stack([np.kron(np.eye(HT), np.eye(D)[:, [n]] * np.ones((1, D))) for n in range(D)],
                          1).astype(np.float32)
    o["c_mask8"] = np.kron(np.eye(16), np.ones((8, 1))).astype(np.float32)
    p64 = np.arange(32, dtype=np.float32) / np.float32(31)
    ang = np.arange(T, dtype=np.float32)[None, :] / (np.float32(10000.0) ** p64)[:, None]
    o["c_cos64"], o["c_sin64"] = (np.tile(f(ang), (4, 1)).astype(np.float32) for f in (np.cos, np.sin))
    t64 = np.zeros((64, 64), np.float32)
    t64[np.arange(32), np.arange(32) + 32] = 1.0
    t64[np.arange(32) + 32, np.arange(32)] = -1.0
    o["c_turn64"] = np.kron(np.eye(2), t64).astype(np.float32)
    o["c_causal"] = np.where(np.arange(P)[:, None] >= np.arange(P)[None, :], 0.0, -1e30).astype(np.float32)
    half = np.arange(D // 2) * 2
    for n, theta, length in (("q", 32.0, T), ("k", 1000.0, S)):
        freqs = np.float32(theta) ** (-half.astype(np.float32) / np.float32(D))
        ang = freqs[:, None] * np.arange(length, dtype=np.float32)[None, :]
        table = np.stack([np.tile(f(ang), (2 * HT, 1)) for f in (np.cos, np.sin)], 1).astype(np.float32)
        o["c_rope_" + n] = np.tile(table, (1, 1, 2)) if n == "q" else table
    t16 = np.zeros((D, D), np.float32)
    t16[np.arange(8) + 8, np.arange(8)] = -1.0
    t16[np.arange(8), np.arange(8) + 8] = 1.0
    o["c_turn16"] = np.kron(np.eye(HT), t16).astype(np.float32)
    rel = np.arange(-256, 256)
    far = np.abs(rel)
    large = 8 + (np.log(np.maximum(far, 1).astype(np.float32) / 8) / np.log(16) * 8).astype(np.int32)
    bucket = (rel > 0) * 16 + np.where(far < 8, far, np.minimum(large, 15))
    hot = np.eye(32)[bucket].T - np.eye(32)[:, [31]]
    o["c_buckets"] = hot.astype(np.float32)
    o["c_mirror"] = np.ascontiguousarray(np.eye(P, dtype=np.float32)[:, ::-1])
    return {k: np.ascontiguousarray(v) for k, v in o.items()}


STAGES = [l0_xattn, l0_attn, l0_ffn, l1_xattn, l1_attn, l1_ffn, l2_xattn, l2_attn, l2_ffn, l3_xattn, l3_attn, l3_ffn]


def perceiver(nc, dram, out, stages=STAGES):
    with ExitStack() as ctx:
        core = Core(nc, ctx, dram)
        setup(core)
        for stage in stages:
            stage(core)
        store(core, out)


def declare(nc, arrays):
    dram = {k: nc.dram_tensor("in_" + k, v.shape, mybir.dt.from_np(v.dtype), kind="ExternalInput").ap()
            for k, v in arrays.items()}
    dram["scratch_tok"] = nc.dram_tensor("scratch_tok", (B, T, C), F32, kind="Internal").ap()
    dram["scratch_bias"] = nc.dram_tensor("scratch_bias", (H, 4 * P), F32, kind="Internal").ap()
    dram["scratch_q"] = nc.dram_tensor("scratch_q", (3, C, N), BF16, kind="Internal").ap()
    dram["scratch_k"] = nc.dram_tensor("scratch_k", (B, 3, C, S), BF16, kind="Internal").ap()
    dram["scratch_w"] = nc.dram_tensor("scratch_w", (66, N), F32, kind="Internal").ap()
    out = nc.dram_tensor("out", (B, T, C), F32, kind="ExternalOutput").ap()
    return dram, out


def kernel(**inputs):
    import numpy as np
    from concourse import bacc
    from concourse.bass_utils import run_bass_kernel_spmd

    nc = bacc.Bacc("TRN2", target_bir_lowering=False, num_devices=1)
    arrays = lay_out({k: np.asarray(v) for k, v in inputs.items()})
    dram, out = declare(nc, arrays)
    perceiver(nc, dram, out)
    r = run_bass_kernel_spmd(nc, [{"in_" + k: v for k, v in arrays.items()}], core_ids=[0])
    return r.results[0]["out"]
```
